# Optimizing a Trainium2 kernel written in Bass

```python
import numpy as np
import jax
import jax.numpy as jnp

def _softmax(x, axis=-1):
    return jax.nn.softmax(x, axis=axis)

def _gelu(x):
    return jax.nn.gelu(x, approximate=True)

def _silu(x):
    return jax.nn.silu(x)

def _sigmoid(x):
    return jax.nn.sigmoid(x)

def _layernorm(x, axis=-1, eps=1e-05):
    m = jnp.mean(x, axis=axis, keepdims=True)
    v = jnp.var(x, axis=axis, keepdims=True)
    return (x - m) / jnp.sqrt(v + eps)

def _scatter_add(tgt, idx, src, axis=0):
    return tgt.at[idx].add(src)

def _segment_sum(src, seg, n):
    return jax.ops.segment_sum(src, seg, n)
kernel_name = 'mk_flamingo_gated_d4_seqx_r8_579d6e'

def setup_inputs(seed: int=0):
    np.random.seed(seed)
    _w = jnp.asarray

    def _rec_inputs():
        import jax
        import jax.numpy as jnp
        _rk = jax.random.key(seed)
        x = 7.22e-05 + 1 * jax.random.normal(jax.random.fold_in(_rk, 1), (4, 256, 128), jnp.float32)
        _lenS = 256 - jax.random.randint(jax.random.fold_in(_rk, 7), (4,), 0, max(1, 256 // 4) + 1, jnp.int32)
        _lenS2 = 64 - jax.random.randint(jax.random.fold_in(_rk, 8), (4,), 0, max(1, 64 // 4) + 1, jnp.int32)
        _ctx_1024P = jax.random.normal(jax.random.fold_in(_rk, 11), (4, 16, 128), jnp.float32)
        _ctx_1024c = jax.random.dirichlet(jax.random.fold_in(_rk, 511), 0.3 * jnp.ones((16,), jnp.float32), (4, 64))
        _ctx_1024t = jnp.einsum('bsk,bkd->bsd', _ctx_1024c, _ctx_1024P)
        _ctx_1024t = _ctx_1024t * jax.lax.rsqrt(jnp.mean(jnp.square(_ctx_1024t)) + 1e-12) * 0.953939
        ctx_1024 = 4.13588e-05 + 0.999923 * (_ctx_1024t + 0.3 * jax.random.normal(jax.random.fold_in(_rk, 611), (4, 64, 128), jnp.float32))
        _validS = jnp.arange(256)[None, :] < _lenS[:, None]
        _validS2 = jnp.arange(64)[None, :] < _lenS2[:, None]
        _causal = jnp.tril(jnp.ones((256, 256), dtype=bool))
        mask_Bx1x1xS2_ff0 = jnp.where(jnp.ones((4, 1, 1, 64), dtype=bool), 0.0, -1000000000.0).astype(jnp.float32)
        mask_SxS_bc0 = jnp.logical_not(jnp.broadcast_to(_causal[:, :], (256, 256)))
        _g = jax.random.normal(jax.random.fold_in(_rk, 9001), (2, 4), jnp.float32)
        _g = jnp.sign(_g) * jnp.maximum(jnp.abs(_g), 1.0) + (_g == 0) * 1.0
        g_xattn = _g[0]
        g_ffn = _g[1]
        return (x, ctx_1024, mask_Bx1x1xS2_ff0, mask_SxS_bc0, g_xattn, g_ffn)
    x, ctx_1024, mask_Bx1x1xS2_ff0, mask_SxS_bc0, g_xattn, g_ffn = _rec_inputs()

    def _L0_xattn_setup():
        import jax, jax.numpy as jnp
        import numpy as np
        B, N, M = (4, 256, 256)
        D_IN = 128
        H, HS = (16, 64)
        D_OUT = 128

        def _xavier(key, shape):
            fan_in, fan_out = (shape[-2], shape[-1])
            limit = float(np.sqrt(6.0 / (fan_in + fan_out)))
            return jax.random.uniform(key, shape, jnp.float32, -limit, limit)
        key = jax.random.key(seed)
        ks = jax.random.split(key, 7)
        return {'query': jax.random.normal(ks[0], (B, N, D_IN), jnp.float32), 'key': jax.random.normal(ks[1], (B, M, D_IN), jnp.float32), 'value': jax.random.normal(ks[2], (B, M, D_IN), jnp.float32), 'query_kernel': _xavier(ks[3], (H, D_IN, HS)), 'key_kernel': _xavier(ks[4], (H, D_IN, HS)), 'value_kernel': _xavier(ks[5], (H, D_IN, HS)), 'projection_kernel': _xavier(ks[6], (H, HS, D_OUT)), 'projection_bias': jnp.zeros((D_OUT,), jnp.float32)}
    _L0_xattn_all = _L0_xattn_setup()
    _L0_xattn_in = {k: v for k, v in _L0_xattn_all.items() if k in ('query_kernel', 'key_kernel', 'value_kernel', 'projection_kernel', 'projection_bias')}
    del _L0_xattn_all

    def _L0_ffn_setup():
        import jax, jax.numpy as jnp
        import numpy as np
        LORA_DIM = 16
        LORA_TOKEN_INDEX = 1
        B, S, D, H = (4, 256, 128, 512)
        key = jax.random.key(seed)
        ks = jax.random.split(key, 6)
        x = jax.random.normal(ks[0], (B, S, D), dtype=jnp.float32)
        W1 = jax.random.normal(ks[1], (H, D), dtype=jnp.float32) * 0.02
        b1 = jnp.zeros((H,), dtype=jnp.float32)
        W2 = jax.random.normal(ks[2], (D, H), dtype=jnp.float32) * 0.02
        b2 = jnp.zeros((D,), dtype=jnp.float32)
        scale = jnp.asarray(0.001, dtype=jnp.float32)
        return {'x': x, 'W1': W1, 'b1': b1, 'W2': W2, 'b2': b2, 'scale': scale}
    _L0_ffn_all = _L0_ffn_setup()
    _L0_ffn_in = {k: v for k, v in _L0_ffn_all.items() if k in ('W1', 'b1', 'W2', 'b2', 'scale')}
    del _L0_ffn_all

    def _L1_xattn_setup():
        import jax, jax.numpy as jnp
        import numpy as np
        NUM_HEADS = 16
        D_K = 64
        D_V = 64
        D_MODEL = 128
        key = jax.random.key(seed)
        ks = jax.random.split(key, 11)
        B, S = (2, 256)
        s = 0.02
        return {'Q': jax.random.normal(ks[0], (B, S, D_MODEL), jnp.float32), 'K': jax.random.normal(ks[1], (B, S, D_MODEL), jnp.float32), 'V': jax.random.normal(ks[2], (B, S, D_MODEL), jnp.float32), 'WQ': jax.random.normal(ks[3], (D_MODEL, NUM_HEADS * D_K), jnp.float32) * s, 'bQ': jnp.zeros((NUM_HEADS * D_K,), jnp.float32), 'WK': jax.random.normal(ks[4], (D_MODEL, NUM_HEADS * D_K), jnp.float32) * s, 'bK': jnp.zeros((NUM_HEADS * D_K,), jnp.float32), 'WV': jax.random.normal(ks[5], (D_MODEL, NUM_HEADS * D_V), jnp.float32) * s, 'bV': jnp.zeros((NUM_HEADS * D_V,), jnp.float32), 'WO': jax.random.normal(ks[6], (NUM_HEADS * D_V, D_MODEL), jnp.float32) * s, 'bO': jnp.zeros((D_MODEL,), jnp.float32)}
    _L1_xattn_all = _L1_xattn_setup()
    _L1_xattn_in = {k: v for k, v in _L1_xattn_all.items() if k in ('WQ', 'bQ', 'WK', 'bK', 'WV', 'bV', 'WO', 'bO')}
    del _L1_xattn_all

    def _L1_ffn_setup():
        import jax, jax.numpy as jnp
        import numpy as np
        D_MODEL = 128
        D_HIDDEN = 512
        NUM_EXPERT = 8
        TOP_K = 2
        B, N = (1, 1024)

        def _expert_mlp(x, W1, b1, W2, b2, W3, b3):
            h = jax.nn.gelu(jnp.einsum('bnd,dh->bnh', x, W1) + b1, approximate=False)
            h = jax.nn.gelu(jnp.einsum('bnh,hk->bnk', h, W2) + b2, approximate=False)
            return jnp.einsum('bnh,hd->bnd', h, W3) + b3
        key = jax.random.key(seed)
        ks = jax.random.split(key, 8)
        s1 = 1.0 / np.sqrt(D_MODEL)
        s2 = 1.0 / np.sqrt(D_HIDDEN)
        return {'x': jax.random.normal(ks[0], (B, N, D_MODEL), jnp.float32), 'expert_tokens': jax.random.normal(ks[1], (NUM_EXPERT, D_MODEL), jnp.float32), 'W1': jax.random.normal(ks[2], (NUM_EXPERT, D_MODEL, D_HIDDEN), jnp.float32) * s1, 'b1': jnp.zeros((NUM_EXPERT, D_HIDDEN), jnp.float32), 'W2': jax.random.normal(ks[3], (NUM_EXPERT, D_HIDDEN, D_HIDDEN), jnp.float32) * s2, 'b2': jnp.zeros((NUM_EXPERT, D_HIDDEN), jnp.float32), 'W3': jax.random.normal(ks[4], (NUM_EXPERT, D_HIDDEN, D_MODEL), jnp.float32) * s2, 'b3': jnp.zeros((NUM_EXPERT, D_MODEL), jnp.float32)}
    _L1_ffn_all = _L1_ffn_setup()
    _L1_ffn_in = {k: v for k, v in _L1_ffn_all.items() if k in ('expert_tokens', 'W1', 'b1', 'W2', 'b2', 'W3', 'b3')}
    del _L1_ffn_all

    def _L2_xattn_setup():
        import jax, jax.numpy as jnp
        import numpy as np
        B, T, D, H = (2, 256, 128, 16)
        DH = D // H

        def _heads(x):
            b, t, _ = x.shape
            return x.reshape(b, t, H, DH).transpose(0, 2, 1, 3)
        key = jax.random.key(seed)
        ks = jax.random.split(key, 8)
        s = 0.02
        return {'query_states': jax.random.normal(ks[0], (B, T, D), jnp.float32), 'key_states': jax.random.normal(ks[1], (B, T, D), jnp.float32), 'attention_mask': jnp.zeros((B, 1, 1, T), jnp.float32), 'Wq': jax.random.normal(ks[2], (D, D), jnp.float32) * s, 'bq': jnp.zeros((D,), jnp.float32), 'Wk': jax.random.normal(ks[3], (D, D), jnp.float32) * s, 'bk': jnp.zeros((D,), jnp.float32), 'Wv': jax.random.normal(ks[4], (D, D), jnp.float32) * s, 'bv': jnp.zeros((D,), jnp.float32), 'mask_future': 0}
    _L2_xattn_all = _L2_xattn_setup()
    _L2_xattn_in = {k: v for k, v in _L2_xattn_all.items() if k in ('Wq', 'bq', 'Wk', 'bk', 'Wv', 'bv')}
    del _L2_xattn_all

    def _L2_ffn_setup():
        import jax, jax.numpy as jnp
        import numpy as np
        TOP_K = 2
        key = jax.random.key(seed)
        k1, k2, k3, k4 = jax.random.split(key, 4)
        B, S, H, I, E = (2, 256, 128, 512, 8)
        return {'hidden_states': jax.random.normal(k1, (B, S, H), jnp.float32), 'gate_w': jax.random.normal(k2, (E, H), jnp.float32) * 0.02, 'gate_up_proj': jax.random.normal(k3, (E, 2 * I, H), jnp.float32) * 0.02, 'down_proj': jax.random.normal(k4, (E, H, I), jnp.float32) * 0.02}
    _L2_ffn_all = _L2_ffn_setup()
    _L2_ffn_in = {k: v for k, v in _L2_ffn_all.items() if k in ('gate_w', 'gate_up_proj', 'down_proj')}
    del _L2_ffn_all

    def _L3_xattn_setup():
        import jax, jax.numpy as jnp
        import numpy as np
        from jax import lax
        H = 16
        K1, K2 = (3, 3)
        LN_EPS = 1e-05

        def _ln(x, g, b):
            m = jnp.mean(x, axis=-1, keepdims=True)
            v = jnp.mean(jnp.square(x - m), axis=-1, keepdims=True)
            return (x - m) * lax.rsqrt(v + LN_EPS) * g + b

        def _gelu(x):
            return jax.nn.gelu(x, approximate=False)
        key = jax.random.key(seed)
        B, T, D, Th = (4, 128, 128, 32)
        C = 2 * D
        ks = jax.random.split(key, 16)

        def w(k, shape):
            fan_in = shape[0]
            return (jax.random.normal(k, shape, jnp.float32) / np.sqrt(fan_in)).astype(jnp.float32)
        inp = {'x': jax.random.normal(ks[0], (B, T, D), jnp.float32), 'historical_data': jax.random.normal(ks[1], (B, Th, D), jnp.float32), 'Wq': w(ks[2], (D, D)), 'Wk': w(ks[3], (D, D)), 'Wv': w(ks[4], (D, D)), 'hist_W': w(ks[5], (D, C)), 'hist_b': jnp.zeros((C,), jnp.float32), 'hist_ln_g': jnp.ones((C,), jnp.float32), 'hist_ln_b': jnp.zeros((C,), jnp.float32), 'ctx_W1': w(ks[6], (C, C // 4)), 'ctx_b1': jnp.zeros((C // 4,), jnp.float32), 'ctx_W2': w(ks[7], (C // 4, 1)), 'ctx_b2': jnp.zeros((1,), jnp.float32), 'kg_W1': w(ks[8], (C, D)), 'kg_b1': jnp.zeros((D,), jnp.float32), 'kg_ln_g': jnp.ones((D,), jnp.float32), 'kg_ln_b': jnp.zeros((D,), jnp.float32), 'kg_W2': w(ks[9], (D, H * K1 * K2)), 'kg_b2': jnp.zeros((H * K1 * K2,), jnp.float32), 'proj_W': w(ks[10], (D, D)), 'proj_b': jnp.zeros((D,), jnp.float32), 'causal_mask': jnp.triu(jnp.ones((T, T), bool), k=1)}
        return inp
    _L3_xattn_all = _L3_xattn_setup()
    _L3_xattn_in = {k: v for k, v in _L3_xattn_all.items() if k in ('Wq', 'Wk', 'Wv', 'hist_W', 'hist_b', 'hist_ln_g', 'hist_ln_b', 'ctx_W1', 'ctx_b1', 'ctx_W2', 'ctx_b2', 'kg_W1', 'kg_b1', 'kg_ln_g', 'kg_ln_b', 'kg_W2', 'kg_b2', 'proj_W', 'proj_b')}
    del _L3_xattn_all

    def _L3_ffn_setup():
        import jax, jax.numpy as jnp
        import numpy as np
        TOP_K = 2
        NUM_EXPERTS = 8
        HIDDEN = 128
        INTER = 256
        key = jax.random.key(seed)
        ks = jax.random.split(key, 5)
        s_h = 1.0 / np.sqrt(HIDDEN)
        s_i = 1.0 / np.sqrt(INTER)
        return {'hidden_states': jax.random.normal(ks[0], (4, 512, HIDDEN), dtype=jnp.float32), 'router_w': jax.random.uniform(ks[1], (NUM_EXPERTS, HIDDEN), minval=-s_h, maxval=s_h, dtype=jnp.float32), 'gate_w': jax.random.uniform(ks[2], (NUM_EXPERTS, HIDDEN, INTER), minval=-s_h, maxval=s_h, dtype=jnp.float32), 'up_w': jax.random.uniform(ks[3], (NUM_EXPERTS, HIDDEN, INTER), minval=-s_h, maxval=s_h, dtype=jnp.float32), 'down_w': jax.random.uniform(ks[4], (NUM_EXPERTS, INTER, HIDDEN), minval=-s_i, maxval=s_i, dtype=jnp.float32)}
    _L3_ffn_all = _L3_ffn_setup()
    _L3_ffn_in = {k: v for k, v in _L3_ffn_all.items() if k in ('router_w', 'gate_w', 'up_w', 'down_w')}
    del _L3_ffn_all
    return {'x': x, 'ctx_1024': ctx_1024, 'mask_Bx1x1xS2_ff0': mask_Bx1x1xS2_ff0, 'mask_SxS_bc0': mask_SxS_bc0, 'g_xattn': g_xattn, 'g_ffn': g_ffn, 'L0_xattn_query_kernel': _L0_xattn_in['query_kernel'], 'L0_xattn_key_kernel': _L0_xattn_in['key_kernel'], 'L0_xattn_value_kernel': _L0_xattn_in['value_kernel'], 'L0_xattn_projection_kernel': _L0_xattn_in['projection_kernel'], 'L0_xattn_projection_bias': _L0_xattn_in['projection_bias'], 'L0_ffn_W1': _L0_ffn_in['W1'], 'L0_ffn_b1': _L0_ffn_in['b1'], 'L0_ffn_W2': _L0_ffn_in['W2'], 'L0_ffn_b2': _L0_ffn_in['b2'], 'L0_ffn_scale': _L0_ffn_in['scale'], 'L1_xattn_WQ': _L1_xattn_in['WQ'], 'L1_xattn_bQ': _L1_xattn_in['bQ'], 'L1_xattn_WK': _L1_xattn_in['WK'], 'L1_xattn_bK': _L1_xattn_in['bK'], 'L1_xattn_WV': _L1_xattn_in['WV'], 'L1_xattn_bV': _L1_xattn_in['bV'], 'L1_xattn_WO': _L1_xattn_in['WO'], 'L1_xattn_bO': _L1_xattn_in['bO'], 'L1_ffn_expert_tokens': _L1_ffn_in['expert_tokens'], 'L1_ffn_W1': _L1_ffn_in['W1'], 'L1_ffn_b1': _L1_ffn_in['b1'], 'L1_ffn_W2': _L1_ffn_in['W2'], 'L1_ffn_b2': _L1_ffn_in['b2'], 'L1_ffn_W3': _L1_ffn_in['W3'], 'L1_ffn_b3': _L1_ffn_in['b3'], 'L2_xattn_Wq': _L2_xattn_in['Wq'], 'L2_xattn_bq': _L2_xattn_in['bq'], 'L2_xattn_Wk': _L2_xattn_in['Wk'], 'L2_xattn_bk': _L2_xattn_in['bk'], 'L2_xattn_Wv': _L2_xattn_in['Wv'], 'L2_xattn_bv': _L2_xattn_in['bv'], 'L2_ffn_gate_w': _L2_ffn_in['gate_w'], 'L2_ffn_gate_up_proj': _L2_ffn_in['gate_up_proj'], 'L2_ffn_down_proj': _L2_ffn_in['down_proj'], 'L3_xattn_Wq': _L3_xattn_in['Wq'], 'L3_xattn_Wk': _L3_xattn_in['Wk'], 'L3_xattn_Wv': _L3_xattn_in['Wv'], 'L3_xattn_hist_W': _L3_xattn_in['hist_W'], 'L3_xattn_hist_b': _L3_xattn_in['hist_b'], 'L3_xattn_hist_ln_g': _L3_xattn_in['hist_ln_g'], 'L3_xattn_hist_ln_b': _L3_xattn_in['hist_ln_b'], 'L3_xattn_ctx_W1': _L3_xattn_in['ctx_W1'], 'L3_xattn_ctx_b1': _L3_xattn_in['ctx_b1'], 'L3_xattn_ctx_W2': _L3_xattn_in['ctx_W2'], 'L3_xattn_ctx_b2': _L3_xattn_in['ctx_b2'], 'L3_xattn_kg_W1': _L3_xattn_in['kg_W1'], 'L3_xattn_kg_b1': _L3_xattn_in['kg_b1'], 'L3_xattn_kg_ln_g': _L3_xattn_in['kg_ln_g'], 'L3_xattn_kg_ln_b': _L3_xattn_in['kg_ln_b'], 'L3_xattn_kg_W2': _L3_xattn_in['kg_W2'], 'L3_xattn_kg_b2': _L3_xattn_in['kg_b2'], 'L3_xattn_proj_W': _L3_xattn_in['proj_W'], 'L3_xattn_proj_b': _L3_xattn_in['proj_b'], 'L3_ffn_router_w': _L3_ffn_in['router_w'], 'L3_ffn_gate_w': _L3_ffn_in['gate_w'], 'L3_ffn_up_w': _L3_ffn_in['up_w'], 'L3_ffn_down_w': _L3_ffn_in['down_w']}

def reference(x, ctx_1024, mask_Bx1x1xS2_ff0, mask_SxS_bc0, g_xattn, g_ffn, L0_xattn_query_kernel, L0_xattn_key_kernel, L0_xattn_value_kernel, L0_xattn_projection_kernel, L0_xattn_projection_bias, L0_ffn_W1, L0_ffn_b1, L0_ffn_W2, L0_ffn_b2, L0_ffn_scale, L1_xattn_WQ, L1_xattn_bQ, L1_xattn_WK, L1_xattn_bK, L1_xattn_WV, L1_xattn_bV, L1_xattn_WO, L1_xattn_bO, L1_ffn_expert_tokens, L1_ffn_W1, L1_ffn_b1, L1_ffn_W2, L1_ffn_b2, L1_ffn_W3, L1_ffn_b3, L2_xattn_Wq, L2_xattn_bq, L2_xattn_Wk, L2_xattn_bk, L2_xattn_Wv, L2_xattn_bv, L2_ffn_gate_w, L2_ffn_gate_up_proj, L2_ffn_down_proj, L3_xattn_Wq, L3_xattn_Wk, L3_xattn_Wv, L3_xattn_hist_W, L3_xattn_hist_b, L3_xattn_hist_ln_g, L3_xattn_hist_ln_b, L3_xattn_ctx_W1, L3_xattn_ctx_b1, L3_xattn_ctx_W2, L3_xattn_ctx_b2, L3_xattn_kg_W1, L3_xattn_kg_b1, L3_xattn_kg_ln_g, L3_xattn_kg_ln_b, L3_xattn_kg_W2, L3_xattn_kg_b2, L3_xattn_proj_W, L3_xattn_proj_b, L3_ffn_router_w, L3_ffn_gate_w, L3_ffn_up_w, L3_ffn_down_w):
    import jax
    import jax.numpy as jnp

    def _L0_xattn_ref(query, key, value, query_kernel, key_kernel, value_kernel, projection_kernel, projection_bias):
        import jax, jax.numpy as jnp
        import numpy as np
        B, N, M = (4, 256, 256)
        D_IN = 128
        H, HS = (16, 64)
        D_OUT = 128

        def _xavier(key, shape):
            fan_in, fan_out = (shape[-2], shape[-1])
            limit = float(np.sqrt(6.0 / (fan_in + fan_out)))
            return jax.random.uniform(key, shape, jnp.float32, -limit, limit)
        q = jnp.einsum('bni,hio->bnho', query, query_kernel)
        k = jnp.einsum('bmi,hio->bmho', key, key_kernel)
        v = jnp.einsum('bmi,hio->bmho', value, value_kernel)
        q = q / jnp.sqrt(jnp.asarray(HS, q.dtype))
        logits = jnp.einsum('bnho,bmho->bhnm', q, k)
        attn = jax.nn.softmax(logits, axis=-1)
        mh = jnp.einsum('bhnm,bmhi->bnhi', attn, v)
        out = jnp.einsum('bnhi,hio->bno', mh, projection_kernel) + projection_bias
        return out

    def _L0_ffn_ref(x, W1, b1, W2, b2, scale):
        import jax, jax.numpy as jnp
        import numpy as np
        LORA_DIM = 16
        LORA_TOKEN_INDEX = 1
        B, S, D, H = (4, 256, 128, 512)
        Bx, Sx, Dx = x.shape
        Hx = W1.shape[0]
        lt = jax.lax.dynamic_slice_in_dim(x, LORA_TOKEN_INDEX, LORA_DIM, axis=1)
        even = lt[:, ::2, :]
        odd = lt[:, 1::2, :]
        m1 = (even[:, :4, :, None] * odd[:, :4, None, :]).reshape(Bx, Hx, Dx)
        m2 = (even[:, 4:, :, None] * odd[:, 4:, None, :]).reshape(Bx, Dx, Hx)
        h = jnp.einsum('bsd,hd->bsh', x, W1) + scale * jnp.einsum('bsd,bhd->bsh', x, m1) + b1
        h = jax.nn.gelu(h, approximate=False)
        out = jnp.einsum('bsh,oh->bso', h, W2) + scale * jnp.einsum('bsh,boh->bso', h, m2) + b2
        return out

    def _L1_xattn_ref(Q, K, V, WQ, bQ, WK, bK, WV, bV, WO, bO):
        import jax, jax.numpy as jnp
        import numpy as np
        NUM_HEADS = 16
        D_K = 64
        D_V = 64
        D_MODEL = 128
        B = Q.shape[0]
        q = (Q @ WQ + bQ).reshape(B, -1, NUM_HEADS, D_K).transpose(0, 2, 1, 3)
        k = (K @ WK + bK).reshape(B, -1, NUM_HEADS, D_K).transpose(0, 2, 1, 3)
        v = (V @ WV + bV).reshape(B, -1, NUM_HEADS, D_V).transpose(0, 2, 1, 3)
        scores = jnp.einsum('bhqd,bhkd->bhqk', q, k) / jnp.sqrt(jnp.float32(D_K))
        attn = jax.nn.softmax(scores, axis=-1)
        out = jnp.einsum('bhqk,bhkd->bhqd', attn, v)
        out = out.transpose(0, 2, 1, 3).reshape(B, -1, NUM_HEADS * D_V)
        return out @ WO + bO

    def _L1_ffn_ref(x, expert_tokens, W1, b1, W2, b2, W3, b3):
        import jax, jax.numpy as jnp
        import numpy as np
        D_MODEL = 128
        D_HIDDEN = 512
        NUM_EXPERT = 8
        TOP_K = 2
        B, N = (1, 1024)

        def _expert_mlp(x, W1, b1, W2, b2, W3, b3):
            h = jax.nn.gelu(jnp.einsum('bnd,dh->bnh', x, W1) + b1, approximate=False)
            h = jax.nn.gelu(jnp.einsum('bnh,hk->bnk', h, W2) + b2, approximate=False)
            return jnp.einsum('bnh,hd->bnd', h, W3) + b3
        scores = jnp.einsum('bnd,ed->bne', x, expert_tokens)
        _, topk_idx = jax.lax.top_k(scores, TOP_K)
        outputs = jnp.zeros_like(x)
        num_expert = W1.shape[0]
        for i in range(num_expert):
            w = jnp.mean((topk_idx == i).astype(x.dtype), axis=-1, keepdims=True)
            y = _expert_mlp(x, W1[i], b1[i], W2[i], b2[i], W3[i], b3[i])
            outputs = outputs + y * w
        return outputs

    def _L2_xattn_ref(query_states, key_states, attention_mask, Wq, bq, Wk, bk, Wv, bv, mask_future):
        import jax, jax.numpy as jnp
        import numpy as np
        B, T, D, H = (2, 256, 128, 16)
        DH = D // H

        def _heads(x):
            b, t, _ = x.shape
            return x.reshape(b, t, H, DH).transpose(0, 2, 1, 3)
        q = _heads(query_states @ Wq + bq)
        k = _heads(key_states @ Wk + bk)
        v = _heads(key_states @ Wv + bv)
        scale = 1.0 / jnp.sqrt(jnp.asarray(DH, jnp.float32))
        scores = jnp.einsum('bhqd,bhkd->bhqk', q, k) * scale + attention_mask
        if mask_future:
            t = scores.shape[-1]
            triu = jnp.triu(jnp.ones((t, t), bool))
            scores = jnp.where(triu, -jnp.inf, scores)
        probs = jax.nn.softmax(scores, axis=-1)
        ctx = jnp.einsum('bhqk,bhkd->bhqd', probs, v)
        b, _, t, _ = ctx.shape
        return ctx.transpose(0, 2, 1, 3).reshape(b, t, H * DH)

    def _L2_ffn_ref(hidden_states, gate_w, gate_up_proj, down_proj):
        import jax, jax.numpy as jnp
        import numpy as np
        TOP_K = 2
        B, S, H = hidden_states.shape
        E = gate_w.shape[0]
        x = hidden_states.reshape(-1, H)
        T = x.shape[0]
        probs = jax.nn.softmax(x @ gate_w.T, axis=-1)
        w, idx = jax.lax.top_k(probs, TOP_K)
        w = w / jnp.sum(w, axis=-1, keepdims=True)
        combine = jnp.zeros((T, E), x.dtype).at[jnp.arange(T)[:, None], idx].add(w)

        def step(acc, inputs):
            gup, dn, ce = inputs
            g, u = jnp.split(x @ gup.T, 2, axis=-1)
            acc = acc + ce[:, None] * (jax.nn.silu(g) * u @ dn.T)
            return (acc, None)
        out, _ = jax.lax.scan(step, jnp.zeros_like(x), (gate_up_proj, down_proj, combine.T))
        return out.reshape(B, S, H)

    def _L3_xattn_ref(x, historical_data, Wq, Wk, Wv, hist_W, hist_b, hist_ln_g, hist_ln_b, ctx_W1, ctx_b1, ctx_W2, ctx_b2, kg_W1, kg_b1, kg_ln_g, kg_ln_b, kg_W2, kg_b2, proj_W, proj_b, causal_mask):
        import jax, jax.numpy as jnp
        import numpy as np
        from jax import lax
        H = 16
        K1, K2 = (3, 3)
        LN_EPS = 1e-05

        def _ln(x, g, b):
            m = jnp.mean(x, axis=-1, keepdims=True)
            v = jnp.mean(jnp.square(x - m), axis=-1, keepdims=True)
            return (x - m) * lax.rsqrt(v + LN_EPS) * g + b

        def _gelu(x):
            return jax.nn.gelu(x, approximate=False)
        B, T, D = x.shape
        hd = D // H
        scale = hd ** (-0.5)
        q = (x @ Wq).reshape(B, T, H, hd).transpose(0, 2, 1, 3)
        k = (x @ Wk).reshape(B, T, H, hd).transpose(0, 2, 1, 3)
        v = (x @ Wv).reshape(B, T, H, hd).transpose(0, 2, 1, 3)
        attn = jnp.einsum('bhqd,bhkd->bhqk', q, k) * scale
        eh = _gelu(_ln(historical_data @ hist_W + hist_b, hist_ln_g, hist_ln_b))
        aw = _gelu(eh @ ctx_W1 + ctx_b1) @ ctx_W2 + ctx_b2
        aw = jax.nn.softmax(aw, axis=1)
        cc = jnp.sum(eh * aw, axis=1)
        kp = _gelu(_ln(cc @ kg_W1 + kg_b1, kg_ln_g, kg_ln_b)) @ kg_W2 + kg_b2
        kernels = jax.nn.softmax(kp.reshape(B, H, K1 * K2), axis=-1)
        kernels = kernels.reshape(B * H, 1, K1, K2)
        mask = causal_mask[None, None]
        attn0 = jnp.where(mask, 0.0, attn).reshape(1, B * H, T, T)
        attn = lax.conv_general_dilated(attn0, kernels, window_strides=(1, 1), padding=((K1 // 2, K1 // 2), (K2 // 2, K2 // 2)), feature_group_count=B * H, dimension_numbers=('NCHW', 'OIHW', 'NCHW')).reshape(B, H, T, T)
        attn = jnp.where(mask, -jnp.inf, attn)
        p = jax.nn.softmax(attn, axis=-1)
        out = jnp.einsum('bhqk,bhkd->bhqd', p, v)
        out = out.transpose(0, 2, 1, 3).reshape(B, T, D)
        return out @ proj_W + proj_b

    def _L3_ffn_ref(hidden_states, router_w, gate_w, up_w, down_w):
        import jax, jax.numpy as jnp
        import numpy as np
        TOP_K = 2
        NUM_EXPERTS = 8
        HIDDEN = 128
        INTER = 256
        B, S, H = hidden_states.shape
        x = hidden_states.reshape(-1, H)
        T = x.shape[0]
        logits = x @ router_w.T
        probs = jax.nn.softmax(logits.astype(jnp.float32), axis=-1)
        w, sel = jax.lax.top_k(probs, TOP_K)
        w = w / jnp.sum(w, axis=-1, keepdims=True)
        w = w.astype(x.dtype)
        combine = jnp.zeros((T, NUM_EXPERTS), dtype=x.dtype)
        combine = combine.at[jnp.arange(T)[:, None], sel].add(w)

        def body(acc, ew):
            g, u, d, c = ew
            h = jax.nn.silu(x @ g) * (x @ u)
            return (acc + c[:, None] * (h @ d), None)
        acc0 = jnp.zeros((T, H), dtype=x.dtype)
        out, _ = jax.lax.scan(body, acc0, (gate_w, up_w, down_w, combine.T))
        return out.reshape(B, S, H)
    x = x + jnp.tanh(g_xattn[0]) * _L0_xattn_ref(_layernorm(x, axis=-1), ctx_1024, ctx_1024, L0_xattn_query_kernel, L0_xattn_key_kernel, L0_xattn_value_kernel, L0_xattn_projection_kernel, L0_xattn_projection_bias)
    x = x + jnp.tanh(g_ffn[0]) * _L0_ffn_ref(_layernorm(x, axis=-1), L0_ffn_W1, L0_ffn_b1, L0_ffn_W2, L0_ffn_b2, L0_ffn_scale)
    x = x + jnp.tanh(g_xattn[1]) * _L1_xattn_ref(_layernorm(x, axis=-1), ctx_1024, ctx_1024, L1_xattn_WQ, L1_xattn_bQ, L1_xattn_WK, L1_xattn_bK, L1_xattn_WV, L1_xattn_bV, L1_xattn_WO, L1_xattn_bO)
    x = x + jnp.tanh(g_ffn[1]) * _L1_ffn_ref(_layernorm(x, axis=-1), L1_ffn_expert_tokens, L1_ffn_W1, L1_ffn_b1, L1_ffn_W2, L1_ffn_b2, L1_ffn_W3, L1_ffn_b3)
    x = x + jnp.tanh(g_xattn[2]) * _L2_xattn_ref(_layernorm(x, axis=-1), ctx_1024, mask_Bx1x1xS2_ff0, L2_xattn_Wq, L2_xattn_bq, L2_xattn_Wk, L2_xattn_bk, L2_xattn_Wv, L2_xattn_bv, 0)
    x = x + jnp.tanh(g_ffn[2]) * _L2_ffn_ref(_layernorm(x, axis=-1), L2_ffn_gate_w, L2_ffn_gate_up_proj, L2_ffn_down_proj)
    x = x + jnp.tanh(g_xattn[3]) * _L3_xattn_ref(_layernorm(x, axis=-1), ctx_1024, L3_xattn_Wq, L3_xattn_Wk, L3_xattn_Wv, L3_xattn_hist_W, L3_xattn_hist_b, L3_xattn_hist_ln_g, L3_xattn_hist_ln_b, L3_xattn_ctx_W1, L3_xattn_ctx_b1, L3_xattn_ctx_W2, L3_xattn_ctx_b2, L3_xattn_kg_W1, L3_xattn_kg_b1, L3_xattn_kg_ln_g, L3_xattn_kg_ln_b, L3_xattn_kg_W2, L3_xattn_kg_b2, L3_xattn_proj_W, L3_xattn_proj_b, mask_SxS_bc0)
    x = x + jnp.tanh(g_ffn[3]) * _L3_ffn_ref(_layernorm(x, axis=-1), L3_ffn_router_w, L3_ffn_gate_w, L3_ffn_up_w, L3_ffn_down_w)
    return x

_drawn_inputs = setup_inputs


def setup_inputs(seed=0):
    import zlib

    import numpy as np

    out = dict(_drawn_inputs(seed))
    spreads = {'L0_xattn_projection_bias': (0.0, 0.1),
     'L0_ffn_b1': (0.0, 0.426),
     'L0_ffn_b2': (0.0, 0.1),
     'L1_xattn_bQ': (0.0, 0.8),
     'L1_xattn_bK': (0.0, 2.0),
     'L1_xattn_bV': (0.0, 0.1),
     'L1_xattn_bO': (0.0, 0.1),
     'L1_ffn_b1': (0.0, 0.547),
     'L1_ffn_b2': (0.0, 0.395),
     'L1_ffn_b3': (0.0, 0.1),
     'L2_xattn_bq': (0.0, 0.8),
     'L2_xattn_bk': (0.0, 2.0),
     'L2_xattn_bv': (0.0, 0.1),
     'L3_xattn_hist_b': (0.0, 0.8),
     'L3_xattn_hist_ln_g': (1.0, 0.6),
     'L3_xattn_hist_ln_b': (0.0, 0.8),
     'L3_xattn_ctx_b1': (0.0, 0.8),
     'L3_xattn_kg_b1': (0.0, 0.8),
     'L3_xattn_kg_ln_g': (1.0, 0.6),
     'L3_xattn_kg_ln_b': (0.0, 0.8),
     'L3_xattn_kg_b2': (0.0, 0.8),
     'L3_xattn_proj_b': (0.0, 0.8)}
    factors = {'g_ffn': 8.0,
     'L1_xattn_WQ': 8.0,
     'L1_xattn_WK': 8.0,
     'L2_xattn_Wq': 8.0,
     'L2_xattn_Wk': 8.0,
     'L2_ffn_gate_w': 8.0,
     'L2_ffn_gate_up_proj': 8.0,
     'L2_ffn_down_proj': 8.0,
     'L3_xattn_Wq': 4.463,
     'L3_xattn_Wk': 4.417,
     'L3_xattn_hist_W': 8.0,
     'L3_xattn_ctx_W1': 8.0,
     'L3_xattn_ctx_W2': 8.0,
     'L3_xattn_kg_W1': 8.0,
     'L3_xattn_kg_W2': 8.0,
     'L3_ffn_router_w': 6.156,
     'L3_ffn_gate_w': 5.379,
     'L3_ffn_up_w': 5.27,
     'L3_ffn_down_w': 5.251}
    for name, (base, spread) in spreads.items():
        noise = np.random.default_rng([zlib.crc32(name.encode()), seed]).standard_normal(out[name].shape)
        drawn = base * np.exp(spread * noise) if base else spread * noise
        out[name] = jnp.asarray(drawn.astype(out[name].dtype))
    for name, factor in factors.items():
        out[name] = (out[name] * factor).astype(out[name].dtype)
    return out
```

```python
import numpy as np
import concourse.bass as bass
from concourse import mybir
from contextlib import ExitStack

F32 = mybir.dt.float32
BF16 = mybir.dt.bfloat16
I32 = mybir.dt.int32
U32 = mybir.dt.uint32
U8 = mybir.dt.uint8
ALU = mybir.AluOpType
ACT = mybir.ActivationFunctionType
AX = mybir.AxisListType.X

P = 128
B, S, D = 4, 256, 128
T = B * S
NT = T // P
C = 64
EPS = 1e-5


class Tally:

    def __init__(self, sem):
        self.sem, self.n, self.top, self.mark = sem, 0, None, 0

    def add(self, instruction, by=1):
        instruction.then_inc(self.sem, by)
        self.n += by
        return instruction

    def enter(self, i, per):
        self.top, self.mark, self.per = self.n + i * per, self.n, per

    def leave(self, times):
        assert self.n - self.mark == self.per, (self.n - self.mark, self.per)
        self.top, self.n = None, self.mark + times * self.per

    def now(self):
        return self.n if self.top is None else self.top + (self.n - self.mark)

    def wait(self, engine):
        engine.wait_ge(self.sem, self.now())


class Scope:

    def __init__(self, nc, name):
        self.nc, self.name, self.stack, self.sems = nc, name, ExitStack(), []

    def __enter__(self):
        self.stack.__enter__()
        return self

    def __exit__(self, *error):
        self.stack.close()
        numbers = sorted(sem.num for sem in self.sems)
        while numbers:
            n = 1
            while n < len(numbers) and numbers[n] == numbers[0] + n:
                n += 1
            self.nc.gpsimd.sem_clear(range(numbers[0], numbers[0] + n))
            numbers = numbers[n:]

    def sb(self, name, shape, dtype=F32):
        return self.stack.enter_context(self.nc.sbuf_tensor(f"{self.name}_{name}", shape, dtype))

    def psum(self, name, shape, dtype=F32):
        return self.stack.enter_context(self.nc.psum_tensor(f"{self.name}_{name}", shape, dtype))

    def sem(self, name):
        self.sems.append(self.stack.enter_context(self.nc.semaphore(f"{self.name}_{name}")))
        return self.sems[-1]

    def gpsimd_dma_sem(self, name):
        return self.nc.alloc_semaphore(f"{self.name}_{name}")

    def block(self):
        return self.nc.Block()


def row(ap):
    return ap.rearrange("(a n) -> a n", a=1)


def setup(nc, a, keep):
    with Scope(nc, "setup") as s:
        gates_raw = s.sb("gates_raw", [P, 2 * B])
        ctx = s.sb("ctx", [P, 2, D])
        ps = s.psum("ps", [P, 2, 512])
        x_loaded, ctx_loaded, gates_loaded = s.sem("x_loaded"), s.sem("ctx_loaded"), s.sem("gates_loaded")
        zeroed, identity_made, ctx_turned = s.sem("zeroed"), s.sem("identity_made"), s.sem("ctx_turned")
        ctx_kept, gates_made, half_made = s.sem("ctx_kept"), s.sem("gates_made"), s.sem("half_made")
        with s.block() as block:

            @block.sync
            def _(sp):
                sp.dma_start(ctx[:], a["ctx_1024"].rearrange("(u b) k d -> (b k) u d", u=2)).then_inc(ctx_loaded, 16)
                sp.dma_start(keep.x[:], a["x"].rearrange("b (u p) d -> p (b u) d", p=P)).then_inc(x_loaded, 16)
                sp.dma_start(gates_raw[:, 0:B], row(a["g_xattn"]).to_broadcast([P, B])).then_inc(gates_loaded, 16)
                sp.dma_start(gates_raw[:, B:2 * B], row(a["g_ffn"]).to_broadcast([P, B])).then_inc(gates_loaded, 16)
                sp.wait_ge(x_loaded, 16)

            @block.gpsimd
            def _(pool):
                pool.iota(keep.iota[:], pattern=[[1, P]], base=0, channel_multiplier=0,
                          allow_small_or_imprecise_dtypes=True)
                pool.iota(keep.iota_tiles[:], pattern=[[P, NT]], base=0, channel_multiplier=0,
                          allow_small_or_imprecise_dtypes=True)
                pool.iota(keep.token[:], pattern=[[P, NT]], base=0, channel_multiplier=1,
                          allow_small_or_imprecise_dtypes=True)
                pool.memset(keep.identity[:], 0.0).then_inc(zeroed, 1)
                pool.memset(keep.neg_half[:], -0.5).then_inc(half_made, 1)
                pool.wait_ge(zeroed, 1)
                pool.affine_select(out=keep.identity[:], in_=keep.identity[:], compare_op=ALU.not_equal, fill=1.0,
                                   base=0, pattern=[[-1, P]], channel_multiplier=1).then_inc(identity_made, 1)

            @block.scalar
            def _(act):
                act.wait_ge(gates_loaded, 32)
                act.activation(keep.gates[:], gates_raw[:], ACT.Tanh).then_inc(gates_made, 1)

            @block.tensor
            def _(pe):
                pe.wait_ge(ctx_loaded, 16)
                pe.wait_ge(identity_made, 1)
                for u in range(2):
                    pe.transpose(ps[:, u, 0:P], ctx[:, u, :], keep.identity[:]).then_inc(ctx_turned, 1)

            @block.vector
            def _(dve):
                for u in range(2):
                    dve.wait_ge(ctx_turned, u + 1)
                    dve.tensor_copy(keep.ctx_t[:, u * P:(u + 1) * P], ps[:, u, 0:P]).then_inc(ctx_kept, 1)


def head_operands(nc, a, keep, name, weights, biases, scale, scores_rhs, values_rhs, score_bias):
    pairs = 8
    with Scope(nc, name) as s:
        wq, wk, wv = (s.sb(n, [P, pairs * P]) for n in ("wq", "wk", "wv"))
        wo = s.sb("wo", [P, pairs, D])
        wq_t = s.sb("wq_t", [P, 2, P])
        k_t = s.sb("k_t", [P, 2, B * C])
        v_diag = s.sb("v_diag", [P, 2, B, 2, C])
        bias_rows = s.sb("bias_rows", [3 * pairs, P])
        bias = s.sb("bias", [P, 3 * pairs])
        ps = s.psum("ps", [P, 8, 512])
        names = ["loaded", "bias_loaded", "bias_turned", "bias_kept", "wq_turned", "wq_kept", "kv_made", "k_kept",
                 "v_kept", "scores_made", "scores_kept", "bias_done", "values_made",
                 "values_kept", "diag_zeroed"]
        sem = {n: s.sem(n) for n in names}
        loads = 4
        with s.block() as block:

            @block.sync
            def _(sp):
                for to, w in zip((wq, wk, wv), weights[:3]):
                    if len(w.shape) == 3:
                        sp.dma_start(to[:].rearrange("i (h o) -> i h o", o=C),
                                     w.rearrange("h i o -> i h o")).then_inc(sem["loaded"], 16)
                    else:
                        sp.dma_start(to[:], w).then_inc(sem["loaded"], 16)
                wo_rows = weights[3].rearrange("h o n -> (h o) n") if len(weights[3].shape) == 3 else weights[3]
                sp.dma_start(wo[:], wo_rows.rearrange("(p r) n -> r p n", r=P)).then_inc(sem["loaded"], 16)
                if biases:
                    for n, v in enumerate(biases):
                        sp.dma_start(bias_rows[n * pairs:(n + 1) * pairs, :],
                                     v.rearrange("(p r) -> p r", r=P)).then_inc(sem["bias_loaded"], 16)

            @block.gpsimd
            def _(pool):
                pool.memset(v_diag[:], 0.0).then_inc(sem["diag_zeroed"], 1)

            @block.tensor
            def _(pe):
                def project(p):
                    u, cols = p % 2, slice(p * P, (p + 1) * P)
                    if p >= 2:
                        pe.wait_ge(sem["wq_kept"], p - 1)
                        pe.wait_ge(sem["k_kept"], p - 1)
                        pe.wait_ge(sem["v_kept"], 2 * (p - 1))
                    pe.transpose(ps[:, 2 + u, 0:P], wq[:, cols], keep.identity[:]).then_inc(sem["wq_turned"], 1)
                    pe.matmul(ps[:, u, 0:256], wk[:, cols], keep.ctx_t[:], start=True, stop=True)
                    pe.matmul(ps[:, u, 256:512], wv[:, cols], keep.ctx_t[:], start=True, stop=True)\
                        .then_inc(sem["kv_made"], 1)

                def fold(p):
                    u = p % 2
                    pe.wait_ge(sem["wq_kept"], p + 1)
                    pe.wait_ge(sem["k_kept"], p + 1)
                    if p >= 1:
                        pe.wait_ge(sem["scores_kept"], p)
                        if biases:
                            pe.wait_ge(sem["bias_done"], p)
                    for e in range(2):
                        rows = slice(e * C, (e + 1) * C)
                        mm = pe.matmul(ps[:, 4 + e, 0:256], wq_t[rows, u, :], k_t[rows, u, :], start=True, stop=True)
                        if biases:
                            mm = pe.matmul(ps[:, 4 + e, 256:512], bias[rows, p:p + 1].to_broadcast([C, P]),
                                           k_t[rows, u, :], start=True, stop=True)
                        mm.then_inc(sem["scores_made"], 1)
                    pe.wait_ge(sem["v_kept"], 2 * (p + 1))
                    if p >= 2:
                        pe.wait_ge(sem["values_kept"], p - 1)
                    for b in range(B):
                        mm = pe.matmul(ps[:, 6 + u, b * D:(b + 1) * D],
                                       v_diag[:, u, b, :, :].rearrange("r e k -> r (e k)"), wo[:, p, :],
                                       start=True, stop=True)
                    mm.then_inc(sem["values_made"], 1)

                pe.wait_ge(sem["loaded"], 16 * loads)
                if biases:
                    pe.wait_ge(sem["bias_loaded"], 48)
                    pe.transpose(ps[:, 7, 0:3 * pairs], bias_rows[:], keep.identity[0:3 * pairs, 0:3 * pairs])\
                        .then_inc(sem["bias_turned"], 1)
                    pe.wait_ge(sem["bias_kept"], 1)
                project(0)
                for p in range(pairs):
                    if p + 1 < pairs:
                        project(p + 1)
                    fold(p)

            @block.scalar
            def _(act):
                def keep_wq(p):
                    act.wait_ge(sem["wq_turned"], p + 1)
                    if p >= 2:
                        act.wait_ge(sem["scores_made"], 2 * (p - 1))
                    act.activation(wq_t[:, p % 2, :], ps[:, 2 + p % 2, 0:P], ACT.Copy).then_inc(sem["wq_kept"], 1)

                keep_wq(0)
                for p in range(pairs):
                    if p + 1 < pairs:
                        keep_wq(p + 1)
                    act.wait_ge(sem["scores_made"], 2 * (p + 1))
                    act.activation(scores_rhs[:, :, p * P:(p + 1) * P].rearrange("i b (e k) -> i e b k", e=2),
                                   ps[:, 4:6, 0:256].rearrange("i e (b k) -> i e b k", b=B), ACT.Copy, scale=scale)\
                        .then_inc(sem["scores_kept"], 1)
                    if biases:
                        act.activation(score_bias[:, :, p * P:(p + 1) * P].rearrange("i b (e k) -> i e b k", e=2),
                                       ps[:, 4:6, 256:512].rearrange("i e (b k) -> i e b k", b=B), ACT.Copy,
                                       scale=scale).then_inc(sem["bias_done"], 1)

            @block.vector
            def _(dve):
                if biases:
                    dve.wait_ge(sem["bias_turned"], 1)
                    dve.tensor_copy(bias[:], ps[:, 7, 0:3 * pairs]).then_inc(sem["bias_kept"], 1)
                    dve.wait_ge(sem["bias_kept"], 1)

                def keep_kv(p):
                    u = p % 2
                    dve.wait_ge(sem["kv_made"], p + 1)
                    if p >= 2:
                        dve.wait_ge(sem["scores_made"], 2 * (p - 1))
                    bk = bias[:, pairs + p:pairs + p + 1] if biases else 0.0
                    dve.tensor_scalar(k_t[:, u, :], ps[:, u, 0:256], bk, None, ALU.add).then_inc(sem["k_kept"], 1)
                    if p >= 2:
                        dve.wait_ge(sem["values_made"], p - 1)
                    for e in range(2):
                        rows = slice(e * C, (e + 1) * C)
                        bv = bias[rows, 2 * pairs + p:2 * pairs + p + 1] if biases else 0.0
                        dve.tensor_scalar(v_diag[rows, u, :, e, :],
                                          ps[rows, u, 256:512].rearrange("r (b k) -> r b k", b=B), bv, None, ALU.add)\
                            .then_inc(sem["v_kept"], 1)

                dve.wait_ge(sem["diag_zeroed"], 1)
                keep_kv(0)
                for p in range(pairs):
                    if p + 1 < pairs:
                        keep_kv(p + 1)
                    dve.wait_ge(sem["values_made"], p + 1)
                    dve.tensor_copy(values_rhs[:, :, p, :], ps[:, 6 + p % 2, :].rearrange("r (b n) -> r b n", b=B))\
                        .then_inc(sem["values_kept"], 1)


def cross_attention(nc, a, keep, name, scores_rhs, values_rhs, score_bias, out_bias, gate, query=None,
                    query_scale=1.0):
    heads, pairs = 16, 8
    width = values_rhs.shape[3]
    own_columns = width < D
    with Scope(nc, name) as s:
        out_bias_rows = s.sb("out_bias_rows", [P, D])
        stats = s.sb("stats", [P, NT, 6])
        moments = s.sb("moments", [P, NT, 2])
        var_eps = s.sb("var_eps", [P, NT])
        rstd = s.sb("rstd", [P, NT])
        xn = s.sb("xn", [P, 2, D])
        xn_t = s.sb("xn_t", [P, 2, P])
        q_t = s.sb("q_t", [P, 2, P]) if query else xn_t
        e = s.sb("e", [P, 2, heads, C])
        probs_t = s.sb("probs_t", [P, 2, pairs, P])
        top = s.sb("top", [P, 2, heads])
        total = s.sb("total", [P, 2, heads])
        inverse = s.sb("inverse", [P, 2, heads])
        change = s.sb("change", [P, 2, D])
        ps_scores = s.psum("ps_scores", [P, 2, heads, C])
        ps_turned = s.psum("ps_turned", [P, 2, 4, P])
        ps_out = s.psum("ps_out", [P, 512])
        ps_xn = s.psum("ps_xn", [P, 512])
        names = ["bias_loaded", "stats_made", "moments_made", "var_ready", "rstd_ready", "xn_ready", "xn_turned",
                 "xn_kept", "q_made", "q_kept", "scores_made", "top_found", "biased", "centred", "exp_done", "total_made",
                 "inverse_made", "probs_ready", "probs_turned", "probs_kept", "out_made", "change_made", "x_done"]
        sem = {n: s.sem(n) for n in names}
        with s.block() as block:

            @block.sync
            def _(sp):
                sp.dma_start(out_bias_rows[:], row(out_bias).to_broadcast([P, D])).then_inc(sem["bias_loaded"], 16)

            @block.gpsimd
            def _(pool):
                pool.wait_ge(sem["var_ready"], 1)
                pool.tensor_tensor(rstd[:], var_eps[:], keep.neg_half[:, 0:NT], ALU.pow).then_inc(sem["rstd_ready"], 1)

                def normalise(t, u):
                    pool.wait_ge(sem["inverse_made"], t + 1)
                    pool.tensor_tensor(e[:, u], e[:, u], inverse[:, u, :, None].to_broadcast([P, heads, C]), ALU.mult)\
                        .then_inc(sem["probs_ready"], 1)

                with pool.Fori(0, NT // 2) as i:
                    for u in range(2):
                        normalise(2 * i + u, u)

            @block.tensor
            def _(pe):
                def turn_xn(t, u, first=False):
                    pe.wait_ge(sem["xn_ready"], t + 1)
                    if not first:
                        pe.wait_ge(sem["xn_kept"], t)
                    if query and not first:
                        pe.wait_ge(sem["q_kept"], t)
                    pe.transpose(ps_xn[:, 0:P], xn[:, u, :], keep.identity[:]).then_inc(sem["xn_turned"], 1)
                    if query:
                        pe.wait_ge(sem["xn_kept"], t + 1)
                        pe.matmul(ps_xn[:, P:2 * P], query[0], xn_t[:, u, :], start=True, stop=True)\
                            .then_inc(sem["q_made"], 1)

                def scores(t, u, b, first=False):
                    pe.wait_ge(sem["q_kept" if query else "xn_kept"], t + 1)
                    if not first:
                        pe.wait_ge(sem["centred"], t - 1)
                    for half in range(2):
                        mm = pe.matmul(ps_scores[:, u, 8 * half:8 * half + 8, :].rearrange("p h k -> p (h k)"),
                                       q_t[:, u, :], scores_rhs[:, b, 512 * half:512 * half + 512],
                                       start=True, stop=True)
                    mm.then_inc(sem["scores_made"], 1)

                def turn_probs(t, u, first=False):
                    pe.wait_ge(sem["probs_ready"], t + 1)
                    for half in range(2):
                        if not first:
                            pe.wait_ge(sem["probs_kept"], 2 * t - 1 + half)
                        for p in range(4 * half, 4 * half + 4):
                            mm = pe.transpose(ps_turned[:, half, p % 4, :],
                                              e[:, u, 2 * p:2 * p + 2, :].rearrange("p h k -> p (h k)"),
                                              keep.identity[:])
                        mm.then_inc(sem["probs_turned"], 1)

                def output(t, u, b, first=False):
                    if not first:
                        pe.wait_ge(sem["change_made"], t)
                    for p in range(pairs):
                        if p % 4 == 0:
                            pe.wait_ge(sem["probs_kept"], 2 * t + 1 + p // 4)
                        to = ps_out[:, p * width:(p + 1) * width] if own_columns else ps_out[:, 0:D]
                        mm = pe.matmul(to, probs_t[:, u, p, :], values_rhs[:, b, p, :],
                                       start=own_columns or p == 0, stop=own_columns or p == pairs - 1)
                    mm.then_inc(sem["out_made"], 1)

                turn_xn(0, 0, True)
                scores(0, 0, 0, True)
                turn_xn(1, 1)
                scores(1, 1, 0, True)

                def step(i, first, last):
                    for u in range(2):
                        t = 2 * i + u
                        if not last:
                            turn_xn(t + 2, u)
                            scores(t + 2, u, i + 1)
                        turn_probs(t, u, first and u == 0)
                        output(t, u, i, first and u == 0)

                step(0, True, False)
                with pe.Fori(1, NT // 2 - 1) as i:
                    step(i, False, False)
                step(NT // 2 - 1, False, True)

            @block.scalar
            def _(act):
                def keep_xn(t, u, first=False):
                    act.wait_ge(sem["xn_turned"], t + 1)
                    if not first:
                        act.wait_ge(sem["q_made" if query else "scores_made"], t - 1)
                    act.activation(xn_t[:, u, :], ps_xn[:, 0:P], ACT.Copy).then_inc(sem["xn_kept"], 1)
                    if query:
                        act.wait_ge(sem["q_made"], t + 1)
                        if not first:
                            act.wait_ge(sem["scores_made"], t - 1)
                        act.activation(q_t[:, u, :], ps_xn[:, P:2 * P], ACT.Identity, bias=query[1],
                                       scale=query_scale)\
                            .then_inc(sem["q_kept"], 1)

                def exp(t, u):
                    act.wait_ge(sem["centred"], t + 1)
                    act.activation(e[:, u], e[:, u], ACT.Exp).then_inc(sem["exp_done"], 1)

                def keep_probs(t, u, first=False):
                    for half in range(2):
                        act.wait_ge(sem["probs_turned"], 2 * t + 1 + half)
                        if not first:
                            act.wait_ge(sem["out_made"], t - 1)
                        act.activation(probs_t[:, u, 4 * half:4 * half + 4, :], ps_turned[:, half], ACT.Copy)\
                            .then_inc(sem["probs_kept"], 1)

                keep_xn(0, 0, True)
                keep_xn(1, 1, True)
                exp(0, 0)

                def step(i, first, last):
                    for u in range(2):
                        t = 2 * i + u
                        if not last:
                            keep_xn(t + 2, u)
                        if not (last and u == 1):
                            exp(t + 1, 1 - u)
                        keep_probs(t, u, first)

                step(0, True, False)
                with act.Fori(1, NT // 2 - 1) as i:
                    step(i, False, False)
                step(NT // 2 - 1, False, True)

            @block.vector
            def _(dve):
                for t in range(NT):
                    dve.bn_stats(stats[:, t, :], keep.x[:, t, :]).then_inc(sem["stats_made"], 1)
                for t in range(NT):
                    dve.wait_ge(sem["stats_made"], t + 1)
                    dve.bn_aggr(moments[:, t, :], stats[:, t, :]).then_inc(sem["moments_made"], 1)
                dve.wait_ge(sem["moments_made"], NT)
                dve.tensor_scalar(var_eps[:], moments[:, :, 1], EPS, None, ALU.add).then_inc(sem["var_ready"], 1)
                dve.wait_ge(sem["rstd_ready"], 1)
                dve.wait_ge(sem["bias_loaded"], 16)

                def normalise(t, u, first=False):
                    if not first:
                        dve.wait_ge(sem["xn_turned"], t - 1)
                    dve.tensor_scalar(xn[:, u, :], keep.x[:, bass.ds(t, 1), :].rearrange("p a d -> p (a d)"),
                                      moments[:, bass.ds(t, 1), 0:1].rearrange("p a d -> p (a d)"),
                                      rstd[:, bass.ds(t, 1)], ALU.subtract, ALU.mult).then_inc(sem["xn_ready"], 1)

                def centre(t, u, b, first=False):
                    dve.wait_ge(sem["scores_made"], t + 1)
                    if not first:
                        dve.wait_ge(sem["probs_turned"], 2 * (t - 1))
                    scored = ps_scores[:, u]
                    if score_bias is not None:
                        dve.tensor_tensor(e[:, u].rearrange("p h k -> p (h k)"),
                                          ps_scores[:, u].rearrange("p h k -> p (h k)"), score_bias[:, b, :],
                                          ALU.add).then_inc(sem["biased"], 1)
                        dve.wait_ge(sem["biased"], t + 1)
                        scored = e[:, u]
                    dve.tensor_reduce(top[:, u, :], scored, AX, ALU.max).then_inc(sem["top_found"], 1)
                    dve.wait_ge(sem["top_found"], t + 1)
                    dve.tensor_tensor(e[:, u], scored, top[:, u, :, None].to_broadcast([P, heads, C]), ALU.subtract)\
                        .then_inc(sem["centred"], 1)

                def sums(t, u, first=False):
                    dve.wait_ge(sem["exp_done"], t + 1)
                    dve.tensor_reduce(total[:, u, :], e[:, u], AX, ALU.add).then_inc(sem["total_made"], 1)
                    dve.wait_ge(sem["total_made"], t + 1)
                    if not first:
                        dve.wait_ge(sem["probs_ready"], t - 1)
                    dve.reciprocal(inverse[:, u, :], total[:, u, :]).then_inc(sem["inverse_made"], 1)

                def update(t, u):
                    dve.wait_ge(sem["out_made"], t + 1)
                    dve.tensor_tensor(change[:, u, :], ps_out[:, 0:D], out_bias_rows[:], ALU.add)\
                        .then_inc(sem["change_made"], 1)
                    dve.wait_ge(sem["change_made"], t + 1)
                    xt = keep.x[:, bass.ds(t, 1), :].rearrange("p a d -> p (a d)")
                    dve.scalar_tensor_tensor(out=xt, in0=change[:, u, :], scalar=gate, in1=xt, op0=ALU.mult,
                                             op1=ALU.add).then_inc(sem["x_done"], 1)

                normalise(0, 0, True)
                normalise(1, 1, True)
                centre(0, 0, 0, True)
                normalise(2, 0)
                centre(1, 1, 0, True)
                sums(0, 0, True)
                normalise(3, 1)
                centre(2, 0, 1)
                sums(1, 1, True)
                update(0, 0)

                def step(i, last):
                    for u in range(2):
                        t = 2 * i + u
                        if not last:
                            normalise(t + 2, u)
                        if u == 0:
                            centre(t + 1, 1, i)
                        elif not last:
                            centre(t + 1, 0, i + 1)
                        sums(t, u)
                        update(t - 1, 1 - u)

                with dve.Fori(1, NT // 2 - 1) as i:
                    step(i, False)
                step(NT // 2 - 1, True)
                update(NT - 1, 1)


EXPERTS, CHOSEN = 8, 2
TILES = CHOSEN * NT + EXPERTS - 1
SLOTS = TILES * P


class Routes:

    def __init__(self, nc, s, name, before=0):
        self.before, self.gathers_before = before, [16 * before * ((TILES + 1) // 2), 16 * before * (TILES // 2)]
        self.weight = s.sb(f"{name}_weight", [P, CHOSEN, NT])
        self.slot = s.sb(f"{name}_slot", [P, CHOSEN, NT], U32)
        self.token_of = s.sb(f"{name}_token", [P, TILES], U32)
        self.expert_of = s.sb(f"{name}_expert", [P, TILES], I32)
        self.tokens = nc.dram_tensor(f"{name}_tokens", [T, D], F32, kind="Internal").ap()
        self.results = nc.dram_tensor(f"{name}_results", [SLOTS, D], F32, kind="Internal").ap()


def route(nc, keep, name, routes, router, gate, weighted):
    with Scope(nc, name) as s:
        ps = s.psum("ps", [P, 6, 512])
        norm = Normed(s, keep, ps[:, 0], ps[:, 1])
        router_rows, router_t = s.sb("router_rows", [EXPERTS, D]), s.sb("router_t", [P, EXPERTS])
        logits, best = s.sb("logits", [P, NT, EXPERTS]), s.sb("best", [P, NT, 8])
        best_at, best_f = s.sb("best_at", [P, NT, 8], U32), s.sb("best_f", [P, CHOSEN, NT])
        chosen, any_chosen = s.sb("chosen", [P, CHOSEN, NT, EXPERTS]), s.sb("any_chosen", [P, NT, EXPERTS])
        before = s.sb("before", [P, P])
        ones = s.sb("ones", [P, P])
        pad = 4
        run = [s.sb(f"run{n}", [P, pad + NT, EXPERTS]) for n in range(2)]
        ends = [s.sb(f"ends{n}", [P, pad + EXPERTS]) for n in range(2)]
        counts = s.sb("counts", [P, NT, EXPERTS])
        over, used = s.sb("over", [P, EXPERTS, EXPERTS]), s.sb("used", [P, EXPERTS])
        rank, slot_of = s.sb("rank", [P, NT, EXPERTS]), s.sb("slot_of", [P, NT, EXPERTS])
        picked, slot_f = s.sb("picked", [P, CHOSEN, NT, EXPERTS]), s.sb("slot_f", [P, CHOSEN, NT])
        slot_i = s.sb("slot_i", [P, 3, CHOSEN * NT], I32)
        place_f = s.sb("place_f", [P, 2, CHOSEN * NT])
        at_row = s.sb("at_row", [P, CHOSEN * NT, P], mybir.dt.float16)
        is_tile = s.sb("is_tile", [P, CHOSEN * NT, TILES])
        at_tile = s.sb("at_tile", [P, CHOSEN * NT, TILES], mybir.dt.float16)
        past, expert_f = s.sb("past", [P, TILES, EXPERTS - 1]), s.sb("expert_f", [P, TILES])
        gap, grown, denominator = (s.sb(n, [P, NT]) for n in ("gap", "grown", "denominator"))
        base = s.sb("base", [P, EXPERTS])
        names = ["router_loaded", "router_turned", "router_kept", "logits_made", "logits_kept", "chosen_ready",
                 "counted", "steps", "gap_ready", "exp_done", "tokens_stored", "order_ready", "order_made",
                 "tables_set", "cut"]
        sem = {n: s.sem(n) for n in names}
        with s.block() as block:

            @block.sync
            def _(sp):
                sp.dma_start(router_rows[:], router).then_inc(sem["router_loaded"], 16)
                sp.wait_ge(norm.xn_ready, NT)
                sp.dma_start(routes.tokens.rearrange("(t p) d -> p t d", p=P), norm.xn[:])\
                    .then_inc(sem["tokens_stored"], 16)
                sp.wait_ge(sem["tokens_stored"], 16)

            @block.gpsimd
            def _(pool):
                norm.gpsimd(pool)
                pool.memset(ones[:], 1.0).then_inc(sem["tables_set"], 1)
                for n in range(2):
                    pool.memset(run[n][:, 0:pad, :], 0.0).then_inc(sem["tables_set"], 1)
                    pool.memset(ends[n][:, 0:pad], 0.0).then_inc(sem["tables_set"], 1)
                pool.wait_ge(sem["tables_set"], 5)
                pool.affine_select(out=before[:], in_=ones[:], compare_op=ALU.is_gt, fill=0.0, base=0,
                                   pattern=[[1, P]], channel_multiplier=-1).then_inc(sem["cut"], 1)

            @block.tensor
            def _(pe):
                pe.wait_ge(sem["router_loaded"], 16)
                pe.transpose(ps[:, 2, 0:EXPERTS], router_rows[:], keep.identity[0:EXPERTS, 0:EXPERTS])\
                    .then_inc(sem["router_turned"], 1)
                norm.tensor(pe)
                pe.wait_ge(sem["router_kept"], 1)
                for t in range(NT):
                    if t % 4 == 0:
                        pe.wait_ge(norm.xt_ready, 1 + t // 4)
                    mm = pe.matmul(ps[:, 3, t * EXPERTS:(t + 1) * EXPERTS], norm.xt[:, t, :], router_t[:],
                                   start=True, stop=True)
                mm.then_inc(sem["logits_made"], 1)
                pe.wait_ge(sem["chosen_ready"], 1)
                pe.wait_ge(sem["cut"], 1)
                flat = any_chosen[:].rearrange("p t e -> p (t e)")
                pe.matmul(ps[:, 4, 0:NT * EXPERTS], before[:], flat, start=True, stop=True)
                pe.matmul(ps[:, 4, 256:256 + NT * EXPERTS], ones[:], flat, start=True, stop=True)\
                    .then_inc(sem["counted"], 1)
                pe.wait_ge(sem["order_ready"], 1)
                for n in range(CHOSEN * NT):
                    mm = pe.matmul(ps[:, 5, 0:TILES], at_row[:, n, :], at_tile[:, n, :], start=(n == 0),
                                   stop=(n == CHOSEN * NT - 1))
                mm.then_inc(sem["order_made"], 1)

            @block.scalar
            def _(act):
                act.wait_ge(sem["router_turned"], 1)
                act.activation(router_t[:], ps[:, 2, 0:EXPERTS], ACT.Copy).then_inc(sem["router_kept"], 1)
                norm.scalar(act)
                if weighted:
                    act.wait_ge(sem["gap_ready"], 1)
                    act.activation(grown[:], gap[:], ACT.Exp).then_inc(sem["exp_done"], 1)

            @block.vector
            def _(dve):
                norm.vector(dve)
                steps = Tally(sem["steps"])

                def then(instruction):
                    steps.add(instruction)
                    steps.wait(dve)

                dve.wait_ge(sem["logits_made"], 1)
                then(dve.tensor_copy(logits[:].rearrange("p t e -> p (t e)"), ps[:, 3, 0:NT * EXPERTS]))
                for t in range(NT):
                    steps.add(dve.max(best[:, t, :], logits[:, t, :]))
                steps.wait(dve)
                for t in range(NT):
                    steps.add(dve.max_index(best_at[:, t, :], best[:, t, :], logits[:, t, :]))
                steps.wait(dve)
                if weighted:
                    dve.tensor_tensor(gap[:], best[:, :, 1], best[:, :, 0], ALU.subtract).then_inc(sem["gap_ready"], 1)
                then(dve.tensor_copy(best_f[:], best_at[:, :, 0:CHOSEN].rearrange("p t k -> p k t")))
                for k in range(CHOSEN):
                    steps.add(dve.tensor_tensor(chosen[:, k], keep.iota[:, None, 0:EXPERTS].to_broadcast([P, NT, EXPERTS]),
                                                best_f[:, k, :, None].to_broadcast([P, NT, EXPERTS]), ALU.is_equal))
                steps.wait(dve)
                dve.tensor_tensor(any_chosen[:], chosen[:, 0], chosen[:, 1], ALU.add).then_inc(sem["chosen_ready"], 1)
                if weighted:
                    dve.wait_ge(sem["exp_done"], 1)
                    then(dve.tensor_scalar(denominator[:], grown[:], 1.0, None, ALU.add))
                    then(dve.reciprocal(gap[:], denominator[:]))
                    then(dve.tensor_scalar(routes.weight[:, 0, :], gap[:], gate, None, ALU.mult))
                    steps.add(dve.tensor_tensor(routes.weight[:, 1, :], grown[:], routes.weight[:, 0, :], ALU.mult))
                else:
                    steps.add(dve.tensor_scalar(routes.weight[:], keep.neg_half[:, 0:CHOSEN * NT].rearrange(
                        "p (k t) -> p k t", k=CHOSEN), gate, -1.0, ALU.mult, ALU.mult))
                dve.wait_ge(sem["counted"], 1)
                dve.wait_ge(sem["tables_set"], 5)
                then(dve.tensor_copy(run[0][:, pad:, :].rearrange("p t e -> p (t e)"), ps[:, 4, 256:256 + NT * EXPERTS]))
                then(dve.tensor_tensor(run[1][:, pad:, :], run[0][:, pad:, :], run[0][:, pad - 1:-1, :], ALU.add))
                steps.add(dve.tensor_copy(counts[:], run[0][:, pad:, :]))
                steps.wait(dve)
                then(dve.tensor_tensor(run[0][:, pad:, :], run[1][:, pad:, :], run[1][:, pad - 2:-2, :], ALU.add))
                then(dve.tensor_tensor(run[1][:, pad:, :], run[0][:, pad:, :], run[0][:, pad - 4:-4, :], ALU.add))
                then(dve.tensor_tensor(over[:], run[1][:, pad + NT - 1, :, None].to_broadcast([P, EXPERTS, NT]),
                                       keep.iota_tiles[:, None, 0:NT].to_broadcast([P, EXPERTS, NT]), ALU.is_gt))
                then(dve.tensor_reduce(used[:], over[:], AX, ALU.add))
                then(dve.tensor_copy(ends[0][:, pad:], used[:]))
                then(dve.tensor_tensor(ends[1][:, pad:], ends[0][:, pad:], ends[0][:, pad - 1:-1], ALU.add))
                then(dve.tensor_tensor(ends[0][:, pad:], ends[1][:, pad:], ends[1][:, pad - 2:-2], ALU.add))
                then(dve.tensor_tensor(ends[1][:, pad:], ends[0][:, pad:], ends[0][:, pad - 4:-4], ALU.add))
                then(dve.tensor_tensor(base[:], ends[1][:, pad:], used[:], ALU.subtract))
                then(dve.tensor_tensor(rank[:], run[1][:, pad:, :], counts[:], ALU.subtract))
                then(dve.tensor_tensor(rank[:].rearrange("p t e -> p (t e)"), rank[:].rearrange("p t e -> p (t e)"),
                                       ps[:, 4, 0:NT * EXPERTS], ALU.add))
                then(dve.scalar_tensor_tensor(out=slot_of[:], in0=base[:, None, :].to_broadcast([P, NT, EXPERTS]),
                                              scalar=float(P), in1=rank[:], op0=ALU.mult, op1=ALU.add))
                for k in range(CHOSEN):
                    steps.add(dve.tensor_tensor(picked[:, k], chosen[:, k], slot_of[:], ALU.mult))
                steps.wait(dve)
                then(dve.tensor_reduce(slot_f[:], picked[:], AX, ALU.add))
                flat_slot = slot_f[:].rearrange("p k t -> p (k t)")
                steps.add(dve.tensor_copy(routes.slot[:].rearrange("p k t -> p (k t)"), flat_slot))
                then(dve.tensor_copy(slot_i[:, 0, :], flat_slot))
                steps.add(dve.tensor_scalar(slot_i[:, 1, :], slot_i[:, 0, :], 7, None, ALU.logical_shift_right))
                then(dve.tensor_scalar(slot_i[:, 2, :], slot_i[:, 0, :], P - 1, None, ALU.bitwise_and))
                then(dve.tensor_copy(place_f[:], slot_i[:, 1:3, :]))
                n = CHOSEN * NT
                for m in range(n):
                    steps.add(dve.tensor_scalar(at_row[:, m, :], keep.iota[:], place_f[:, 1, m:m + 1], None, ALU.is_equal))
                then(dve.tensor_tensor(is_tile[:], keep.iota[:, None, 0:TILES].to_broadcast([P, n, TILES]),
                                       place_f[:, 0, :, None].to_broadcast([P, n, TILES]), ALU.is_equal))
                for k in range(CHOSEN):
                    half = slice(k * NT, (k + 1) * NT)
                    ins = steps.add(dve.tensor_tensor(at_tile[:, half, :], is_tile[:, half, :],
                                                      keep.token[:, :, None].to_broadcast([P, NT, TILES]), ALU.mult))
                steps.wait(dve)
                dve.engine_nop().then_inc(sem["order_ready"], 1)
                then(dve.tensor_tensor(past[:], keep.iota[:, 0:TILES, None].to_broadcast([P, TILES, EXPERTS - 1]),
                                       ends[1][:, None, pad:pad + EXPERTS - 1].to_broadcast([P, TILES, EXPERTS - 1]),
                                       ALU.is_ge))
                then(dve.tensor_reduce(expert_f[:], past[:], AX, ALU.add))
                steps.add(dve.tensor_copy(routes.expert_of[:], expert_f[:]))
                dve.wait_ge(sem["order_made"], 1)
                steps.add(dve.tensor_copy(routes.token_of[:], ps[:, 5, 0:TILES]))


def pairs_of_tiles(engine, first, last, step):
    pairs = (last - first + 1) // 2
    with engine.Fori(0, pairs) as i:
        for u in range(2):
            step(first + 2 * i + u, (first + u) % 2)
    for j in range(first + 2 * pairs, last + 1):
        step(j, j % 2)


def expert_index(engine, routes, j):
    return engine.value_load(routes.expert_of[0:1, bass.ds(j, 1)], min_val=0, max_val=EXPERTS - 1)


def gather_tiles(pool, keep, sem, routes, slots):
    for j in range(TILES):
        u = j % 2
        if j >= 2:
            pool.wait_ge(sem["turned"], j - 1)
            pool.wait_ge(keep.gathered[u], routes.gathers_before[u] + 16 * (j // 2))
        pool.indirect_dma_start(slots[:, u, :], None, routes.tokens,
                                bass.IndirectOffsetOnAxis(ap=routes.token_of[:, j:j + 1], axis=0))\
            .then_inc(keep.gathered[u], 16)


def store_results(sp, sem, routes, results):
    def step(j, u):
        sp.wait_ge(sem["result_kept"], j + 1)
        sp.dma_start(routes.results[bass.ds(j * P, P), :], results[:, u, :]).then_inc(sem["stored"][u], 16)

    step(0, 0)
    pairs_of_tiles(sp, 1, TILES - 1, step)
    sp.wait_ge(sem["stored"][0], 16 * ((TILES + 1) // 2))
    sp.wait_ge(sem["stored"][1], 16 * (TILES // 2))


def gelu_experts(nc, keep, name, routes, w1, w2, w3, b1, b2, b3):
    hidden = w1.shape[2]
    chunks = hidden // P
    with Scope(nc, name) as s:
        slots, slots_t = s.sb("slots", [P, 2, D]), s.sb("slots_t", [P, 2, P])
        rows1, rows2 = s.sb("rows1", [P, 2, hidden]), s.sb("rows2", [P, 2, hidden])
        act1, act2 = s.sb("act1", [P, 2, chunks, P]), s.sb("act2", [P, 2, chunks, P])
        results = s.sb("results", [P, 2, D])
        ps = s.psum("ps", [P, 6, 512])
        ps_x, ps_1, ps_1t, ps_2, ps_2t, ps_y = (ps[:, n] for n in range(6))
        names = ["turned", "slots_kept", "rows1_made", "rows1_kept", "rows1_turned", "act1_done", "rows2_made",
                 "rows2_kept", "rows2_turned", "act2_done", "result_made", "result_kept"]
        sem = {n: s.sem(n) for n in names}
        sem["stored"] = [s.sem("stored0"), s.sem("stored1")]
        with s.block() as block:

            @block.gpsimd
            def _(pool):
                gather_tiles(pool, keep, sem, routes, slots)

            @block.sync
            def _(sp):
                store_results(sp, sem, routes, results)

            @block.tensor
            def _(pe):
                def turn_slots(j, u, half, first=False):
                    pe.wait_ge(keep.gathered[u], 16 * (half + 1) + routes.gathers_before[u])
                    if not first:
                        pe.wait_ge(sem["slots_kept"], j)
                    pe.transpose(ps_x[:, 0:P], slots[:, u, :], keep.identity[:]).then_inc(sem["turned"], 1)

                def layer1(j, u, first=False):
                    e = expert_index(pe, routes, j)
                    pe.wait_ge(sem["slots_kept"], j + 1)
                    if not first:
                        pe.wait_ge(sem["rows1_kept"], j)
                    pe.matmul(ps_1, slots_t[:, u, :], w1[:, bass.ds(e, 1), :].rearrange("d a h -> d (a h)"),
                              start=True, stop=True).then_inc(sem["rows1_made"], 1)

                def turn1(j, u, first=False):
                    pe.wait_ge(sem["rows1_kept"], j + 1)
                    if not first:
                        pe.wait_ge(sem["act1_done"], chunks * j)
                    for c in range(chunks):
                        mm = pe.transpose(ps_1t[:, c * P:(c + 1) * P], rows1[:, u, c * P:(c + 1) * P], keep.identity[:])
                    mm.then_inc(sem["rows1_turned"], 1)

                def layer2(j, u, first=False):
                    e = expert_index(pe, routes, j)
                    pe.wait_ge(sem["act1_done"], chunks * (j + 1))
                    if not first:
                        pe.wait_ge(sem["rows2_kept"], j)
                    for c in range(chunks):
                        mm = pe.matmul(ps_2, act1[:, u, c, :],
                                       w2[:, bass.ds(e, 1), c, :].rearrange("d a h -> d (a h)"),
                                       start=(c == 0), stop=(c == chunks - 1))
                    mm.then_inc(sem["rows2_made"], 1)

                def turn2(j, u, first=False):
                    pe.wait_ge(sem["rows2_kept"], j + 1)
                    if not first:
                        pe.wait_ge(sem["act2_done"], chunks * j)
                    for c in range(chunks):
                        mm = pe.transpose(ps_2t[:, c * P:(c + 1) * P], rows2[:, u, c * P:(c + 1) * P], keep.identity[:])
                    mm.then_inc(sem["rows2_turned"], 1)

                def layer3(j, u, first=False):
                    e = expert_index(pe, routes, j)
                    pe.wait_ge(sem["act2_done"], chunks * (j + 1))
                    if not first:
                        pe.wait_ge(sem["result_kept"], j)
                    for c in range(chunks):
                        mm = pe.matmul(ps_y[:, 0:D], act2[:, u, c, :],
                                       w3[:, bass.ds(e, 1), c, :].rearrange("d a h -> d (a h)"),
                                       start=(c == 0), stop=(c == chunks - 1))
                    mm.then_inc(sem["result_made"], 1)

                turn_slots(0, 0, 0, True)
                layer1(0, 0, True)
                turn_slots(1, 1, 0)
                turn1(0, 0, True)
                layer1(1, 1)
                layer2(0, 0, True)
                turn1(1, 1)
                turn_slots(2, 0, 1)
                turn2(0, 0, True)

                def steady(i):
                    for u in range(2):
                        j = 1 + 2 * i + u
                        layer1(j + 1, u)
                        layer2(j, 1 - u)
                        turn1(j + 1, u)
                        turn_slots(j + 2, 1 - u, i + 1 + u)
                        layer3(j - 1, u, False) if not isinstance(j, int) else layer3(j - 1, u, j == 1)
                        turn2(j, 1 - u)

                steady(0)
                with pe.Fori(1, (TILES - 3) // 2) as i:
                    steady(i)
                j = TILES - 2
                layer1(j + 1, 0)
                layer2(j, 1)
                turn1(j + 1, 0)
                layer3(j - 1, 0)
                turn2(j, 1)
                layer2(j + 1, 0)
                layer3(j, 1)
                turn2(j + 1, 0)
                layer3(j + 1, 0)

            @block.scalar
            def _(act):
                def gelu(j, u, rows_turned, read, source, to, bias, done, first):
                    e = expert_index(act, routes, j)
                    act.wait_ge(rows_turned, j + 1)
                    if not first:
                        act.wait_ge(read, j - 1)
                    for c in range(chunks):
                        act.activation(to[:, u, c, :], source[:, c * P:(c + 1) * P], ACT.Gelu,
                                       bias=bias[:, bass.ds(e * chunks + c, 1)]).then_inc(done, 1)

                def gelu1(j, u, first=False):
                    gelu(j, u, sem["rows1_turned"], sem["rows2_made"], ps_1t, act1, b1, sem["act1_done"], first)

                def gelu2(j, u, first=False):
                    gelu(j, u, sem["rows2_turned"], sem["result_made"], ps_2t, act2, b2, sem["act2_done"], first)

                gelu1(0, 0, True)
                gelu1(1, 1, True)
                gelu2(0, 0, True)
                gelu1(2, 0)
                gelu2(1, 1, True)

                def step(j, u):
                    gelu1(j + 1, 1 - u)
                    gelu2(j, u)

                with act.Fori(0, (TILES - 3) // 2) as i:
                    step(2 + 2 * i, 0)
                    step(3 + 2 * i, 1)
                gelu2(TILES - 1, (TILES - 1) % 2)

            @block.vector
            def _(dve):
                def keep_slots(j, u, first=False):
                    dve.wait_ge(sem["turned"], j + 1)
                    if not first:
                        dve.wait_ge(sem["rows1_made"], j - 1)
                    dve.tensor_copy(slots_t[:, u, :], ps_x[:, 0:P]).then_inc(sem["slots_kept"], 1)

                def keep1(j, u, first=False):
                    dve.wait_ge(sem["rows1_made"], j + 1)
                    if not first:
                        dve.wait_ge(sem["rows1_turned"], j - 1)
                    dve.tensor_copy(rows1[:, u, :], ps_1).then_inc(sem["rows1_kept"], 1)

                def keep2(j, u, first=False):
                    dve.wait_ge(sem["rows2_made"], j + 1)
                    if not first:
                        dve.wait_ge(sem["rows2_turned"], j - 1)
                    dve.tensor_copy(rows2[:, u, :], ps_2).then_inc(sem["rows2_kept"], 1)

                def keep_result(j, u, half, first=False):
                    e = expert_index(dve, routes, j)
                    dve.wait_ge(sem["result_made"], j + 1)
                    if not first:
                        dve.wait_ge(sem["stored"][u], 16 * half)
                    dve.tensor_tensor(results[:, u, :], ps_y[:, 0:D],
                                      b3[:, bass.ds(e, 1), :].rearrange("p a d -> p (a d)"), ALU.add)\
                        .then_inc(sem["result_kept"], 1)

                keep_slots(0, 0, True)
                keep1(0, 0, True)
                keep_slots(1, 1, True)
                keep1(1, 1, True)
                keep2(0, 0, True)
                keep_slots(2, 0)

                def steady(i, first):
                    for u in range(2):
                        j = 1 + 2 * i + u
                        keep1(j + 1, u)
                        keep2(j, 1 - u, first and u == 0)
                        keep_slots(j + 2, 1 - u)
                        keep_result(j - 1, u, i, first)

                steady(0, True)
                with dve.Fori(1, (TILES - 3) // 2) as i:
                    steady(i, False)
                j = TILES - 2
                keep1(j + 1, 0)
                keep2(j, 1)
                keep_result(j - 1, 0, (j - 1) // 2)
                keep2(j + 1, 0)
                keep_result(j, 1, j // 2)
                keep_result(j + 1, 0, (j + 1) // 2)


def gated_experts(nc, keep, name, routes, w_in, w_out):
    width = w_in.shape[2] // 2
    chunks = width // P
    banks = 2 * width // 512
    with Scope(nc, name) as s:
        slots, slots_t = s.sb("slots", [P, 2, D]), s.sb("slots_t", [P, 2, P])
        gated, gated_t = s.sb("gated", [P, 2, width]), s.sb("gated_t", [P, 2, chunks, P])
        results = s.sb("results", [P, 2, D])
        ps_in = s.psum("ps_in", [P, 2, 512])
        ps_x, ps_t, ps_y = s.psum("ps_x", [P, 512]), s.psum("ps_t", [P, 512]), s.psum("ps_y", [P, 512])
        names = ["turned", "slots_kept", "in_made", "silu_done", "gated_ready", "gated_turned", "gated_kept",
                 "result_made", "result_kept"]
        sem = {n: s.sem(n) for n in names}
        sem["stored"] = [s.sem("stored0"), s.sem("stored1")]
        flat_in = ps_in[:].rearrange("p b n -> p (b n)")
        def gate_part(u):
            return flat_in[:, 0:width] if banks == 2 else flat_in[:, 512 * u:512 * u + width]

        def up_part(u):
            return flat_in[:, width:2 * width] if banks == 2 else flat_in[:, 512 * u + width:512 * u + 2 * width]

        lag = 0 if banks == 2 else 1
        with s.block() as block:

            @block.gpsimd
            def _(pool):
                gather_tiles(pool, keep, sem, routes, slots)

            @block.sync
            def _(sp):
                store_results(sp, sem, routes, results)

            @block.tensor
            def _(pe):
                def turn_slots(j, u, half, first=False):
                    pe.wait_ge(keep.gathered[u], 16 * (half + 1) + routes.gathers_before[u])
                    if not first:
                        pe.wait_ge(sem["slots_kept"], j)
                    pe.transpose(ps_x[:, 0:P], slots[:, u, :], keep.identity[:]).then_inc(sem["turned"], 1)

                def up(j, u, first=False):
                    e = expert_index(pe, routes, j)
                    pe.wait_ge(sem["slots_kept"], j + 1)
                    if not first:
                        pe.wait_ge(sem["gated_ready"], j - lag)
                    for n in range(banks):
                        bank = n if banks == 2 else u
                        mm = pe.matmul(ps_in[:, bank], slots_t[:, u, :],
                                       w_in[:, bass.ds(e, 1), 512 * n:512 * n + 512].rearrange("d a h -> d (a h)"),
                                       start=True, stop=True)
                    mm.then_inc(sem["in_made"], 1)

                def turn(j, u, first=False):
                    pe.wait_ge(sem["gated_ready"], j + 1)
                    if not first:
                        pe.wait_ge(sem["gated_kept"], j)
                    for c in range(chunks):
                        mm = pe.transpose(ps_t[:, c * P:(c + 1) * P], gated[:, u, c * P:(c + 1) * P], keep.identity[:])
                    mm.then_inc(sem["gated_turned"], 1)

                def down(j, u, first=False):
                    e = expert_index(pe, routes, j)
                    pe.wait_ge(sem["gated_kept"], j + 1)
                    if not first:
                        pe.wait_ge(sem["result_kept"], j)
                    for c in range(chunks):
                        mm = pe.matmul(ps_y[:, 0:D], gated_t[:, u, c, :],
                                       w_out[:, bass.ds(e, 1), c, :].rearrange("d a h -> d (a h)"),
                                       start=(c == 0), stop=(c == chunks - 1))
                    mm.then_inc(sem["result_made"], 1)

                turn_slots(0, 0, 0, True)
                up(0, 0, True)
                turn_slots(1, 1, 0)
                up(1, 1, lag == 1)
                turn(0, 0, True)
                turn_slots(2, 0, 1)

                def steady(i, first):
                    for u in range(2):
                        j = 1 + 2 * i + u
                        up(j + 1, u)
                        down(j - 1, u, first and u == 0)
                        turn(j, 1 - u)
                        turn_slots(j + 2, 1 - u, i + 1 + u)

                steady(0, True)
                with pe.Fori(1, (TILES - 3) // 2) as i:
                    steady(i, False)
                j = TILES - 2
                up(j + 1, 0)
                down(j - 1, 0)
                turn(j, 1)
                down(j, 1)
                turn(j + 1, 0)
                down(j + 1, 0)

            @block.scalar
            def _(act):
                def silu(j, u, first=False):
                    act.wait_ge(sem["in_made"], j + 1)
                    if not first:
                        act.wait_ge(sem["gated_turned"], j - 1)
                    act.activation(gated[:, u, :], gate_part(u), ACT.Silu).then_inc(sem["silu_done"], 1)

                def keep_gated(j, u, first=False):
                    act.wait_ge(sem["gated_turned"], j + 1)
                    if not first:
                        act.wait_ge(sem["result_made"], j - 1)
                    act.activation(gated_t[:, u, :, :].rearrange("p c k -> p (c k)"), ps_t[:, 0:width], ACT.Copy)\
                        .then_inc(sem["gated_kept"], 1)

                silu(0, 0, True)
                silu(1, 1, True)
                keep_gated(0, 0, True)
                silu(2, 0)
                keep_gated(1, 1, True)
                with act.Fori(0, (TILES - 3) // 2) as i:
                    for u in range(2):
                        silu(3 + 2 * i + u, 1 - u)
                        keep_gated(2 + 2 * i + u, u)
                keep_gated(TILES - 1, 0)

            @block.vector
            def _(dve):
                def keep_slots(j, u, first=False):
                    dve.wait_ge(sem["turned"], j + 1)
                    if not first:
                        dve.wait_ge(sem["in_made"], j - 1)
                    dve.tensor_copy(slots_t[:, u, :], ps_x[:, 0:P]).then_inc(sem["slots_kept"], 1)

                def multiply(j, u):
                    dve.wait_ge(sem["silu_done"], j + 1)
                    dve.tensor_tensor(gated[:, u, :], gated[:, u, :], up_part(u), ALU.mult)\
                        .then_inc(sem["gated_ready"], 1)

                def keep_result(j, u, half, first=False):
                    dve.wait_ge(sem["result_made"], j + 1)
                    if not first:
                        dve.wait_ge(sem["stored"][u], 16 * half)
                    dve.tensor_copy(results[:, u, :], ps_y[:, 0:D]).then_inc(sem["result_kept"], 1)

                keep_slots(0, 0, True)
                keep_slots(1, 1, True)
                multiply(0, 0)
                multiply(1, 1)
                keep_slots(2, 0)

                def steady(i, first):
                    for u in range(2):
                        j = 1 + 2 * i + u
                        multiply(j + 1, u)
                        keep_result(j - 1, u, i, first)
                        keep_slots(j + 2, 1 - u)

                steady(0, True)
                with dve.Fori(1, (TILES - 3) // 2) as i:
                    steady(i, False)
                j = TILES - 2
                multiply(j + 1, 0)
                keep_result(j - 1, 0, (j - 1) // 2)
                keep_result(j, 1, j // 2)
                keep_result(j + 1, 0, (j + 1) // 2)


def combine(nc, keep, name, routes):
    with Scope(nc, name) as s:
        mine = s.sb("mine", [P, CHOSEN, NT, D])
        got = keep.got
        added = s.sem("added")
        with s.block() as block:

            @block.gpsimd
            def _(pool):
                for t in range(NT):
                    for k in range(CHOSEN):
                        pool.indirect_dma_start(mine[:, k, t, :], None, routes.results,
                                                bass.IndirectOffsetOnAxis(ap=routes.slot[:, k, t:t + 1], axis=0))\
                            .then_inc(got[CHOSEN * t + k], 16)

            @block.vector
            def _(dve):
                for t in range(NT):
                    for k in range(CHOSEN):
                        dve.wait_ge(got[CHOSEN * t + k], 16 * (routes.before + 1))
                        if k:
                            dve.wait_ge(added, CHOSEN * t + k)
                        dve.scalar_tensor_tensor(out=keep.x[:, t, :], in0=mine[:, k, t, :],
                                                 scalar=routes.weight[:, k, t:t + 1], in1=keep.x[:, t, :],
                                                 op0=ALU.mult, op1=ALU.add).then_inc(added, 1)



def turn_gated_weights(nc, a, keep, name, gate_up, down, w_in, w_out):
    width = down.shape[2]
    jobs = []
    for e in range(EXPERTS):
        for n in range(2 * width // 512):
            jobs.append((gate_up[:, e, 4 * n:4 * n + 4, :], w_in[:, e, 512 * n:512 * n + 512]))
        jobs.append((down[:, e, :].rearrange("o (c k) -> o c k", k=P), w_out[:, e, :, :].rearrange("k c o -> k (c o)")))
    with Scope(nc, name) as s:
        ps = s.psum("ps", [P, 4, 512])
        turned, kept_act, kept_dve = s.sem("turned"), s.sem("kept_act"), s.sem("kept_dve")
        with s.block() as block:

            @block.tensor
            def _(pe):
                for e, n in enumerate(keep.raw_loaded):
                    pe.wait_ge(n, 16)
                for m, (source, _) in enumerate(jobs):
                    if m >= 4:
                        pe.wait_ge(kept_dve if m % 2 else kept_act, m // 2 - 1)
                    for c in range(4):
                        mm = pe.transpose(ps[:, m % 4, c * P:(c + 1) * P], source[:, c, :], keep.identity[:])
                    mm.then_inc(turned, 1)

            @block.scalar
            def _(act):
                for m in range(0, len(jobs), 2):
                    act.wait_ge(turned, m + 1)
                    act.activation(jobs[m][1], ps[:, m % 4, :], ACT.Copy).then_inc(kept_act, 1)

            @block.vector
            def _(dve):
                for m in range(1, len(jobs), 2):
                    dve.wait_ge(turned, m + 1)
                    dve.tensor_copy(jobs[m][1], ps[:, m % 4, :]).then_inc(kept_dve, 1)



TAPS = 9


def conv_kernels(nc, a, keep, name, taps):
    heads, wide, inner = 16, 2 * D, 64
    with Scope(nc, name) as s:
        hist_w = s.sb("hist_w", [P, wide])
        hist_rows = s.sb("hist_rows", [P, 3, wide])
        ctx_w1, ctx_b1 = s.sb("ctx_w1", [P, 2, inner]), s.sb("ctx_b1", [inner, 1])
        ctx_w2, ctx_b2 = s.sb("ctx_w2", [inner, 1]), s.sb("ctx_b2", [1, 1])
        kg_w1, kg_rows = s.sb("kg_w1", [P, 2, D]), s.sb("kg_rows", [B, 3, D])
        kg_w2, kg_b2 = s.sb("kg_w2", [P, heads * TAPS]), s.sb("kg_b2", [B, heads * TAPS])
        eh, eh_t = s.sb("eh", [P, 2, wide]), s.sb("eh_t", [P, 2, 2, P])
        stats, moments, rstd = s.sb("stats", [P, 2, 6]), s.sb("moments", [P, 2, 2]), s.sb("rstd", [P, 2, 1])
        inner_act, one = s.sb("inner_act", [inner, B * C]), s.sb("one", [1, 1])
        aw, aw_top, aw_sum = s.sb("aw", [1, B, C]), s.sb("aw_top", [1, B]), s.sb("aw_sum", [1, B])
        aw_cols, cc_t = s.sb("aw_cols", [P, 2, 2]), s.sb("cc_t", [P, 2, B])
        kp, kp_stats, kp_moments = s.sb("kp", [B, D]), s.sb("kp_stats", [B, 6]), s.sb("kp_moments", [B, 2])
        kp_rstd, kp_t = s.sb("kp_rstd", [B, 1]), s.sb("kp_t", [P, B])
        kernels = s.sb("kernels", [B, heads, TAPS])
        k_top, k_sum = s.sb("k_top", [B, heads]), s.sb("k_sum", [B, heads])
        ps = s.psum("ps", [P, 8, 512])
        ones = s.sb("ones", [P, 2])
        names = ["hist_loaded", "ctx_loaded", "kg_loaded", "hist_made", "eh_steps", "var_ready", "rstd_ready", "gelu_in",
                 "eh_ready", "eh_turned", "eh_kept", "inner_made", "inner_ready", "aw_made", "aw_steps", "aw_centred",
                 "aw_exp", "aw_ready", "ones_set", "cols_made", "cols_ready", "cc_made", "cc_ready", "kp_made",
                 "kp_steps", "kp_var", "kp_rstd_ready", "kp_gelu_in", "kp_ready", "kp_turned", "kp_kept", "k_made",
                 "k_centred", "k_exp", "k_ready", "taps_made", "taps_ready"]
        sem = {n: s.sem(n) for n in names}

        def rows_of(v, rows, n):
            return row(a[v]).to_broadcast([rows, n])

        with s.block() as block:

            @block.sync
            def _(sp):
                sp.dma_start(hist_w[:], a["L3_xattn_hist_W"]).then_inc(sem["hist_loaded"], 16)
                for n, v in enumerate(("hist_b", "hist_ln_g", "hist_ln_b")):
                    sp.dma_start(hist_rows[:, n, :], rows_of("L3_xattn_" + v, P, wide)).then_inc(sem["hist_loaded"], 16)
                sp.dma_start(ctx_w1[:], a["L3_xattn_ctx_W1"].rearrange("(c d) n -> d c n", d=P))\
                    .then_inc(sem["ctx_loaded"], 16)
                sp.dma_start(ctx_b1[:], a["L3_xattn_ctx_b1"].rearrange("(p c) -> p c", c=1)).then_inc(sem["ctx_loaded"], 16)
                sp.dma_start(ctx_w2[:], a["L3_xattn_ctx_W2"]).then_inc(sem["ctx_loaded"], 16)
                sp.dma_start(ctx_b2[:], row(a["L3_xattn_ctx_b2"])).then_inc(sem["ctx_loaded"], 16)
                sp.dma_start(kg_w1[:], a["L3_xattn_kg_W1"].rearrange("(c d) n -> d c n", d=P)).then_inc(sem["kg_loaded"], 16)
                for n, v in enumerate(("kg_b1", "kg_ln_g", "kg_ln_b")):
                    sp.dma_start(kg_rows[:, n, :], rows_of("L3_xattn_" + v, B, D)).then_inc(sem["kg_loaded"], 16)
                sp.dma_start(kg_w2[:], a["L3_xattn_kg_W2"]).then_inc(sem["kg_loaded"], 16)
                sp.dma_start(kg_b2[:], rows_of("L3_xattn_kg_b2", B, heads * TAPS)).then_inc(sem["kg_loaded"], 16)

            @block.gpsimd
            def _(pool):
                pool.memset(one[:], 1.0).then_inc(sem["ones_set"], 1)
                pool.memset(ones[:], 0.0).then_inc(sem["ones_set"], 1)
                pool.wait_ge(sem["ones_set"], 2)
                pool.memset(ones[0:C, 0:1], 1.0).then_inc(sem["ones_set"], 1)
                pool.memset(ones[C:P, 1:2], 1.0).then_inc(sem["ones_set"], 1)
                pool.wait_ge(sem["ones_set"], 4)
                pool.wait_ge(sem["var_ready"], 1)
                pool.tensor_tensor(rstd[:, :, 0], rstd[:, :, 0], keep.neg_half[:, 0:2], ALU.pow)\
                    .then_inc(sem["rstd_ready"], 1)
                pool.wait_ge(sem["kp_var"], 1)
                pool.tensor_tensor(kp_rstd[:], kp_rstd[:], keep.neg_half[0:B, 0:1], ALU.pow)\
                    .then_inc(sem["kp_rstd_ready"], 1)

            @block.tensor
            def _(pe):
                pe.wait_ge(sem["hist_loaded"], 64)
                for u in range(2):
                    mm = pe.matmul(ps[:, 0, u * wide:(u + 1) * wide], keep.ctx_t[:, u * P:(u + 1) * P], hist_w[:],
                                   start=True, stop=True)
                mm.then_inc(sem["hist_made"], 1)
                pe.wait_ge(sem["eh_ready"], 1)
                for c in range(2):
                    for u in range(2):
                        mm = pe.transpose(ps[:, 1, (2 * c + u) * P:(2 * c + u + 1) * P], eh[:, u, c * P:(c + 1) * P],
                                          keep.identity[:])
                mm.then_inc(sem["eh_turned"], 1)
                pe.wait_ge(sem["eh_kept"], 1)
                pe.wait_ge(sem["ctx_loaded"], 64)
                for c in range(2):
                    mm = pe.matmul(ps[0:inner, 2, 0:B * C], ctx_w1[:, c, :], eh_t[:, c].rearrange("p u k -> p (u k)"),
                                   start=(c == 0), stop=(c == 1))
                mm.then_inc(sem["inner_made"], 1)
                pe.wait_ge(sem["inner_ready"], 1)
                pe.matmul(ps[0:1, 3, 0:B * C], ctx_w2[:], inner_act[:], start=True, stop=True).then_inc(sem["aw_made"], 1)
                pe.wait_ge(sem["aw_ready"], 1)
                for u in range(2):
                    mm = pe.matmul(ps[:, 4, u:u + 1], aw[:, 2 * u:2 * u + 2, :].rearrange("p b k -> p (b k)"), one[:],
                                   start=True, stop=True)
                mm.then_inc(sem["cols_made"], 1)
                pe.wait_ge(sem["cols_ready"], 2)
                for c in range(2):
                    for u in range(2):
                        mm = pe.matmul(ps[:, 5, c * B + 2 * u:c * B + 2 * u + 2], eh[:, u, c * P:(c + 1) * P],
                                       aw_cols[:, u, :], start=True, stop=True)
                mm.then_inc(sem["cc_made"], 1)
                pe.wait_ge(sem["cc_ready"], 1)
                pe.wait_ge(sem["kg_loaded"], 96)
                for c in range(2):
                    mm = pe.matmul(ps[0:B, 6, 0:D], cc_t[:, c, :], kg_w1[:, c, :], start=(c == 0), stop=(c == 1))
                mm.then_inc(sem["kp_made"], 1)
                pe.wait_ge(sem["kp_ready"], 1)
                pe.transpose(ps[:, 7, 0:B], kp[:], keep.identity[0:B, 0:B]).then_inc(sem["kp_turned"], 1)
                pe.wait_ge(sem["kp_kept"], 1)
                pe.matmul(ps[0:B, 0, 0:heads * TAPS], kp_t[:], kg_w2[:], start=True, stop=True).then_inc(sem["k_made"], 1)
                pe.wait_ge(sem["k_ready"], 1)
                for b in range(B):
                    mm = pe.matmul(ps[:, 1 + b // 2, (b % 2) * 256:(b % 2) * 256 + heads * TAPS],
                                   keep.identity[0:B, b:b + 1].to_broadcast([B, P]),
                                   kernels[:].rearrange("b h n -> b (h n)"), start=True, stop=True)
                mm.then_inc(sem["taps_made"], 1)

            @block.scalar
            def _(act):
                act.wait_ge(sem["gelu_in"], 1)
                act.activation(eh[:], eh[:], ACT.Gelu).then_inc(sem["eh_ready"], 1)
                act.wait_ge(sem["inner_made"], 1)
                act.wait_ge(sem["ctx_loaded"], 64)
                act.activation(inner_act[:], ps[0:inner, 2, 0:B * C], ACT.Gelu, bias=ctx_b1[:, 0:1])\
                    .then_inc(sem["inner_ready"], 1)
                act.wait_ge(sem["aw_centred"], 1)
                act.activation(aw[:], aw[:], ACT.Exp).then_inc(sem["aw_exp"], 1)
                act.wait_ge(sem["kp_gelu_in"], 1)
                act.activation(kp[:], kp[:], ACT.Gelu).then_inc(sem["kp_ready"], 1)
                act.wait_ge(sem["k_centred"], 1)
                act.activation(kernels[:], kernels[:], ACT.Exp).then_inc(sem["k_exp"], 1)

            @block.vector
            def _(dve):
                steps = Tally(sem["eh_steps"])

                def then(instruction):
                    steps.add(instruction)
                    steps.wait(dve)

                dve.wait_ge(sem["hist_made"], 1)
                then(dve.tensor_tensor(eh[:], ps[:, 0, :].rearrange("p (u n) -> p u n", u=2),
                                       hist_rows[:, 0:1, :].to_broadcast([P, 2, wide]), ALU.add))
                for u in range(2):
                    steps.add(dve.bn_stats(stats[:, u, :], eh[:, u, :]))
                steps.wait(dve)
                for u in range(2):
                    steps.add(dve.bn_aggr(moments[:, u, :], stats[:, u, :]))
                steps.wait(dve)
                dve.tensor_scalar(rstd[:, :, 0], moments[:, :, 1], EPS, None, ALU.add).then_inc(sem["var_ready"], 1)
                dve.wait_ge(sem["rstd_ready"], 1)
                for u in range(2):
                    steps.add(dve.tensor_scalar(eh[:, u, :], eh[:, u, :], moments[:, u, 0:1], rstd[:, u, :],
                                                ALU.subtract, ALU.mult))
                steps.wait(dve)
                then(dve.tensor_tensor(eh[:], eh[:], hist_rows[:, 1:2, :].to_broadcast([P, 2, wide]), ALU.mult))
                dve.tensor_tensor(eh[:], eh[:], hist_rows[:, 2:3, :].to_broadcast([P, 2, wide]), ALU.add)\
                    .then_inc(sem["gelu_in"], 1)
                dve.wait_ge(sem["eh_turned"], 1)
                dve.tensor_copy(eh_t[:].rearrange("p c u k -> p (c u k)"), ps[:, 1, :]).then_inc(sem["eh_kept"], 1)
                dve.wait_ge(sem["aw_made"], 1)
                then(dve.tensor_scalar(aw[:].rearrange("p b k -> p (b k)"), ps[0:1, 3, 0:B * C], ctx_b2[:, 0:1], None,
                                       ALU.add))
                then(dve.tensor_reduce(aw_top[:], aw[:], AX, ALU.max))
                dve.tensor_tensor(aw[:], aw[:], aw_top[:, :, None].to_broadcast([1, B, C]), ALU.subtract)\
                    .then_inc(sem["aw_centred"], 1)
                dve.wait_ge(sem["aw_exp"], 1)
                then(dve.tensor_reduce(aw_sum[:], aw[:], AX, ALU.add))
                then(dve.reciprocal(aw_top[:], aw_sum[:]))
                dve.tensor_tensor(aw[:], aw[:], aw_top[:, :, None].to_broadcast([1, B, C]), ALU.mult)\
                    .then_inc(sem["aw_ready"], 1)
                dve.wait_ge(sem["cols_made"], 1)
                dve.wait_ge(sem["ones_set"], 4)
                for u in range(2):
                    dve.tensor_scalar(aw_cols[:, u, :], ones[:], ps[:, 4, u:u + 1], None, ALU.mult)\
                        .then_inc(sem["cols_ready"], 1)
                dve.wait_ge(sem["cc_made"], 1)
                dve.tensor_copy(cc_t[:].rearrange("p c b -> p (c b)"), ps[:, 5, 0:2 * B]).then_inc(sem["cc_ready"], 1)
                dve.wait_ge(sem["kp_made"], 1)
                dve.wait_ge(sem["kg_loaded"], 96)
                then(dve.tensor_tensor(kp[:], ps[0:B, 6, 0:D], kg_rows[:, 0, :], ALU.add))
                then(dve.bn_stats(kp_stats[:], kp[:]))
                then(dve.bn_aggr(kp_moments[:], kp_stats[:]))
                dve.tensor_scalar(kp_rstd[:], kp_moments[:, 1:2], EPS, None, ALU.add).then_inc(sem["kp_var"], 1)
                dve.wait_ge(sem["kp_rstd_ready"], 1)
                then(dve.tensor_scalar(kp[:], kp[:], kp_moments[:, 0:1], kp_rstd[:, 0:1], ALU.subtract, ALU.mult))
                then(dve.tensor_tensor(kp[:], kp[:], kg_rows[:, 1, :], ALU.mult))
                dve.tensor_tensor(kp[:], kp[:], kg_rows[:, 2, :], ALU.add).then_inc(sem["kp_gelu_in"], 1)
                dve.wait_ge(sem["kp_turned"], 1)
                dve.tensor_copy(kp_t[:], ps[:, 7, 0:B]).then_inc(sem["kp_kept"], 1)
                dve.wait_ge(sem["k_made"], 1)
                flat = kernels[:].rearrange("b h n -> b (h n)")
                then(dve.tensor_tensor(flat, ps[0:B, 0, 0:heads * TAPS], kg_b2[:], ALU.add))
                then(dve.tensor_reduce(k_top[:], kernels[:], AX, ALU.max))
                dve.tensor_tensor(kernels[:], kernels[:], k_top[:, :, None].to_broadcast([B, heads, TAPS]),
                                  ALU.subtract).then_inc(sem["k_centred"], 1)
                dve.wait_ge(sem["k_exp"], 1)
                then(dve.tensor_reduce(k_sum[:], kernels[:], AX, ALU.add))
                then(dve.reciprocal(k_top[:], k_sum[:]))
                dve.tensor_tensor(kernels[:], kernels[:], k_top[:, :, None].to_broadcast([B, heads, TAPS]), ALU.mult)\
                    .then_inc(sem["k_ready"], 1)
                dve.wait_ge(sem["taps_made"], 1)
                for n in range(2):
                    dve.tensor_copy(taps[:, 2 * n:2 * n + 2, :, :].rearrange("p b h n -> p b (h n)"),
                                    ps[:, 1 + n, :].rearrange("p (b n) -> p b n", b=2)[:, :, 0:heads * TAPS])\
                        .then_inc(sem["taps_ready"], 1)


def conv_attention_any_mask(nc, a, keep, name, taps, gate):
    heads, wide = 16, 8
    scale = float(wide) ** -0.5
    with Scope(nc, name) as s:
        ps = s.psum("ps", [P, 8, 512])
        norm = Normed(s, keep, ps[:, 0], ps[:, 1])
        wq, wk, wv, proj = (s.sb(n, [P, D]) for n in ("wq", "wk", "wv", "proj"))
        proj_rows, head_mask = s.sb("proj_rows", [P, D]), s.sb("head_mask", [P, heads])
        mask_u8, masked, open_ = s.sb("mask_u8", [P, 2, S], U8), s.sb("masked", [P, 2, S]), s.sb("open", [P, 2, S])
        bands, edge = s.sb("bands", [P, 3, P]), s.sb("edge", [P, 2, P])
        q_t, k_t, v = s.sb("q_t", [P, S]), s.sb("k_t", [P, S]), s.sb("v", [P, 2, D])
        k_spread = s.sb("k_spread", [P, heads, S])
        scored = s.sb("scored", [P, 2, S + 2])
        along, tmp = s.sb("along", [P, 3, P]), s.sb("tmp", [P, 3, P])
        over_edge = s.sb("over_edge", [P, 2, 3, P])
        e, e_t = s.sb("e", [P, 2, S]), s.sb("e_t", [P, 2, 2, P])
        top, total, inverse = s.sb("top", [P, 2]), s.sb("total", [P, 2]), s.sb("inverse", [P, 2])
        mixed, mixed_t = s.sb("mixed", [P, 2, D]), s.sb("mixed_t", [P, 2, P])
        change = s.sb("change", [P, 2, D])
        names = ["loaded", "mask_loaded", "tables", "tables_done", "mask_ready", "q_made", "q_kept", "v_kept", "k_ready",
                 "spread", "scores_made", "scored_ready", "kernel_steps", "kernel_ready", "conv_made", "biased", "topped",
                 "exp_done", "turned", "turned_kept", "mixed_made", "inverted", "band_made", "mixed_ready", "mixed_turned",
                 "mixed_kept", "out_made", "changed", "x_done", "zeroed"]
        sem = {n: s.sem(n) for n in names}
        with s.block() as block:

            @block.sync
            def _(sp):
                for to, w in zip((wq, wk, wv, proj), ("Wq", "Wk", "Wv", "proj_W")):
                    sp.dma_start(to[:], a["L3_xattn_" + w]).then_inc(sem["loaded"], 16)
                sp.dma_start(proj_rows[:], row(a["L3_xattn_proj_b"]).to_broadcast([P, D])).then_inc(sem["loaded"], 16)
                sp.dma_start(mask_u8[:], a["mask_SxS_bc0"].rearrange("(u i) j -> i u j", i=P))\
                    .then_inc(sem["mask_loaded"], 16)

            @block.gpsimd
            def _(pool):
                norm.gpsimd(pool)
                tables = Tally(sem["tables"])
                tables.add(pool.memset(head_mask[:], 1.0))
                tables.add(pool.memset(bands[:], 0.0))
                tables.add(pool.memset(edge[:], 0.0))
                tables.add(pool.memset(scored[:], 0.0))
                tables.wait(pool)
                tables.add(pool.affine_select(out=head_mask[:], in_=head_mask[:], compare_op=ALU.is_ge, fill=0.0,
                                              base=0, pattern=[[-wide, heads]], channel_multiplier=1))
                tables.wait(pool)
                pool.affine_select(out=head_mask[:], in_=head_mask[:], compare_op=ALU.is_ge, fill=0.0, base=wide - 1,
                                   pattern=[[wide, heads]], channel_multiplier=-1).then_inc(sem["tables_done"], 1)
                for n in range(3):
                    pool.affine_select(out=bands[:, n, :], in_=bands[:, n, :], compare_op=ALU.not_equal, fill=1.0,
                                       base=1 - n, pattern=[[-1, P]], channel_multiplier=1)\
                        .then_inc(sem["tables_done"], 1)
                for n, base in enumerate((P - 1, 1 - P)):
                    pool.affine_select(out=edge[:, n, :], in_=edge[:, n, :], compare_op=ALU.not_equal, fill=1.0,
                                       base=base, pattern=[[-1, P]], channel_multiplier=1)\
                        .then_inc(sem["tables_done"], 1)

            @block.tensor
            def _(pe):
                norm.tensor(pe)
                for free in ("conv_made", "turned", "mixed_made"):
                    pe.sem_inc(sem[free], 1)
                pe.wait_ge(sem["loaded"], 80)
                pe.wait_ge(norm.xt_ready, 2)
                with pe.Fori(0, B) as b:
                    xt = norm.xt[:, bass.ds(2 * b, 2), :].rearrange("p t k -> p (t k)")
                    pe.wait_ge(sem["x_done"], b + 1)
                    pe.matmul(ps[:, 2, 0:S], wq[:], xt, start=True, stop=True)
                    pe.matmul(ps[:, 2, S:2 * S], wk[:], xt, start=True, stop=True)
                    pe.matmul(ps[:, 3, 0:S], wv[:], xt, start=True, stop=True).then_inc(sem["q_made"], 1)
                    pe.wait_ge(sem["q_kept"], 3 * (b + 1))
                    for u in range(2):
                        mm = pe.transpose(ps[:, 4, u * D:(u + 1) * D], e[:, 0, u * P:(u + 1) * P], keep.identity[:])
                    mm.then_inc(sem["q_made"], 1)
                    with pe.Fori(0, heads) as h:
                        n = b * heads + h
                        pe.wait_ge(sem["spread"], b + 1)
                        pe.wait_ge(sem["v_kept"], b + 1)
                        pe.wait_ge(sem["scored_ready"], n + 1)
                        for u in range(2):
                            mm = pe.matmul(ps[:, 5, u * S:(u + 1) * S], q_t[:, u * P:(u + 1) * P],
                                           k_spread[:, bass.ds(h, 1), :].rearrange("p a j -> p (a j)"),
                                           start=True, stop=True)
                        mm.then_inc(sem["scores_made"], 1)
                        pe.wait_ge(sem["scored_ready"], n + 2)
                        pe.wait_ge(sem["kernel_ready"], 3 * (n + 1))
                        for u in range(2):
                            to = ps[:, 6, u * S:(u + 1) * S]
                            for c in range(3):
                                pe.matmul(to, along[:, c, :], scored[:, u, c:c + S], start=(c == 0), stop=False)
                            for c in range(3):
                                mm = pe.matmul(to, over_edge[:, u, c, :], scored[:, 1 - u, c:c + S], start=False,
                                               stop=(c == 2))
                        mm.then_inc(sem["conv_made"], 1)
                        pe.wait_ge(sem["exp_done"], 2 * (n + 1))
                        for u in range(2):
                            for j in range(2):
                                mm = pe.transpose(ps[:, 7, (2 * u + j) * P:(2 * u + j + 1) * P],
                                                  e[:, u, j * P:(j + 1) * P], keep.identity[:])
                        mm.then_inc(sem["turned"], 1)
                        pe.wait_ge(sem["turned_kept"], n + 1)
                        for u in range(2):
                            for j in range(2):
                                mm = pe.matmul(ps[:, 4, u * wide:(u + 1) * wide], e_t[:, u, j, :],
                                               v[:, j, bass.ds(h * wide, wide)], start=(j == 0), stop=(j == 1))
                        mm.then_inc(sem["mixed_made"], 1)
                    pe.wait_ge(sem["mixed_ready"], 2 * heads * (b + 1) + 1)
                    for u in range(2):
                        mm = pe.transpose(ps[:, 2, u * P:(u + 1) * P], mixed[:, u, :], keep.identity[:])
                    mm.then_inc(sem["mixed_turned"], 1)
                    pe.wait_ge(sem["mixed_kept"], b + 1)
                    for u in range(2):
                        mm = pe.matmul(ps[:, 3, u * D:(u + 1) * D], mixed_t[:, u, :], proj[:], start=True, stop=True)
                    mm.then_inc(sem["out_made"], 1)

            @block.scalar
            def _(act):
                norm.scalar(act)
                act.wait_ge(sem["loaded"], 80)
                with act.Fori(0, B * heads) as n:
                    act.wait_ge(sem["topped"], n + 1)
                    act.wait_ge(sem["mixed_made"], n + 1)
                    for u in range(2):
                        act.activation(e[:, u, :], e[:, u, :], ACT.Exp, bias=top[:, u:u + 1],
                                       accum_out=total[:, u:u + 1]).then_inc(sem["exp_done"], 1)

            @block.vector
            def _(dve):
                norm.vector(dve)
                for free in ("x_done", "scored_ready", "mixed_ready"):
                    dve.sem_inc(sem[free], 1)
                steps = Tally(sem["kernel_steps"])

                def then(instruction):
                    steps.add(instruction)
                    steps.wait(dve)

                dve.wait_ge(sem["mask_loaded"], 16)
                then(dve.tensor_copy(masked[:], mask_u8[:]))
                then(dve.tensor_scalar(open_[:], masked[:], -1.0, 1.0, ALU.mult, ALU.add))
                then(dve.tensor_scalar(masked[:], masked[:], -1e30, None, ALU.mult))
                dve.wait_ge(sem["tables_done"], 6)
                with dve.Fori(0, B) as b:
                    dve.wait_ge(sem["q_made"], 2 * b + 1)
                    dve.tensor_scalar(q_t[:], ps[:, 2, 0:S], scale, None, ALU.mult).then_inc(sem["q_kept"], 1)
                    dve.tensor_copy(k_t[:], ps[:, 2, S:2 * S]).then_inc(sem["q_kept"], 1)
                    dve.tensor_copy(e[:, 0, :], ps[:, 3, 0:S]).then_inc(sem["q_kept"], 1)
                    dve.wait_ge(sem["q_kept"], 3 * (b + 1))
                    dve.tensor_tensor(k_spread[:], k_t[:, None, :].to_broadcast([P, heads, S]),
                                      head_mask[:, :, None].to_broadcast([P, heads, S]), ALU.mult)\
                        .then_inc(sem["spread"], 1)
                    dve.wait_ge(sem["q_made"], 2 * b + 2)
                    dve.tensor_copy(v[:].rearrange("p u d -> p (u d)"), ps[:, 4, 0:2 * D]).then_inc(sem["v_kept"], 1)
                    with dve.Fori(0, heads) as h:
                        n = b * heads + h
                        def tap(k):
                            return taps[:, bass.ds(b, 1), bass.ds(h, 1), 3 * k:3 * k + 3].rearrange(
                                "p x y c -> p (x y c)")[:, :, None].to_broadcast([P, 3, P])

                        def spread(to, table, k):
                            return dve.tensor_tensor(to, table.to_broadcast([P, 3, P]), tap(k), ALU.mult)

                        dve.wait_ge(sem["conv_made"], n + 1)
                        spread(along[:], bands[:, 0:1, :], 0).then_inc(sem["band_made"], 1)
                        spread(tmp[:], bands[:, 1:2, :], 1).then_inc(sem["band_made"], 1)
                        dve.wait_ge(sem["band_made"], 4 * n + 2)
                        dve.tensor_tensor(along[:], along[:], tmp[:], ALU.add).then_inc(sem["band_made"], 1)
                        dve.wait_ge(sem["band_made"], 4 * n + 3)
                        spread(tmp[:], bands[:, 2:3, :], 2).then_inc(sem["band_made"], 1)
                        dve.wait_ge(sem["band_made"], 4 * n + 4)
                        dve.tensor_tensor(along[:], along[:], tmp[:], ALU.add).then_inc(sem["kernel_ready"], 1)
                        spread(over_edge[:, 0], edge[:, 0:1, :], 2).then_inc(sem["kernel_ready"], 1)
                        spread(over_edge[:, 1], edge[:, 1:2, :], 0).then_inc(sem["kernel_ready"], 1)
                        dve.wait_ge(sem["scores_made"], n + 1)
                        dve.tensor_tensor(scored[:, :, 1:S + 1], ps[:, 5, :].rearrange("p (u j) -> p u j", u=2),
                                          open_[:], ALU.mult).then_inc(sem["scored_ready"], 1)
                        dve.wait_ge(sem["conv_made"], n + 2)
                        dve.wait_ge(sem["turned"], n + 1)
                        dve.tensor_tensor(e[:], ps[:, 6, :].rearrange("p (u j) -> p u j", u=2), masked[:], ALU.add)\
                            .then_inc(sem["biased"], 1)
                        dve.wait_ge(sem["biased"], n + 1)
                        dve.tensor_reduce(top[:], e[:], AX, ALU.max, negate=True).then_inc(sem["topped"], 1)
                        dve.wait_ge(sem["turned"], n + 2)
                        dve.tensor_copy(e_t[:].rearrange("p u j k -> p (u j k)"), ps[:, 7, :])\
                            .then_inc(sem["turned_kept"], 1)
                        dve.wait_ge(sem["mixed_ready"], 2 * n + 1)
                        dve.reciprocal(inverse[:], total[:]).then_inc(sem["inverted"], 1)
                        dve.wait_ge(sem["inverted"], n + 1)
                        dve.wait_ge(sem["mixed_made"], n + 2)
                        for u in range(2):
                            dve.tensor_scalar(mixed[:, u, bass.ds(h * wide, wide)], ps[:, 4, u * wide:(u + 1) * wide],
                                              inverse[:, u:u + 1], None, ALU.mult).then_inc(sem["mixed_ready"], 1)
                    dve.wait_ge(sem["mixed_turned"], b + 1)
                    dve.tensor_copy(mixed_t[:].rearrange("p u k -> p (u k)"), ps[:, 2, 0:2 * P])\
                        .then_inc(sem["mixed_kept"], 1)
                    dve.wait_ge(sem["out_made"], b + 1)
                    dve.tensor_tensor(change[:], ps[:, 3, 0:2 * D].rearrange("p (u d) -> p u d", u=2),
                                      proj_rows[:, None, :].to_broadcast([P, 2, D]), ALU.add).then_inc(sem["changed"], 1)
                    dve.wait_ge(sem["changed"], b + 1)
                    xb = keep.x[:, bass.ds(2 * b, 2), :]
                    dve.scalar_tensor_tensor(out=xb, in0=change[:], scalar=gate, in1=xb, op0=ALU.mult, op1=ALU.add)\
                        .then_inc(sem["x_done"], 1)



class Keep:

    def __init__(self, s):
        self.x = s.sb("x", [P, NT, D])
        self.ctx_t = s.sb("ctx_t", [P, B * C])
        self.identity = s.sb("identity", [P, P])
        self.gates = s.sb("gates", [P, 2 * B])
        self.neg_half = s.sb("neg_half", [P, 16])
        self.iota = s.sb("iota", [P, P])
        self.iota_tiles = s.sb("iota_tiles", [P, NT])
        self.token = s.sb("token", [P, NT])
        self.gathered = [s.gpsimd_dma_sem(f"gathered{u}") for u in range(2)]
        self.got = [s.gpsimd_dma_sem(f"got{k}{t}") for t in range(NT) for k in range(CHOSEN)]


def store(nc, a, keep, out):
    with Scope(nc, "store") as s:
        stored = s.sem("stored")
        with s.block() as block:

            @block.sync
            def _(sp):
                sp.dma_start(out.rearrange("b (u p) d -> p (b u) d", p=P), keep.x[:]).then_inc(stored, 16)
                sp.wait_ge(stored, 16)


def latent_operands(nc, a, keep, name, scores_rhs, values_rhs, score_bias, wq, bias_q, scale):
    heads = 16
    wide = D // heads
    with Scope(nc, name) as s:
        wk, wv, mask = s.sb("wk", [P, D]), s.sb("wv", [P, D]), s.sb("mask", [P, B * C])
        ctx_twice = s.sb("ctx_twice", [P, B, 2, C])
        bias_k, head_mask, k_t = s.sb("bias_k", [P, 1]), s.sb("head_mask", [P, heads]), s.sb("k_t", [P, B * C])
        ps = s.psum("ps", [P, 2, 512])
        names = ["weights_loaded", "bias_loaded", "mask_loaded", "ones_set", "lower_cut", "mask_made", "k_made",
                 "k_kept", "v_made", "rhs_zeroed", "v_kept", "k_spread", "bias_spread", "q_scaled", "ctx_doubled"]
        sem = {n: s.sem(n) for n in names}
        with s.block() as block:

            @block.sync
            def _(sp):
                sp.dma_start(wk[:], a["L2_xattn_Wk"]).then_inc(sem["weights_loaded"], 16)
                sp.dma_start(wv[:], a["L2_xattn_Wv"]).then_inc(sem["weights_loaded"], 16)
                sp.dma_start(wq[:], a["L2_xattn_Wq"]).then_inc(sem["weights_loaded"], 16)
                sp.dma_start(mask[:], a["mask_Bx1x1xS2_ff0"].rearrange("b x y k -> (x y) (b k)").to_broadcast([P, B * C]))\
                    .then_inc(sem["mask_loaded"], 16)
                for to, v in ((bias_k, "L2_xattn_bk"), (bias_q, "L2_xattn_bq")):
                    sp.dma_start(to[:], a[v].rearrange("(p c) -> p c", c=1)).then_inc(sem["bias_loaded"], 16)
                sp.wait_ge(sem["weights_loaded"], 48)

            @block.gpsimd
            def _(pool):
                pool.memset(head_mask[:], 1.0).then_inc(sem["ones_set"], 1)
                pool.memset(values_rhs[:], 0.0).then_inc(sem["rhs_zeroed"], 1)
                pool.wait_ge(sem["ones_set"], 1)
                pool.affine_select(out=head_mask[:], in_=head_mask[:], compare_op=ALU.is_ge, fill=0.0, base=0,
                                   pattern=[[-wide, heads]], channel_multiplier=1).then_inc(sem["lower_cut"], 1)
                pool.wait_ge(sem["lower_cut"], 1)
                pool.affine_select(out=head_mask[:], in_=head_mask[:], compare_op=ALU.is_ge, fill=0.0, base=wide - 1,
                                   pattern=[[wide, heads]], channel_multiplier=-1).then_inc(sem["mask_made"], 1)
                pool.wait_ge(sem["mask_loaded"], 16)
                for b in range(B):
                    pool.tensor_copy(score_bias[:, b, :].rearrange("p (h k) -> p h k", h=heads),
                                     mask[:, None, b * C:(b + 1) * C].to_broadcast([P, heads, C]))\
                        .then_inc(sem["bias_spread"], 1)

            @block.tensor
            def _(pe):
                pe.wait_ge(sem["weights_loaded"], 48)
                pe.matmul(ps[:, 0, 0:B * C], wk[:], keep.ctx_t[:], start=True, stop=True).then_inc(sem["k_made"], 1)
                pe.wait_ge(sem["ctx_doubled"], 1)
                for b in range(B):
                    mm = pe.matmul(ps[:, 1, b * D:(b + 1) * D], ctx_twice[:, b, :, :].rearrange("p e k -> p (e k)"),
                                   wv[:], start=True, stop=True)
                mm.then_inc(sem["v_made"], 1)

            @block.scalar
            def _(act):
                act.wait_ge(sem["bias_loaded"], 32)
                act.activation(bias_q[:], bias_q[:], ACT.Copy, scale=scale).then_inc(sem["q_scaled"], 1)
                act.wait_ge(sem["v_made"], 1)
                act.wait_ge(sem["rhs_zeroed"], 1)
                for e in range(2):
                    rows = slice(e * C, (e + 1) * C)
                    act.activation(values_rhs[rows, :, :, e * wide:(e + 1) * wide],
                                   ps[rows, 1, :].rearrange("r (b p e d) -> r b p e d", b=B, e=2, d=wide)[:, :, :, e, :],
                                   ACT.Copy).then_inc(sem["v_kept"], 1)

            @block.vector
            def _(dve):
                dve.tensor_copy(ctx_twice[:], keep.ctx_t[:].rearrange("p (b k) -> p b k", b=B)[:, :, None, :]
                                .to_broadcast([P, B, 2, C])).then_inc(sem["ctx_doubled"], 1)
                dve.wait_ge(sem["k_made"], 1)
                dve.wait_ge(sem["bias_loaded"], 32)
                dve.tensor_scalar(k_t[:], ps[:, 0, 0:B * C], bias_k[:, 0:1], None, ALU.add).then_inc(sem["k_kept"], 1)
                dve.wait_ge(sem["k_kept"], 1)
                dve.wait_ge(sem["mask_made"], 1)
                for b in range(B):
                    dve.tensor_tensor(scores_rhs[:, b, :].rearrange("p (h k) -> p h k", h=heads),
                                      k_t[:, None, b * C:(b + 1) * C].to_broadcast([P, heads, C]),
                                      head_mask[:, :, None].to_broadcast([P, heads, C]), ALU.mult)\
                        .then_inc(sem["k_spread"], 1)


class Normed:

    def __init__(self, s, keep, bank_a, bank_b):
        self.keep, self.banks = keep, (bank_a, bank_b)
        self.xn, self.xt = s.sb("xn", [P, NT, D]), s.sb("xt", [P, NT, P])
        self.stats, self.moments = s.sb("stats", [P, NT, 6]), s.sb("moments", [P, NT, 2])
        self.var_eps, self.rstd = s.sb("var_eps", [P, NT]), s.sb("rstd", [P, NT])
        self.stats_made, self.moments_made = s.sem("stats_made"), s.sem("moments_made")
        self.var_ready, self.rstd_ready = s.sem("var_ready"), s.sem("rstd_ready")
        self.xn_ready, self.xn_turned, self.xt_ready = s.sem("xn_ready"), s.sem("xn_turned"), s.sem("xt_ready")

    def vector(self, dve):
        x = self.keep.x
        for t in range(NT):
            dve.bn_stats(self.stats[:, t, :], x[:, t, :]).then_inc(self.stats_made, 1)
        for t in range(NT):
            dve.wait_ge(self.stats_made, t + 1)
            dve.bn_aggr(self.moments[:, t, :], self.stats[:, t, :]).then_inc(self.moments_made, 1)
        dve.wait_ge(self.moments_made, NT)
        dve.tensor_scalar(self.var_eps[:], self.moments[:, :, 1], EPS, None, ALU.add).then_inc(self.var_ready, 1)
        dve.wait_ge(self.rstd_ready, 1)
        for t in range(NT):
            dve.tensor_scalar(self.xn[:, t, :], x[:, t, :], self.moments[:, t, 0:1], self.rstd[:, t:t + 1],
                              ALU.subtract, ALU.mult).then_inc(self.xn_ready, 1)

    def gpsimd(self, pool):
        pool.wait_ge(self.var_ready, 1)
        pool.tensor_tensor(self.rstd[:], self.var_eps[:], self.keep.neg_half[:, 0:NT], ALU.pow)\
            .then_inc(self.rstd_ready, 1)

    def tensor(self, pe):
        for t in range(NT):
            pe.wait_ge(self.xn_ready, t + 1)
            mm = pe.transpose(self.banks[t // 4][:, (t % 4) * P:(t % 4 + 1) * P], self.xn[:, t, :],
                              self.keep.identity[:])
            if t % 4 == 3:
                mm.then_inc(self.xn_turned, 1)

    def scalar(self, act):
        for n in range(2):
            act.wait_ge(self.xn_turned, n + 1)
            act.activation(self.xt[:, 4 * n:4 * n + 4, :].rearrange("p t k -> p (t k)"), self.banks[n][:],
                           ACT.Copy).then_inc(self.xt_ready, 1)


def lora_ffn(nc, a, keep, name, gate):
    with Scope(nc, name) as s:
        ps = s.psum("ps", [P, 8, 512])
        norm = Normed(s, keep, ps[:, 0], ps[:, 1])
        w1, w1_t = s.sb("w1", [P, 4, D]), s.sb("w1_t", [P, 4, P])
        w2, w2_t = s.sb("w2", [P, 4, P]), s.sb("w2_t", [P, 4, D])
        b1_rows, b1, b2 = s.sb("b1_rows", [4, P]), s.sb("b1", [P, 4]), s.sb("b2", [P, D])
        scale, odd = s.sb("scale", [P, 1]), s.sb("odd", [P, B, 8])
        w1_own, w2_own = s.sb("w1_own", [P, 2, 4, P]), s.sb("w2_own", [P, 2, 4, D])
        hidden, change = s.sb("hidden", [P, 2, 4, S]), s.sb("change", [P, 2, 2, D])
        names = ["loaded", "w_turned", "w_kept", "b1_turned", "b1_kept", "odd_scaled", "even_made", "own_made",
                 "hidden_made", "gelu_done", "out_made", "change_made", "x_done"]
        sem = {n: s.sem(n) for n in names}
        with s.block() as block:

            @block.sync
            def _(sp):
                sp.dma_start(w1[:], a["L0_ffn_W1"].rearrange("(j h) d -> h j d", h=P)).then_inc(sem["loaded"], 16)
                sp.dma_start(w2[:], a["L0_ffn_W2"].rearrange("o (g c) -> o g c", c=P)).then_inc(sem["loaded"], 16)
                sp.dma_start(b1_rows[:], a["L0_ffn_b1"].rearrange("(j h) -> j h", h=P)).then_inc(sem["loaded"], 16)
                sp.dma_start(b2[:], row(a["L0_ffn_b2"]).to_broadcast([P, D])).then_inc(sem["loaded"], 16)
                sp.dma_start(scale[:], row(a["L0_ffn_scale"]).to_broadcast([P, 1])).then_inc(sem["loaded"], 16)

            @block.gpsimd
            def _(pool):
                norm.gpsimd(pool)

            @block.tensor
            def _(pe):
                pe.wait_ge(sem["loaded"], 80)
                for j in range(4):
                    pe.transpose(ps[:, 2, j * P:(j + 1) * P], w1[:, j, :], keep.identity[:])
                    mm = pe.transpose(ps[:, 3, j * P:(j + 1) * P], w2[:, j, :], keep.identity[:])
                mm.then_inc(sem["w_turned"], 1)
                pe.transpose(ps[:, 4, 0:4], b1_rows[:], keep.identity[0:4, 0:4]).then_inc(sem["b1_turned"], 1)
                norm.tensor(pe)

                def even(b):
                    if b == 0:
                        pe.wait_ge(sem["w_kept"], 2)
                    else:
                        pe.wait_ge(sem["own_made"], 8 * b)
                    for j in range(8):
                        mm = pe.matmul(ps[:, 2 + j // 4, (j % 4) * D:(j % 4 + 1) * D],
                                       keep.identity[:, 1 + 2 * j:2 + 2 * j].to_broadcast([P, P]),
                                       norm.xn[:, 2 * b, :], start=True, stop=True)
                    mm.then_inc(sem["even_made"], 1)

                def up(b):
                    pe.wait_ge(sem["own_made"], 8 * (b + 1))
                    pe.wait_ge(norm.xt_ready, 2)
                    if b >= 1:
                        pe.wait_ge(sem["gelu_done"], 4 * b)
                    for j in range(4):
                        mm = pe.matmul(ps[:, 4 + j // 2, (j % 2) * S:(j % 2 + 1) * S], w1_own[:, b % 2, j, :],
                                       norm.xt[:, 2 * b:2 * b + 2, :].rearrange("p t k -> p (t k)"),
                                       start=True, stop=True)
                    mm.then_inc(sem["hidden_made"], 1)

                def down(b):
                    pe.wait_ge(sem["gelu_done"], 4 * (b + 1))
                    if b >= 2:
                        pe.wait_ge(sem["change_made"], b - 1)
                    for u in range(2):
                        for g in range(4):
                            mm = pe.matmul(ps[:, 6 + b % 2, u * D:(u + 1) * D],
                                           hidden[:, b % 2, g, u * P:(u + 1) * P], w2_own[:, b % 2, g, :],
                                           start=(g == 0), stop=(g == 3))
                    mm.then_inc(sem["out_made"], 1)

                pe.wait_ge(sem["b1_kept"], 1)
                even(0)
                for b in range(B):
                    up(b)
                    if b + 1 < B:
                        even(b + 1)
                    down(b)

            @block.scalar
            def _(act):
                act.wait_ge(sem["b1_turned"], 1)
                act.activation(b1[:], ps[:, 4, 0:4], ACT.Copy).then_inc(sem["b1_kept"], 1)
                norm.scalar(act)
                act.wait_ge(sem["b1_kept"], 1)
                for b in range(B):
                    act.wait_ge(sem["hidden_made"], b + 1)
                    if b >= 2:
                        act.wait_ge(sem["out_made"], b - 1)
                    for j in range(4):
                        act.activation(hidden[:, b % 2, j, :], ps[:, 4 + j // 2, (j % 2) * S:(j % 2 + 1) * S],
                                       ACT.Gelu, bias=b1[:, j:j + 1]).then_inc(sem["gelu_done"], 1)

            @block.vector
            def _(dve):
                dve.wait_ge(sem["w_turned"], 1)
                dve.tensor_copy(w1_t[:].rearrange("p j h -> p (j h)"), ps[:, 2]).then_inc(sem["w_kept"], 1)
                dve.tensor_copy(w2_t[:].rearrange("p j h -> p (j h)"), ps[:, 3]).then_inc(sem["w_kept"], 1)
                norm.vector(dve)
                dve.wait_ge(norm.xt_ready, 2)
                for b in range(B):
                    dve.tensor_scalar(odd[:, b, :], norm.xt[:, 2 * b, 2:18:2], scale[:, 0:1], None, ALU.mult)\
                        .then_inc(sem["odd_scaled"], 1)

                def own(b):
                    dve.wait_ge(sem["odd_scaled"], B)
                    dve.wait_ge(sem["w_kept"], 2)
                    dve.wait_ge(sem["even_made"], b + 1)
                    if b >= 2:
                        dve.wait_ge(sem["out_made"], b - 1)
                    for j in range(4):
                        dve.scalar_tensor_tensor(out=w1_own[:, b % 2, j, :], in0=ps[:, 2, j * D:(j + 1) * D],
                                                 scalar=odd[:, b, j:j + 1], in1=w1_t[:, j, :], op0=ALU.mult,
                                                 op1=ALU.add).then_inc(sem["own_made"], 1)
                    for m in range(4):
                        cols = slice(32 * m, 32 * m + 32)
                        dve.scalar_tensor_tensor(
                            out=w2_own[:, b % 2, :, cols],
                            in0=ps[:, 3, m * D:(m + 1) * D].rearrange("c (o g) -> c g o", g=4),
                            scalar=odd[:, b, 4 + m:5 + m], in1=w2_t[:, :, cols], op0=ALU.mult,
                            op1=ALU.add).then_inc(sem["own_made"], 1)

                def update(b):
                    dve.wait_ge(sem["out_made"], b + 1)
                    dve.tensor_tensor(change[:, b % 2], ps[:, 6 + b % 2, 0:2 * D].rearrange("p (u d) -> p u d", u=2),
                                      b2[:, None, :].to_broadcast([P, 2, D]), ALU.add).then_inc(sem["change_made"], 1)
                    dve.wait_ge(sem["change_made"], b + 1)
                    dve.scalar_tensor_tensor(out=keep.x[:, 2 * b:2 * b + 2, :], in0=change[:, b % 2], scalar=gate,
                                             in1=keep.x[:, 2 * b:2 * b + 2, :], op0=ALU.mult, op1=ALU.add)\
                        .then_inc(sem["x_done"], 1)

                own(0)
                for b in range(B):
                    if b + 1 < B:
                        own(b + 1)
                    update(b)


class GeluWeights:

    def __init__(self, s):
        self.w1, self.w2 = s.sb("w1", [P, EXPERTS, 512]), s.sb("w2", [P, EXPERTS, 4, 512])
        self.w3, self.b3 = s.sb("w3", [P, EXPERTS, 4, D]), s.sb("b3", [P, EXPERTS, D])
        self.b_rows, self.b = s.sb("b_rows", [2 * EXPERTS * 4, P]), s.sb("b", [P, 2 * EXPERTS * 4])
        self.loaded = s.gpsimd_dma_sem("loaded")


def load_gelu_weights(nc, a, s):
    w = GeluWeights(s)
    with nc.Block() as block:

        @block.gpsimd
        def _(pool):
            for n, v in enumerate(("L1_ffn_b1", "L1_ffn_b2")):
                pool.dma_start(w.b_rows[32 * n:32 * n + 32, :], a[v].rearrange("e (c d) -> (e c) d", d=P))\
                    .then_inc(w.loaded, 16)
            pool.dma_start(w.b3[:], a["L1_ffn_b3"].rearrange("(o e) d -> o e d", o=1).to_broadcast([P, EXPERTS, D]))\
                .then_inc(w.loaded, 16)
            pool.dma_start(w.w1[:], a["L1_ffn_W1"].rearrange("e d h -> d e h")).then_inc(w.loaded, 16)
            pool.dma_start(w.w3[:], a["L1_ffn_W3"].rearrange("e (c d) h -> d e c h", d=P)).then_inc(w.loaded, 16)
            pool.dma_start(w.w2[:], a["L1_ffn_W2"].rearrange("e (c d) h -> d e c h", d=P)).then_inc(w.loaded, 16)
    return w


def turn_expert_biases(nc, keep, name, w):
    with Scope(nc, name) as s:
        ps = s.psum("ps", [P, 512])
        turned, kept = s.sem("turned"), s.sem("kept")
        with s.block() as block:

            @block.tensor
            def _(pe):
                pe.wait_ge(w.loaded, 96)
                pe.transpose(ps[:, 0:64], w.b_rows[:], keep.identity[0:64, 0:64]).then_inc(turned, 1)

            @block.vector
            def _(dve):
                dve.wait_ge(turned, 1)
                dve.tensor_copy(w.b[:], ps[:, 0:64]).then_inc(kept, 1)


def program(nc, a, out):
    with Scope(nc, "keep") as s:
        keep = Keep(s)
        setup(nc, a, keep)

        def gate(kind, layer):
            return keep.gates[:, B * kind + layer:B * kind + layer + 1]

        with Scope(nc, "experts1") as own:
            w = load_gelu_weights(nc, a, own)
            with Scope(nc, "attention01") as q:
                scores_rhs, values_rhs = q.sb("scores_rhs", [P, B, 16 * C]), q.sb("values_rhs", [P, B, 8, D])
                head_operands(nc, a, keep, "operands0",
                              [a[f"L0_xattn_{n}_kernel"] for n in ("query", "key", "value", "projection")], None,
                              0.125, scores_rhs, values_rhs, None)
                cross_attention(nc, a, keep, "attention0", scores_rhs, values_rhs, None,
                                a["L0_xattn_projection_bias"], gate(0, 0))
            lora_ffn(nc, a, keep, "ffn0", gate(1, 0))
            with Scope(nc, "attention1") as q:
                scores_rhs, values_rhs = q.sb("scores_rhs", [P, B, 16 * C]), q.sb("values_rhs", [P, B, 8, D])
                score_bias = q.sb("score_bias", [P, B, 16 * C])
                head_operands(nc, a, keep, "operands1", [a[f"L1_xattn_{n}"] for n in ("WQ", "WK", "WV", "WO")],
                              [a[f"L1_xattn_{n}"] for n in ("bQ", "bK", "bV")], 0.125, scores_rhs, values_rhs,
                              score_bias)
                cross_attention(nc, a, keep, "attention1", scores_rhs, values_rhs, score_bias, a["L1_xattn_bO"],
                                gate(0, 1))
            routes = Routes(nc, own, "ffn1")
            turn_expert_biases(nc, keep, "biases1", w)
            route(nc, keep, "route1", routes, a["L1_ffn_expert_tokens"], gate(1, 1), False)
            gelu_experts(nc, keep, "experts1", routes, w.w1, w.w2, w.w3, w.b[:, 0:32], w.b[:, 32:64], w.b3)
            combine(nc, keep, "combine1", routes)
        with Scope(nc, "experts23") as own:
            w_in2, w_out2 = own.sb("w_in2", [P, EXPERTS, 1024]), own.sb("w_out2", [P, EXPERTS, 4, D])
            w_in3, w_out3 = own.sb("w_in3", [P, EXPERTS, 512]), own.sb("w_out3", [P, EXPERTS, 2, D])
            loaded3 = own.gpsimd_dma_sem("loaded3")
            with Scope(nc, "raw2") as raw:
                gate_up, down = raw.sb("gate_up", [P, EXPERTS, 8, D]), raw.sb("down", [P, EXPERTS, 512])
                keep.raw_loaded = [raw.gpsimd_dma_sem("gate_up_loaded"), raw.gpsimd_dma_sem("down_loaded")]
                with nc.Block() as block:

                    @block.gpsimd
                    def _(pool):
                        pool.dma_start(gate_up[:], a["L2_ffn_gate_up_proj"].rearrange("e (c i) h -> i e c h", i=P))\
                            .then_inc(keep.raw_loaded[0], 16)
                        pool.dma_start(down[:], a["L2_ffn_down_proj"].rearrange("e h i -> h e i"))\
                            .then_inc(keep.raw_loaded[1], 16)
                        pool.dma_start(w_in3[:, :, 0:256], a["L3_ffn_gate_w"].rearrange("e d i -> d e i"))\
                            .then_inc(loaded3, 16)
                        pool.dma_start(w_in3[:, :, 256:512], a["L3_ffn_up_w"].rearrange("e d i -> d e i"))\
                            .then_inc(loaded3, 16)
                        pool.dma_start(w_out3[:], a["L3_ffn_down_w"].rearrange("e (c i) d -> i e c d", i=P))\
                            .then_inc(loaded3, 16)

                with Scope(nc, "attention2") as q:
                    scores_rhs, values_rhs = q.sb("scores_rhs", [P, B, 16 * C]), q.sb("values_rhs", [P, B, 8, 16])
                    score_bias, wq, bias_q = q.sb("score_bias", [P, B, 16 * C]), q.sb("wq", [P, D]), q.sb("bias_q", [P, 1])
                    latent_operands(nc, a, keep, "operands2", scores_rhs, values_rhs, score_bias, wq, bias_q, 8 ** -0.5)
                    cross_attention(nc, a, keep, "attention2", scores_rhs, values_rhs, score_bias, a["L2_xattn_bv"],
                                    gate(0, 2), (wq[:], bias_q[:]), 8 ** -0.5)
                turn_gated_weights(nc, a, keep, "weights2", gate_up, down, w_in2, w_out2)
            routes = Routes(nc, own, "ffn2", 1)
            route(nc, keep, "route2", routes, a["L2_ffn_gate_w"], gate(1, 2), True)
            gated_experts(nc, keep, "gated2", routes, w_in2, w_out2)
            combine(nc, keep, "combine2", routes)
            with Scope(nc, "attention3") as q:
                taps = q.sb("taps", [P, B, 16, TAPS])
                conv_kernels(nc, a, keep, "kernels3", taps)
                conv_attention_any_mask(nc, a, keep, "masked3", taps, gate(0, 3))
            routes = Routes(nc, own, "ffn3", 2)
            with nc.Block() as block:

                @block.tensor
                def _(pe):
                    pe.wait_ge(loaded3, 48)

            route(nc, keep, "route3", routes, a["L3_ffn_router_w"], gate(1, 3), True)
            gated_experts(nc, keep, "gated3", routes, w_in3, w_out3)
            combine(nc, keep, "combine3", routes)
        store(nc, a, keep, out)


def kernel(**inputs):
    import concourse.bacc as bacc
    from concourse.bass_utils import run_bass_kernel_spmd

    nc = bacc.Bacc("TRN2", target_bir_lowering=False, num_devices=1)
    arrays, a = {}, {}
    for name, value in inputs.items():
        value = np.ascontiguousarray(value)
        if not value.shape:
            value = value.reshape(1)
        arrays["in_" + name] = value
        a[name] = nc.dram_tensor("in_" + name, value.shape, mybir.dt.from_np(value.dtype), kind="ExternalInput").ap()
    out = nc.dram_tensor("out", (B, S, D), F32, kind="ExternalOutput").ap()
    program(nc, a, out)
    return run_bass_kernel_spmd(nc, [arrays], core_ids=[0]).results[0]["out"]
```

```python
import numpy as np
import concourse.bass as bass
from concourse import mybir
from contextlib import ExitStack

F32 = mybir.dt.float32
BF16 = mybir.dt.bfloat16
I32 = mybir.dt.int32
U32 = mybir.dt.uint32
U8 = mybir.dt.uint8
ALU = mybir.AluOpType
ACT = mybir.ActivationFunctionType
AX = mybir.AxisListType.X

P = 128
B, S, D = 4, 256, 128
T = B * S
NT = T // P
C = 64
EPS = 1e-5


class Tally:

    def __init__(self, sem):
        self.sem, self.n, self.top, self.mark = sem, 0, None, 0

    def add(self, instruction, by=1):
        instruction.then_inc(self.sem, by)
        self.n += by
        return instruction

    def enter(self, i, per):
        self.top, self.mark, self.per = self.n + i * per, self.n, per

    def leave(self, times):
        assert self.n - self.mark == self.per, (self.n - self.mark, self.per)
        self.top, self.n = None, self.mark + times * self.per

    def now(self):
        return self.n if self.top is None else self.top + (self.n - self.mark)

    def wait(self, engine):
        engine.wait_ge(self.sem, self.now())


class Scope:

    def __init__(self, nc, name):
        self.nc, self.name, self.stack, self.sems = nc, name, ExitStack(), []

    def __enter__(self):
        self.stack.__enter__()
        return self

    def __exit__(self, *error):
        self.stack.close()
        numbers = sorted(sem.num for sem in self.sems)
        while numbers:
            n = 1
            while n < len(numbers) and numbers[n] == numbers[0] + n:
                n += 1
            self.nc.gpsimd.sem_clear(range(numbers[0], numbers[0] + n))
            numbers = numbers[n:]

    def sb(self, name, shape, dtype=F32):
        return self.stack.enter_context(self.nc.sbuf_tensor(f"{self.name}_{name}", shape, dtype))

    def psum(self, name, shape, dtype=F32):
        return self.stack.enter_context(self.nc.psum_tensor(f"{self.name}_{name}", shape, dtype))

    def sem(self, name):
        self.sems.append(self.stack.enter_context(self.nc.semaphore(f"{self.name}_{name}")))
        return self.sems[-1]

    def gpsimd_dma_sem(self, name):
        return self.nc.alloc_semaphore(f"{self.name}_{name}")

    def block(self):
        return self.nc.Block()


def row(ap):
    return ap.rearrange("(a n) -> a n", a=1)


def setup(nc, a, keep):
    with Scope(nc, "setup") as s:
        gates_raw = s.sb("gates_raw", [P, 2 * B])
        ctx = s.sb("ctx", [P, 2, D])
        ps = s.psum("ps", [P, 2, 512])
        x_loaded, ctx_loaded, gates_loaded = s.sem("x_loaded"), s.sem("ctx_loaded"), s.sem("gates_loaded")
        zeroed, identity_made, ctx_turned = s.sem("zeroed"), s.sem("identity_made"), s.sem("ctx_turned")
        ctx_kept, gates_made, half_made = s.sem("ctx_kept"), s.sem("gates_made"), s.sem("half_made")
        with s.block() as block:

            @block.sync
            def _(sp):
                sp.dma_start(ctx[:], a["ctx_1024"].rearrange("(u b) k d -> (b k) u d", u=2)).then_inc(ctx_loaded, 16)
                sp.dma_start(keep.x[:], a["x"].rearrange("b (u p) d -> p (b u) d", p=P)).then_inc(x_loaded, 16)
                sp.dma_start(gates_raw[:, 0:B], row(a["g_xattn"]).to_broadcast([P, B])).then_inc(gates_loaded, 16)
                sp.dma_start(gates_raw[:, B:2 * B], row(a["g_ffn"]).to_broadcast([P, B])).then_inc(gates_loaded, 16)
                sp.wait_ge(x_loaded, 16)

            @block.gpsimd
            def _(pool):
                pool.iota(keep.iota[:], pattern=[[1, P]], base=0, channel_multiplier=0,
                          allow_small_or_imprecise_dtypes=True)
                pool.iota(keep.iota_tiles[:], pattern=[[P, NT]], base=0, channel_multiplier=0,
                          allow_small_or_imprecise_dtypes=True)
                pool.iota(keep.token[:], pattern=[[P, NT]], base=0, channel_multiplier=1,
                          allow_small_or_imprecise_dtypes=True)
                pool.memset(keep.identity[:], 0.0).then_inc(zeroed, 1)
                pool.memset(keep.neg_half[:], -0.5).then_inc(half_made, 1)
                pool.wait_ge(zeroed, 1)
                pool.affine_select(out=keep.identity[:], in_=keep.identity[:], compare_op=ALU.not_equal, fill=1.0,
                                   base=0, pattern=[[-1, P]], channel_multiplier=1).then_inc(identity_made, 1)

            @block.scalar
            def _(act):
                act.wait_ge(gates_loaded, 32)
                act.activation(keep.gates[:], gates_raw[:], ACT.Tanh).then_inc(gates_made, 1)

            @block.tensor
            def _(pe):
                pe.wait_ge(ctx_loaded, 16)
                pe.wait_ge(identity_made, 1)
                for u in range(2):
                    pe.transpose(ps[:, u, 0:P], ctx[:, u, :], keep.identity[:]).then_inc(ctx_turned, 1)

            @block.vector
            def _(dve):
                for u in range(2):
                    dve.wait_ge(ctx_turned, u + 1)
                    dve.tensor_copy(keep.ctx_t[:, u * P:(u + 1) * P], ps[:, u, 0:P]).then_inc(ctx_kept, 1)


def head_operands(nc, a, keep, name, weights, biases, scale, scores_rhs, values_rhs, score_bias):
    pairs = 8
    with Scope(nc, name) as s:
        wq, wk, wv = (s.sb(n, [P, pairs * P]) for n in ("wq", "wk", "wv"))
        wo = s.sb("wo", [P, pairs, D])
        wq_t = s.sb("wq_t", [P, 2, P])
        k_t = s.sb("k_t", [P, 2, B * C])
        v_diag = s.sb("v_diag", [P, 2, B, 2, C])
        bias_rows = s.sb("bias_rows", [3 * pairs, P])
        bias = s.sb("bias", [P, 3 * pairs])
        ps = s.psum("ps", [P, 8, 512])
        names = ["loaded", "bias_loaded", "bias_turned", "bias_kept", "wq_turned", "wq_kept", "kv_made", "k_kept",
                 "v_kept", "scores_made", "scores_kept", "bias_done", "values_made",
                 "values_kept", "diag_zeroed"]
        sem = {n: s.sem(n) for n in names}
        loads = 4
        with s.block() as block:

            @block.sync
            def _(sp):
                for to, w in zip((wq, wk, wv), weights[:3]):
                    if len(w.shape) == 3:
                        sp.dma_start(to[:].rearrange("i (h o) -> i h o", o=C),
                                     w.rearrange("h i o -> i h o")).then_inc(sem["loaded"], 16)
                    else:
                        sp.dma_start(to[:], w).then_inc(sem["loaded"], 16)
                wo_rows = weights[3].rearrange("h o n -> (h o) n") if len(weights[3].shape) == 3 else weights[3]
                sp.dma_start(wo[:], wo_rows.rearrange("(p r) n -> r p n", r=P)).then_inc(sem["loaded"], 16)
                if biases:
                    for n, v in enumerate(biases):
                        sp.dma_start(bias_rows[n * pairs:(n + 1) * pairs, :],
                                     v.rearrange("(p r) -> p r", r=P)).then_inc(sem["bias_loaded"], 16)

            @block.gpsimd
            def _(pool):
                pool.memset(v_diag[:], 0.0).then_inc(sem["diag_zeroed"], 1)

            @block.tensor
            def _(pe):
                def project(p):
                    u, cols = p % 2, slice(p * P, (p + 1) * P)
                    if p >= 2:
                        pe.wait_ge(sem["wq_kept"], p - 1)
                        pe.wait_ge(sem["k_kept"], p - 1)
                        pe.wait_ge(sem["v_kept"], 2 * (p - 1))
                    pe.transpose(ps[:, 2 + u, 0:P], wq[:, cols], keep.identity[:]).then_inc(sem["wq_turned"], 1)
                    pe.matmul(ps[:, u, 0:256], wk[:, cols], keep.ctx_t[:], start=True, stop=True)
                    pe.matmul(ps[:, u, 256:512], wv[:, cols], keep.ctx_t[:], start=True, stop=True)\
                        .then_inc(sem["kv_made"], 1)

                def fold(p):
                    u = p % 2
                    pe.wait_ge(sem["wq_kept"], p + 1)
                    pe.wait_ge(sem["k_kept"], p + 1)
                    if p >= 1:
                        pe.wait_ge(sem["scores_kept"], p)
                        if biases:
                            pe.wait_ge(sem["bias_done"], p)
                    for e in range(2):
                        rows = slice(e * C, (e + 1) * C)
                        mm = pe.matmul(ps[:, 4 + e, 0:256], wq_t[rows, u, :], k_t[rows, u, :], start=True, stop=True)
                        if biases:
                            mm = pe.matmul(ps[:, 4 + e, 256:512], bias[rows, p:p + 1].to_broadcast([C, P]),
                                           k_t[rows, u, :], start=True, stop=True)
                        mm.then_inc(sem["scores_made"], 1)
                    pe.wait_ge(sem["v_kept"], 2 * (p + 1))
                    if p >= 2:
                        pe.wait_ge(sem["values_kept"], p - 1)
                    for b in range(B):
                        mm = pe.matmul(ps[:, 6 + u, b * D:(b + 1) * D],
                                       v_diag[:, u, b, :, :].rearrange("r e k -> r (e k)"), wo[:, p, :],
                                       start=True, stop=True)
                    mm.then_inc(sem["values_made"], 1)

                pe.wait_ge(sem["loaded"], 16 * loads)
                if biases:
                    pe.wait_ge(sem["bias_loaded"], 48)
                    pe.transpose(ps[:, 7, 0:3 * pairs], bias_rows[:], keep.identity[0:3 * pairs, 0:3 * pairs])\
                        .then_inc(sem["bias_turned"], 1)
                    pe.wait_ge(sem["bias_kept"], 1)
                project(0)
                for p in range(pairs):
                    if p + 1 < pairs:
                        project(p + 1)
                    fold(p)

            @block.scalar
            def _(act):
                def keep_wq(p):
                    act.wait_ge(sem["wq_turned"], p + 1)
                    if p >= 2:
                        act.wait_ge(sem["scores_made"], 2 * (p - 1))
                    act.activation(wq_t[:, p % 2, :], ps[:, 2 + p % 2, 0:P], ACT.Copy).then_inc(sem["wq_kept"], 1)

                keep_wq(0)
                for p in range(pairs):
                    if p + 1 < pairs:
                        keep_wq(p + 1)
                    act.wait_ge(sem["scores_made"], 2 * (p + 1))
                    act.activation(scores_rhs[:, :, p * P:(p + 1) * P].rearrange("i b (e k) -> i e b k", e=2),
                                   ps[:, 4:6, 0:256].rearrange("i e (b k) -> i e b k", b=B), ACT.Copy, scale=scale)\
                        .then_inc(sem["scores_kept"], 1)
                    if biases:
                        act.activation(score_bias[:, :, p * P:(p + 1) * P].rearrange("i b (e k) -> i e b k", e=2),
                                       ps[:, 4:6, 256:512].rearrange("i e (b k) -> i e b k", b=B), ACT.Copy,
                                       scale=scale).then_inc(sem["bias_done"], 1)

            @block.vector
            def _(dve):
                if biases:
                    dve.wait_ge(sem["bias_turned"], 1)
                    dve.tensor_copy(bias[:], ps[:, 7, 0:3 * pairs]).then_inc(sem["bias_kept"], 1)
                    dve.wait_ge(sem["bias_kept"], 1)

                def keep_kv(p):
                    u = p % 2
                    dve.wait_ge(sem["kv_made"], p + 1)
                    if p >= 2:
                        dve.wait_ge(sem["scores_made"], 2 * (p - 1))
                    bk = bias[:, pairs + p:pairs + p + 1] if biases else 0.0
                    dve.tensor_scalar(k_t[:, u, :], ps[:, u, 0:256], bk, None, ALU.add).then_inc(sem["k_kept"], 1)
                    if p >= 2:
                        dve.wait_ge(sem["values_made"], p - 1)
                    for e in range(2):
                        rows = slice(e * C, (e + 1) * C)
                        bv = bias[rows, 2 * pairs + p:2 * pairs + p + 1] if biases else 0.0
                        dve.tensor_scalar(v_diag[rows, u, :, e, :],
                                          ps[rows, u, 256:512].rearrange("r (b k) -> r b k", b=B), bv, None, ALU.add)\
                            .then_inc(sem["v_kept"], 1)

                dve.wait_ge(sem["diag_zeroed"], 1)
                keep_kv(0)
                for p in range(pairs):
                    if p + 1 < pairs:
                        keep_kv(p + 1)
                    dve.wait_ge(sem["values_made"], p + 1)
                    dve.tensor_copy(values_rhs[:, :, p, :], ps[:, 6 + p % 2, :].rearrange("r (b n) -> r b n", b=B))\
                        .then_inc(sem["values_kept"], 1)


def cross_attention(nc, a, keep, name, scores_rhs, values_rhs, score_bias, out_bias, gate, query=None,
                    query_scale=1.0):
    heads, pairs = 16, 8
    width = values_rhs.shape[3]
    own_columns = width < D
    with Scope(nc, name) as s:
        out_bias_rows = s.sb("out_bias_rows", [P, D])
        stats = s.sb("stats", [P, NT, 6])
        moments = s.sb("moments", [P, NT, 2])
        var_eps = s.sb("var_eps", [P, NT])
        rstd = s.sb("rstd", [P, NT])
        xn = s.sb("xn", [P, 2, D])
        xn_t = s.sb("xn_t", [P, 2, P])
        q_t = s.sb("q_t", [P, 2, P]) if query else xn_t
        e = s.sb("e", [P, 2, heads, C])
        probs_t = s.sb("probs_t", [P, 2, pairs, P])
        top = s.sb("top", [P, 2, heads])
        total = s.sb("total", [P, 2, heads])
        inverse = s.sb("inverse", [P, 2, heads])
        change = s.sb("change", [P, 2, D])
        ps_scores = s.psum("ps_scores", [P, 2, heads, C])
        ps_turned = s.psum("ps_turned", [P, 2, 4, P])
        ps_out = s.psum("ps_out", [P, 512])
        ps_xn = s.psum("ps_xn", [P, 512])
        names = ["bias_loaded", "stats_made", "moments_made", "var_ready", "rstd_ready", "xn_ready", "xn_turned",
                 "xn_kept", "q_made", "q_kept", "scores_made", "top_found", "biased", "centred", "exp_done", "total_made",
                 "inverse_made", "probs_ready", "probs_turned", "probs_kept", "out_made", "change_made", "x_done"]
        sem = {n: s.sem(n) for n in names}
        with s.block() as block:

            @block.sync
            def _(sp):
                sp.dma_start(out_bias_rows[:], row(out_bias).to_broadcast([P, D])).then_inc(sem["bias_loaded"], 16)

            @block.gpsimd
            def _(pool):
                pool.wait_ge(sem["var_ready"], 1)
                pool.tensor_tensor(rstd[:], var_eps[:], keep.neg_half[:, 0:NT], ALU.pow).then_inc(sem["rstd_ready"], 1)

                def normalise(t, u):
                    pool.wait_ge(sem["inverse_made"], t + 1)
                    pool.tensor_tensor(e[:, u], e[:, u], inverse[:, u, :, None].to_broadcast([P, heads, C]), ALU.mult)\
                        .then_inc(sem["probs_ready"], 1)

                with pool.Fori(0, NT // 2) as i:
                    for u in range(2):
                        normalise(2 * i + u, u)

            @block.tensor
            def _(pe):
                def turn_xn(t, u, first=False):
                    pe.wait_ge(sem["xn_ready"], t + 1)
                    if not first:
                        pe.wait_ge(sem["xn_kept"], t)
                    if query and not first:
                        pe.wait_ge(sem["q_kept"], t)
                    pe.transpose(ps_xn[:, 0:P], xn[:, u, :], keep.identity[:]).then_inc(sem["xn_turned"], 1)
                    if query:
                        pe.wait_ge(sem["xn_kept"], t + 1)
                        pe.matmul(ps_xn[:, P:2 * P], query[0], xn_t[:, u, :], start=True, stop=True)\
                            .then_inc(sem["q_made"], 1)

                def scores(t, u, b, first=False):
                    pe.wait_ge(sem["q_kept" if query else "xn_kept"], t + 1)
                    if not first:
                        pe.wait_ge(sem["centred"], t - 1)
                    for half in range(2):
                        mm = pe.matmul(ps_scores[:, u, 8 * half:8 * half + 8, :].rearrange("p h k -> p (h k)"),
                                       q_t[:, u, :], scores_rhs[:, b, 512 * half:512 * half + 512],
                                       start=True, stop=True)
                    mm.then_inc(sem["scores_made"], 1)

                def turn_probs(t, u, first=False):
                    pe.wait_ge(sem["probs_ready"], t + 1)
                    for half in range(2):
                        if not first:
                            pe.wait_ge(sem["probs_kept"], 2 * t - 1 + half)
                        for p in range(4 * half, 4 * half + 4):
                            mm = pe.transpose(ps_turned[:, half, p % 4, :],
                                              e[:, u, 2 * p:2 * p + 2, :].rearrange("p h k -> p (h k)"),
                                              keep.identity[:])
                        mm.then_inc(sem["probs_turned"], 1)

                def output(t, u, b, first=False):
                    if not first:
                        pe.wait_ge(sem["change_made"], t)
                    for p in range(pairs):
                        if p % 4 == 0:
                            pe.wait_ge(sem["probs_kept"], 2 * t + 1 + p // 4)
                        to = ps_out[:, p * width:(p + 1) * width] if own_columns else ps_out[:, 0:D]
                        mm = pe.matmul(to, probs_t[:, u, p, :], values_rhs[:, b, p, :],
                                       start=own_columns or p == 0, stop=own_columns or p == pairs - 1)
                    mm.then_inc(sem["out_made"], 1)

                turn_xn(0, 0, True)
                scores(0, 0, 0, True)
                turn_xn(1, 1)
                scores(1, 1, 0, True)

                def step(i, first, last):
                    for u in range(2):
                        t = 2 * i + u
                        if not last:
                            turn_xn(t + 2, u)
                            scores(t + 2, u, i + 1)
                        turn_probs(t, u, first and u == 0)
                        output(t, u, i, first and u == 0)

                step(0, True, False)
                with pe.Fori(1, NT // 2 - 1) as i:
                    step(i, False, False)
                step(NT // 2 - 1, False, True)

            @block.scalar
            def _(act):
                def keep_xn(t, u, first=False):
                    act.wait_ge(sem["xn_turned"], t + 1)
                    if not first:
                        act.wait_ge(sem["q_made" if query else "scores_made"], t - 1)
                    act.activation(xn_t[:, u, :], ps_xn[:, 0:P], ACT.Copy).then_inc(sem["xn_kept"], 1)
                    if query:
                        act.wait_ge(sem["q_made"], t + 1)
                        if not first:
                            act.wait_ge(sem["scores_made"], t - 1)
                        act.activation(q_t[:, u, :], ps_xn[:, P:2 * P], ACT.Identity, bias=query[1],
                                       scale=query_scale)\
                            .then_inc(sem["q_kept"], 1)

                def exp(t, u):
                    act.wait_ge(sem["centred"], t + 1)
                    act.activation(e[:, u], e[:, u], ACT.Exp).then_inc(sem["exp_done"], 1)

                def keep_probs(t, u, first=False):
                    for half in range(2):
                        act.wait_ge(sem["probs_turned"], 2 * t + 1 + half)
                        if not first:
                            act.wait_ge(sem["out_made"], t - 1)
                        act.activation(probs_t[:, u, 4 * half:4 * half + 4, :], ps_turned[:, half], ACT.Copy)\
                            .then_inc(sem["probs_kept"], 1)

                keep_xn(0, 0, True)
                keep_xn(1, 1, True)
                exp(0, 0)

                def step(i, first, last):
                    for u in range(2):
                        t = 2 * i + u
                        if not last:
                            keep_xn(t + 2, u)
                        if not (last and u == 1):
                            exp(t + 1, 1 - u)
                        keep_probs(t, u, first)

                step(0, True, False)
                with act.Fori(1, NT // 2 - 1) as i:
                    step(i, False, False)
                step(NT // 2 - 1, False, True)

            @block.vector
            def _(dve):
                for t in range(NT):
                    dve.bn_stats(stats[:, t, :], keep.x[:, t, :]).then_inc(sem["stats_made"], 1)
                for t in range(NT):
                    dve.wait_ge(sem["stats_made"], t + 1)
                    dve.bn_aggr(moments[:, t, :], stats[:, t, :]).then_inc(sem["moments_made"], 1)
                dve.wait_ge(sem["moments_made"], NT)
                dve.tensor_scalar(var_eps[:], moments[:, :, 1], EPS, None, ALU.add).then_inc(sem["var_ready"], 1)
                dve.wait_ge(sem["rstd_ready"], 1)
                dve.wait_ge(sem["bias_loaded"], 16)

                def normalise(t, u, first=False):
                    if not first:
                        dve.wait_ge(sem["xn_turned"], t - 1)
                    dve.tensor_scalar(xn[:, u, :], keep.x[:, bass.ds(t, 1), :].rearrange("p a d -> p (a d)"),
                                      moments[:, bass.ds(t, 1), 0:1].rearrange("p a d -> p (a d)"),
                                      rstd[:, bass.ds(t, 1)], ALU.subtract, ALU.mult).then_inc(sem["xn_ready"], 1)

                def centre(t, u, b, first=False):
                    dve.wait_ge(sem["scores_made"], t + 1)
                    if not first:
                        dve.wait_ge(sem["probs_turned"], 2 * (t - 1))
                    scored = ps_scores[:, u]
                    if score_bias is not None:
                        dve.tensor_tensor(e[:, u].rearrange("p h k -> p (h k)"),
                                          ps_scores[:, u].rearrange("p h k -> p (h k)"), score_bias[:, b, :],
                                          ALU.add).then_inc(sem["biased"], 1)
                        dve.wait_ge(sem["biased"], t + 1)
                        scored = e[:, u]
                    dve.tensor_reduce(top[:, u, :], scored, AX, ALU.max).then_inc(sem["top_found"], 1)
                    dve.wait_ge(sem["top_found"], t + 1)
                    dve.tensor_tensor(e[:, u], scored, top[:, u, :, None].to_broadcast([P, heads, C]), ALU.subtract)\
                        .then_inc(sem["centred"], 1)

                def sums(t, u, first=False):
                    dve.wait_ge(sem["exp_done"], t + 1)
                    dve.tensor_reduce(total[:, u, :], e[:, u], AX, ALU.add).then_inc(sem["total_made"], 1)
                    dve.wait_ge(sem["total_made"], t + 1)
                    if not first:
                        dve.wait_ge(sem["probs_ready"], t - 1)
                    dve.reciprocal(inverse[:, u, :], total[:, u, :]).then_inc(sem["inverse_made"], 1)

                def update(t, u):
                    dve.wait_ge(sem["out_made"], t + 1)
                    dve.tensor_tensor(change[:, u, :], ps_out[:, 0:D], out_bias_rows[:], ALU.add)\
                        .then_inc(sem["change_made"], 1)
                    dve.wait_ge(sem["change_made"], t + 1)
                    xt = keep.x[:, bass.ds(t, 1), :].rearrange("p a d -> p (a d)")
                    dve.scalar_tensor_tensor(out=xt, in0=change[:, u, :], scalar=gate, in1=xt, op0=ALU.mult,
                                             op1=ALU.add).then_inc(sem["x_done"], 1)

                normalise(0, 0, True)
                normalise(1, 1, True)
                centre(0, 0, 0, True)
                normalise(2, 0)
                centre(1, 1, 0, True)
                sums(0, 0, True)
                normalise(3, 1)
                centre(2, 0, 1)
                sums(1, 1, True)
                update(0, 0)

                def step(i, last):
                    for u in range(2):
                        t = 2 * i + u
                        if not last:
                            normalise(t + 2, u)
                        if u == 0:
                            centre(t + 1, 1, i)
                        elif not last:
                            centre(t + 1, 0, i + 1)
                        sums(t, u)
                        update(t - 1, 1 - u)

                with dve.Fori(1, NT // 2 - 1) as i:
                    step(i, False)
                step(NT // 2 - 1, True)
                update(NT - 1, 1)


EXPERTS, CHOSEN = 8, 2
TILES = CHOSEN * NT + EXPERTS - 1
SLOTS = TILES * P


class Routes:

    def __init__(self, nc, s, name, before=0):
        self.before, self.gathers_before = before, [16 * before * ((TILES + 1) // 2), 16 * before * (TILES // 2)]
        self.weight = s.sb(f"{name}_weight", [P, CHOSEN, NT])
        self.slot = s.sb(f"{name}_slot", [P, CHOSEN, NT], U32)
        self.token_of = s.sb(f"{name}_token", [P, TILES], U32)
        self.expert_of = s.sb(f"{name}_expert", [P, TILES], I32)
        self.tokens = nc.dram_tensor(f"{name}_tokens", [T, D], F32, kind="Internal").ap()
        self.results = nc.dram_tensor(f"{name}_results", [SLOTS, D], F32, kind="Internal").ap()


def route(nc, keep, name, routes, router, gate, weighted):
    with Scope(nc, name) as s:
        ps = s.psum("ps", [P, 6, 512])
        norm = Normed(s, keep, ps[:, 0], ps[:, 1])
        router_rows, router_t = s.sb("router_rows", [EXPERTS, D]), s.sb("router_t", [P, EXPERTS])
        logits, best = s.sb("logits", [P, NT, EXPERTS]), s.sb("best", [P, NT, 8])
        best_at, best_f = s.sb("best_at", [P, NT, 8], U32), s.sb("best_f", [P, CHOSEN, NT])
        chosen, any_chosen = s.sb("chosen", [P, CHOSEN, NT, EXPERTS]), s.sb("any_chosen", [P, NT, EXPERTS])
        before = s.sb("before", [P, P])
        ones = s.sb("ones", [P, P])
        pad = 4
        run = [s.sb(f"run{n}", [P, pad + NT, EXPERTS]) for n in range(2)]
        ends = [s.sb(f"ends{n}", [P, pad + EXPERTS]) for n in range(2)]
        counts = s.sb("counts", [P, NT, EXPERTS])
        over, used = s.sb("over", [P, EXPERTS, EXPERTS]), s.sb("used", [P, EXPERTS])
        rank, slot_of = s.sb("rank", [P, NT, EXPERTS]), s.sb("slot_of", [P, NT, EXPERTS])
        picked, slot_f = s.sb("picked", [P, CHOSEN, NT, EXPERTS]), s.sb("slot_f", [P, CHOSEN, NT])
        slot_i = s.sb("slot_i", [P, 3, CHOSEN * NT], I32)
        place_f = s.sb("place_f", [P, 2, CHOSEN * NT])
        at_row = s.sb("at_row", [P, CHOSEN * NT, P], mybir.dt.float16)
        is_tile = s.sb("is_tile", [P, CHOSEN * NT, TILES])
        at_tile = s.sb("at_tile", [P, CHOSEN * NT, TILES], mybir.dt.float16)
        past, expert_f = s.sb("past", [P, TILES, EXPERTS - 1]), s.sb("expert_f", [P, TILES])
        gap, grown, denominator = (s.sb(n, [P, NT]) for n in ("gap", "grown", "denominator"))
        base = s.sb("base", [P, EXPERTS])
        names = ["router_loaded", "router_turned", "router_kept", "logits_made", "logits_kept", "chosen_ready",
                 "counted", "steps", "gap_ready", "exp_done", "tokens_stored", "order_ready", "order_made",
                 "tables_set", "cut"]
        sem = {n: s.sem(n) for n in names}
        with s.block() as block:

            @block.sync
            def _(sp):
                sp.dma_start(router_rows[:], router).then_inc(sem["router_loaded"], 16)
                sp.wait_ge(norm.xn_ready, NT)
                sp.dma_start(routes.tokens.rearrange("(t p) d -> p t d", p=P), norm.xn[:])\
                    .then_inc(sem["tokens_stored"], 16)
                sp.wait_ge(sem["tokens_stored"], 16)

            @block.gpsimd
            def _(pool):
                norm.gpsimd(pool)
                pool.memset(ones[:], 1.0).then_inc(sem["tables_set"], 1)
                for n in range(2):
                    pool.memset(run[n][:, 0:pad, :], 0.0).then_inc(sem["tables_set"], 1)
                    pool.memset(ends[n][:, 0:pad], 0.0).then_inc(sem["tables_set"], 1)
                pool.wait_ge(sem["tables_set"], 5)
                pool.affine_select(out=before[:], in_=ones[:], compare_op=ALU.is_gt, fill=0.0, base=0,
                                   pattern=[[1, P]], channel_multiplier=-1).then_inc(sem["cut"], 1)

            @block.tensor
            def _(pe):
                pe.wait_ge(sem["router_loaded"], 16)
                pe.transpose(ps[:, 2, 0:EXPERTS], router_rows[:], keep.identity[0:EXPERTS, 0:EXPERTS])\
                    .then_inc(sem["router_turned"], 1)
                norm.tensor(pe)
                pe.wait_ge(sem["router_kept"], 1)
                for t in range(NT):
                    if t % 4 == 0:
                        pe.wait_ge(norm.xt_ready, 1 + t // 4)
                    mm = pe.matmul(ps[:, 3, t * EXPERTS:(t + 1) * EXPERTS], norm.xt[:, t, :], router_t[:],
                                   start=True, stop=True)
                mm.then_inc(sem["logits_made"], 1)
                pe.wait_ge(sem["chosen_ready"], 1)
                pe.wait_ge(sem["cut"], 1)
                flat = any_chosen[:].rearrange("p t e -> p (t e)")
                pe.matmul(ps[:, 4, 0:NT * EXPERTS], before[:], flat, start=True, stop=True)
                pe.matmul(ps[:, 4, 256:256 + NT * EXPERTS], ones[:], flat, start=True, stop=True)\
                    .then_inc(sem["counted"], 1)
                pe.wait_ge(sem["order_ready"], 1)
                for n in range(CHOSEN * NT):
                    mm = pe.matmul(ps[:, 5, 0:TILES], at_row[:, n, :], at_tile[:, n, :], start=(n == 0),
                                   stop=(n == CHOSEN * NT - 1))
                mm.then_inc(sem["order_made"], 1)

            @block.scalar
            def _(act):
                act.wait_ge(sem["router_turned"], 1)
                act.activation(router_t[:], ps[:, 2, 0:EXPERTS], ACT.Copy).then_inc(sem["router_kept"], 1)
                norm.scalar(act)
                if weighted:
                    act.wait_ge(sem["gap_ready"], 1)
                    act.activation(grown[:], gap[:], ACT.Exp).then_inc(sem["exp_done"], 1)

            @block.vector
            def _(dve):
                norm.vector(dve)
                steps = Tally(sem["steps"])

                def then(instruction):
                    steps.add(instruction)
                    steps.wait(dve)

                dve.wait_ge(sem["logits_made"], 1)
                then(dve.tensor_copy(logits[:].rearrange("p t e -> p (t e)"), ps[:, 3, 0:NT * EXPERTS]))
                for t in range(NT):
                    steps.add(dve.max(best[:, t, :], logits[:, t, :]))
                steps.wait(dve)
                for t in range(NT):
                    steps.add(dve.max_index(best_at[:, t, :], best[:, t, :], logits[:, t, :]))
                steps.wait(dve)
                if weighted:
                    dve.tensor_tensor(gap[:], best[:, :, 1], best[:, :, 0], ALU.subtract).then_inc(sem["gap_ready"], 1)
                then(dve.tensor_copy(best_f[:], best_at[:, :, 0:CHOSEN].rearrange("p t k -> p k t")))
                for k in range(CHOSEN):
                    steps.add(dve.tensor_tensor(chosen[:, k], keep.iota[:, None, 0:EXPERTS].to_broadcast([P, NT, EXPERTS]),
                                                best_f[:, k, :, None].to_broadcast([P, NT, EXPERTS]), ALU.is_equal))
                steps.wait(dve)
                dve.tensor_tensor(any_chosen[:], chosen[:, 0], chosen[:, 1], ALU.add).then_inc(sem["chosen_ready"], 1)
                if weighted:
                    dve.wait_ge(sem["exp_done"], 1)
                    then(dve.tensor_scalar(denominator[:], grown[:], 1.0, None, ALU.add))
                    then(dve.reciprocal(gap[:], denominator[:]))
                    then(dve.tensor_scalar(routes.weight[:, 0, :], gap[:], gate, None, ALU.mult))
                    steps.add(dve.tensor_tensor(routes.weight[:, 1, :], grown[:], routes.weight[:, 0, :], ALU.mult))
                else:
                    steps.add(dve.tensor_scalar(routes.weight[:], keep.neg_half[:, 0:CHOSEN * NT].rearrange(
                        "p (k t) -> p k t", k=CHOSEN), gate, -1.0, ALU.mult, ALU.mult))
                dve.wait_ge(sem["counted"], 1)
                dve.wait_ge(sem["tables_set"], 5)
                then(dve.tensor_copy(run[0][:, pad:, :].rearrange("p t e -> p (t e)"), ps[:, 4, 256:256 + NT * EXPERTS]))
                then(dve.tensor_tensor(run[1][:, pad:, :], run[0][:, pad:, :], run[0][:, pad - 1:-1, :], ALU.add))
                steps.add(dve.tensor_copy(counts[:], run[0][:, pad:, :]))
                steps.wait(dve)
                then(dve.tensor_tensor(run[0][:, pad:, :], run[1][:, pad:, :], run[1][:, pad - 2:-2, :], ALU.add))
                then(dve.tensor_tensor(run[1][:, pad:, :], run[0][:, pad:, :], run[0][:, pad - 4:-4, :], ALU.add))
                then(dve.tensor_tensor(over[:], run[1][:, pad + NT - 1, :, None].to_broadcast([P, EXPERTS, NT]),
                                       keep.iota_tiles[:, None, 0:NT].to_broadcast([P, EXPERTS, NT]), ALU.is_gt))
                then(dve.tensor_reduce(used[:], over[:], AX, ALU.add))
                then(dve.tensor_copy(ends[0][:, pad:], used[:]))
                then(dve.tensor_tensor(ends[1][:, pad:], ends[0][:, pad:], ends[0][:, pad - 1:-1], ALU.add))
                then(dve.tensor_tensor(ends[0][:, pad:], ends[1][:, pad:], ends[1][:, pad - 2:-2], ALU.add))
                then(dve.tensor_tensor(ends[1][:, pad:], ends[0][:, pad:], ends[0][:, pad - 4:-4], ALU.add))
                then(dve.tensor_tensor(base[:], ends[1][:, pad:], used[:], ALU.subtract))
                then(dve.tensor_tensor(rank[:], run[1][:, pad:, :], counts[:], ALU.subtract))
                then(dve.tensor_tensor(rank[:].rearrange("p t e -> p (t e)"), rank[:].rearrange("p t e -> p (t e)"),
                                       ps[:, 4, 0:NT * EXPERTS], ALU.add))
                then(dve.scalar_tensor_tensor(out=slot_of[:], in0=base[:, None, :].to_broadcast([P, NT, EXPERTS]),
                                              scalar=float(P), in1=rank[:], op0=ALU.mult, op1=ALU.add))
                for k in range(CHOSEN):
                    steps.add(dve.tensor_tensor(picked[:, k], chosen[:, k], slot_of[:], ALU.mult))
                steps.wait(dve)
                then(dve.tensor_reduce(slot_f[:], picked[:], AX, ALU.add))
                flat_slot = slot_f[:].rearrange("p k t -> p (k t)")
                steps.add(dve.tensor_copy(routes.slot[:].rearrange("p k t -> p (k t)"), flat_slot))
                then(dve.tensor_copy(slot_i[:, 0, :], flat_slot))
                steps.add(dve.tensor_scalar(slot_i[:, 1, :], slot_i[:, 0, :], 7, None, ALU.logical_shift_right))
                then(dve.tensor_scalar(slot_i[:, 2, :], slot_i[:, 0, :], P - 1, None, ALU.bitwise_and))
                then(dve.tensor_copy(place_f[:], slot_i[:, 1:3, :]))
                n = CHOSEN * NT
                for m in range(n):
                    steps.add(dve.tensor_scalar(at_row[:, m, :], keep.iota[:], place_f[:, 1, m:m + 1], None, ALU.is_equal))
                then(dve.tensor_tensor(is_tile[:], keep.iota[:, None, 0:TILES].to_broadcast([P, n, TILES]),
                                       place_f[:, 0, :, None].to_broadcast([P, n, TILES]), ALU.is_equal))
                for k in range(CHOSEN):
                    half = slice(k * NT, (k + 1) * NT)
                    ins = steps.add(dve.tensor_tensor(at_tile[:, half, :], is_tile[:, half, :],
                                                      keep.token[:, :, None].to_broadcast([P, NT, TILES]), ALU.mult))
                steps.wait(dve)
                dve.engine_nop().then_inc(sem["order_ready"], 1)
                then(dve.tensor_tensor(past[:], keep.iota[:, 0:TILES, None].to_broadcast([P, TILES, EXPERTS - 1]),
                                       ends[1][:, None, pad:pad + EXPERTS - 1].to_broadcast([P, TILES, EXPERTS - 1]),
                                       ALU.is_ge))
                then(dve.tensor_reduce(expert_f[:], past[:], AX, ALU.add))
                steps.add(dve.tensor_copy(routes.expert_of[:], expert_f[:]))
                dve.wait_ge(sem["order_made"], 1)
                steps.add(dve.tensor_copy(routes.token_of[:], ps[:, 5, 0:TILES]))


def pairs_of_tiles(engine, first, last, step):
    pairs = (last - first + 1) // 2
    with engine.Fori(0, pairs) as i:
        for u in range(2):
            step(first + 2 * i + u, (first + u) % 2)
    for j in range(first + 2 * pairs, last + 1):
        step(j, j % 2)


def expert_index(engine, routes, j):
    return engine.value_load(routes.expert_of[0:1, bass.ds(j, 1)], min_val=0, max_val=EXPERTS - 1)


def gather_tiles(pool, keep, sem, routes, slots):
    for j in range(TILES):
        u = j % 2
        if j >= 2:
            pool.wait_ge(sem["turned"], j - 1)
            pool.wait_ge(keep.gathered[u], routes.gathers_before[u] + 16 * (j // 2))
        pool.indirect_dma_start(slots[:, u, :], None, routes.tokens,
                                bass.IndirectOffsetOnAxis(ap=routes.token_of[:, j:j + 1], axis=0))\
            .then_inc(keep.gathered[u], 16)


def store_results(sp, sem, routes, results):
    def step(j, u):
        sp.wait_ge(sem["result_kept"], j + 1)
        sp.dma_start(routes.results[bass.ds(j * P, P), :], results[:, u, :]).then_inc(sem["stored"][u], 16)

    step(0, 0)
    pairs_of_tiles(sp, 1, TILES - 1, step)
    sp.wait_ge(sem["stored"][0], 16 * ((TILES + 1) // 2))
    sp.wait_ge(sem["stored"][1], 16 * (TILES // 2))


def gelu_experts(nc, keep, name, routes, w1, w2, w3, b1, b2, b3):
    hidden = w1.shape[2]
    chunks = hidden // P
    with Scope(nc, name) as s:
        slots, slots_t = s.sb("slots", [P, 2, D]), s.sb("slots_t", [P, 2, P])
        rows1, rows2 = s.sb("rows1", [P, 2, hidden]), s.sb("rows2", [P, 2, hidden])
        act1, act2 = s.sb("act1", [P, 2, chunks, P]), s.sb("act2", [P, 2, chunks, P])
        results = s.sb("results", [P, 2, D])
        ps = s.psum("ps", [P, 6, 512])
        ps_x, ps_1, ps_1t, ps_2, ps_2t, ps_y = (ps[:, n] for n in range(6))
        names = ["turned", "slots_kept", "rows1_made", "rows1_kept", "rows1_turned", "act1_done", "rows2_made",
                 "rows2_kept", "rows2_turned", "act2_done", "result_made", "result_kept"]
        sem = {n: s.sem(n) for n in names}
        sem["stored"] = [s.sem("stored0"), s.sem("stored1")]
        with s.block() as block:

            @block.gpsimd
            def _(pool):
                gather_tiles(pool, keep, sem, routes, slots)

            @block.sync
            def _(sp):
                store_results(sp, sem, routes, results)

            @block.tensor
            def _(pe):
                def turn_slots(j, u, half, first=False):
                    pe.wait_ge(keep.gathered[u], 16 * (half + 1) + routes.gathers_before[u])
                    if not first:
                        pe.wait_ge(sem["slots_kept"], j)
                    pe.transpose(ps_x[:, 0:P], slots[:, u, :], keep.identity[:]).then_inc(sem["turned"], 1)

                def layer1(j, u, first=False):
                    e = expert_index(pe, routes, j)
                    pe.wait_ge(sem["slots_kept"], j + 1)
                    if not first:
                        pe.wait_ge(sem["rows1_kept"], j)
                    pe.matmul(ps_1, slots_t[:, u, :], w1[:, bass.ds(e, 1), :].rearrange("d a h -> d (a h)"),
                              start=True, stop=True).then_inc(sem["rows1_made"], 1)

                def turn1(j, u, first=False):
                    pe.wait_ge(sem["rows1_kept"], j + 1)
                    if not first:
                        pe.wait_ge(sem["act1_done"], chunks * j)
                    for c in range(chunks):
                        mm = pe.transpose(ps_1t[:, c * P:(c + 1) * P], rows1[:, u, c * P:(c + 1) * P], keep.identity[:])
                    mm.then_inc(sem["rows1_turned"], 1)

                def layer2(j, u, first=False):
                    e = expert_index(pe, routes, j)
                    pe.wait_ge(sem["act1_done"], chunks * (j + 1))
                    if not first:
                        pe.wait_ge(sem["rows2_kept"], j)
                    for c in range(chunks):
                        mm = pe.matmul(ps_2, act1[:, u, c, :],
                                       w2[:, bass.ds(e, 1), c, :].rearrange("d a h -> d (a h)"),
                                       start=(c == 0), stop=(c == chunks - 1))
                    mm.then_inc(sem["rows2_made"], 1)

                def turn2(j, u, first=False):
                    pe.wait_ge(sem["rows2_kept"], j + 1)
                    if not first:
                        pe.wait_ge(sem["act2_done"], chunks * j)
                    for c in range(chunks):
                        mm = pe.transpose(ps_2t[:, c * P:(c + 1) * P], rows2[:, u, c * P:(c + 1) * P], keep.identity[:])
                    mm.then_inc(sem["rows2_turned"], 1)

                def layer3(j, u, first=False):
                    e = expert_index(pe, routes, j)
                    pe.wait_ge(sem["act2_done"], chunks * (j + 1))
                    if not first:
                        pe.wait_ge(sem["result_kept"], j)
                    for c in range(chunks):
                        mm = pe.matmul(ps_y[:, 0:D], act2[:, u, c, :],
                                       w3[:, bass.ds(e, 1), c, :].rearrange("d a h -> d (a h)"),
                                       start=(c == 0), stop=(c == chunks - 1))
                    mm.then_inc(sem["result_made"], 1)

                turn_slots(0, 0, 0, True)
                layer1(0, 0, True)
                turn_slots(1, 1, 0)
                turn1(0, 0, True)
                layer1(1, 1)
                layer2(0, 0, True)
                turn1(1, 1)
                turn_slots(2, 0, 1)
                turn2(0, 0, True)

                def steady(i):
                    for u in range(2):
                        j = 1 + 2 * i + u
                        layer1(j + 1, u)
                        layer2(j, 1 - u)
                        turn1(j + 1, u)
                        turn_slots(j + 2, 1 - u, i + 1 + u)
                        layer3(j - 1, u, False) if not isinstance(j, int) else layer3(j - 1, u, j == 1)
                        turn2(j, 1 - u)

                steady(0)
                with pe.Fori(1, (TILES - 3) // 2) as i:
                    steady(i)
                j = TILES - 2
                layer1(j + 1, 0)
                layer2(j, 1)
                turn1(j + 1, 0)
                layer3(j - 1, 0)
                turn2(j, 1)
                layer2(j + 1, 0)
                layer3(j, 1)
                turn2(j + 1, 0)
                layer3(j + 1, 0)

            @block.scalar
            def _(act):
                def gelu(j, u, rows_turned, read, source, to, bias, done, first):
                    e = expert_index(act, routes, j)
                    act.wait_ge(rows_turned, j + 1)
                    if not first:
                        act.wait_ge(read, j - 1)
                    for c in range(chunks):
                        act.activation(to[:, u, c, :], source[:, c * P:(c + 1) * P], ACT.Gelu,
                                       bias=bias[:, bass.ds(e * chunks + c, 1)]).then_inc(done, 1)

                def gelu1(j, u, first=False):
                    gelu(j, u, sem["rows1_turned"], sem["rows2_made"], ps_1t, act1, b1, sem["act1_done"], first)

                def gelu2(j, u, first=False):
                    gelu(j, u, sem["rows2_turned"], sem["result_made"], ps_2t, act2, b2, sem["act2_done"], first)

                gelu1(0, 0, True)
                gelu1(1, 1, True)
                gelu2(0, 0, True)
                gelu1(2, 0)
                gelu2(1, 1, True)

                def step(j, u):
                    gelu1(j + 1, 1 - u)
                    gelu2(j, u)

                with act.Fori(0, (TILES - 3) // 2) as i:
                    step(2 + 2 * i, 0)
                    step(3 + 2 * i, 1)
                gelu2(TILES - 1, (TILES - 1) % 2)

            @block.vector
            def _(dve):
                def keep_slots(j, u, first=False):
                    dve.wait_ge(sem["turned"], j + 1)
                    if not first:
                        dve.wait_ge(sem["rows1_made"], j - 1)
                    dve.tensor_copy(slots_t[:, u, :], ps_x[:, 0:P]).then_inc(sem["slots_kept"], 1)

                def keep1(j, u, first=False):
                    dve.wait_ge(sem["rows1_made"], j + 1)
                    if not first:
                        dve.wait_ge(sem["rows1_turned"], j - 1)
                    dve.tensor_copy(rows1[:, u, :], ps_1).then_inc(sem["rows1_kept"], 1)

                def keep2(j, u, first=False):
                    dve.wait_ge(sem["rows2_made"], j + 1)
                    if not first:
                        dve.wait_ge(sem["rows2_turned"], j - 1)
                    dve.tensor_copy(rows2[:, u, :], ps_2).then_inc(sem["rows2_kept"], 1)

                def keep_result(j, u, half, first=False):
                    e = expert_index(dve, routes, j)
                    dve.wait_ge(sem["result_made"], j + 1)
                    if not first:
                        dve.wait_ge(sem["stored"][u], 16 * half)
                    dve.tensor_tensor(results[:, u, :], ps_y[:, 0:D],
                                      b3[:, bass.ds(e, 1), :].rearrange("p a d -> p (a d)"), ALU.add)\
                        .then_inc(sem["result_kept"], 1)

                keep_slots(0, 0, True)
                keep1(0, 0, True)
                keep_slots(1, 1, True)
                keep1(1, 1, True)
                keep2(0, 0, True)
                keep_slots(2, 0)

                def steady(i, first):
                    for u in range(2):
                        j = 1 + 2 * i + u
                        keep1(j + 1, u)
                        keep2(j, 1 - u, first and u == 0)
                        keep_slots(j + 2, 1 - u)
                        keep_result(j - 1, u, i, first)

                steady(0, True)
                with dve.Fori(1, (TILES - 3) // 2) as i:
                    steady(i, False)
                j = TILES - 2
                keep1(j + 1, 0)
                keep2(j, 1)
                keep_result(j - 1, 0, (j - 1) // 2)
                keep2(j + 1, 0)
                keep_result(j, 1, j // 2)
                keep_result(j + 1, 0, (j + 1) // 2)


def gated_experts(nc, keep, name, routes, w_in, w_out):
    width = w_in.shape[2] // 2
    chunks = width // P
    banks = 2 * width // 512
    with Scope(nc, name) as s:
        slots, slots_t = s.sb("slots", [P, 2, D]), s.sb("slots_t", [P, 2, P])
        gated, gated_t = s.sb("gated", [P, 2, width]), s.sb("gated_t", [P, 2, chunks, P])
        results = s.sb("results", [P, 2, D])
        ps_in = s.psum("ps_in", [P, 2, 512])
        ps_x, ps_t, ps_y = s.psum("ps_x", [P, 512]), s.psum("ps_t", [P, 512]), s.psum("ps_y", [P, 512])
        names = ["turned", "slots_kept", "in_made", "silu_done", "gated_ready", "gated_turned", "gated_kept",
                 "result_made", "result_kept"]
        sem = {n: s.sem(n) for n in names}
        sem["stored"] = [s.sem("stored0"), s.sem("stored1")]
        flat_in = ps_in[:].rearrange("p b n -> p (b n)")
        def gate_part(u):
            return flat_in[:, 0:width] if banks == 2 else flat_in[:, 512 * u:512 * u + width]

        def up_part(u):
            return flat_in[:, width:2 * width] if banks == 2 else flat_in[:, 512 * u + width:512 * u + 2 * width]

        lag = 0 if banks == 2 else 1
        with s.block() as block:

            @block.gpsimd
            def _(pool):
                gather_tiles(pool, keep, sem, routes, slots)

            @block.sync
            def _(sp):
                store_results(sp, sem, routes, results)

            @block.tensor
            def _(pe):
                def turn_slots(j, u, half, first=False):
                    pe.wait_ge(keep.gathered[u], 16 * (half + 1) + routes.gathers_before[u])
                    if not first:
                        pe.wait_ge(sem["slots_kept"], j)
                    pe.transpose(ps_x[:, 0:P], slots[:, u, :], keep.identity[:]).then_inc(sem["turned"], 1)

                def up(j, u, first=False):
                    e = expert_index(pe, routes, j)
                    pe.wait_ge(sem["slots_kept"], j + 1)
                    if not first:
                        pe.wait_ge(sem["gated_ready"], j - lag)
                    for n in range(banks):
                        bank = n if banks == 2 else u
                        mm = pe.matmul(ps_in[:, bank], slots_t[:, u, :],
                                       w_in[:, bass.ds(e, 1), 512 * n:512 * n + 512].rearrange("d a h -> d (a h)"),
                                       start=True, stop=True)
                    mm.then_inc(sem["in_made"], 1)

                def turn(j, u, first=False):
                    pe.wait_ge(sem["gated_ready"], j + 1)
                    if not first:
                        pe.wait_ge(sem["gated_kept"], j)
                    for c in range(chunks):
                        mm = pe.transpose(ps_t[:, c * P:(c + 1) * P], gated[:, u, c * P:(c + 1) * P], keep.identity[:])
                    mm.then_inc(sem["gated_turned"], 1)

                def down(j, u, first=False):
                    e = expert_index(pe, routes, j)
                    pe.wait_ge(sem["gated_kept"], j + 1)
                    if not first:
                        pe.wait_ge(sem["result_kept"], j)
                    for c in range(chunks):
                        mm = pe.matmul(ps_y[:, 0:D], gated_t[:, u, c, :],
                                       w_out[:, bass.ds(e, 1), c, :].rearrange("d a h -> d (a h)"),
                                       start=(c == 0), stop=(c == chunks - 1))
                    mm.then_inc(sem["result_made"], 1)

                turn_slots(0, 0, 0, True)
                up(0, 0, True)
                turn_slots(1, 1, 0)
                up(1, 1, lag == 1)
                turn(0, 0, True)
                turn_slots(2, 0, 1)

                def steady(i, first):
                    for u in range(2):
                        j = 1 + 2 * i + u
                        up(j + 1, u)
                        down(j - 1, u, first and u == 0)
                        turn(j, 1 - u)
                        turn_slots(j + 2, 1 - u, i + 1 + u)

                steady(0, True)
                with pe.Fori(1, (TILES - 3) // 2) as i:
                    steady(i, False)
                j = TILES - 2
                up(j + 1, 0)
                down(j - 1, 0)
                turn(j, 1)
                down(j, 1)
                turn(j + 1, 0)
                down(j + 1, 0)

            @block.scalar
            def _(act):
                def silu(j, u, first=False):
                    act.wait_ge(sem["in_made"], j + 1)
                    if not first:
                        act.wait_ge(sem["gated_turned"], j - 1)
                    act.activation(gated[:, u, :], gate_part(u), ACT.Silu).then_inc(sem["silu_done"], 1)

                def keep_gated(j, u, first=False):
                    act.wait_ge(sem["gated_turned"], j + 1)
                    if not first:
                        act.wait_ge(sem["result_made"], j - 1)
                    act.activation(gated_t[:, u, :, :].rearrange("p c k -> p (c k)"), ps_t[:, 0:width], ACT.Copy)\
                        .then_inc(sem["gated_kept"], 1)

                silu(0, 0, True)
                silu(1, 1, True)
                keep_gated(0, 0, True)
                silu(2, 0)
                keep_gated(1, 1, True)
                with act.Fori(0, (TILES - 3) // 2) as i:
                    for u in range(2):
                        silu(3 + 2 * i + u, 1 - u)
                        keep_gated(2 + 2 * i + u, u)
                keep_gated(TILES - 1, 0)

            @block.vector
            def _(dve):
                def keep_slots(j, u, first=False):
                    dve.wait_ge(sem["turned"], j + 1)
                    if not first:
                        dve.wait_ge(sem["in_made"], j - 1)
                    dve.tensor_copy(slots_t[:, u, :], ps_x[:, 0:P]).then_inc(sem["slots_kept"], 1)

                def multiply(j, u):
                    dve.wait_ge(sem["silu_done"], j + 1)
                    dve.tensor_tensor(gated[:, u, :], gated[:, u, :], up_part(u), ALU.mult)\
                        .then_inc(sem["gated_ready"], 1)

                def keep_result(j, u, half, first=False):
                    dve.wait_ge(sem["result_made"], j + 1)
                    if not first:
                        dve.wait_ge(sem["stored"][u], 16 * half)
                    dve.tensor_copy(results[:, u, :], ps_y[:, 0:D]).then_inc(sem["result_kept"], 1)

                keep_slots(0, 0, True)
                keep_slots(1, 1, True)
                multiply(0, 0)
                multiply(1, 1)
                keep_slots(2, 0)

                def steady(i, first):
                    for u in range(2):
                        j = 1 + 2 * i + u
                        multiply(j + 1, u)
                        keep_result(j - 1, u, i, first)
                        keep_slots(j + 2, 1 - u)

                steady(0, True)
                with dve.Fori(1, (TILES - 3) // 2) as i:
                    steady(i, False)
                j = TILES - 2
                multiply(j + 1, 0)
                keep_result(j - 1, 0, (j - 1) // 2)
                keep_result(j, 1, j // 2)
                keep_result(j + 1, 0, (j + 1) // 2)


def combine(nc, keep, name, routes):
    with Scope(nc, name) as s:
        mine = s.sb("mine", [P, CHOSEN, NT, D])
        got = keep.got
        added = s.sem("added")
        with s.block() as block:

            @block.gpsimd
            def _(pool):
                for t in range(NT):
                    for k in range(CHOSEN):
                        pool.indirect_dma_start(mine[:, k, t, :], None, routes.results,
                                                bass.IndirectOffsetOnAxis(ap=routes.slot[:, k, t:t + 1], axis=0))\
                            .then_inc(got[CHOSEN * t + k], 16)

            @block.vector
            def _(dve):
                for t in range(NT):
                    for k in range(CHOSEN):
                        dve.wait_ge(got[CHOSEN * t + k], 16 * (routes.before + 1))
                        if k:
                            dve.wait_ge(added, CHOSEN * t + k)
                        dve.scalar_tensor_tensor(out=keep.x[:, t, :], in0=mine[:, k, t, :],
                                                 scalar=routes.weight[:, k, t:t + 1], in1=keep.x[:, t, :],
                                                 op0=ALU.mult, op1=ALU.add).then_inc(added, 1)



def turn_gated_weights(nc, a, keep, name, gate_up, down, w_in, w_out):
    width = down.shape[2]
    jobs = []
    for e in range(EXPERTS):
        for n in range(2 * width // 512):
            jobs.append((gate_up[:, e, 4 * n:4 * n + 4, :], w_in[:, e, 512 * n:512 * n + 512]))
        jobs.append((down[:, e, :].rearrange("o (c k) -> o c k", k=P), w_out[:, e, :, :].rearrange("k c o -> k (c o)")))
    with Scope(nc, name) as s:
        ps = s.psum("ps", [P, 4, 512])
        turned, kept_act, kept_dve = s.sem("turned"), s.sem("kept_act"), s.sem("kept_dve")
        with s.block() as block:

            @block.tensor
            def _(pe):
                for e, n in enumerate(keep.raw_loaded):
                    pe.wait_ge(n, 16)
                for m, (source, _) in enumerate(jobs):
                    if m >= 4:
                        pe.wait_ge(kept_dve if m % 2 else kept_act, m // 2 - 1)
                    for c in range(4):
                        mm = pe.transpose(ps[:, m % 4, c * P:(c + 1) * P], source[:, c, :], keep.identity[:])
                    mm.then_inc(turned, 1)

            @block.scalar
            def _(act):
                for m in range(0, len(jobs), 2):
                    act.wait_ge(turned, m + 1)
                    act.activation(jobs[m][1], ps[:, m % 4, :], ACT.Copy).then_inc(kept_act, 1)

            @block.vector
            def _(dve):
                for m in range(1, len(jobs), 2):
                    dve.wait_ge(turned, m + 1)
                    dve.tensor_copy(jobs[m][1], ps[:, m % 4, :]).then_inc(kept_dve, 1)



TAPS = 9


def conv_kernels(nc, a, keep, name, taps):
    heads, wide, inner = 16, 2 * D, 64
    with Scope(nc, name) as s:
        hist_w = s.sb("hist_w", [P, wide])
        hist_rows = s.sb("hist_rows", [P, 3, wide])
        ctx_w1, ctx_b1 = s.sb("ctx_w1", [P, 2, inner]), s.sb("ctx_b1", [inner, 1])
        ctx_w2, ctx_b2 = s.sb("ctx_w2", [inner, 1]), s.sb("ctx_b2", [1, 1])
        kg_w1, kg_rows = s.sb("kg_w1", [P, 2, D]), s.sb("kg_rows", [B, 3, D])
        kg_w2, kg_b2 = s.sb("kg_w2", [P, heads * TAPS]), s.sb("kg_b2", [B, heads * TAPS])
        eh, eh_t = s.sb("eh", [P, 2, wide]), s.sb("eh_t", [P, 2, 2, P])
        stats, moments, rstd = s.sb("stats", [P, 2, 6]), s.sb("moments", [P, 2, 2]), s.sb("rstd", [P, 2, 1])
        inner_act, one = s.sb("inner_act", [inner, B * C]), s.sb("one", [1, 1])
        aw, aw_top, aw_sum = s.sb("aw", [1, B, C]), s.sb("aw_top", [1, B]), s.sb("aw_sum", [1, B])
        aw_cols, cc_t = s.sb("aw_cols", [P, 2, 2]), s.sb("cc_t", [P, 2, B])
        kp, kp_stats, kp_moments = s.sb("kp", [B, D]), s.sb("kp_stats", [B, 6]), s.sb("kp_moments", [B, 2])
        kp_rstd, kp_t = s.sb("kp_rstd", [B, 1]), s.sb("kp_t", [P, B])
        kernels = s.sb("kernels", [B, heads, TAPS])
        k_top, k_sum = s.sb("k_top", [B, heads]), s.sb("k_sum", [B, heads])
        ps = s.psum("ps", [P, 8, 512])
        ones = s.sb("ones", [P, 2])
        names = ["hist_loaded", "ctx_loaded", "kg_loaded", "hist_made", "eh_steps", "var_ready", "rstd_ready", "gelu_in",
                 "eh_ready", "eh_turned", "eh_kept", "inner_made", "inner_ready", "aw_made", "aw_steps", "aw_centred",
                 "aw_exp", "aw_ready", "ones_set", "cols_made", "cols_ready", "cc_made", "cc_ready", "kp_made",
                 "kp_steps", "kp_var", "kp_rstd_ready", "kp_gelu_in", "kp_ready", "kp_turned", "kp_kept", "k_made",
                 "k_centred", "k_exp", "k_ready", "taps_made", "taps_ready"]
        sem = {n: s.sem(n) for n in names}

        def rows_of(v, rows, n):
            return row(a[v]).to_broadcast([rows, n])

        with s.block() as block:

            @block.sync
            def _(sp):
                sp.dma_start(hist_w[:], a["L3_xattn_hist_W"]).then_inc(sem["hist_loaded"], 16)
                for n, v in enumerate(("hist_b", "hist_ln_g", "hist_ln_b")):
                    sp.dma_start(hist_rows[:, n, :], rows_of("L3_xattn_" + v, P, wide)).then_inc(sem["hist_loaded"], 16)
                sp.dma_start(ctx_w1[:], a["L3_xattn_ctx_W1"].rearrange("(c d) n -> d c n", d=P))\
                    .then_inc(sem["ctx_loaded"], 16)
                sp.dma_start(ctx_b1[:], a["L3_xattn_ctx_b1"].rearrange("(p c) -> p c", c=1)).then_inc(sem["ctx_loaded"], 16)
                sp.dma_start(ctx_w2[:], a["L3_xattn_ctx_W2"]).then_inc(sem["ctx_loaded"], 16)
                sp.dma_start(ctx_b2[:], row(a["L3_xattn_ctx_b2"])).then_inc(sem["ctx_loaded"], 16)
                sp.dma_start(kg_w1[:], a["L3_xattn_kg_W1"].rearrange("(c d) n -> d c n", d=P)).then_inc(sem["kg_loaded"], 16)
                for n, v in enumerate(("kg_b1", "kg_ln_g", "kg_ln_b")):
                    sp.dma_start(kg_rows[:, n, :], rows_of("L3_xattn_" + v, B, D)).then_inc(sem["kg_loaded"], 16)
                sp.dma_start(kg_w2[:], a["L3_xattn_kg_W2"]).then_inc(sem["kg_loaded"], 16)
                sp.dma_start(kg_b2[:], rows_of("L3_xattn_kg_b2", B, heads * TAPS)).then_inc(sem["kg_loaded"], 16)

            @block.gpsimd
            def _(pool):
                pool.memset(one[:], 1.0).then_inc(sem["ones_set"], 1)
                pool.memset(ones[:], 0.0).then_inc(sem["ones_set"], 1)
                pool.wait_ge(sem["ones_set"], 2)
                pool.memset(ones[0:C, 0:1], 1.0).then_inc(sem["ones_set"], 1)
                pool.memset(ones[C:P, 1:2], 1.0).then_inc(sem["ones_set"], 1)
                pool.wait_ge(sem["ones_set"], 4)
                pool.wait_ge(sem["var_ready"], 1)
                pool.tensor_tensor(rstd[:, :, 0], rstd[:, :, 0], keep.neg_half[:, 0:2], ALU.pow)\
                    .then_inc(sem["rstd_ready"], 1)
                pool.wait_ge(sem["kp_var"], 1)
                pool.tensor_tensor(kp_rstd[:], kp_rstd[:], keep.neg_half[0:B, 0:1], ALU.pow)\
                    .then_inc(sem["kp_rstd_ready"], 1)

            @block.tensor
            def _(pe):
                pe.wait_ge(sem["hist_loaded"], 64)
                for u in range(2):
                    mm = pe.matmul(ps[:, 0, u * wide:(u + 1) * wide], keep.ctx_t[:, u * P:(u + 1) * P], hist_w[:],
                                   start=True, stop=True)
                mm.then_inc(sem["hist_made"], 1)
                pe.wait_ge(sem["eh_ready"], 1)
                for c in range(2):
                    for u in range(2):
                        mm = pe.transpose(ps[:, 1, (2 * c + u) * P:(2 * c + u + 1) * P], eh[:, u, c * P:(c + 1) * P],
                                          keep.identity[:])
                mm.then_inc(sem["eh_turned"], 1)
                pe.wait_ge(sem["eh_kept"], 1)
                pe.wait_ge(sem["ctx_loaded"], 64)
                for c in range(2):
                    mm = pe.matmul(ps[0:inner, 2, 0:B * C], ctx_w1[:, c, :], eh_t[:, c].rearrange("p u k -> p (u k)"),
                                   start=(c == 0), stop=(c == 1))
                mm.then_inc(sem["inner_made"], 1)
                pe.wait_ge(sem["inner_ready"], 1)
                pe.matmul(ps[0:1, 3, 0:B * C], ctx_w2[:], inner_act[:], start=True, stop=True).then_inc(sem["aw_made"], 1)
                pe.wait_ge(sem["aw_ready"], 1)
                for u in range(2):
                    mm = pe.matmul(ps[:, 4, u:u + 1], aw[:, 2 * u:2 * u + 2, :].rearrange("p b k -> p (b k)"), one[:],
                                   start=True, stop=True)
                mm.then_inc(sem["cols_made"], 1)
                pe.wait_ge(sem["cols_ready"], 2)
                for c in range(2):
                    for u in range(2):
                        mm = pe.matmul(ps[:, 5, c * B + 2 * u:c * B + 2 * u + 2], eh[:, u, c * P:(c + 1) * P],
                                       aw_cols[:, u, :], start=True, stop=True)
                mm.then_inc(sem["cc_made"], 1)
                pe.wait_ge(sem["cc_ready"], 1)
                pe.wait_ge(sem["kg_loaded"], 96)
                for c in range(2):
                    mm = pe.matmul(ps[0:B, 6, 0:D], cc_t[:, c, :], kg_w1[:, c, :], start=(c == 0), stop=(c == 1))
                mm.then_inc(sem["kp_made"], 1)
                pe.wait_ge(sem["kp_ready"], 1)
                pe.transpose(ps[:, 7, 0:B], kp[:], keep.identity[0:B, 0:B]).then_inc(sem["kp_turned"], 1)
                pe.wait_ge(sem["kp_kept"], 1)
                pe.matmul(ps[0:B, 0, 0:heads * TAPS], kp_t[:], kg_w2[:], start=True, stop=True).then_inc(sem["k_made"], 1)
                pe.wait_ge(sem["k_ready"], 1)
                for b in range(B):
                    mm = pe.matmul(ps[:, 1 + b // 2, (b % 2) * 256:(b % 2) * 256 + heads * TAPS],
                                   keep.identity[0:B, b:b + 1].to_broadcast([B, P]),
                                   kernels[:].rearrange("b h n -> b (h n)"), start=True, stop=True)
                mm.then_inc(sem["taps_made"], 1)

            @block.scalar
            def _(act):
                act.wait_ge(sem["gelu_in"], 1)
                act.activation(eh[:], eh[:], ACT.Gelu).then_inc(sem["eh_ready"], 1)
                act.wait_ge(sem["inner_made"], 1)
                act.wait_ge(sem["ctx_loaded"], 64)
                act.activation(inner_act[:], ps[0:inner, 2, 0:B * C], ACT.Gelu, bias=ctx_b1[:, 0:1])\
                    .then_inc(sem["inner_ready"], 1)
                act.wait_ge(sem["aw_centred"], 1)
                act.activation(aw[:], aw[:], ACT.Exp).then_inc(sem["aw_exp"], 1)
                act.wait_ge(sem["kp_gelu_in"], 1)
                act.activation(kp[:], kp[:], ACT.Gelu).then_inc(sem["kp_ready"], 1)
                act.wait_ge(sem["k_centred"], 1)
                act.activation(kernels[:], kernels[:], ACT.Exp).then_inc(sem["k_exp"], 1)

            @block.vector
            def _(dve):
                steps = Tally(sem["eh_steps"])

                def then(instruction):
                    steps.add(instruction)
                    steps.wait(dve)

                dve.wait_ge(sem["hist_made"], 1)
                then(dve.tensor_tensor(eh[:], ps[:, 0, :].rearrange("p (u n) -> p u n", u=2),
                                       hist_rows[:, 0:1, :].to_broadcast([P, 2, wide]), ALU.add))
                for u in range(2):
                    steps.add(dve.bn_stats(stats[:, u, :], eh[:, u, :]))
                steps.wait(dve)
                for u in range(2):
                    steps.add(dve.bn_aggr(moments[:, u, :], stats[:, u, :]))
                steps.wait(dve)
                dve.tensor_scalar(rstd[:, :, 0], moments[:, :, 1], EPS, None, ALU.add).then_inc(sem["var_ready"], 1)
                dve.wait_ge(sem["rstd_ready"], 1)
                for u in range(2):
                    steps.add(dve.tensor_scalar(eh[:, u, :], eh[:, u, :], moments[:, u, 0:1], rstd[:, u, :],
                                                ALU.subtract, ALU.mult))
                steps.wait(dve)
                then(dve.tensor_tensor(eh[:], eh[:], hist_rows[:, 1:2, :].to_broadcast([P, 2, wide]), ALU.mult))
                dve.tensor_tensor(eh[:], eh[:], hist_rows[:, 2:3, :].to_broadcast([P, 2, wide]), ALU.add)\
                    .then_inc(sem["gelu_in"], 1)
                dve.wait_ge(sem["eh_turned"], 1)
                dve.tensor_copy(eh_t[:].rearrange("p c u k -> p (c u k)"), ps[:, 1, :]).then_inc(sem["eh_kept"], 1)
                dve.wait_ge(sem["aw_made"], 1)
                then(dve.tensor_scalar(aw[:].rearrange("p b k -> p (b k)"), ps[0:1, 3, 0:B * C], ctx_b2[:, 0:1], None,
                                       ALU.add))
                then(dve.tensor_reduce(aw_top[:], aw[:], AX, ALU.max))
                dve.tensor_tensor(aw[:], aw[:], aw_top[:, :, None].to_broadcast([1, B, C]), ALU.subtract)\
                    .then_inc(sem["aw_centred"], 1)
                dve.wait_ge(sem["aw_exp"], 1)
                then(dve.tensor_reduce(aw_sum[:], aw[:], AX, ALU.add))
                then(dve.reciprocal(aw_top[:], aw_sum[:]))
                dve.tensor_tensor(aw[:], aw[:], aw_top[:, :, None].to_broadcast([1, B, C]), ALU.mult)\
                    .then_inc(sem["aw_ready"], 1)
                dve.wait_ge(sem["cols_made"], 1)
                dve.wait_ge(sem["ones_set"], 4)
                for u in range(2):
                    dve.tensor_scalar(aw_cols[:, u, :], ones[:], ps[:, 4, u:u + 1], None, ALU.mult)\
                        .then_inc(sem["cols_ready"], 1)
                dve.wait_ge(sem["cc_made"], 1)
                dve.tensor_copy(cc_t[:].rearrange("p c b -> p (c b)"), ps[:, 5, 0:2 * B]).then_inc(sem["cc_ready"], 1)
                dve.wait_ge(sem["kp_made"], 1)
                dve.wait_ge(sem["kg_loaded"], 96)
                then(dve.tensor_tensor(kp[:], ps[0:B, 6, 0:D], kg_rows[:, 0, :], ALU.add))
                then(dve.bn_stats(kp_stats[:], kp[:]))
                then(dve.bn_aggr(kp_moments[:], kp_stats[:]))
                dve.tensor_scalar(kp_rstd[:], kp_moments[:, 1:2], EPS, None, ALU.add).then_inc(sem["kp_var"], 1)
                dve.wait_ge(sem["kp_rstd_ready"], 1)
                then(dve.tensor_scalar(kp[:], kp[:], kp_moments[:, 0:1], kp_rstd[:, 0:1], ALU.subtract, ALU.mult))
                then(dve.tensor_tensor(kp[:], kp[:], kg_rows[:, 1, :], ALU.mult))
                dve.tensor_tensor(kp[:], kp[:], kg_rows[:, 2, :], ALU.add).then_inc(sem["kp_gelu_in"], 1)
                dve.wait_ge(sem["kp_turned"], 1)
                dve.tensor_copy(kp_t[:], ps[:, 7, 0:B]).then_inc(sem["kp_kept"], 1)
                dve.wait_ge(sem["k_made"], 1)
                flat = kernels[:].rearrange("b h n -> b (h n)")
                then(dve.tensor_tensor(flat, ps[0:B, 0, 0:heads * TAPS], kg_b2[:], ALU.add))
                then(dve.tensor_reduce(k_top[:], kernels[:], AX, ALU.max))
                dve.tensor_tensor(kernels[:], kernels[:], k_top[:, :, None].to_broadcast([B, heads, TAPS]),
                                  ALU.subtract).then_inc(sem["k_centred"], 1)
                dve.wait_ge(sem["k_exp"], 1)
                then(dve.tensor_reduce(k_sum[:], kernels[:], AX, ALU.add))
                then(dve.reciprocal(k_top[:], k_sum[:]))
                dve.tensor_tensor(kernels[:], kernels[:], k_top[:, :, None].to_broadcast([B, heads, TAPS]), ALU.mult)\
                    .then_inc(sem["k_ready"], 1)
                dve.wait_ge(sem["taps_made"], 1)
                for n in range(2):
                    dve.tensor_copy(taps[:, 2 * n:2 * n + 2, :, :].rearrange("p b h n -> p b (h n)"),
                                    ps[:, 1 + n, :].rearrange("p (b n) -> p b n", b=2)[:, :, 0:heads * TAPS])\
                        .then_inc(sem["taps_ready"], 1)


def conv_attention_any_mask(nc, a, keep, name, taps, gate):
    heads, wide = 16, 8
    scale = float(wide) ** -0.5
    with Scope(nc, name) as s:
        ps = s.psum("ps", [P, 8, 512])
        norm = Normed(s, keep, ps[:, 0], ps[:, 1])
        wq, wk, wv, proj = (s.sb(n, [P, D]) for n in ("wq", "wk", "wv", "proj"))
        proj_rows, head_mask = s.sb("proj_rows", [P, D]), s.sb("head_mask", [P, heads])
        mask_u8, masked, open_ = s.sb("mask_u8", [P, 2, S], U8), s.sb("masked", [P, 2, S]), s.sb("open", [P, 2, S])
        bands, edge = s.sb("bands", [P, 3, P]), s.sb("edge", [P, 2, P])
        q_t, k_t, v = s.sb("q_t", [P, S]), s.sb("k_t", [P, S]), s.sb("v", [P, 2, D])
        k_spread = s.sb("k_spread", [P, heads, S])
        scored = s.sb("scored", [P, 2, S + 2])
        along, tmp = s.sb("along", [P, 3, P]), s.sb("tmp", [P, 3, P])
        over_edge = s.sb("over_edge", [P, 2, 3, P])
        e, e_t = s.sb("e", [P, 2, S]), s.sb("e_t", [P, 2, 2, P])
        top, total, inverse = s.sb("top", [P, 2]), s.sb("total", [P, 2]), s.sb("inverse", [P, 2])
        mixed, mixed_t = s.sb("mixed", [P, 2, D]), s.sb("mixed_t", [P, 2, P])
        change = s.sb("change", [P, 2, D])
        names = ["loaded", "mask_loaded", "tables", "tables_done", "mask_ready", "q_made", "q_kept", "v_kept", "k_ready",
                 "spread", "scores_made", "scored_ready", "kernel_steps", "kernel_ready", "conv_made", "biased", "topped",
                 "exp_done", "turned", "turned_kept", "mixed_made", "inverted", "band_made", "mixed_ready", "mixed_turned",
                 "mixed_kept", "out_made", "changed", "x_done", "zeroed"]
        sem = {n: s.sem(n) for n in names}
        with s.block() as block:

            @block.sync
            def _(sp):
                with sp.If(keep.mask_is_odd(sp) > 0):
                    for to, w in zip((wq, wk, wv, proj), ("Wq", "Wk", "Wv", "proj_W")):
                        sp.dma_start(to[:], a["L3_xattn_" + w]).then_inc(sem["loaded"], 16)
                    sp.dma_start(proj_rows[:], row(a["L3_xattn_proj_b"]).to_broadcast([P, D])).then_inc(sem["loaded"], 16)
                    sp.dma_start(mask_u8[:], a["mask_SxS_bc0"].rearrange("(u i) j -> i u j", i=P))\
                        .then_inc(sem["mask_loaded"], 16)

            @block.gpsimd
            def _(pool):
                with pool.If(keep.mask_is_odd(pool) > 0):
                    norm.gpsimd(pool)
                    tables = Tally(sem["tables"])
                    tables.add(pool.memset(head_mask[:], 1.0))
                    tables.add(pool.memset(bands[:], 0.0))
                    tables.add(pool.memset(edge[:], 0.0))
                    tables.add(pool.memset(scored[:], 0.0))
                    tables.wait(pool)
                    tables.add(pool.affine_select(out=head_mask[:], in_=head_mask[:], compare_op=ALU.is_ge, fill=0.0,
                                                  base=0, pattern=[[-wide, heads]], channel_multiplier=1))
                    tables.wait(pool)
                    pool.affine_select(out=head_mask[:], in_=head_mask[:], compare_op=ALU.is_ge, fill=0.0, base=wide - 1,
                                       pattern=[[wide, heads]], channel_multiplier=-1).then_inc(sem["tables_done"], 1)
                    for n in range(3):
                        pool.affine_select(out=bands[:, n, :], in_=bands[:, n, :], compare_op=ALU.not_equal, fill=1.0,
                                           base=1 - n, pattern=[[-1, P]], channel_multiplier=1)\
                            .then_inc(sem["tables_done"], 1)
                    for n, base in enumerate((P - 1, 1 - P)):
                        pool.affine_select(out=edge[:, n, :], in_=edge[:, n, :], compare_op=ALU.not_equal, fill=1.0,
                                           base=base, pattern=[[-1, P]], channel_multiplier=1)\
                            .then_inc(sem["tables_done"], 1)

            @block.tensor
            def _(pe):
                with pe.If(keep.mask_is_odd(pe) > 0):
                    norm.tensor(pe)
                    for free in ("conv_made", "turned", "mixed_made"):
                        pe.sem_inc(sem[free], 1)
                    pe.wait_ge(sem["loaded"], 80)
                    pe.wait_ge(norm.xt_ready, 2)
                    with pe.Fori(0, B) as b:
                        xt = norm.xt[:, bass.ds(2 * b, 2), :].rearrange("p t k -> p (t k)")
                        pe.wait_ge(sem["x_done"], b + 1)
                        pe.matmul(ps[:, 2, 0:S], wq[:], xt, start=True, stop=True)
                        pe.matmul(ps[:, 2, S:2 * S], wk[:], xt, start=True, stop=True)
                        pe.matmul(ps[:, 3, 0:S], wv[:], xt, start=True, stop=True).then_inc(sem["q_made"], 1)
                        pe.wait_ge(sem["q_kept"], 3 * (b + 1))
                        for u in range(2):
                            mm = pe.transpose(ps[:, 4, u * D:(u + 1) * D], e[:, 0, u * P:(u + 1) * P], keep.identity[:])
                        mm.then_inc(sem["q_made"], 1)
                        with pe.Fori(0, heads) as h:
                            n = b * heads + h
                            pe.wait_ge(sem["spread"], b + 1)
                            pe.wait_ge(sem["v_kept"], b + 1)
                            pe.wait_ge(sem["scored_ready"], n + 1)
                            for u in range(2):
                                mm = pe.matmul(ps[:, 5, u * S:(u + 1) * S], q_t[:, u * P:(u + 1) * P],
                                               k_spread[:, bass.ds(h, 1), :].rearrange("p a j -> p (a j)"),
                                               start=True, stop=True)
                            mm.then_inc(sem["scores_made"], 1)
                            pe.wait_ge(sem["scored_ready"], n + 2)
                            pe.wait_ge(sem["kernel_ready"], 3 * (n + 1))
                            for u in range(2):
                                to = ps[:, 6, u * S:(u + 1) * S]
                                for c in range(3):
                                    pe.matmul(to, along[:, c, :], scored[:, u, c:c + S], start=(c == 0), stop=False)
                                for c in range(3):
                                    mm = pe.matmul(to, over_edge[:, u, c, :], scored[:, 1 - u, c:c + S], start=False,
                                                   stop=(c == 2))
                            mm.then_inc(sem["conv_made"], 1)
                            pe.wait_ge(sem["exp_done"], 2 * (n + 1))
                            for u in range(2):
                                for j in range(2):
                                    mm = pe.transpose(ps[:, 7, (2 * u + j) * P:(2 * u + j + 1) * P],
                                                      e[:, u, j * P:(j + 1) * P], keep.identity[:])
                            mm.then_inc(sem["turned"], 1)
                            pe.wait_ge(sem["turned_kept"], n + 1)
                            for u in range(2):
                                for j in range(2):
                                    mm = pe.matmul(ps[:, 4, u * wide:(u + 1) * wide], e_t[:, u, j, :],
                                                   v[:, j, bass.ds(h * wide, wide)], start=(j == 0), stop=(j == 1))
                            mm.then_inc(sem["mixed_made"], 1)
                        pe.wait_ge(sem["mixed_ready"], 2 * heads * (b + 1) + 1)
                        for u in range(2):
                            mm = pe.transpose(ps[:, 2, u * P:(u + 1) * P], mixed[:, u, :], keep.identity[:])
                        mm.then_inc(sem["mixed_turned"], 1)
                        pe.wait_ge(sem["mixed_kept"], b + 1)
                        for u in range(2):
                            mm = pe.matmul(ps[:, 3, u * D:(u + 1) * D], mixed_t[:, u, :], proj[:], start=True, stop=True)
                        mm.then_inc(sem["out_made"], 1)

            @block.scalar
            def _(act):
                with act.If(keep.mask_is_odd(act) > 0):
                    norm.scalar(act)
                    act.wait_ge(sem["loaded"], 80)
                    with act.Fori(0, B * heads) as n:
                        act.wait_ge(sem["topped"], n + 1)
                        act.wait_ge(sem["mixed_made"], n + 1)
                        for u in range(2):
                            act.activation(e[:, u, :], e[:, u, :], ACT.Exp, bias=top[:, u:u + 1],
                                           accum_out=total[:, u:u + 1]).then_inc(sem["exp_done"], 1)

            @block.vector
            def _(dve):
                with dve.If(keep.mask_is_odd(dve) > 0):
                    norm.vector(dve)
                    for free in ("x_done", "scored_ready", "mixed_ready"):
                        dve.sem_inc(sem[free], 1)
                    steps = Tally(sem["kernel_steps"])

                    def then(instruction):
                        steps.add(instruction)
                        steps.wait(dve)

                    dve.wait_ge(sem["mask_loaded"], 16)
                    then(dve.tensor_copy(masked[:], mask_u8[:]))
                    then(dve.tensor_scalar(open_[:], masked[:], -1.0, 1.0, ALU.mult, ALU.add))
                    then(dve.tensor_scalar(masked[:], masked[:], -1e30, None, ALU.mult))
                    dve.wait_ge(sem["tables_done"], 6)
                    with dve.Fori(0, B) as b:
                        dve.wait_ge(sem["q_made"], 2 * b + 1)
                        dve.tensor_scalar(q_t[:], ps[:, 2, 0:S], scale, None, ALU.mult).then_inc(sem["q_kept"], 1)
                        dve.tensor_copy(k_t[:], ps[:, 2, S:2 * S]).then_inc(sem["q_kept"], 1)
                        dve.tensor_copy(e[:, 0, :], ps[:, 3, 0:S]).then_inc(sem["q_kept"], 1)
                        dve.wait_ge(sem["q_kept"], 3 * (b + 1))
                        dve.tensor_tensor(k_spread[:], k_t[:, None, :].to_broadcast([P, heads, S]),
                                          head_mask[:, :, None].to_broadcast([P, heads, S]), ALU.mult)\
                            .then_inc(sem["spread"], 1)
                        dve.wait_ge(sem["q_made"], 2 * b + 2)
                        dve.tensor_copy(v[:].rearrange("p u d -> p (u d)"), ps[:, 4, 0:2 * D]).then_inc(sem["v_kept"], 1)
                        with dve.Fori(0, heads) as h:
                            n = b * heads + h
                            def tap(k):
                                return taps[:, bass.ds(b, 1), bass.ds(h, 1), 3 * k:3 * k + 3].rearrange(
                                    "p x y c -> p (x y c)")[:, :, None].to_broadcast([P, 3, P])

                            def spread(to, table, k):
                                return dve.tensor_tensor(to, table.to_broadcast([P, 3, P]), tap(k), ALU.mult)

                            dve.wait_ge(sem["conv_made"], n + 1)
                            spread(along[:], bands[:, 0:1, :], 0).then_inc(sem["band_made"], 1)
                            spread(tmp[:], bands[:, 1:2, :], 1).then_inc(sem["band_made"], 1)
                            dve.wait_ge(sem["band_made"], 4 * n + 2)
                            dve.tensor_tensor(along[:], along[:], tmp[:], ALU.add).then_inc(sem["band_made"], 1)
                            dve.wait_ge(sem["band_made"], 4 * n + 3)
                            spread(tmp[:], bands[:, 2:3, :], 2).then_inc(sem["band_made"], 1)
                            dve.wait_ge(sem["band_made"], 4 * n + 4)
                            dve.tensor_tensor(along[:], along[:], tmp[:], ALU.add).then_inc(sem["kernel_ready"], 1)
                            spread(over_edge[:, 0], edge[:, 0:1, :], 2).then_inc(sem["kernel_ready"], 1)
                            spread(over_edge[:, 1], edge[:, 1:2, :], 0).then_inc(sem["kernel_ready"], 1)
                            dve.wait_ge(sem["scores_made"], n + 1)
                            dve.tensor_tensor(scored[:, :, 1:S + 1], ps[:, 5, :].rearrange("p (u j) -> p u j", u=2),
                                              open_[:], ALU.mult).then_inc(sem["scored_ready"], 1)
                            dve.wait_ge(sem["conv_made"], n + 2)
                            dve.wait_ge(sem["turned"], n + 1)
                            dve.tensor_tensor(e[:], ps[:, 6, :].rearrange("p (u j) -> p u j", u=2), masked[:], ALU.add)\
                                .then_inc(sem["biased"], 1)
                            dve.wait_ge(sem["biased"], n + 1)
                            dve.tensor_reduce(top[:], e[:], AX, ALU.max, negate=True).then_inc(sem["topped"], 1)
                            dve.wait_ge(sem["turned"], n + 2)
                            dve.tensor_copy(e_t[:].rearrange("p u j k -> p (u j k)"), ps[:, 7, :])\
                                .then_inc(sem["turned_kept"], 1)
                            dve.wait_ge(sem["mixed_ready"], 2 * n + 1)
                            dve.reciprocal(inverse[:], total[:]).then_inc(sem["inverted"], 1)
                            dve.wait_ge(sem["inverted"], n + 1)
                            dve.wait_ge(sem["mixed_made"], n + 2)
                            for u in range(2):
                                dve.tensor_scalar(mixed[:, u, bass.ds(h * wide, wide)], ps[:, 4, u * wide:(u + 1) * wide],
                                                  inverse[:, u:u + 1], None, ALU.mult).then_inc(sem["mixed_ready"], 1)
                        dve.wait_ge(sem["mixed_turned"], b + 1)
                        dve.tensor_copy(mixed_t[:].rearrange("p u k -> p (u k)"), ps[:, 2, 0:2 * P])\
                            .then_inc(sem["mixed_kept"], 1)
                        dve.wait_ge(sem["out_made"], b + 1)
                        dve.tensor_tensor(change[:], ps[:, 3, 0:2 * D].rearrange("p (u d) -> p u d", u=2),
                                          proj_rows[:, None, :].to_broadcast([P, 2, D]), ALU.add).then_inc(sem["changed"], 1)
                        dve.wait_ge(sem["changed"], b + 1)
                        xb = keep.x[:, bass.ds(2 * b, 2), :]
                        dve.scalar_tensor_tensor(out=xb, in0=change[:], scalar=gate, in1=xb, op0=ALU.mult, op1=ALU.add)\
                            .then_inc(sem["x_done"], 1)


def check_mask(nc, a, keep, name):
    with Scope(nc, name) as s:
        mask_u8, given, causal = s.sb("mask_u8", [P, 2, S], U8), s.sb("given", [P, 2, S]), s.sb("causal", [P, 2, S])
        ones, off = s.sb("ones", [P, 1]), s.sb("off", [P, 1])
        ps = s.psum("ps", [1, 1])
        names = ["loaded", "ones_set", "causal_set", "causal_made", "steps", "off_ready", "off_counted", "flagged"]
        sem = {n: s.sem(n) for n in names}
        with s.block() as block:

            @block.sync
            def _(sp):
                sp.dma_start(mask_u8[:], a["mask_SxS_bc0"].rearrange("(u i) j -> i u j", i=P)).then_inc(sem["loaded"], 16)

            @block.gpsimd
            def _(pool):
                pool.memset(ones[:], 1.0).then_inc(sem["ones_set"], 1)
                pool.memset(causal[:], 1.0).then_inc(sem["causal_set"], 1)
                pool.wait_ge(sem["causal_set"], 1)
                pool.affine_select(out=causal[:], in_=causal[:], compare_op=ALU.is_ge, fill=0.0, base=-1,
                                   pattern=[[-P, 2], [1, S]], channel_multiplier=-1).then_inc(sem["causal_made"], 1)

            @block.tensor
            def _(pe):
                pe.wait_ge(sem["ones_set"], 1)
                pe.wait_ge(sem["off_ready"], 1)
                pe.matmul(ps[:], off[:], ones[:], start=True, stop=True).then_inc(sem["off_counted"], 1)

            @block.vector
            def _(dve):
                steps = Tally(sem["steps"])
                dve.wait_ge(sem["loaded"], 16)
                steps.add(dve.tensor_copy(given[:], mask_u8[:]))
                steps.wait(dve)
                dve.wait_ge(sem["causal_made"], 1)
                steps.add(dve.tensor_tensor(given[:], given[:], causal[:], ALU.not_equal))
                steps.wait(dve)
                dve.tensor_reduce(off[:], given[:].rearrange("p u j -> p (u j)"), AX, ALU.max)\
                    .then_inc(sem["off_ready"], 1)
                dve.wait_ge(sem["off_counted"], 1)
                dve.tensor_scalar(keep.odd_mask[:], ps[:], 1.0, None, ALU.min).then_inc(sem["flagged"], 1)
                dve.wait_ge(sem["flagged"], 1)


def conv_attention_causal(nc, a, keep, name, taps, gate):
    heads, wide, R, G = 16, 8, 4, 4
    scale = float(wide) ** -0.5
    closest = [(shift, tap_a) for shift in range(4) for tap_a in (-1, 0, 1)
               if abs(tap_a - shift) <= 1 or abs(tap_a - shift + 1) <= 1]
    units = [(b, t, j) for b in range(B) for t, j in ((0, 0), (1, 0), (1, 1))]
    with Scope(nc, name) as s:
        ps = s.psum("ps", [P, 8, 512])
        norm = Normed(s, keep, ps[:, 0], ps[:, 1], True)
        xt = norm.xt
        wq, wk, wv, proj, bias = (s.sb(n, [P, D]) for n in ("wq", "wk", "wv", "proj", "bias"))
        head_mask, mask_rg = s.sb("head_mask", [P, heads]), s.sb("mask_rg", [P, R, G])
        near_taps = s.sb("near_taps", [P, B, len(closest), 2, heads])
        wq_wide, wk_wide = s.sb("wq_wide", [P, 3, G, R, 32]), s.sb("wk_wide", [P, 2, 3, G, R, 32])
        below, one_below = s.sb("below", [P, P], BF16), s.sb("one_below", [P, 1], BF16)
        identity16 = s.sb("identity16", [P, P], BF16)
        zeros16 = s.sb("zeros16", [P, P], BF16)
        q_f, k_f = s.sb("q_f", [P, B, S + 2]), s.sb("k_f", [P, B, S + 5])
        products = s.sb("products", [P, 4, B, S + 2])
        stacks = s.sb("stacks", [P, 2, 2, G, S])
        v, v_before = s.sb("v", [P, NT, heads, wide + 1]), s.sb("v_before", [P, NT, heads, wide + 1])
        near = s.sb("near", [P, NT, 2, heads])
        near_e = s.sb("near_e", [P, NT, 2, heads])
        near_v = s.sb("near_v", [P, NT, 2, heads, wide + 1])
        top = s.sb("top", [P, len(units), heads])
        tmp_top = s.sb("tmp_top", [P, B, 3, heads])
        e, e_t = s.sb("e", [P, 2, R, G, P]), s.sb("e_t", [P, 2, R, G, P])
        acc = s.sb("acc", [P, len(units), heads, wide + 1])
        inverse = s.sb("inverse", [P, NT, heads])
        mixed, mixed_t, change = s.sb("mixed", [P, NT, D]), s.sb("mixed_t", [P, NT, P]), s.sb("change", [P, NT, D])
        names = ["loaded", "padded", "tables", "tables_made", "near_taps_made", "wq_widened", "wk_widened", "features_made",
                 "features_kept", "products_made", "v_made", "v_kept", "near_made", "near_kept", "misc_made",
                 "misc_read", "scores_made", "maxed", "centred", "near_centred", "exp_done", "near_exp",
                 "near_steps", "near_ready", "turned", "turned_kept", "pv_made", "acc_made", "gap_ready", "gap_exp",
                 "joined", "inverted", "mixed_ready", "biased_x", "x_done"]
        sem = {n: s.sem(n) for n in names}

        def misc_uses():
            uses = [("stack", 0, part) for part in range(4)]
            for n in range(len(units)):
                b, kind = n // 3, n % 3
                if b + 1 < B and kind < 2:
                    uses += [("stack", b + 1, 2 * kind + part) for part in range(2)]
                if b and kind == 0:
                    uses += [("turn", b - 1, 0), ("project", b - 1, 0)]
            return uses + [("turn", B - 1, 0), ("project", B - 1, 0)]

        uses = misc_uses()

        with s.block() as block:

            @block.sync
            def _(sp):
                with sp.If(keep.mask_is_odd(sp) < 1):
                    for to, w in zip((wq, wk, wv, proj), ("Wq", "Wk", "Wv", "proj_W")):
                        sp.dma_start(to[:], a["L3_xattn_" + w]).then_inc(sem["loaded"], 16)
                    sp.dma_start(bias[:], row(a["L3_xattn_proj_b"]).to_broadcast([P, D])).then_inc(sem["loaded"], 16)
                    sp.wait_ge(sem["loaded"], 80)

            @block.gpsimd
            def _(pool):
                with pool.If(keep.mask_is_odd(pool) < 1):
                    steps = Tally(sem["tables"])
                    norm_pads = (xt[:, :, 0:1], xt[:, :, S + 1:S + 2])
                    for pad in norm_pads + (q_f[:, :, 0:1], q_f[:, :, S + 1:S + 2], k_f[:, :, 0:4],
                                            k_f[:, :, S + 4:S + 5], wq_wide[:], wk_wide[:]):
                        pool.memset(pad, 0.0).then_inc(sem["padded"], 1)
                    norm.gpsimd(pool)
                    steps.add(pool.memset(head_mask[:], 1.0))
                    steps.add(pool.memset(zeros16[:], 0.0))
                    steps.add(pool.memset(near_taps[:], 0.0))
                    steps.add(pool.memset(v[:, :, :, wide:wide + 1], 1.0))
                    steps.add(pool.memset(v_before[:, :, :, wide:wide + 1], 1.0))
                    steps.wait(pool)
                    pool.affine_select(out=below[:], in_=zeros16[:], compare_op=ALU.is_ge, fill=-1e30, base=-2,
                                       pattern=[[-1, P]], channel_multiplier=1).then_inc(sem["tables_made"], 1)
                    pool.affine_select(out=one_below[:], in_=zeros16[:, 0:1], compare_op=ALU.not_equal, fill=-1e30,
                                       base=0, pattern=[[0, 1]], channel_multiplier=1).then_inc(sem["tables_made"], 1)
                    pool.affine_select(out=identity16[:], in_=zeros16[:], compare_op=ALU.not_equal, fill=1.0, base=0,
                                       pattern=[[-1, P]], channel_multiplier=1).then_inc(sem["tables_made"], 1)
                    steps.add(pool.affine_select(out=head_mask[:], in_=head_mask[:], compare_op=ALU.is_ge, fill=0.0,
                                                 base=0, pattern=[[-wide, heads]], channel_multiplier=1))
                    steps.wait(pool)
                    steps.add(pool.affine_select(out=head_mask[:], in_=head_mask[:], compare_op=ALU.is_ge, fill=0.0,
                                                 base=wide - 1, pattern=[[wide, heads]], channel_multiplier=-1))
                    steps.wait(pool)
                    steps.add(pool.tensor_copy(mask_rg[:], head_mask[:].rearrange("p (g r) -> p r g", r=R)))
                    steps.wait(pool)
                    for n, (shift, tap_a) in enumerate(closest):
                        for below_by in range(2):
                            tap_c = tap_a - shift + below_by
                            if abs(tap_c) <= 1:
                                at = 3 * (tap_a + 1) + tap_c + 1
                                for b in range(B):
                                    steps.add(pool.tensor_tensor(
                                        near_taps[:, b, n, below_by, :].rearrange("p (r g) -> p r g", r=R),
                                        taps[:, b, :, at].rearrange("p (g r) -> p r g", r=R), mask_rg[:], ALU.mult))
                    steps.wait(pool)
                    pool.tensor_copy(one_below[:], one_below[:]).then_inc(sem["near_taps_made"], 1)

                    def near_values(b, t):
                        n = 2 * b + t
                        pool.wait_ge(sem["near_exp"], n + 1)
                        pool.wait_ge(sem["v_kept"], 4)
                        near_steps = Tally(sem["near_steps"])
                        near_steps.n = 2 * n
                        for below_by, rows in enumerate((v, v_before)):
                            near_steps.add(pool.tensor_tensor(
                                near_v[:, n, below_by], rows[:, n],
                                near_e[:, n, below_by, :, None].to_broadcast([P, heads, wide + 1]), ALU.mult))
                        near_steps.wait(pool)
                        pool.tensor_tensor(near_v[:, n, 0], near_v[:, n, 0], near_v[:, n, 1], ALU.add)\
                            .then_inc(sem["near_ready"], 1)

                    def join(b):
                        n = 3 * b + 1
                        joined = Tally(sem["joined"])
                        joined.n = 3 * b
                        pool.wait_ge(sem["gap_exp"], b + 1)
                        pool.wait_ge(sem["acc_made"], n + 2)
                        for k in range(2):
                            joined.add(pool.tensor_tensor(
                                acc[:, n + k], acc[:, n + k],
                                tmp_top[:, b, k, :, None].to_broadcast([P, heads, wide + 1]), ALU.mult))
                        joined.wait(pool)
                        joined.add(pool.tensor_tensor(acc[:, n + 1], acc[:, n + 1], acc[:, n], ALU.add))

                    def add_change(b):
                        pool.wait_ge(sem["misc_read"], uses.index(("project", b, 0)) + 1)
                        pool.wait_ge(sem["biased_x"], 1)
                        pool.tensor_tensor(keep.x[:, 2 * b:2 * b + 2], keep.x[:, 2 * b:2 * b + 2],
                                           change[:, 2 * b:2 * b + 2], ALU.add).then_inc(sem["x_done"], 1)

                    for b in range(B):
                        near_values(b, 0)
                        if b:
                            add_change(b - 1)
                        near_values(b, 1)
                        join(b)
                    add_change(B - 1)

            @block.tensor
            def _(pe):
                with pe.If(keep.mask_is_odd(pe) < 1):
                    norm.tensor(pe)
                    pe.wait_ge(sem["loaded"], 80)
                    pe.wait_ge(norm.xt_ready, 2)
                    pe.wait_ge(sem["padded"], 8)
                    for n, w in enumerate((wq, wk)):
                        for b in range(B):
                            mm = pe.matmul(ps[:, 2 * n + b // 2, (b % 2) * S:(b % 2 + 1) * S], w[:],
                                           xt[:, b, 1:S + 1], start=True, stop=True)
                        mm.then_inc(sem["features_made"], 1)
                    for before in range(2):
                        for t in range(NT):
                            at = (t % 2) * P + 1 - before
                            mm = pe.matmul(ps[:, 4 + 2 * before + t // 4, (t % 4) * D:(t % 4 + 1) * D],
                                           xt[:, t // 2, at:at + P], wv[:], start=True, stop=True)
                            if t % 4 == 3:
                                mm.then_inc(sem["v_made"], 1)

                    def stack(use):
                        b, part = uses[use][1:]
                        of_k, pair = part // 2, part % 2
                        pe.wait_ge(sem["wk_widened" if of_k else "wq_widened"], 3 * (b + 1) if of_k else 3)
                        if use:
                            pe.wait_ge(sem["misc_read"], use)
                        else:
                            pe.wait_ge(sem["v_kept"], 4)
                        for g in range(2):
                            for shift in range(3):
                                w = wk_wide[:, b % 2, shift, 2 * pair + g] if of_k else wq_wide[:, shift, 2 * pair + g]
                                mm = pe.matmul(ps[:, 6, g * S:(g + 1) * S], w.rearrange("p r d -> p (r d)"),
                                               xt[:, b, shift:shift + S], start=(shift == 0), stop=(shift == 2))
                        mm.then_inc(sem["misc_made"], 1)

                    def finish(use):
                        b = uses[use][1]
                        pe.wait_ge(sem["misc_read"], use)
                        pe.wait_ge(sem["mixed_ready"], 2 * (b + 1))
                        for t in range(2):
                            mm = pe.transpose(ps[:, 6, t * P:(t + 1) * P], mixed[:, 2 * b + t, :], keep.identity[:])
                        mm.then_inc(sem["misc_made"], 1)
                        pe.wait_ge(sem["misc_read"], use + 1)
                        for t in range(2):
                            mm = pe.matmul(ps[:, 6, t * D:(t + 1) * D], mixed_t[:, 2 * b + t, :], proj[:],
                                           start=True, stop=True)
                        mm.then_inc(sem["misc_made"], 1)

                    def scores(n):
                        b, t, j = units[n]
                        last_stack = max(k for k, use in enumerate(uses) if use[0:2] == ("stack", b))
                        pe.wait_ge(sem["misc_read"], last_stack + 1)
                        for r in range(R):
                            if n:
                                pe.wait_ge(sem["centred"], R * (n - 1) + r + 1)
                            rows = slice(32 * r, 32 * r + 32)
                            for g in range(G):
                                to = ps[:, r, g * P:(g + 1) * P]
                                if t == j:
                                    pe.matmul(to, identity16[:], below[:], start=True, stop=False)
                                mm = pe.matmul(to, stacks[rows, b % 2, 0, g, t * P:(t + 1) * P],
                                               stacks[rows, b % 2, 1, g, j * P:(j + 1) * P], start=(t != j),
                                               stop=(t == j))
                                if t != j:
                                    mm = pe.matmul(to[:, P - 1:P], identity16[:], one_below[:], start=False, stop=True)
                            mm.then_inc(sem["scores_made"], 1)

                    def turn(n):
                        for r in range(R):
                            if r % 2 == 0:
                                pe.wait_ge(sem["exp_done"], 2 * n + r // 2 + 1)
                            if R * n + r >= 2:
                                pe.wait_ge(sem["turned_kept"], R * n + r - 1)
                            else:
                                pe.wait_ge(sem["v_kept"], 4)
                            for g in range(G):
                                mm = pe.transpose(ps[:, 4 + r % 2, g * P:(g + 1) * P], e[:, n % 2, r, g, :],
                                                  keep.identity[:])
                            mm.then_inc(sem["turned"], 1)

                    def values(n):
                        b, t, j = units[n]
                        if n:
                            pe.wait_ge(sem["acc_made"], n)
                        for r in range(R):
                            pe.wait_ge(sem["turned_kept"], R * n + r + 1)
                            for g in range(G):
                                h = G * r + g
                                mm = pe.matmul(ps[:, 7, (wide + 1) * h:(wide + 1) * (h + 1)], e_t[:, n % 2, r, g, :],
                                               v[:, 2 * b + j, h, :], start=True, stop=True)
                        mm.then_inc(sem["pv_made"], 1)

                    use = 0
                    while use < 4:
                        stack(use)
                        use += 1
                    pe.wait_ge(sem["near_taps_made"], 1)
                    pe.wait_ge(sem["products_made"], 4)
                    for t in range(NT):
                        for n, (shift, tap_a) in enumerate(closest):
                            at = (t % 2) * P + 1 + tap_a
                            mm = pe.matmul(ps[:, 7, t * 2 * heads:(t + 1) * 2 * heads],
                                           products[:, shift, t // 2, at:at + P],
                                           near_taps[:, t // 2, n].rearrange("p x h -> p (x h)"),
                                           start=(n == 0), stop=(n == len(closest) - 1))
                    mm.then_inc(sem["near_made"], 1)
                    pe.wait_ge(sem["tables_made"], 3)
                    pe.wait_ge(sem["features_kept"], 2)
                    scores(0)
                    for n in range(len(units)):
                        if n + 1 < len(units):
                            scores(n + 1)
                        while use < len(uses) and uses[use][0] == "stack":
                            stack(use)
                            use += 1
                            if uses[use][1:] == (n // 3 + 1, 2):
                                break
                        turn(n)
                        if n == 0:
                            pe.wait_ge(sem["near_kept"], 1)
                        values(n)
                        if n % 3 == 0 and n:
                            finish(use)
                            use += 2
                    finish(use)

            @block.scalar
            def _(act):
                with act.If(keep.mask_is_odd(act) < 1):
                    norm.scalar(act)
                    act.wait_ge(sem["padded"], 8)
                    act.wait_ge(sem["features_made"], 1)
                    act.activation(q_f[:, :, 1:S + 1], ps[:, 0:2, :].rearrange("p u (b i) -> p (u b) i", b=2), ACT.Copy,
                                   scale=scale).then_inc(sem["features_kept"], 1)
                    act.wait_ge(sem["tables"], 5)
                    for before, rows in enumerate((v, v_before)):
                        for half in range(2):
                            act.wait_ge(sem["v_made"], 2 * before + half + 1)
                            for t in range(4 * half, 4 * half + 4):
                                done = act.activation(
                                    rows[:, t, :, 0:wide].rearrange("p (r g) d -> p r g d", r=R),
                                    ps[:, 4 + 2 * before + half, (t % 4) * D:(t % 4 + 1) * D].rearrange(
                                        "p (g r d) -> p r g d", r=R, g=G), ACT.Copy)
                            done.then_inc(sem["v_kept"], 1)

                    def misc(use):
                        kind, b, part = uses[use]
                        act.wait_ge(sem["misc_made"], use + 1)
                        if kind == "stack":
                            of_k, pair = part // 2, part % 2
                            if b >= 2:
                                act.wait_ge(sem["scores_made"], R * 3 * (b - 1))
                            act.activation(stacks[:, b % 2, of_k, 2 * pair:2 * pair + 2, :].rearrange("p g i -> p (g i)"),
                                           ps[:, 6, :], ACT.Copy, scale=1.0 if of_k else scale)\
                                .then_inc(sem["misc_read"], 1)
                        elif kind == "turn":
                            act.activation(mixed_t[:, 2 * b:2 * b + 2].rearrange("p t k -> p (t k)"), ps[:, 6, 0:2 * P],
                                           ACT.Copy).then_inc(sem["misc_read"], 1)
                        else:
                            act.activation(change[:, 2 * b:2 * b + 2].rearrange("p t k -> p (t k)"), ps[:, 6, 0:2 * D],
                                           ACT.Copy, scale=gate).then_inc(sem["misc_read"], 1)

                    def exp(n):
                        b, t, j = units[n]
                        for half in range(2):
                            act.wait_ge(sem["centred"], R * n + 2 * half + 2)
                            act.activation(e[:, n % 2, 2 * half:2 * half + 2], e[:, n % 2, 2 * half:2 * half + 2], ACT.Exp)\
                                .then_inc(sem["exp_done"], 1)
                        if t == j:
                            act.wait_ge(sem["near_centred"], 2 * b + t + 1)
                            act.activation(near_e[:, 2 * b + t], near_e[:, 2 * b + t], ACT.Exp)\
                                .then_inc(sem["near_exp"], 1)
                        if (t, j) == (1, 1):
                            act.wait_ge(sem["gap_ready"], b + 1)
                            act.activation(tmp_top[:, b, 0:2], tmp_top[:, b, 0:2], ACT.Exp).then_inc(sem["gap_exp"], 1)

                    def keep_turned(n):
                        for r in range(R):
                            act.wait_ge(sem["turned"], R * n + r + 1)
                            if n >= 2:
                                act.wait_ge(sem["pv_made"], n - 1)
                            act.activation(e_t[:, n % 2, r].rearrange("p g k -> p (g k)"), ps[:, 4 + r % 2, :], ACT.Copy)\
                                .then_inc(sem["turned_kept"], 1)

                    use = 0
                    while use < 4:
                        misc(use)
                        use += 1
                    exp(0)
                    for n in range(len(units)):
                        while use < len(uses) and uses[use][0] == "stack":
                            misc(use)
                            use += 1
                            if uses[use][1:] == (n // 3 + 1, 2):
                                break
                        keep_turned(n)
                        if n + 1 < len(units):
                            exp(n + 1)
                        if n % 3 == 0 and n:
                            misc(use)
                            misc(use + 1)
                            use += 2
                    misc(use)
                    misc(use + 1)

            @block.vector
            def _(dve):
                with dve.If(keep.mask_is_odd(dve) < 1):
                    norm.vector(dve)
                    dve.wait_ge(sem["loaded"], 80)
                    dve.wait_ge(sem["padded"], 8)
                    for shift in range(3):
                        dve.tensor_copy(wq_wide[:, shift, :, :, wide * shift:wide * (shift + 1)],
                                        wq[:].rearrange("p (g r d) -> p g r d", g=G, r=R)).then_inc(sem["wq_widened"], 1)

                    def widen(b):
                        if b >= 2:
                            last = max(k for k, use in enumerate(uses) if use[0:2] == ("stack", b - 2))
                            dve.wait_ge(sem["misc_made"], last + 1)
                        for c in range(3):
                            dve.tensor_tensor(
                                wk_wide[:, b % 2, c, :, :, 0:3 * wide].rearrange("p g r (x d) -> p (g r) x d", x=3),
                                wk[:].rearrange("p (h d) -> p h d", h=heads)[:, :, None, :].to_broadcast([P, heads, 3, wide]),
                                taps[:, b, :, c::3, None].to_broadcast([P, heads, 3, wide]), ALU.mult)\
                                .then_inc(sem["wk_widened"], 1)

                    widen(0)
                    dve.wait_ge(sem["features_made"], 2)
                    dve.tensor_copy(k_f[:, :, 4:S + 4], ps[:, 2:4, :].rearrange("p u (b i) -> p (u b) i", b=2))\
                        .then_inc(sem["features_kept"], 1)
                    dve.wait_ge(sem["features_kept"], 2)
                    for shift in range(4):
                        dve.tensor_tensor(products[:, shift], q_f[:], k_f[:, :, 3 - shift:3 - shift + S + 2], ALU.mult)\
                            .then_inc(sem["products_made"], 1)
                    dve.wait_ge(norm.xn_ready, NT)
                    dve.scalar_tensor_tensor(out=keep.x[:], in0=bias[:, None, :].to_broadcast([P, NT, D]), scalar=gate,
                                             in1=keep.x[:], op0=ALU.mult, op1=ALU.add).then_inc(sem["biased_x"], 1)
                    widen(1)
                    dve.wait_ge(sem["near_made"], 1)
                    dve.tensor_copy(near[:].rearrange("p t x h -> p (t x h)"), ps[:, 7, 0:NT * 2 * heads])\
                        .then_inc(sem["near_kept"], 1)
                    dve.wait_ge(sem["near_kept"], 1)
                    dve.tensor_scalar(near[0:1, 0::2, 1, :], near[0:1, 0::2, 1, :], -1e30, None, ALU.add)\
                        .then_inc(sem["near_kept"], 1)
                    dve.wait_ge(sem["near_kept"], 2)
                    maxed = Tally(sem["maxed"])

                    def centre(n):
                        b, t, j = units[n]
                        for r in range(R):
                            dve.wait_ge(sem["scores_made"], R * n + r + 1)
                            maxed.add(dve.tensor_reduce(top[:, n, G * r:G * (r + 1)],
                                                        ps[:, r, :].rearrange("p (g k) -> p g k", g=G), AX, ALU.max))
                        maxed.wait(dve)
                        if t == j:
                            for x in range(2):
                                maxed.add(dve.tensor_tensor(top[:, n], top[:, n], near[:, 2 * b + t, x], ALU.max))
                                maxed.wait(dve)
                        if n >= 2:
                            dve.wait_ge(sem["turned"], R * (n - 1))
                        for r in range(R):
                            done = dve.tensor_tensor(e[:, n % 2, r], ps[:, r, :].rearrange("p (g k) -> p g k", g=G),
                                                     top[:, n, G * r:G * (r + 1), None].to_broadcast([P, G, P]),
                                                     ALU.subtract)
                            done.then_inc(sem["centred"], 1)
                        if t == j:
                            dve.tensor_tensor(near_e[:, 2 * b + t], near[:, 2 * b + t],
                                              top[:, n:n + 1].to_broadcast([P, 2, heads]), ALU.subtract)\
                                .then_inc(sem["near_centred"], 1)
                        if (t, j) == (1, 1):
                            maxed.add(dve.tensor_tensor(tmp_top[:, b, 2], top[:, n - 1], top[:, n], ALU.max))
                            maxed.wait(dve)
                            dve.tensor_tensor(tmp_top[:, b, 0:2], top[:, n - 1:n + 1],
                                              tmp_top[:, b, 2:3].to_broadcast([P, 2, heads]), ALU.subtract)\
                                .then_inc(sem["gap_ready"], 1)

                    def gather(n):
                        b, t, j = units[n]
                        dve.wait_ge(sem["pv_made"], n + 1)
                        flat = acc[:, n].rearrange("p h d -> p (h d)")
                        if t == j:
                            dve.wait_ge(sem["near_ready"], 2 * b + t + 1)
                            dve.tensor_tensor(flat, ps[:, 7, 0:heads * (wide + 1)],
                                              near_v[:, 2 * b + t, 0].rearrange("p h d -> p (h d)"), ALU.add)\
                                .then_inc(sem["acc_made"], 1)
                        else:
                            dve.tensor_copy(flat, ps[:, 7, 0:heads * (wide + 1)]).then_inc(sem["acc_made"], 1)

                    def normalise(n):
                        b, t, j = units[n]
                        m = 2 * b + t
                        if t:
                            dve.wait_ge(sem["joined"], 3 * (b + 1))
                        else:
                            dve.wait_ge(sem["acc_made"], n + 1)
                        dve.reciprocal(inverse[:, m], acc[:, n, :, wide]).then_inc(sem["inverted"], 1)
                        dve.wait_ge(sem["inverted"], m + 1)
                        dve.tensor_tensor(mixed[:, m].rearrange("p (g r d) -> p r g d", g=G, r=R),
                                          acc[:, n, :, 0:wide].rearrange("p (r g) d -> p r g d", r=R),
                                          inverse[:, m].rearrange("p (r g) -> p r g", r=R)[:, :, :, None].to_broadcast(
                                              [P, R, G, wide]), ALU.mult).then_inc(sem["mixed_ready"], 1)

                    centre(0)
                    for n in range(len(units)):
                        if n + 1 < len(units):
                            centre(n + 1)
                        gather(n)
                        if n % 3 == 0:
                            if n:
                                normalise(n - 1)
                            normalise(n)
                        if n % 3 == 1 and n // 3 + 2 < B:
                            widen(n // 3 + 2)
                    normalise(len(units) - 1)



class Keep:

    def __init__(self, s):
        self.x = s.sb("x", [P, NT, D])
        self.ctx_t = s.sb("ctx_t", [P, B * C])
        self.identity = s.sb("identity", [P, P])
        self.gates = s.sb("gates", [P, 2 * B])
        self.neg_half = s.sb("neg_half", [P, 16])
        self.iota = s.sb("iota", [P, P])
        self.iota_tiles = s.sb("iota_tiles", [P, NT])
        self.token = s.sb("token", [P, NT])
        self.odd_mask = s.sb("odd_mask", [1, 1], I32)
        self.gathered = [s.gpsimd_dma_sem(f"gathered{u}") for u in range(2)]
        self.got = [s.gpsimd_dma_sem(f"got{k}{t}") for t in range(NT) for k in range(CHOSEN)]

    def mask_is_odd(self, engine):
        return engine.value_load(self.odd_mask[0:1, 0:1], min_val=0, max_val=1)


def store(nc, a, keep, out):
    with Scope(nc, "store") as s:
        stored = s.sem("stored")
        with s.block() as block:

            @block.sync
            def _(sp):
                sp.dma_start(out.rearrange("b (u p) d -> p (b u) d", p=P), keep.x[:]).then_inc(stored, 16)
                sp.wait_ge(stored, 16)


def latent_operands(nc, a, keep, name, scores_rhs, values_rhs, score_bias, wq, bias_q, scale):
    heads = 16
    wide = D // heads
    with Scope(nc, name) as s:
        wk, wv, mask = s.sb("wk", [P, D]), s.sb("wv", [P, D]), s.sb("mask", [P, B * C])
        ctx_twice = s.sb("ctx_twice", [P, B, 2, C])
        bias_k, head_mask, k_t = s.sb("bias_k", [P, 1]), s.sb("head_mask", [P, heads]), s.sb("k_t", [P, B * C])
        ps = s.psum("ps", [P, 2, 512])
        names = ["weights_loaded", "bias_loaded", "mask_loaded", "ones_set", "lower_cut", "mask_made", "k_made",
                 "k_kept", "v_made", "rhs_zeroed", "v_kept", "k_spread", "bias_spread", "q_scaled", "ctx_doubled"]
        sem = {n: s.sem(n) for n in names}
        with s.block() as block:

            @block.sync
            def _(sp):
                sp.dma_start(wk[:], a["L2_xattn_Wk"]).then_inc(sem["weights_loaded"], 16)
                sp.dma_start(wv[:], a["L2_xattn_Wv"]).then_inc(sem["weights_loaded"], 16)
                sp.dma_start(wq[:], a["L2_xattn_Wq"]).then_inc(sem["weights_loaded"], 16)
                sp.dma_start(mask[:], a["mask_Bx1x1xS2_ff0"].rearrange("b x y k -> (x y) (b k)").to_broadcast([P, B * C]))\
                    .then_inc(sem["mask_loaded"], 16)
                for to, v in ((bias_k, "L2_xattn_bk"), (bias_q, "L2_xattn_bq")):
                    sp.dma_start(to[:], a[v].rearrange("(p c) -> p c", c=1)).then_inc(sem["bias_loaded"], 16)
                sp.wait_ge(sem["weights_loaded"], 48)

            @block.gpsimd
            def _(pool):
                pool.memset(head_mask[:], 1.0).then_inc(sem["ones_set"], 1)
                pool.memset(values_rhs[:], 0.0).then_inc(sem["rhs_zeroed"], 1)
                pool.wait_ge(sem["ones_set"], 1)
                pool.affine_select(out=head_mask[:], in_=head_mask[:], compare_op=ALU.is_ge, fill=0.0, base=0,
                                   pattern=[[-wide, heads]], channel_multiplier=1).then_inc(sem["lower_cut"], 1)
                pool.wait_ge(sem["lower_cut"], 1)
                pool.affine_select(out=head_mask[:], in_=head_mask[:], compare_op=ALU.is_ge, fill=0.0, base=wide - 1,
                                   pattern=[[wide, heads]], channel_multiplier=-1).then_inc(sem["mask_made"], 1)
                pool.wait_ge(sem["mask_loaded"], 16)
                for b in range(B):
                    pool.tensor_copy(score_bias[:, b, :].rearrange("p (h k) -> p h k", h=heads),
                                     mask[:, None, b * C:(b + 1) * C].to_broadcast([P, heads, C]))\
                        .then_inc(sem["bias_spread"], 1)

            @block.tensor
            def _(pe):
                pe.wait_ge(sem["weights_loaded"], 48)
                pe.matmul(ps[:, 0, 0:B * C], wk[:], keep.ctx_t[:], start=True, stop=True).then_inc(sem["k_made"], 1)
                pe.wait_ge(sem["ctx_doubled"], 1)
                for b in range(B):
                    mm = pe.matmul(ps[:, 1, b * D:(b + 1) * D], ctx_twice[:, b, :, :].rearrange("p e k -> p (e k)"),
                                   wv[:], start=True, stop=True)
                mm.then_inc(sem["v_made"], 1)

            @block.scalar
            def _(act):
                act.wait_ge(sem["bias_loaded"], 32)
                act.activation(bias_q[:], bias_q[:], ACT.Copy, scale=scale).then_inc(sem["q_scaled"], 1)
                act.wait_ge(sem["v_made"], 1)
                act.wait_ge(sem["rhs_zeroed"], 1)
                for e in range(2):
                    rows = slice(e * C, (e + 1) * C)
                    act.activation(values_rhs[rows, :, :, e * wide:(e + 1) * wide],
                                   ps[rows, 1, :].rearrange("r (b p e d) -> r b p e d", b=B, e=2, d=wide)[:, :, :, e, :],
                                   ACT.Copy).then_inc(sem["v_kept"], 1)

            @block.vector
            def _(dve):
                dve.tensor_copy(ctx_twice[:], keep.ctx_t[:].rearrange("p (b k) -> p b k", b=B)[:, :, None, :]
                                .to_broadcast([P, B, 2, C])).then_inc(sem["ctx_doubled"], 1)
                dve.wait_ge(sem["k_made"], 1)
                dve.wait_ge(sem["bias_loaded"], 32)
                dve.tensor_scalar(k_t[:], ps[:, 0, 0:B * C], bias_k[:, 0:1], None, ALU.add).then_inc(sem["k_kept"], 1)
                dve.wait_ge(sem["k_kept"], 1)
                dve.wait_ge(sem["mask_made"], 1)
                for b in range(B):
                    dve.tensor_tensor(scores_rhs[:, b, :].rearrange("p (h k) -> p h k", h=heads),
                                      k_t[:, None, b * C:(b + 1) * C].to_broadcast([P, heads, C]),
                                      head_mask[:, :, None].to_broadcast([P, heads, C]), ALU.mult)\
                        .then_inc(sem["k_spread"], 1)


class Normed:

    def __init__(self, s, keep, bank_a, bank_b, padded=False):
        self.keep, self.banks, self.padded = keep, (bank_a, bank_b), padded
        self.xn, self.xt = s.sb("xn", [P, NT, D]), s.sb("xt", [P, B, S + 2] if padded else [P, NT, P])
        self.stats, self.moments = s.sb("stats", [P, NT, 6]), s.sb("moments", [P, NT, 2])
        self.var_eps, self.rstd = s.sb("var_eps", [P, NT]), s.sb("rstd", [P, NT])
        self.stats_made, self.moments_made = s.sem("stats_made"), s.sem("moments_made")
        self.var_ready, self.rstd_ready = s.sem("var_ready"), s.sem("rstd_ready")
        self.xn_ready, self.xn_turned, self.xt_ready = s.sem("xn_ready"), s.sem("xn_turned"), s.sem("xt_ready")

    def vector(self, dve):
        x = self.keep.x
        for t in range(NT):
            dve.bn_stats(self.stats[:, t, :], x[:, t, :]).then_inc(self.stats_made, 1)
        for t in range(NT):
            dve.wait_ge(self.stats_made, t + 1)
            dve.bn_aggr(self.moments[:, t, :], self.stats[:, t, :]).then_inc(self.moments_made, 1)
        dve.wait_ge(self.moments_made, NT)
        dve.tensor_scalar(self.var_eps[:], self.moments[:, :, 1], EPS, None, ALU.add).then_inc(self.var_ready, 1)
        dve.wait_ge(self.rstd_ready, 1)
        for t in range(NT):
            dve.tensor_scalar(self.xn[:, t, :], x[:, t, :], self.moments[:, t, 0:1], self.rstd[:, t:t + 1],
                              ALU.subtract, ALU.mult).then_inc(self.xn_ready, 1)

    def gpsimd(self, pool):
        pool.wait_ge(self.var_ready, 1)
        pool.tensor_tensor(self.rstd[:], self.var_eps[:], self.keep.neg_half[:, 0:NT], ALU.pow)\
            .then_inc(self.rstd_ready, 1)

    def tensor(self, pe):
        for t in range(NT):
            pe.wait_ge(self.xn_ready, t + 1)
            mm = pe.transpose(self.banks[t // 4][:, (t % 4) * P:(t % 4 + 1) * P], self.xn[:, t, :],
                              self.keep.identity[:])
            if t % 4 == 3:
                mm.then_inc(self.xn_turned, 1)

    def scalar(self, act):
        for n in range(2):
            act.wait_ge(self.xn_turned, n + 1)
            if self.padded:
                act.activation(self.xt[:, 2 * n:2 * n + 2, 1:S + 1], self.banks[n].rearrange("p (b k) -> p b k", b=2),
                               ACT.Copy).then_inc(self.xt_ready, 1)
            else:
                act.activation(self.xt[:, 4 * n:4 * n + 4, :].rearrange("p t k -> p (t k)"), self.banks[n][:],
                               ACT.Copy).then_inc(self.xt_ready, 1)


def lora_ffn(nc, a, keep, name, gate):
    with Scope(nc, name) as s:
        ps = s.psum("ps", [P, 8, 512])
        norm = Normed(s, keep, ps[:, 0], ps[:, 1])
        w1, w1_t = s.sb("w1", [P, 4, D]), s.sb("w1_t", [P, 4, P])
        w2, w2_t = s.sb("w2", [P, 4, P]), s.sb("w2_t", [P, 4, D])
        b1_rows, b1, b2 = s.sb("b1_rows", [4, P]), s.sb("b1", [P, 4]), s.sb("b2", [P, D])
        scale, odd = s.sb("scale", [P, 1]), s.sb("odd", [P, B, 8])
        w1_own, w2_own = s.sb("w1_own", [P, 2, 4, P]), s.sb("w2_own", [P, 2, 4, D])
        hidden, change = s.sb("hidden", [P, 2, 4, S]), s.sb("change", [P, 2, 2, D])
        names = ["loaded", "w_turned", "w_kept", "b1_turned", "b1_kept", "odd_scaled", "even_made", "own_made",
                 "hidden_made", "gelu_done", "out_made", "change_made", "x_done"]
        sem = {n: s.sem(n) for n in names}
        with s.block() as block:

            @block.sync
            def _(sp):
                sp.dma_start(w1[:], a["L0_ffn_W1"].rearrange("(j h) d -> h j d", h=P)).then_inc(sem["loaded"], 16)
                sp.dma_start(w2[:], a["L0_ffn_W2"].rearrange("o (g c) -> o g c", c=P)).then_inc(sem["loaded"], 16)
                sp.dma_start(b1_rows[:], a["L0_ffn_b1"].rearrange("(j h) -> j h", h=P)).then_inc(sem["loaded"], 16)
                sp.dma_start(b2[:], row(a["L0_ffn_b2"]).to_broadcast([P, D])).then_inc(sem["loaded"], 16)
                sp.dma_start(scale[:], row(a["L0_ffn_scale"]).to_broadcast([P, 1])).then_inc(sem["loaded"], 16)

            @block.gpsimd
            def _(pool):
                norm.gpsimd(pool)

            @block.tensor
            def _(pe):
                pe.wait_ge(sem["loaded"], 80)
                for j in range(4):
                    pe.transpose(ps[:, 2, j * P:(j + 1) * P], w1[:, j, :], keep.identity[:])
                    mm = pe.transpose(ps[:, 3, j * P:(j + 1) * P], w2[:, j, :], keep.identity[:])
                mm.then_inc(sem["w_turned"], 1)
                pe.transpose(ps[:, 4, 0:4], b1_rows[:], keep.identity[0:4, 0:4]).then_inc(sem["b1_turned"], 1)
                norm.tensor(pe)

                def even(b):
                    if b == 0:
                        pe.wait_ge(sem["w_kept"], 2)
                    else:
                        pe.wait_ge(sem["own_made"], 8 * b)
                    for j in range(8):
                        mm = pe.matmul(ps[:, 2 + j // 4, (j % 4) * D:(j % 4 + 1) * D],
                                       keep.identity[:, 1 + 2 * j:2 + 2 * j].to_broadcast([P, P]),
                                       norm.xn[:, 2 * b, :], start=True, stop=True)
                    mm.then_inc(sem["even_made"], 1)

                def up(b):
                    pe.wait_ge(sem["own_made"], 8 * (b + 1))
                    pe.wait_ge(norm.xt_ready, 2)
                    if b >= 1:
                        pe.wait_ge(sem["gelu_done"], 4 * b)
                    for j in range(4):
                        mm = pe.matmul(ps[:, 4 + j // 2, (j % 2) * S:(j % 2 + 1) * S], w1_own[:, b % 2, j, :],
                                       norm.xt[:, 2 * b:2 * b + 2, :].rearrange("p t k -> p (t k)"),
                                       start=True, stop=True)
                    mm.then_inc(sem["hidden_made"], 1)

                def down(b):
                    pe.wait_ge(sem["gelu_done"], 4 * (b + 1))
                    if b >= 2:
                        pe.wait_ge(sem["change_made"], b - 1)
                    for u in range(2):
                        for g in range(4):
                            mm = pe.matmul(ps[:, 6 + b % 2, u * D:(u + 1) * D],
                                           hidden[:, b % 2, g, u * P:(u + 1) * P], w2_own[:, b % 2, g, :],
                                           start=(g == 0), stop=(g == 3))
                    mm.then_inc(sem["out_made"], 1)

                pe.wait_ge(sem["b1_kept"], 1)
                even(0)
                for b in range(B):
                    up(b)
                    if b + 1 < B:
                        even(b + 1)
                    down(b)

            @block.scalar
            def _(act):
                act.wait_ge(sem["b1_turned"], 1)
                act.activation(b1[:], ps[:, 4, 0:4], ACT.Copy).then_inc(sem["b1_kept"], 1)
                norm.scalar(act)
                act.wait_ge(sem["b1_kept"], 1)
                for b in range(B):
                    act.wait_ge(sem["hidden_made"], b + 1)
                    if b >= 2:
                        act.wait_ge(sem["out_made"], b - 1)
                    for j in range(4):
                        act.activation(hidden[:, b % 2, j, :], ps[:, 4 + j // 2, (j % 2) * S:(j % 2 + 1) * S],
                                       ACT.Gelu, bias=b1[:, j:j + 1]).then_inc(sem["gelu_done"], 1)

            @block.vector
            def _(dve):
                dve.wait_ge(sem["w_turned"], 1)
                dve.tensor_copy(w1_t[:].rearrange("p j h -> p (j h)"), ps[:, 2]).then_inc(sem["w_kept"], 1)
                dve.tensor_copy(w2_t[:].rearrange("p j h -> p (j h)"), ps[:, 3]).then_inc(sem["w_kept"], 1)
                norm.vector(dve)
                dve.wait_ge(norm.xt_ready, 2)
                for b in range(B):
                    dve.tensor_scalar(odd[:, b, :], norm.xt[:, 2 * b, 2:18:2], scale[:, 0:1], None, ALU.mult)\
                        .then_inc(sem["odd_scaled"], 1)

                def own(b):
                    dve.wait_ge(sem["odd_scaled"], B)
                    dve.wait_ge(sem["w_kept"], 2)
                    dve.wait_ge(sem["even_made"], b + 1)
                    if b >= 2:
                        dve.wait_ge(sem["out_made"], b - 1)
                    for j in range(4):
                        dve.scalar_tensor_tensor(out=w1_own[:, b % 2, j, :], in0=ps[:, 2, j * D:(j + 1) * D],
                                                 scalar=odd[:, b, j:j + 1], in1=w1_t[:, j, :], op0=ALU.mult,
                                                 op1=ALU.add).then_inc(sem["own_made"], 1)
                    for m in range(4):
                        cols = slice(32 * m, 32 * m + 32)
                        dve.scalar_tensor_tensor(
                            out=w2_own[:, b % 2, :, cols],
                            in0=ps[:, 3, m * D:(m + 1) * D].rearrange("c (o g) -> c g o", g=4),
                            scalar=odd[:, b, 4 + m:5 + m], in1=w2_t[:, :, cols], op0=ALU.mult,
                            op1=ALU.add).then_inc(sem["own_made"], 1)

                def update(b):
                    dve.wait_ge(sem["out_made"], b + 1)
                    dve.tensor_tensor(change[:, b % 2], ps[:, 6 + b % 2, 0:2 * D].rearrange("p (u d) -> p u d", u=2),
                                      b2[:, None, :].to_broadcast([P, 2, D]), ALU.add).then_inc(sem["change_made"], 1)
                    dve.wait_ge(sem["change_made"], b + 1)
                    dve.scalar_tensor_tensor(out=keep.x[:, 2 * b:2 * b + 2, :], in0=change[:, b % 2], scalar=gate,
                                             in1=keep.x[:, 2 * b:2 * b + 2, :], op0=ALU.mult, op1=ALU.add)\
                        .then_inc(sem["x_done"], 1)

                own(0)
                for b in range(B):
                    if b + 1 < B:
                        own(b + 1)
                    update(b)


class GeluWeights:

    def __init__(self, s):
        self.w1, self.w2 = s.sb("w1", [P, EXPERTS, 512]), s.sb("w2", [P, EXPERTS, 4, 512])
        self.w3, self.b3 = s.sb("w3", [P, EXPERTS, 4, D]), s.sb("b3", [P, EXPERTS, D])
        self.b_rows, self.b = s.sb("b_rows", [2 * EXPERTS * 4, P]), s.sb("b", [P, 2 * EXPERTS * 4])
        self.loaded = s.gpsimd_dma_sem("loaded")


def load_gelu_weights(nc, a, s):
    w = GeluWeights(s)
    with nc.Block() as block:

        @block.gpsimd
        def _(pool):
            for n, v in enumerate(("L1_ffn_b1", "L1_ffn_b2")):
                pool.dma_start(w.b_rows[32 * n:32 * n + 32, :], a[v].rearrange("e (c d) -> (e c) d", d=P))\
                    .then_inc(w.loaded, 16)
            pool.dma_start(w.b3[:], a["L1_ffn_b3"].rearrange("(o e) d -> o e d", o=1).to_broadcast([P, EXPERTS, D]))\
                .then_inc(w.loaded, 16)
            pool.dma_start(w.w1[:], a["L1_ffn_W1"].rearrange("e d h -> d e h")).then_inc(w.loaded, 16)
            pool.dma_start(w.w3[:], a["L1_ffn_W3"].rearrange("e (c d) h -> d e c h", d=P)).then_inc(w.loaded, 16)
            pool.dma_start(w.w2[:], a["L1_ffn_W2"].rearrange("e (c d) h -> d e c h", d=P)).then_inc(w.loaded, 16)
    return w


def turn_expert_biases(nc, keep, name, w):
    with Scope(nc, name) as s:
        ps = s.psum("ps", [P, 512])
        turned, kept = s.sem("turned"), s.sem("kept")
        with s.block() as block:

            @block.tensor
            def _(pe):
                pe.wait_ge(w.loaded, 96)
                pe.transpose(ps[:, 0:64], w.b_rows[:], keep.identity[0:64, 0:64]).then_inc(turned, 1)

            @block.vector
            def _(dve):
                dve.wait_ge(turned, 1)
                dve.tensor_copy(w.b[:], ps[:, 0:64]).then_inc(kept, 1)


def program(nc, a, out):
    with Scope(nc, "keep") as s:
        keep = Keep(s)
        setup(nc, a, keep)
        check_mask(nc, a, keep, "mask")

        def gate(kind, layer):
            return keep.gates[:, B * kind + layer:B * kind + layer + 1]

        with Scope(nc, "experts1") as own:
            w = load_gelu_weights(nc, a, own)
            with Scope(nc, "attention01") as q:
                scores_rhs, values_rhs = q.sb("scores_rhs", [P, B, 16 * C]), q.sb("values_rhs", [P, B, 8, D])
                head_operands(nc, a, keep, "operands0",
                              [a[f"L0_xattn_{n}_kernel"] for n in ("query", "key", "value", "projection")], None,
                              0.125, scores_rhs, values_rhs, None)
                cross_attention(nc, a, keep, "attention0", scores_rhs, values_rhs, None,
                                a["L0_xattn_projection_bias"], gate(0, 0))
            lora_ffn(nc, a, keep, "ffn0", gate(1, 0))
            with Scope(nc, "attention1") as q:
                scores_rhs, values_rhs = q.sb("scores_rhs", [P, B, 16 * C]), q.sb("values_rhs", [P, B, 8, D])
                score_bias = q.sb("score_bias", [P, B, 16 * C])
                head_operands(nc, a, keep, "operands1", [a[f"L1_xattn_{n}"] for n in ("WQ", "WK", "WV", "WO")],
                              [a[f"L1_xattn_{n}"] for n in ("bQ", "bK", "bV")], 0.125, scores_rhs, values_rhs,
                              score_bias)
                cross_attention(nc, a, keep, "attention1", scores_rhs, values_rhs, score_bias, a["L1_xattn_bO"],
                                gate(0, 1))
            routes = Routes(nc, own, "ffn1")
            turn_expert_biases(nc, keep, "biases1", w)
            route(nc, keep, "route1", routes, a["L1_ffn_expert_tokens"], gate(1, 1), False)
            gelu_experts(nc, keep, "experts1", routes, w.w1, w.w2, w.w3, w.b[:, 0:32], w.b[:, 32:64], w.b3)
            combine(nc, keep, "combine1", routes)
        with Scope(nc, "experts23") as own:
            experts2 = Scope(nc, "experts2")
            w_in3, w_out3 = own.sb("w_in3", [P, EXPERTS, 512]), own.sb("w_out3", [P, EXPERTS, 2, D])
            loaded3 = own.gpsimd_dma_sem("loaded3")
            experts2.__enter__()
            w_in2, w_out2 = experts2.sb("w_in2", [P, EXPERTS, 1024]), experts2.sb("w_out2", [P, EXPERTS, 4, D])
            with Scope(nc, "raw2") as raw:
                gate_up, down = raw.sb("gate_up", [P, EXPERTS, 8, D]), raw.sb("down", [P, EXPERTS, 512])
                keep.raw_loaded = [raw.gpsimd_dma_sem("gate_up_loaded"), raw.gpsimd_dma_sem("down_loaded")]
                with nc.Block() as block:

                    @block.gpsimd
                    def _(pool):
                        pool.dma_start(gate_up[:], a["L2_ffn_gate_up_proj"].rearrange("e (c i) h -> i e c h", i=P))\
                            .then_inc(keep.raw_loaded[0], 16)
                        pool.dma_start(down[:], a["L2_ffn_down_proj"].rearrange("e h i -> h e i"))\
                            .then_inc(keep.raw_loaded[1], 16)
                        pool.dma_start(w_in3[:, :, 0:256], a["L3_ffn_gate_w"].rearrange("e d i -> d e i"))\
                            .then_inc(loaded3, 16)
                        pool.dma_start(w_in3[:, :, 256:512], a["L3_ffn_up_w"].rearrange("e d i -> d e i"))\
                            .then_inc(loaded3, 16)
                        pool.dma_start(w_out3[:], a["L3_ffn_down_w"].rearrange("e (c i) d -> i e c d", i=P))\
                            .then_inc(loaded3, 16)

                with Scope(nc, "attention2") as q:
                    scores_rhs, values_rhs = q.sb("scores_rhs", [P, B, 16 * C]), q.sb("values_rhs", [P, B, 8, 16])
                    score_bias, wq, bias_q = q.sb("score_bias", [P, B, 16 * C]), q.sb("wq", [P, D]), q.sb("bias_q", [P, 1])
                    latent_operands(nc, a, keep, "operands2", scores_rhs, values_rhs, score_bias, wq, bias_q, 8 ** -0.5)
                    cross_attention(nc, a, keep, "attention2", scores_rhs, values_rhs, score_bias, a["L2_xattn_bv"],
                                    gate(0, 2), (wq[:], bias_q[:]), 8 ** -0.5)
                turn_gated_weights(nc, a, keep, "weights2", gate_up, down, w_in2, w_out2)
            routes = Routes(nc, experts2, "ffn2", 1)
            route(nc, keep, "route2", routes, a["L2_ffn_gate_w"], gate(1, 2), True)
            gated_experts(nc, keep, "gated2", routes, w_in2, w_out2)
            combine(nc, keep, "combine2", routes)
            experts2.__exit__()
            with Scope(nc, "attention3") as q:
                taps = q.sb("taps", [P, B, 16, TAPS])
                conv_kernels(nc, a, keep, "kernels3", taps)
                conv_attention_any_mask(nc, a, keep, "masked3", taps, gate(0, 3))
                conv_attention_causal(nc, a, keep, "causal3", taps, gate(0, 3))
            routes = Routes(nc, own, "ffn3", 2)
            with nc.Block() as block:

                @block.tensor
                def _(pe):
                    pe.wait_ge(loaded3, 48)

            route(nc, keep, "route3", routes, a["L3_ffn_router_w"], gate(1, 3), True)
            gated_experts(nc, keep, "gated3", routes, w_in3, w_out3)
            combine(nc, keep, "combine3", routes)
        store(nc, a, keep, out)


def kernel(**inputs):
    import concourse.bacc as bacc
    from concourse.bass_utils import run_bass_kernel_spmd

    nc = bacc.Bacc("TRN2", target_bir_lowering=False, num_devices=1)
    arrays, a = {}, {}
    for name, value in inputs.items():
        value = np.ascontiguousarray(value)
        if not value.shape:
            value = value.reshape(1)
        arrays["in_" + name] = value
        a[name] = nc.dram_tensor("in_" + name, value.shape, mybir.dt.from_np(value.dtype), kind="ExternalInput").ap()
    out = nc.dram_tensor("out", (B, S, D), F32, kind="ExternalOutput").ap()
    program(nc, a, out)
    return run_bass_kernel_spmd(nc, [arrays], core_ids=[0]).results[0]["out"]
```

```python
import numpy as np
import concourse.bass as bass
from concourse import mybir
from contextlib import ExitStack, nullcontext

F32 = mybir.dt.float32
BF16 = mybir.dt.bfloat16
I32 = mybir.dt.int32
U32 = mybir.dt.uint32
U8 = mybir.dt.uint8
ALU = mybir.AluOpType
ACT = mybir.ActivationFunctionType
AX = mybir.AxisListType.X

P = 128
B, S, D = 4, 256, 128
T = B * S
NT = T // P
C = 64
EPS = 1e-5


class Tally:

    def __init__(self, sem):
        self.sem, self.n, self.top, self.mark = sem, 0, None, 0

    def add(self, instruction, by=1):
        instruction.then_inc(self.sem, by)
        self.n += by
        return instruction

    def enter(self, i, per):
        self.top, self.mark, self.per = self.n + i * per, self.n, per

    def leave(self, times):
        assert self.n - self.mark == self.per, (self.n - self.mark, self.per)
        self.top, self.n = None, self.mark + times * self.per

    def now(self):
        return self.n if self.top is None else self.top + (self.n - self.mark)

    def wait(self, engine):
        engine.wait_ge(self.sem, self.now())


class Together:

    current = None

    def __init__(self, nc):
        self.nc, self.scopes, self.block = nc, [], nc.Block()

    def __enter__(self):
        Together.current = self
        self.opened = self.block.__enter__()
        return self.opened

    def __exit__(self, *error):
        Together.current = None
        self.block.__exit__(*error)
        for scope in reversed(self.scopes):
            scope.free()


class Scope:

    def __init__(self, nc, name):
        self.nc, self.name, self.stack, self.sems = nc, name, ExitStack(), []

    def __enter__(self):
        self.stack.__enter__()
        if Together.current:
            Together.current.scopes.append(self)
        return self

    def __exit__(self, *error):
        if not Together.current:
            self.free()

    def free(self):
        self.stack.close()
        numbers = sorted(sem.num for sem in self.sems)
        while numbers:
            n = 1
            while n < len(numbers) and numbers[n] == numbers[0] + n:
                n += 1
            self.nc.gpsimd.sem_clear(range(numbers[0], numbers[0] + n))
            numbers = numbers[n:]

    def sb(self, name, shape, dtype=F32):
        return self.stack.enter_context(self.nc.sbuf_tensor(f"{self.name}_{name}", shape, dtype))

    def psum(self, name, shape, dtype=F32):
        return self.stack.enter_context(self.nc.psum_tensor(f"{self.name}_{name}", shape, dtype))

    def sem(self, name):
        self.sems.append(self.stack.enter_context(self.nc.semaphore(f"{self.name}_{name}")))
        return self.sems[-1]

    def gpsimd_dma_sem(self, name):
        return self.nc.alloc_semaphore(f"{self.name}_{name}")

    def block(self):
        return nullcontext(Together.current.opened) if Together.current else self.nc.Block()


def row(ap):
    return ap.rearrange("(a n) -> a n", a=1)


def setup(nc, a, keep, heads0):
    with Scope(nc, "setup") as s:
        gates_raw = s.sb("gates_raw", [P, 2 * B])
        ctx = s.sb("ctx", [P, 2, D])
        ps = s.psum("ps", [P, 2, 512])
        ctx_loaded, gates_loaded = s.sem("ctx_loaded"), s.sem("gates_loaded")
        zeroed, identity_made, ctx_turned = s.sem("zeroed"), s.sem("identity_made"), s.sem("ctx_turned")
        ctx_kept, gates_made, half_made = s.sem("ctx_kept"), s.sem("gates_made"), s.sem("half_made")
        with s.block() as block:

            @block.sync
            def _(sp):
                sp.dma_start(ctx[:], a["ctx_1024"].rearrange("(u b) k d -> (b k) u d", u=2)).then_inc(ctx_loaded, 16)
                sp.dma_start(gates_raw[:, 0:B], row(a["g_xattn"]).to_broadcast([P, B])).then_inc(gates_loaded, 16)
                sp.dma_start(gates_raw[:, B:2 * B], row(a["g_ffn"]).to_broadcast([P, B])).then_inc(gates_loaded, 16)
                sp.dma_start(keep.x[:], a["x"].rearrange("b (u p) d -> p (b u) d", p=P)).then_inc(keep.x_loaded, 16)
                heads0.load(sp)

            @block.gpsimd
            def _(pool):
                pool.iota(keep.iota[:], pattern=[[1, P]], base=0, channel_multiplier=0,
                          allow_small_or_imprecise_dtypes=True)
                pool.iota(keep.iota_tiles[:], pattern=[[P, NT]], base=0, channel_multiplier=0,
                          allow_small_or_imprecise_dtypes=True)
                pool.iota(keep.token[:], pattern=[[P, NT]], base=0, channel_multiplier=1,
                          allow_small_or_imprecise_dtypes=True)
                pool.memset(keep.identity[:], 0.0).then_inc(zeroed, 1)
                pool.memset(keep.neg_half[:], -0.5).then_inc(half_made, 1)
                pool.wait_ge(zeroed, 1)
                pool.affine_select(out=keep.identity[:], in_=keep.identity[:], compare_op=ALU.not_equal, fill=1.0,
                                   base=0, pattern=[[-1, P]], channel_multiplier=1).then_inc(identity_made, 1)

            @block.scalar
            def _(act):
                act.wait_ge(gates_loaded, 32)
                act.activation(keep.gates[:], gates_raw[:], ACT.Tanh).then_inc(gates_made, 1)

            @block.tensor
            def _(pe):
                pe.wait_ge(ctx_loaded, 16)
                pe.wait_ge(identity_made, 1)
                for u in range(2):
                    pe.transpose(ps[:, u, 0:P], ctx[:, u, :], keep.identity[:]).then_inc(ctx_turned, 1)

            @block.vector
            def _(dve):
                for u in range(2):
                    dve.wait_ge(ctx_turned, u + 1)
                    dve.tensor_copy(keep.ctx_t[:, u * P:(u + 1) * P], ps[:, u, 0:P]).then_inc(ctx_kept, 1)


class RowStats:

    def __init__(self, keep, s):
        self.keep = keep
        self.stats, self.moments = s.sb("stats", [P, NT, 6]), s.sb("moments", [P, NT, 2])
        self.var_eps, self.rstd = s.sb("var_eps", [P, NT]), s.sb("rstd", [P, NT])
        self.stats_made, self.moments_made = s.sem("stats_made"), s.sem("moments_made")
        self.var_ready, self.rstd_ready = s.sem("var_ready"), s.sem("rstd_ready")

    def vector(self, dve):
        dve.wait_ge(self.keep.x_loaded, 16)
        for t in range(NT):
            self.stats_of_tile(dve, t)
        self.join_stats(dve)

    def stats_of_tile(self, dve, t):
        dve.bn_stats(self.stats[:, t, :], self.keep.x[:, t, :]).then_inc(self.stats_made, 1)

    def join_stats(self, dve):
        for t in range(NT):
            dve.wait_ge(self.stats_made, t + 1)
            dve.bn_aggr(self.moments[:, t, :], self.stats[:, t, :]).then_inc(self.moments_made, 1)
        dve.wait_ge(self.moments_made, NT)
        dve.tensor_scalar(self.var_eps[:], self.moments[:, :, 1], EPS, None, ALU.add).then_inc(self.var_ready, 1)

    def gpsimd(self, pool):
        pool.wait_ge(self.var_ready, 1)
        pool.tensor_tensor(self.rstd[:], self.var_eps[:], self.keep.neg_half[:, 0:NT], ALU.pow)\
            .then_inc(self.rstd_ready, 1)


class HeadWeights:

    def __init__(self, s, weights, biases, out_bias):
        self.weights, self.biases, self.out_bias = weights, biases, out_bias
        self.wq, self.wk, self.wv = (s.sb(n, [P, 16 * C]) for n in ("wq", "wk", "wv"))
        self.wo = s.sb("wo", [P, 8, D])
        self.bias_rows = s.sb("bias_rows", [24, P])
        self.out_bias_rows = s.sb("out_bias_rows", [P, D])
        self.loaded, self.bias_loaded = s.sem("loaded"), s.sem("bias_loaded")
        self.out_bias_loaded, self.wo_loaded = s.sem("out_bias_loaded"), s.sem("wo_loaded")

    def load(self, sp):
        for to, w in zip((self.wq, self.wk, self.wv), self.weights[:3]):
            if len(w.shape) == 3:
                sp.dma_start(to[:].rearrange("i (h o) -> i h o", o=C), w.rearrange("h i o -> i h o"))\
                    .then_inc(self.loaded, 16)
            else:
                sp.dma_start(to[:], w).then_inc(self.loaded, 16)
        wo = self.weights[3]
        wo = wo.rearrange("h o n -> (h o) n") if len(wo.shape) == 3 else wo
        sp.dma_start(self.wo[:], wo.rearrange("(p r) n -> r p n", r=P)).then_inc(self.wo_loaded, 16)
        for n, v in enumerate(self.biases or ()):
            sp.dma_start(self.bias_rows[n * 8:(n + 1) * 8, :], v.rearrange("(p r) -> p r", r=P))\
                .then_inc(self.bias_loaded, 16)
        sp.dma_start(self.out_bias_rows[:], row(self.out_bias).to_broadcast([P, D])).then_inc(self.out_bias_loaded, 16)


def head_operands(nc, keep, name, w, scale, scores_rhs, values_rhs, score_bias, load_ahead=None):
    pairs = 8
    with Scope(nc, name) as s:
        wq, wk, wv, wo, bias_rows, biases = w.wq, w.wk, w.wv, w.wo, w.bias_rows, w.biases
        wq_t = s.sb("wq_t", [P, 2, P])
        k_t = s.sb("k_t", [P, 2, B * C])
        v_diag = s.sb("v_diag", [P, 2, B, 2, C])
        bias = s.sb("bias", [P, 3 * pairs])
        ps = s.psum("ps", [P, 8, 512])
        names = ["bias_turned", "bias_kept", "wq_turned", "wq_kept", "kv_made", "k_kept",
                 "v_kept", "scores_made", "scores_kept", "bias_done", "values_made",
                 "values_kept", "diag_zeroed"]
        sem = {n: s.sem(n) for n in names}
        sem.update(loaded=w.loaded, bias_loaded=w.bias_loaded)
        loads = 3
        with s.block() as block:

            @block.sync
            def _(sp):
                sp.wait_ge(sem["loaded"], 16 * loads)
                sp.wait_ge(w.wo_loaded, 16)
                sp.wait_ge(w.out_bias_loaded, 16)
                if load_ahead:
                    load_ahead(sp)

            @block.gpsimd
            def _(pool):
                pool.memset(v_diag[:], 0.0).then_inc(sem["diag_zeroed"], 1)

            @block.tensor
            def _(pe):
                def project(p):
                    u, cols = p % 2, slice(p * P, (p + 1) * P)
                    if p >= 2:
                        pe.wait_ge(sem["wq_kept"], p - 1)
                        pe.wait_ge(sem["k_kept"], p - 1)
                        pe.wait_ge(sem["v_kept"], 2 * (p - 1))
                    pe.transpose(ps[:, 2 + u, 0:P], wq[:, cols], keep.identity[:]).then_inc(sem["wq_turned"], 1)
                    pe.matmul(ps[:, u, 0:256], wk[:, cols], keep.ctx_t[:], start=True, stop=True)
                    pe.matmul(ps[:, u, 256:512], wv[:, cols], keep.ctx_t[:], start=True, stop=True)\
                        .then_inc(sem["kv_made"], 1)

                def fold(p):
                    u = p % 2
                    pe.wait_ge(sem["wq_kept"], p + 1)
                    pe.wait_ge(sem["k_kept"], p + 1)
                    if p >= 1:
                        pe.wait_ge(sem["scores_kept"], p)
                        if biases:
                            pe.wait_ge(sem["bias_done"], p)
                    for e in range(2):
                        rows = slice(e * C, (e + 1) * C)
                        mm = pe.matmul(ps[:, 4 + e, 0:256], wq_t[rows, u, :], k_t[rows, u, :], start=True, stop=True)
                        if biases:
                            mm = pe.matmul(ps[:, 4 + e, 256:512], bias[rows, p:p + 1].to_broadcast([C, P]),
                                           k_t[rows, u, :], start=True, stop=True)
                        mm.then_inc(sem["scores_made"], 1)
                    pe.wait_ge(sem["v_kept"], 2 * (p + 1))
                    if p == 0:
                        pe.wait_ge(w.wo_loaded, 16)
                    if p >= 2:
                        pe.wait_ge(sem["values_kept"], p - 1)
                    for b in range(B):
                        mm = pe.matmul(ps[:, 6 + u, b * D:(b + 1) * D],
                                       v_diag[:, u, b, :, :].rearrange("r e k -> r (e k)"), wo[:, p, :],
                                       start=True, stop=True)
                    mm.then_inc(sem["values_made"], 1)

                pe.wait_ge(sem["loaded"], 16 * loads)
                if biases:
                    pe.wait_ge(sem["bias_loaded"], 48)
                    pe.transpose(ps[:, 7, 0:3 * pairs], bias_rows[:], keep.identity[0:3 * pairs, 0:3 * pairs])\
                        .then_inc(sem["bias_turned"], 1)
                    pe.wait_ge(sem["bias_kept"], 1)
                project(0)
                for p in range(pairs):
                    if p + 1 < pairs:
                        project(p + 1)
                    fold(p)

            @block.scalar
            def _(act):
                def keep_wq(p):
                    act.wait_ge(sem["wq_turned"], p + 1)
                    if p >= 2:
                        act.wait_ge(sem["scores_made"], 2 * (p - 1))
                    act.activation(wq_t[:, p % 2, :], ps[:, 2 + p % 2, 0:P], ACT.Copy).then_inc(sem["wq_kept"], 1)

                keep_wq(0)
                for p in range(pairs):
                    if p + 1 < pairs:
                        keep_wq(p + 1)
                    act.wait_ge(sem["scores_made"], 2 * (p + 1))
                    act.activation(scores_rhs[:, :, p * P:(p + 1) * P].rearrange("i b (e k) -> i e b k", e=2),
                                   ps[:, 4:6, 0:256].rearrange("i e (b k) -> i e b k", b=B), ACT.Copy, scale=scale)\
                        .then_inc(sem["scores_kept"], 1)
                    if biases:
                        act.activation(score_bias[:, :, p * P:(p + 1) * P].rearrange("i b (e k) -> i e b k", e=2),
                                       ps[:, 4:6, 256:512].rearrange("i e (b k) -> i e b k", b=B), ACT.Copy,
                                       scale=scale).then_inc(sem["bias_done"], 1)

            @block.vector
            def _(dve):
                if biases:
                    dve.wait_ge(sem["bias_turned"], 1)
                    dve.tensor_copy(bias[:], ps[:, 7, 0:3 * pairs]).then_inc(sem["bias_kept"], 1)
                    dve.wait_ge(sem["bias_kept"], 1)

                def keep_kv(p):
                    u = p % 2
                    dve.wait_ge(sem["kv_made"], p + 1)
                    if p >= 2:
                        dve.wait_ge(sem["scores_made"], 2 * (p - 1))
                    bk = bias[:, pairs + p:pairs + p + 1] if biases else 0.0
                    dve.tensor_scalar(k_t[:, u, :], ps[:, u, 0:256], bk, None, ALU.add).then_inc(sem["k_kept"], 1)
                    if p >= 2:
                        dve.wait_ge(sem["values_made"], p - 1)
                    for e in range(2):
                        rows = slice(e * C, (e + 1) * C)
                        bv = bias[rows, 2 * pairs + p:2 * pairs + p + 1] if biases else 0.0
                        dve.tensor_scalar(v_diag[rows, u, :, e, :],
                                          ps[rows, u, 256:512].rearrange("r (b k) -> r b k", b=B), bv, None, ALU.add)\
                            .then_inc(sem["v_kept"], 1)

                dve.wait_ge(sem["diag_zeroed"], 1)
                keep_kv(0)
                for p in range(pairs):
                    if p + 1 < pairs:
                        keep_kv(p + 1)
                    dve.wait_ge(sem["values_made"], p + 1)
                    dve.tensor_copy(values_rhs[:, :, p, :], ps[:, 6 + p % 2, :].rearrange("r (b n) -> r b n", b=B))\
                        .then_inc(sem["values_kept"], 1)


def cross_attention(nc, a, keep, name, scores_rhs, values_rhs, score_bias, out_bias_rows, gate, rows, query=None,
                    query_scale=1.0, load_ahead=None):
    heads, pairs = 16, 8
    width = values_rhs.shape[3]
    own_columns = width < D
    with Scope(nc, name) as s:
        moments, rstd = rows.moments, rows.rstd
        xn = s.sb("xn", [P, 2, D])
        xn_t = s.sb("xn_t", [P, 2, P])
        q_t = s.sb("q_t", [P, 2, P]) if query else xn_t
        e = s.sb("e", [P, 2, heads, C])
        probs_t = s.sb("probs_t", [P, 2, pairs, P])
        top = s.sb("top", [P, 2, heads])
        total = s.sb("total", [P, 2, heads])
        inverse = s.sb("inverse", [P, 2, heads])
        change = s.sb("change", [P, 2, D])
        ps_scores = s.psum("ps_scores", [P, 2, heads, C])
        ps_turned = s.psum("ps_turned", [P, 2, 4, P])
        ps_out = s.psum("ps_out", [P, 512])
        ps_xn = s.psum("ps_xn", [P, 512])
        names = ["xn_ready", "xn_turned",
                 "xn_kept", "q_made", "q_kept", "scores_made", "top_found", "biased", "centred", "exp_done", "total_made",
                 "inverse_made", "probs_ready", "probs_turned", "probs_kept", "out_made", "change_made", "x_done"]
        sem = {n: s.sem(n) for n in names}
        with s.block() as block:

            @block.gpsimd
            def _(pool):
                def normalise(t, u):
                    pool.wait_ge(sem["inverse_made"], t + 1)
                    pool.tensor_tensor(e[:, u], e[:, u], inverse[:, u, :, None].to_broadcast([P, heads, C]), ALU.mult)\
                        .then_inc(sem["probs_ready"], 1)

                if not own_columns:
                    with pool.Fori(0, NT // 2) as i:
                        for u in range(2):
                            normalise(2 * i + u, u)

            if load_ahead:
                block.sync(load_ahead)

            @block.tensor
            def _(pe):
                def turn_xn(t, u, first=False):
                    pe.wait_ge(sem["xn_ready"], t + 1)
                    if not first:
                        pe.wait_ge(sem["xn_kept"], t)
                    if query and not first:
                        pe.wait_ge(sem["q_kept"], t)
                    pe.transpose(ps_xn[:, 0:P], xn[:, u, :], keep.identity[:]).then_inc(sem["xn_turned"], 1)

                def queries(t, u):
                    if query:
                        pe.wait_ge(sem["xn_kept"], t + 1)
                        pe.matmul(ps_xn[:, P:2 * P], query[0], xn_t[:, u, :], start=True, stop=True)\
                            .then_inc(sem["q_made"], 1)

                def scores(t, u, b, first=False):
                    pe.wait_ge(sem["q_kept" if query else "xn_kept"], t + 1)
                    if not first:
                        pe.wait_ge(sem["centred"], t - 1)
                    for half in range(2):
                        mm = pe.matmul(ps_scores[:, u, 8 * half:8 * half + 8, :].rearrange("p h k -> p (h k)"),
                                       q_t[:, u, :], scores_rhs[:, b, 512 * half:512 * half + 512],
                                       start=True, stop=True)
                    mm.then_inc(sem["scores_made"], 1)

                def turn_probs(t, u, first=False):
                    pe.wait_ge(sem["exp_done" if own_columns else "probs_ready"], t + 1)
                    for half in range(2):
                        if not first:
                            pe.wait_ge(sem["probs_kept"], 2 * t - 1 + half)
                        for p in range(4 * half, 4 * half + 4):
                            mm = pe.transpose(ps_turned[:, half, p % 4, :],
                                              e[:, u, 2 * p:2 * p + 2, :].rearrange("p h k -> p (h k)"),
                                              keep.identity[:])
                        mm.then_inc(sem["probs_turned"], 1)

                def output(t, u, b, first=False):
                    if not first:
                        pe.wait_ge(sem["change_made"], t)
                    for p in range(pairs):
                        if p % 4 == 0:
                            pe.wait_ge(sem["probs_kept"], 2 * t + 1 + p // 4)
                        to = ps_out[:, p * width:(p + 1) * width] if own_columns else ps_out[:, 0:D]
                        mm = pe.matmul(to, probs_t[:, u, p, :], values_rhs[:, b, p, :],
                                       start=own_columns or p == 0, stop=own_columns or p == pairs - 1)
                    mm.then_inc(sem["out_made"], 1)

                turn_xn(0, 0, True)
                queries(0, 0)
                scores(0, 0, 0, True)
                turn_xn(1, 1)
                queries(1, 1)
                scores(1, 1, 0, True)

                def step(i, first, last):
                    for u in range(2):
                        t = 2 * i + u
                        if not last:
                            turn_xn(t + 2, u)
                        turn_probs(t, u, first and u == 0)
                        if not last:
                            queries(t + 2, u)
                            scores(t + 2, u, i + 1)
                        output(t, u, i, first and u == 0)

                step(0, True, False)
                with pe.Fori(1, NT // 2 - 1) as i:
                    step(i, False, False)
                step(NT // 2 - 1, False, True)

            @block.scalar
            def _(act):
                def keep_xn(t, u, first=False):
                    act.wait_ge(sem["xn_turned"], t + 1)
                    if not first:
                        act.wait_ge(sem["q_made" if query else "scores_made"], t - 1)
                    act.activation(xn_t[:, u, :], ps_xn[:, 0:P], ACT.Copy).then_inc(sem["xn_kept"], 1)

                def keep_q(t, u, first=False):
                    if query:
                        act.wait_ge(sem["q_made"], t + 1)
                        if not first:
                            act.wait_ge(sem["scores_made"], t - 1)
                        act.activation(q_t[:, u, :], ps_xn[:, P:2 * P], ACT.Identity, bias=query[1],
                                       scale=query_scale)\
                            .then_inc(sem["q_kept"], 1)

                def exp(t, u):
                    act.wait_ge(sem["centred"], t + 1)
                    act.activation(e[:, u], e[:, u], ACT.Exp).then_inc(sem["exp_done"], 1)

                def keep_probs(t, u, first=False):
                    for half in range(2):
                        act.wait_ge(sem["probs_turned"], 2 * t + 1 + half)
                        if not first:
                            act.wait_ge(sem["out_made"], t - 1)
                        act.activation(probs_t[:, u, 4 * half:4 * half + 4, :], ps_turned[:, half], ACT.Copy)\
                            .then_inc(sem["probs_kept"], 1)

                for t in range(2):
                    keep_xn(t, t, True)
                    keep_q(t, t, True)
                exp(0, 0)

                def step(i, first, last):
                    for u in range(2):
                        t = 2 * i + u
                        if not last:
                            keep_xn(t + 2, u)
                        if not own_columns and not (last and u == 1):
                            exp(t + 1, 1 - u)
                        if not last:
                            keep_q(t + 2, u)
                        keep_probs(t, u, first)
                        if own_columns and not (last and u == 1):
                            exp(t + 1, 1 - u)

                step(0, True, False)
                with act.Fori(1, NT // 2 - 1) as i:
                    step(i, False, False)
                step(NT // 2 - 1, False, True)

            @block.vector
            def _(dve):
                dve.wait_ge(rows.rstd_ready, 1)

                def normalise(t, u, first=False):
                    if not first:
                        dve.wait_ge(sem["xn_turned"], t - 1)
                    dve.tensor_scalar(xn[:, u, :], keep.x[:, bass.ds(t, 1), :].rearrange("p a d -> p (a d)"),
                                      moments[:, bass.ds(t, 1), 0:1].rearrange("p a d -> p (a d)"),
                                      rstd[:, bass.ds(t, 1)], ALU.subtract, ALU.mult).then_inc(sem["xn_ready"], 1)

                def centre(t, u, b, first=False):
                    dve.wait_ge(sem["scores_made"], t + 1)
                    if not first:
                        dve.wait_ge(sem["probs_turned"], 2 * (t - 1))
                    scored = ps_scores[:, u]
                    if score_bias is not None:
                        bias = score_bias[:, b, :]
                        bias = (bias.rearrange("p (h k) -> p h k", h=heads) if score_bias.shape[2] > C else
                                bias.rearrange("p (x k) -> p x k", x=1).to_broadcast([P, heads, C]))
                        dve.tensor_tensor(e[:, u], ps_scores[:, u], bias, ALU.add).then_inc(sem["biased"], 1)
                        dve.wait_ge(sem["biased"], t + 1)
                        scored = e[:, u]
                    dve.tensor_reduce(top[:, u, :], scored, AX, ALU.max).then_inc(sem["top_found"], 1)
                    dve.wait_ge(sem["top_found"], t + 1)
                    dve.tensor_tensor(e[:, u], scored, top[:, u, :, None].to_broadcast([P, heads, C]), ALU.subtract)\
                        .then_inc(sem["centred"], 1)

                def sums(t, u, first=False):
                    if own_columns:
                        return
                    dve.wait_ge(sem["exp_done"], t + 1)
                    dve.tensor_reduce(total[:, u, :], e[:, u], AX, ALU.add).then_inc(sem["total_made"], 1)
                    dve.wait_ge(sem["total_made"], t + 1)
                    if not first:
                        dve.wait_ge(sem["probs_ready"], t - 1)
                    dve.reciprocal(inverse[:, u, :], total[:, u, :]).then_inc(sem["inverse_made"], 1)

                def update(t, u):
                    dve.wait_ge(sem["out_made"], t + 1)
                    made = ps_out[:, 0:D]
                    if own_columns:
                        parts = ps_out[:, 0:pairs * width].rearrange("p (x w) -> p x w", w=width)
                        split = change[:, u, :].rearrange("p (h d) -> p h d", h=heads)
                        dve.reciprocal(inverse[:, u, :].rearrange("p (x e) -> p x e", e=2), parts[:, :, width - 2:width])\
                            .then_inc(sem["inverse_made"], 1)
                        dve.wait_ge(sem["inverse_made"], t + 1)
                        dve.tensor_tensor(split.rearrange("p (x e) d -> p x e d", e=2),
                                          parts[:, :, 0:width - 2].rearrange("p x (e d) -> p x e d", e=2),
                                          inverse[:, u, :].rearrange("p (x e y) -> p x e y", e=2, y=1).to_broadcast(
                                              [P, pairs, 2, (width - 2) // 2]), ALU.mult).then_inc(sem["total_made"], 1)
                        dve.wait_ge(sem["total_made"], t + 1)
                        made = change[:, u, :]
                    dve.tensor_tensor(change[:, u, :], made, out_bias_rows[:], ALU.add)\
                        .then_inc(sem["change_made"], 1)
                    dve.wait_ge(sem["change_made"], t + 1)
                    xt = keep.x[:, bass.ds(t, 1), :].rearrange("p a d -> p (a d)")
                    dve.scalar_tensor_tensor(out=xt, in0=change[:, u, :], scalar=gate, in1=xt, op0=ALU.mult,
                                             op1=ALU.add).then_inc(sem["x_done"], 1)

                normalise(0, 0, True)
                normalise(1, 1, True)
                for t in range(2):
                    centre(t, t, 0, t == 0)
                    normalise(t + 2, t)
                    sums(t, t, t == 0)

                def step(i, last):
                    for u in range(2):
                        t = 2 * i + u
                        centre(t, u, i)
                        if not last:
                            normalise(t + 2, u)
                        update(t - 2, u)
                        sums(t, u)

                with dve.Fori(1, NT // 2 - 1) as i:
                    step(i, False)
                step(NT // 2 - 1, True)
                update(NT - 2, 0)
                update(NT - 1, 1)


EXPERTS, CHOSEN = 8, 2
TILES = CHOSEN * NT + EXPERTS - 1
SLOTS = TILES * P


class Routes:

    def __init__(self, nc, s, name, before=0):
        self.before, self.gathers_before = before, [16 * before * len(range(u, TILES, 4)) for u in range(4)]
        self.weight = s.sb(f"{name}_weight", [P, CHOSEN, NT])
        self.slot = s.sb(f"{name}_slot", [P, CHOSEN, NT], U32)
        self.token_of = s.sb(f"{name}_token", [P, TILES], U32)
        self.expert_of = s.sb(f"{name}_expert", [P, TILES], I32)
        self.tokens = nc.dram_tensor(f"{name}_tokens", [T, D], F32, kind="Internal").ap()
        self.results = nc.dram_tensor(f"{name}_results", [SLOTS, D], F32, kind="Internal").ap()


def route(nc, keep, name, routes, router, gate, weighted):
    with Scope(nc, name) as s:
        ps = s.psum("ps", [P, 6, 512])
        norm = Normed(s, keep, ps[:, 0], ps[:, 1])
        router_rows, router_t = s.sb("router_rows", [EXPERTS, D]), s.sb("router_t", [P, EXPERTS])
        logits, best = s.sb("logits", [P, NT, EXPERTS]), s.sb("best", [P, NT, 8])
        best_at, best_f = s.sb("best_at", [P, NT, 8], U32), s.sb("best_f", [P, CHOSEN, NT])
        chosen, any_chosen = s.sb("chosen", [P, CHOSEN, NT, EXPERTS]), s.sb("any_chosen", [P, NT, EXPERTS])
        before = s.sb("before", [P, P])
        ones = s.sb("ones", [P, P])
        pad = 4
        run = [s.sb(f"run{n}", [P, pad + NT, EXPERTS]) for n in range(2)]
        ends = [s.sb(f"ends{n}", [P, pad + EXPERTS]) for n in range(2)]
        counts = s.sb("counts", [P, NT, EXPERTS])
        over, used = s.sb("over", [P, EXPERTS, EXPERTS]), s.sb("used", [P, EXPERTS])
        rank, slot_of = s.sb("rank", [P, NT, EXPERTS]), s.sb("slot_of", [P, NT, EXPERTS])
        picked, slot_f = s.sb("picked", [P, CHOSEN, NT, EXPERTS]), s.sb("slot_f", [P, CHOSEN, NT])
        slot_i = s.sb("slot_i", [P, 3, CHOSEN * NT], I32)
        place_f = s.sb("place_f", [P, 2, CHOSEN * NT])
        at_row = s.sb("at_row", [P, CHOSEN * NT, P], mybir.dt.float16)
        is_tile = s.sb("is_tile", [P, CHOSEN * NT, TILES])
        at_tile = s.sb("at_tile", [P, CHOSEN * NT, TILES], mybir.dt.float16)
        past, expert_f = s.sb("past", [P, TILES, EXPERTS - 1]), s.sb("expert_f", [P, TILES])
        gap, grown, denominator = (s.sb(n, [P, NT]) for n in ("gap", "grown", "denominator"))
        base = s.sb("base", [P, EXPERTS])
        names = ["router_loaded", "router_turned", "router_kept", "logits_made", "chosen_ready",
                 "counted", "steps", "gap_ready", "exp_done", "tokens_stored", "order_ready", "order_made",
                 "tables_set", "cut"]
        sem = {n: s.sem(n) for n in names}
        with s.block() as block:

            @block.sync
            def _(sp):
                sp.dma_start(router_rows[:], router).then_inc(sem["router_loaded"], 16)
                sp.wait_ge(norm.xn_ready, NT)
                sp.dma_start(routes.tokens.rearrange("(t p) d -> p t d", p=P), norm.xn[:])\
                    .then_inc(sem["tokens_stored"], 16)
                sp.wait_ge(sem["tokens_stored"], 16)

            @block.gpsimd
            def _(pool):
                norm.gpsimd(pool)
                pool.memset(ones[:], 1.0).then_inc(sem["tables_set"], 1)
                for n in range(2):
                    pool.memset(run[n][:, 0:pad, :], 0.0).then_inc(sem["tables_set"], 1)
                    pool.memset(ends[n][:, 0:pad], 0.0).then_inc(sem["tables_set"], 1)
                pool.wait_ge(sem["tables_set"], 5)
                pool.affine_select(out=before[:], in_=ones[:], compare_op=ALU.is_gt, fill=0.0, base=0,
                                   pattern=[[1, P]], channel_multiplier=-1).then_inc(sem["cut"], 1)

            @block.tensor
            def _(pe):
                pe.wait_ge(sem["router_loaded"], 16)
                pe.transpose(ps[:, 2, 0:EXPERTS], router_rows[:], keep.identity[0:EXPERTS, 0:EXPERTS])\
                    .then_inc(sem["router_turned"], 1)
                norm.tensor(pe)
                pe.wait_ge(sem["router_kept"], 1)
                for t in range(NT):
                    if t % 4 == 0:
                        pe.wait_ge(norm.xt_ready, 1 + t // 4)
                    mm = pe.matmul(ps[:, 3, t * EXPERTS:(t + 1) * EXPERTS], norm.xt[:, t, :], router_t[:],
                                   start=True, stop=True)
                mm.then_inc(sem["logits_made"], 1)
                pe.wait_ge(sem["chosen_ready"], 1)
                pe.wait_ge(sem["cut"], 1)
                flat = any_chosen[:].rearrange("p t e -> p (t e)")
                pe.matmul(ps[:, 4, 0:NT * EXPERTS], before[:], flat, start=True, stop=True)
                pe.matmul(ps[:, 4, 256:256 + NT * EXPERTS], ones[:], flat, start=True, stop=True)\
                    .then_inc(sem["counted"], 1)
                pe.wait_ge(sem["order_ready"], 1)
                for n in range(CHOSEN * NT):
                    mm = pe.matmul(ps[:, 5, 0:TILES], at_row[:, n, :], at_tile[:, n, :], start=(n == 0),
                                   stop=(n == CHOSEN * NT - 1))
                mm.then_inc(sem["order_made"], 1)

            @block.scalar
            def _(act):
                act.wait_ge(sem["router_turned"], 1)
                act.activation(router_t[:], ps[:, 2, 0:EXPERTS], ACT.Copy).then_inc(sem["router_kept"], 1)
                norm.scalar(act)
                if weighted:
                    act.wait_ge(sem["gap_ready"], 1)
                    act.activation(grown[:], gap[:], ACT.Exp).then_inc(sem["exp_done"], 1)

            @block.vector
            def _(dve):
                norm.vector(dve)
                steps = Tally(sem["steps"])

                def then(instruction):
                    steps.add(instruction)
                    steps.wait(dve)

                dve.wait_ge(sem["logits_made"], 1)
                then(dve.tensor_copy(logits[:].rearrange("p t e -> p (t e)"), ps[:, 3, 0:NT * EXPERTS]))
                for t in range(NT):
                    steps.add(dve.max(best[:, t, :], logits[:, t, :]))
                steps.wait(dve)
                for t in range(NT):
                    steps.add(dve.max_index(best_at[:, t, :], best[:, t, :], logits[:, t, :]))
                steps.wait(dve)
                if weighted:
                    dve.tensor_tensor(gap[:], best[:, :, 1], best[:, :, 0], ALU.subtract).then_inc(sem["gap_ready"], 1)
                then(dve.tensor_copy(best_f[:], best_at[:, :, 0:CHOSEN].rearrange("p t k -> p k t")))
                for k in range(CHOSEN):
                    steps.add(dve.tensor_tensor(chosen[:, k], keep.iota[:, None, 0:EXPERTS].to_broadcast([P, NT, EXPERTS]),
                                                best_f[:, k, :, None].to_broadcast([P, NT, EXPERTS]), ALU.is_equal))
                steps.wait(dve)
                dve.tensor_tensor(any_chosen[:], chosen[:, 0], chosen[:, 1], ALU.add).then_inc(sem["chosen_ready"], 1)
                if weighted:
                    dve.wait_ge(sem["exp_done"], 1)
                    then(dve.tensor_scalar(denominator[:], grown[:], 1.0, None, ALU.add))
                    then(dve.reciprocal(gap[:], denominator[:]))
                    then(dve.tensor_scalar(routes.weight[:, 0, :], gap[:], gate, None, ALU.mult))
                    steps.add(dve.tensor_tensor(routes.weight[:, 1, :], grown[:], routes.weight[:, 0, :], ALU.mult))
                else:
                    steps.add(dve.tensor_scalar(routes.weight[:], keep.neg_half[:, 0:CHOSEN * NT].rearrange(
                        "p (k t) -> p k t", k=CHOSEN), gate, -1.0, ALU.mult, ALU.mult))
                dve.wait_ge(sem["counted"], 1)
                dve.wait_ge(sem["tables_set"], 5)
                then(dve.tensor_copy(run[0][:, pad:, :].rearrange("p t e -> p (t e)"), ps[:, 4, 256:256 + NT * EXPERTS]))
                then(dve.tensor_tensor(run[1][:, pad:, :], run[0][:, pad:, :], run[0][:, pad - 1:-1, :], ALU.add))
                steps.add(dve.tensor_copy(counts[:], run[0][:, pad:, :]))
                steps.wait(dve)
                then(dve.tensor_tensor(run[0][:, pad:, :], run[1][:, pad:, :], run[1][:, pad - 2:-2, :], ALU.add))
                then(dve.tensor_tensor(run[1][:, pad:, :], run[0][:, pad:, :], run[0][:, pad - 4:-4, :], ALU.add))
                then(dve.tensor_tensor(over[:], run[1][:, pad + NT - 1, :, None].to_broadcast([P, EXPERTS, NT]),
                                       keep.iota_tiles[:, None, 0:NT].to_broadcast([P, EXPERTS, NT]), ALU.is_gt))
                then(dve.tensor_reduce(used[:], over[:], AX, ALU.add))
                then(dve.tensor_copy(ends[0][:, pad:], used[:]))
                then(dve.tensor_tensor(ends[1][:, pad:], ends[0][:, pad:], ends[0][:, pad - 1:-1], ALU.add))
                then(dve.tensor_tensor(ends[0][:, pad:], ends[1][:, pad:], ends[1][:, pad - 2:-2], ALU.add))
                then(dve.tensor_tensor(ends[1][:, pad:], ends[0][:, pad:], ends[0][:, pad - 4:-4], ALU.add))
                then(dve.tensor_tensor(base[:], ends[1][:, pad:], used[:], ALU.subtract))
                then(dve.tensor_tensor(rank[:], run[1][:, pad:, :], counts[:], ALU.subtract))
                then(dve.tensor_tensor(rank[:].rearrange("p t e -> p (t e)"), rank[:].rearrange("p t e -> p (t e)"),
                                       ps[:, 4, 0:NT * EXPERTS], ALU.add))
                then(dve.scalar_tensor_tensor(out=slot_of[:], in0=base[:, None, :].to_broadcast([P, NT, EXPERTS]),
                                              scalar=float(P), in1=rank[:], op0=ALU.mult, op1=ALU.add))
                for k in range(CHOSEN):
                    steps.add(dve.tensor_tensor(picked[:, k], chosen[:, k], slot_of[:], ALU.mult))
                steps.wait(dve)
                then(dve.tensor_reduce(slot_f[:], picked[:], AX, ALU.add))
                flat_slot = slot_f[:].rearrange("p k t -> p (k t)")
                steps.add(dve.tensor_copy(routes.slot[:].rearrange("p k t -> p (k t)"), flat_slot))
                then(dve.tensor_copy(slot_i[:, 0, :], flat_slot))
                steps.add(dve.tensor_scalar(slot_i[:, 1, :], slot_i[:, 0, :], 7, None, ALU.logical_shift_right))
                then(dve.tensor_scalar(slot_i[:, 2, :], slot_i[:, 0, :], P - 1, None, ALU.bitwise_and))
                then(dve.tensor_copy(place_f[:], slot_i[:, 1:3, :]))
                n = CHOSEN * NT
                steps.add(dve.tensor_tensor(at_row[:], keep.iota[:, None, :].to_broadcast([P, n, P]),
                                            place_f[:, 1, :, None].to_broadcast([P, n, P]), ALU.is_equal))
                then(dve.tensor_tensor(is_tile[:], keep.iota[:, None, 0:TILES].to_broadcast([P, n, TILES]),
                                       place_f[:, 0, :, None].to_broadcast([P, n, TILES]), ALU.is_equal))
                for k in range(CHOSEN):
                    half = slice(k * NT, (k + 1) * NT)
                    ins = steps.add(dve.tensor_tensor(at_tile[:, half, :], is_tile[:, half, :],
                                                      keep.token[:, :, None].to_broadcast([P, NT, TILES]), ALU.mult))
                steps.wait(dve)
                dve.engine_nop().then_inc(sem["order_ready"], 1)
                then(dve.tensor_tensor(past[:], keep.iota[:, 0:TILES, None].to_broadcast([P, TILES, EXPERTS - 1]),
                                       ends[1][:, None, pad:pad + EXPERTS - 1].to_broadcast([P, TILES, EXPERTS - 1]),
                                       ALU.is_ge))
                then(dve.tensor_reduce(expert_f[:], past[:], AX, ALU.add))
                steps.add(dve.tensor_copy(routes.expert_of[:], expert_f[:]))
                dve.wait_ge(sem["order_made"], 1)
                steps.add(dve.tensor_copy(routes.token_of[:], ps[:, 5, 0:TILES]))


AHEAD = 4


def turn_ahead(turn_slots, i, v):
    return [lambda n=3 + 2 * v + u: turn_slots(AHEAD * i + n, n % AHEAD, i + n // AHEAD) for u in range(2)]


def pairs_of_tiles(engine, first, last, step):
    pairs = (last - first + 1) // 2
    with engine.Fori(0, pairs) as i:
        for u in range(2):
            step(first + 2 * i + u, (first + u) % 2)
    for j in range(first + 2 * pairs, last + 1):
        step(j, j % 2)


def expert_index(engine, routes, j):
    return engine.value_load(routes.expert_of[0:1, bass.ds(j, 1)], min_val=0, max_val=EXPERTS - 1)


def gather_tiles(pool, keep, sem, routes, slots):
    for j in range(TILES):
        u = j % AHEAD
        if j >= AHEAD:
            pool.wait_ge(sem["turned"], j - AHEAD + 1)
            pool.wait_ge(keep.gathered[u], routes.gathers_before[u] + 16 * (j // AHEAD))
        pool.indirect_dma_start(slots[:, u, :], None, routes.tokens,
                                bass.IndirectOffsetOnAxis(ap=routes.token_of[:, j:j + 1], axis=0))\
            .then_inc(keep.gathered[u], 16)


def store_results(sp, sem, routes, results):
    def step(j, u):
        sp.wait_ge(sem["result_kept"], j + 1)
        sp.dma_start(routes.results[bass.ds(j * P, P), :], results[:, u, :]).then_inc(sem["stored"][u], 16)

    step(0, 0)
    pairs_of_tiles(sp, 1, TILES - 1, step)
    sp.wait_ge(sem["stored"][0], 16 * ((TILES + 1) // 2))
    sp.wait_ge(sem["stored"][1], 16 * (TILES // 2))


def gelu_experts(nc, keep, name, routes, w1, w2, w3, b1, b2, b3):
    hidden = w1.shape[2]
    chunks = hidden // P
    with Scope(nc, name) as s:
        slots, slots_t = s.sb("slots", [P, AHEAD, D]), s.sb("slots_t", [P, 2, P])
        rows1, rows2 = s.sb("rows1", [P, 2, hidden]), s.sb("rows2", [P, 2, hidden])
        act1, act2 = s.sb("act1", [P, 2, chunks, P]), s.sb("act2", [P, 2, chunks, P])
        results = s.sb("results", [P, 2, D])
        ps = s.psum("ps", [P, 6, 512])
        ps_x, ps_1, ps_1t, ps_2, ps_2t, ps_y = (ps[:, n] for n in range(6))
        names = ["turned", "slots_kept", "rows1_made", "rows1_kept", "rows1_turned", "act1_done", "rows2_made",
                 "rows2_kept", "rows2_turned", "act2_done", "result_made", "result_kept"]
        sem = {n: s.sem(n) for n in names}
        sem["stored"] = [s.sem("stored0"), s.sem("stored1")]
        with s.block() as block:

            @block.gpsimd
            def _(pool):
                gather_tiles(pool, keep, sem, routes, slots)

            @block.sync
            def _(sp):
                store_results(sp, sem, routes, results)

            @block.tensor
            def _(pe):
                def turn_slots(j, u, round, first=False):
                    pe.wait_ge(keep.gathered[u], 16 * (round + 1) + routes.gathers_before[u])
                    if not first:
                        pe.wait_ge(sem["slots_kept"], j)
                    pe.transpose(ps_x[:, 0:P], slots[:, u, :], keep.identity[:]).then_inc(sem["turned"], 1)

                def layer1(j, u, first=False):
                    e = expert_index(pe, routes, j)
                    pe.wait_ge(sem["slots_kept"], j + 1)
                    if not first:
                        pe.wait_ge(sem["rows1_kept"], j)
                    pe.matmul(ps_1, slots_t[:, u, :], w1[:, bass.ds(e, 1), :].rearrange("d a h -> d (a h)"),
                              start=True, stop=True).then_inc(sem["rows1_made"], 1)

                def turn1(j, u, first=False):
                    pe.wait_ge(sem["rows1_kept"], j + 1)
                    if not first:
                        pe.wait_ge(sem["act1_done"], chunks * j)
                    for c in range(chunks):
                        mm = pe.transpose(ps_1t[:, c * P:(c + 1) * P], rows1[:, u, c * P:(c + 1) * P], keep.identity[:])
                    mm.then_inc(sem["rows1_turned"], 1)

                def layer2(j, u, first=False):
                    e = expert_index(pe, routes, j)
                    pe.wait_ge(sem["act1_done"], chunks * (j + 1))
                    if not first:
                        pe.wait_ge(sem["rows2_kept"], j)
                    for c in range(chunks):
                        mm = pe.matmul(ps_2, act1[:, u, c, :],
                                       w2[:, bass.ds(e, 1), c, :].rearrange("d a h -> d (a h)"),
                                       start=(c == 0), stop=(c == chunks - 1))
                    mm.then_inc(sem["rows2_made"], 1)

                def turn2(j, u, first=False):
                    pe.wait_ge(sem["rows2_kept"], j + 1)
                    if not first:
                        pe.wait_ge(sem["act2_done"], chunks * j)
                    for c in range(chunks):
                        mm = pe.transpose(ps_2t[:, c * P:(c + 1) * P], rows2[:, u, c * P:(c + 1) * P], keep.identity[:])
                    mm.then_inc(sem["rows2_turned"], 1)

                def layer3(j, u, first=False):
                    e = expert_index(pe, routes, j)
                    pe.wait_ge(sem["act2_done"], chunks * (j + 1))
                    if not first:
                        pe.wait_ge(sem["result_kept"], j)
                    for c in range(chunks):
                        mm = pe.matmul(ps_y[:, 0:D], act2[:, u, c, :],
                                       w3[:, bass.ds(e, 1), c, :].rearrange("d a h -> d (a h)"),
                                       start=(c == 0), stop=(c == chunks - 1))
                    mm.then_inc(sem["result_made"], 1)

                turn_slots(0, 0, 0, True)
                layer1(0, 0, True)
                turn_slots(1, 1, 0)
                turn1(0, 0, True)
                layer1(1, 1)
                layer2(0, 0, True)
                turn1(1, 1)
                turn_slots(2, 2, 0)
                turn2(0, 0, True)

                def steady(i, v):
                    for u in range(2):
                        j = 1 + 2 * (2 * i + v) + u
                        layer1(j + 1, u)
                        layer2(j, 1 - u)
                        turn1(j + 1, u)
                        turn_ahead(turn_slots, i, v)[u]()
                        layer3(j - 1, u, False) if not isinstance(j, int) else layer3(j - 1, u, j == 1)
                        turn2(j, 1 - u)

                steady(0, 0)
                steady(0, 1)
                with pe.Fori(1, (TILES - 3) // 4) as i:
                    for v in range(2):
                        steady(i, v)
                j = TILES - 2
                layer1(j + 1, 0)
                layer2(j, 1)
                turn1(j + 1, 0)
                layer3(j - 1, 0)
                turn2(j, 1)
                layer2(j + 1, 0)
                layer3(j, 1)
                turn2(j + 1, 0)
                layer3(j + 1, 0)

            @block.scalar
            def _(act):
                def gelu(j, u, rows_turned, read, source, to, bias, done, first):
                    e = expert_index(act, routes, j)
                    act.wait_ge(rows_turned, j + 1)
                    if not first:
                        act.wait_ge(read, j - 1)
                    for c in range(chunks):
                        act.activation(to[:, u, c, :], source[:, c * P:(c + 1) * P], ACT.Gelu,
                                       bias=bias[:, bass.ds(e * chunks + c, 1)]).then_inc(done, 1)

                def gelu1(j, u, first=False):
                    gelu(j, u, sem["rows1_turned"], sem["rows2_made"], ps_1t, act1, b1, sem["act1_done"], first)

                def gelu2(j, u, first=False):
                    gelu(j, u, sem["rows2_turned"], sem["result_made"], ps_2t, act2, b2, sem["act2_done"], first)

                gelu1(0, 0, True)
                gelu1(1, 1, True)
                gelu2(0, 0, True)
                gelu1(2, 0)
                gelu2(1, 1, True)

                def step(j, u):
                    gelu1(j + 1, 1 - u)
                    gelu2(j, u)

                with act.Fori(0, (TILES - 3) // 2) as i:
                    step(2 + 2 * i, 0)
                    step(3 + 2 * i, 1)
                gelu2(TILES - 1, (TILES - 1) % 2)

            @block.vector
            def _(dve):
                def keep_slots(j, u, first=False):
                    dve.wait_ge(sem["turned"], j + 1)
                    if not first:
                        dve.wait_ge(sem["rows1_made"], j - 1)
                    dve.tensor_copy(slots_t[:, u, :], ps_x[:, 0:P]).then_inc(sem["slots_kept"], 1)

                def keep1(j, u, first=False):
                    dve.wait_ge(sem["rows1_made"], j + 1)
                    if not first:
                        dve.wait_ge(sem["rows1_turned"], j - 1)
                    dve.tensor_copy(rows1[:, u, :], ps_1).then_inc(sem["rows1_kept"], 1)

                def keep2(j, u, first=False):
                    dve.wait_ge(sem["rows2_made"], j + 1)
                    if not first:
                        dve.wait_ge(sem["rows2_turned"], j - 1)
                    dve.tensor_copy(rows2[:, u, :], ps_2).then_inc(sem["rows2_kept"], 1)

                def keep_result(j, u, half, first=False):
                    e = expert_index(dve, routes, j)
                    dve.wait_ge(sem["result_made"], j + 1)
                    if not first:
                        dve.wait_ge(sem["stored"][u], 16 * half)
                    dve.tensor_tensor(results[:, u, :], ps_y[:, 0:D],
                                      b3[:, bass.ds(e, 1), :].rearrange("p a d -> p (a d)"), ALU.add)\
                        .then_inc(sem["result_kept"], 1)

                keep_slots(0, 0, True)
                keep1(0, 0, True)
                keep_slots(1, 1, True)
                keep1(1, 1, True)
                keep2(0, 0, True)
                keep_slots(2, 0)

                def steady(i, first):
                    for u in range(2):
                        j = 1 + 2 * i + u
                        keep1(j + 1, u)
                        keep2(j, 1 - u, first and u == 0)
                        keep_slots(j + 2, 1 - u)
                        keep_result(j - 1, u, i, first)

                steady(0, True)
                with dve.Fori(1, (TILES - 3) // 2) as i:
                    steady(i, False)
                j = TILES - 2
                keep1(j + 1, 0)
                keep2(j, 1)
                keep_result(j - 1, 0, (j - 1) // 2)
                keep2(j + 1, 0)
                keep_result(j, 1, j // 2)
                keep_result(j + 1, 0, (j + 1) // 2)


def gated_experts(nc, keep, name, routes, w_in, w_out):
    width = w_in.shape[2] // 2
    chunks = width // P
    banks = 2 * width // 512
    with Scope(nc, name) as s:
        slots, slots_t = s.sb("slots", [P, AHEAD, D]), s.sb("slots_t", [P, 2, P])
        gated, gated_t = s.sb("gated", [P, 2, width]), s.sb("gated_t", [P, 2, chunks, P])
        results = s.sb("results", [P, 2, D])
        ps_in = s.psum("ps_in", [P, 2 * banks, 512])
        ps_x, ps_t, ps_y = s.psum("ps_x", [P, 512]), s.psum("ps_t", [P, 512]), s.psum("ps_y", [P, 512])
        names = ["turned", "slots_kept", "in_made", "silu_done", "gated_ready", "gated_turned", "gated_kept",
                 "result_made", "result_kept"]
        sem = {n: s.sem(n) for n in names}
        sem["stored"] = [s.sem("stored0"), s.sem("stored1")]
        flat_in = ps_in[:].rearrange("p b n -> p (b n)")

        def gate_part(u):
            return flat_in[:, 2 * width * u:2 * width * u + width]

        def up_part(u):
            return flat_in[:, 2 * width * u + width:2 * width * (u + 1)]

        with s.block() as block:

            @block.gpsimd
            def _(pool):
                gather_tiles(pool, keep, sem, routes, slots)

            @block.sync
            def _(sp):
                store_results(sp, sem, routes, results)

            @block.tensor
            def _(pe):
                def turn_slots(j, u, round, first=False):
                    pe.wait_ge(keep.gathered[u], 16 * (round + 1) + routes.gathers_before[u])
                    if not first:
                        pe.wait_ge(sem["slots_kept"], j)
                    pe.transpose(ps_x[:, 0:P], slots[:, u, :], keep.identity[:]).then_inc(sem["turned"], 1)

                def up(j, u, first=False):
                    e = expert_index(pe, routes, j)
                    pe.wait_ge(sem["slots_kept"], j + 1)
                    if not first:
                        pe.wait_ge(sem["gated_ready"], j - 1)
                    for n in range(banks):
                        mm = pe.matmul(ps_in[:, banks * u + n], slots_t[:, u, :],
                                       w_in[:, bass.ds(e, 1), 512 * n:512 * n + 512].rearrange("d a h -> d (a h)"),
                                       start=True, stop=True)
                    mm.then_inc(sem["in_made"], 1)

                def turn(j, u, first=False):
                    pe.wait_ge(sem["gated_ready"], j + 1)
                    if not first:
                        pe.wait_ge(sem["gated_kept"], j)
                    for c in range(chunks):
                        mm = pe.transpose(ps_t[:, c * P:(c + 1) * P], gated[:, u, c * P:(c + 1) * P], keep.identity[:])
                    mm.then_inc(sem["gated_turned"], 1)

                def down(j, u, first=False):
                    e = expert_index(pe, routes, j)
                    pe.wait_ge(sem["gated_kept"], j + 1)
                    if not first:
                        pe.wait_ge(sem["result_kept"], j)
                    for c in range(chunks):
                        mm = pe.matmul(ps_y[:, 0:D], gated_t[:, u, c, :],
                                       w_out[:, bass.ds(e, 1), c, :].rearrange("d a h -> d (a h)"),
                                       start=(c == 0), stop=(c == chunks - 1))
                    mm.then_inc(sem["result_made"], 1)

                turn_slots(0, 0, 0, True)
                up(0, 0, True)
                turn_slots(1, 1, 0)
                up(1, 1, True)
                turn(0, 0, True)
                turn_slots(2, 2, 0)

                def steady(i, v, first=False):
                    for u in range(2):
                        j = 1 + 2 * (2 * i + v) + u
                        up(j + 1, u)
                        turn_ahead(turn_slots, i, v)[u]()
                        down(j - 1, u, first and u == 0)
                        turn(j, 1 - u)

                steady(0, 0, True)
                steady(0, 1)
                with pe.Fori(1, (TILES - 3) // 4) as i:
                    for v in range(2):
                        steady(i, v)
                j = TILES - 2
                up(j + 1, 0)
                down(j - 1, 0)
                turn(j, 1)
                down(j, 1)
                turn(j + 1, 0)
                down(j + 1, 0)

            @block.scalar
            def _(act):
                def silu(j, u, first=False):
                    act.wait_ge(sem["in_made"], j + 1)
                    if not first:
                        act.wait_ge(sem["gated_turned"], j - 1)
                    act.activation(gated[:, u, :], gate_part(u), ACT.Silu).then_inc(sem["silu_done"], 1)

                def keep_gated(j, u, first=False):
                    act.wait_ge(sem["gated_turned"], j + 1)
                    if not first:
                        act.wait_ge(sem["result_made"], j - 1)
                    act.activation(gated_t[:, u, :, :].rearrange("p c k -> p (c k)"), ps_t[:, 0:width], ACT.Copy)\
                        .then_inc(sem["gated_kept"], 1)

                silu(0, 0, True)
                silu(1, 1, True)
                keep_gated(0, 0, True)
                silu(2, 0)
                keep_gated(1, 1, True)
                with act.Fori(0, (TILES - 3) // 2) as i:
                    for u in range(2):
                        silu(3 + 2 * i + u, 1 - u)
                        keep_gated(2 + 2 * i + u, u)
                keep_gated(TILES - 1, 0)

            @block.vector
            def _(dve):
                def keep_slots(j, u, first=False):
                    dve.wait_ge(sem["turned"], j + 1)
                    if not first:
                        dve.wait_ge(sem["in_made"], j - 1)
                    dve.tensor_copy(slots_t[:, u, :], ps_x[:, 0:P]).then_inc(sem["slots_kept"], 1)

                def multiply(j, u):
                    dve.wait_ge(sem["silu_done"], j + 1)
                    dve.tensor_tensor(gated[:, u, :], gated[:, u, :], up_part(u), ALU.mult)\
                        .then_inc(sem["gated_ready"], 1)

                def keep_result(j, u, half, first=False):
                    dve.wait_ge(sem["result_made"], j + 1)
                    if not first:
                        dve.wait_ge(sem["stored"][u], 16 * half)
                    dve.tensor_copy(results[:, u, :], ps_y[:, 0:D]).then_inc(sem["result_kept"], 1)

                keep_slots(0, 0, True)
                keep_slots(1, 1, True)
                multiply(0, 0)
                multiply(1, 1)
                keep_slots(2, 0)

                def steady(i, first):
                    for u in range(2):
                        j = 1 + 2 * i + u
                        keep_slots(j + 2, 1 - u)
                        multiply(j + 1, u)
                        keep_result(j - 1, u, i, first)

                steady(0, True)
                with dve.Fori(1, (TILES - 3) // 2) as i:
                    steady(i, False)
                j = TILES - 2
                multiply(j + 1, 0)
                keep_result(j - 1, 0, (j - 1) // 2)
                keep_result(j, 1, j // 2)
                keep_result(j + 1, 0, (j + 1) // 2)


class Combine:

    def __init__(self, keep, s, routes, out=None):
        self.keep, self.routes, self.out = keep, routes, out
        self.mine = s.sb("mine", [P, CHOSEN, NT, D])
        self.added, self.stored = s.sem("added"), s.sem("stored")

    def gather(self, pool):
        for t in range(NT):
            for k in range(CHOSEN):
                pool.indirect_dma_start(self.mine[:, k, t, :], None, self.routes.results,
                                        bass.IndirectOffsetOnAxis(ap=self.routes.slot[:, k, t:t + 1], axis=0))\
                    .then_inc(self.keep.got[CHOSEN * t + k], 16)

    def add_tile(self, dve, t):
        x, routes = self.keep.x, self.routes
        for k in range(CHOSEN):
            dve.wait_ge(self.keep.got[CHOSEN * t + k], 16 * (routes.before + 1))
            if k:
                dve.wait_ge(self.added, CHOSEN * t + k)
            dve.scalar_tensor_tensor(out=x[:, t, :], in0=self.mine[:, k, t, :], scalar=routes.weight[:, k, t:t + 1],
                                     in1=x[:, t, :], op0=ALU.mult, op1=ALU.add).then_inc(self.added, 1)

    def add(self, block, rows=None):
        x = self.keep.x

        def stats(dve, t):
            dve.wait_ge(self.added, CHOSEN * (t + 1))
            rows.stats_of_tile(dve, t)

        @block.vector
        def _(dve):
            for t in range(NT):
                self.add_tile(dve, t)
                if rows and t:
                    stats(dve, t - 1)
            if rows:
                stats(dve, NT - 1)
                rows.join_stats(dve)

        if rows:
            block.gpsimd(rows.gpsimd)

        if self.out is not None:

            @block.sync
            def _(sp):
                for b in range(B):
                    sp.wait_ge(self.added, 2 * CHOSEN * (b + 1))
                    sp.dma_start(self.out[b].rearrange("(u p) d -> p u d", p=P), x[:, 2 * b:2 * b + 2, :])\
                        .then_inc(self.stored, 16)
                sp.wait_ge(self.stored, 16 * B)


def turn_gated_weights(nc, a, keep, name, gate_up, down, w_in, w_out):
    width = down.shape[2]
    jobs = []
    for e in range(EXPERTS):
        for n in range(2 * width // 512):
            jobs.append((gate_up[:, e, 4 * n:4 * n + 4, :], w_in[:, e, 512 * n:512 * n + 512]))
        jobs.append((down[:, e, :].rearrange("o (c k) -> o c k", k=P), w_out[:, e, :, :].rearrange("k c o -> k (c o)")))
    with Scope(nc, name) as s:
        ps = s.psum("ps", [P, 2, 512])
        turned, kept = s.sem("turned"), s.sem("kept")
        with s.block() as block:

            @block.tensor
            def _(pe):
                for e, n in enumerate(keep.raw_loaded):
                    pe.wait_ge(n, 16)
                for m, (source, _) in enumerate(jobs):
                    if m >= 2:
                        pe.wait_ge(kept, m - 1)
                    for c in range(4):
                        mm = pe.transpose(ps[:, m % 2, c * P:(c + 1) * P], source[:, c, :], keep.identity[:])
                    mm.then_inc(turned, 1)

            @block.scalar
            def _(act):
                for m, (_, to) in enumerate(jobs):
                    act.wait_ge(turned, m + 1)
                    act.activation(to, ps[:, m % 2, :], ACT.Copy).then_inc(kept, 1)



TAPS = 9


class ConvWeights:

    def __init__(self, s):
        heads, wide, inner = 16, 2 * D, 64
        self.hist_w = s.sb("hist_w", [P, wide])
        self.hist_rows = s.sb("hist_rows", [P, 3, wide])
        self.ctx_w1, self.ctx_b1 = s.sb("ctx_w1", [P, 2, inner]), s.sb("ctx_b1", [inner, 1])
        self.ctx_w2, self.ctx_b2 = s.sb("ctx_w2", [inner, 1]), s.sb("ctx_b2", [1, 1])
        self.kg_w1, self.kg_rows = s.sb("kg_w1", [P, 2, D]), s.sb("kg_rows", [B, 3, D])
        self.kg_w2, self.kg_b2 = s.sb("kg_w2", [P, heads * TAPS]), s.sb("kg_b2", [B, heads * TAPS])
        self.hist_loaded, self.ctx_loaded, self.kg_loaded = s.sem("hist_loaded"), s.sem("ctx_loaded"), s.sem("kg_loaded")

    def load(self, a, sp):
        def rows_of(v, rows, n):
            return row(a[v]).to_broadcast([rows, n])

        wide = 2 * D
        sp.dma_start(self.hist_w[:], a["L3_xattn_hist_W"]).then_inc(self.hist_loaded, 16)
        for n, v in enumerate(("hist_b", "hist_ln_g", "hist_ln_b")):
            sp.dma_start(self.hist_rows[:, n, :], rows_of("L3_xattn_" + v, P, wide)).then_inc(self.hist_loaded, 16)
        sp.dma_start(self.ctx_w1[:], a["L3_xattn_ctx_W1"].rearrange("(c d) n -> d c n", d=P)).then_inc(self.ctx_loaded, 16)
        sp.dma_start(self.ctx_b1[:], a["L3_xattn_ctx_b1"].rearrange("(p c) -> p c", c=1)).then_inc(self.ctx_loaded, 16)
        sp.dma_start(self.ctx_w2[:], a["L3_xattn_ctx_W2"]).then_inc(self.ctx_loaded, 16)
        sp.dma_start(self.ctx_b2[:], row(a["L3_xattn_ctx_b2"])).then_inc(self.ctx_loaded, 16)
        sp.dma_start(self.kg_w1[:], a["L3_xattn_kg_W1"].rearrange("(c d) n -> d c n", d=P)).then_inc(self.kg_loaded, 16)
        for n, v in enumerate(("kg_b1", "kg_ln_g", "kg_ln_b")):
            sp.dma_start(self.kg_rows[:, n, :], rows_of("L3_xattn_" + v, B, D)).then_inc(self.kg_loaded, 16)
        sp.dma_start(self.kg_w2[:], a["L3_xattn_kg_W2"]).then_inc(self.kg_loaded, 16)
        sp.dma_start(self.kg_b2[:], rows_of("L3_xattn_kg_b2", B, 16 * TAPS)).then_inc(self.kg_loaded, 16)


def conv_kernels(nc, keep, name, w, taps, combine, rows):
    heads, wide, inner = 16, 2 * D, 64
    with Scope(nc, name) as s:
        hist_w, hist_rows, ctx_w1, ctx_b1, ctx_w2, ctx_b2 = w.hist_w, w.hist_rows, w.ctx_w1, w.ctx_b1, w.ctx_w2, w.ctx_b2
        kg_w1, kg_rows, kg_w2, kg_b2 = w.kg_w1, w.kg_rows, w.kg_w2, w.kg_b2
        eh, eh_t = s.sb("eh", [P, 2, wide]), s.sb("eh_t", [P, 2, 2, P])
        stats, moments, rstd = s.sb("stats", [P, 2, 6]), s.sb("moments", [P, 2, 2]), s.sb("rstd", [P, 2, 1])
        inner_act, one = s.sb("inner_act", [inner, B * C]), s.sb("one", [1, 1])
        aw, aw_top, aw_sum = s.sb("aw", [1, B, C]), s.sb("aw_top", [1, B]), s.sb("aw_sum", [1, B])
        aw_cols, cc_t = s.sb("aw_cols", [P, 2, 2]), s.sb("cc_t", [P, 2, B])
        kp, kp_stats, kp_moments = s.sb("kp", [B, D]), s.sb("kp_stats", [B, 6]), s.sb("kp_moments", [B, 2])
        kp_rstd, kp_t = s.sb("kp_rstd", [B, 1]), s.sb("kp_t", [P, B])
        kernels = s.sb("kernels", [B, heads, TAPS])
        k_top, k_sum = s.sb("k_top", [B, heads]), s.sb("k_sum", [B, heads])
        ps = s.psum("ps", [P, 8, 512])
        ones = s.sb("ones", [P, 2])
        names = ["hist_made", "eh_steps", "var_ready", "rstd_ready", "gelu_in",
                 "eh_ready", "eh_turned", "eh_kept", "inner_made", "inner_ready", "aw_made", "aw_centred",
                 "aw_exp", "aw_ready", "ones_set", "cols_made", "cols_ready", "cc_made", "cc_ready", "kp_made",
                 "kp_var", "kp_rstd_ready", "kp_gelu_in", "kp_ready", "kp_turned", "kp_kept", "k_made",
                 "k_centred", "k_exp", "k_ready", "taps_made", "taps_ready"]
        sem = {n: s.sem(n) for n in names}

        sem.update(hist_loaded=w.hist_loaded, ctx_loaded=w.ctx_loaded, kg_loaded=w.kg_loaded)
        with s.block() as block:

            @block.gpsimd
            def _(pool):
                pool.memset(one[:], 1.0).then_inc(sem["ones_set"], 1)
                pool.memset(ones[:], 0.0).then_inc(sem["ones_set"], 1)
                pool.wait_ge(sem["ones_set"], 2)
                pool.memset(ones[0:C, 0:1], 1.0).then_inc(sem["ones_set"], 1)
                pool.memset(ones[C:P, 1:2], 1.0).then_inc(sem["ones_set"], 1)
                pool.wait_ge(sem["ones_set"], 4)
                pool.wait_ge(sem["var_ready"], 1)
                pool.tensor_tensor(rstd[:, :, 0], rstd[:, :, 0], keep.neg_half[:, 0:2], ALU.pow)\
                    .then_inc(sem["rstd_ready"], 1)
                combine.gather(pool)
                pool.wait_ge(sem["kp_var"], 1)
                pool.tensor_tensor(kp_rstd[:], kp_rstd[:], keep.neg_half[0:B, 0:1], ALU.pow)\
                    .then_inc(sem["kp_rstd_ready"], 1)
                pool.wait_ge(sem["kp_rstd_ready"], 1)
                rows.gpsimd(pool)

            @block.tensor
            def _(pe):
                pe.wait_ge(sem["hist_loaded"], 64)
                for u in range(2):
                    mm = pe.matmul(ps[:, 0, u * wide:(u + 1) * wide], keep.ctx_t[:, u * P:(u + 1) * P], hist_w[:],
                                   start=True, stop=True)
                mm.then_inc(sem["hist_made"], 1)
                pe.wait_ge(sem["eh_ready"], 1)
                for c in range(2):
                    for u in range(2):
                        mm = pe.transpose(ps[:, 1, (2 * c + u) * P:(2 * c + u + 1) * P], eh[:, u, c * P:(c + 1) * P],
                                          keep.identity[:])
                mm.then_inc(sem["eh_turned"], 1)
                pe.wait_ge(sem["eh_kept"], 1)
                pe.wait_ge(sem["ctx_loaded"], 64)
                for c in range(2):
                    mm = pe.matmul(ps[0:inner, 2, 0:B * C], ctx_w1[:, c, :], eh_t[:, c].rearrange("p u k -> p (u k)"),
                                   start=(c == 0), stop=(c == 1))
                mm.then_inc(sem["inner_made"], 1)
                pe.wait_ge(sem["inner_ready"], 1)
                pe.matmul(ps[0:1, 3, 0:B * C], ctx_w2[:], inner_act[:], start=True, stop=True).then_inc(sem["aw_made"], 1)
                pe.wait_ge(sem["aw_ready"], 1)
                for u in range(2):
                    mm = pe.matmul(ps[:, 4, u:u + 1], aw[:, 2 * u:2 * u + 2, :].rearrange("p b k -> p (b k)"), one[:],
                                   start=True, stop=True)
                mm.then_inc(sem["cols_made"], 1)
                pe.wait_ge(sem["cols_ready"], 2)
                for c in range(2):
                    for u in range(2):
                        mm = pe.matmul(ps[:, 5, c * B + 2 * u:c * B + 2 * u + 2], eh[:, u, c * P:(c + 1) * P],
                                       aw_cols[:, u, :], start=True, stop=True)
                mm.then_inc(sem["cc_made"], 1)
                pe.wait_ge(sem["cc_ready"], 1)
                pe.wait_ge(sem["kg_loaded"], 96)
                for c in range(2):
                    mm = pe.matmul(ps[0:B, 6, 0:D], cc_t[:, c, :], kg_w1[:, c, :], start=(c == 0), stop=(c == 1))
                mm.then_inc(sem["kp_made"], 1)
                pe.wait_ge(sem["kp_ready"], 1)
                pe.transpose(ps[:, 7, 0:B], kp[:], keep.identity[0:B, 0:B]).then_inc(sem["kp_turned"], 1)
                pe.wait_ge(sem["kp_kept"], 1)
                pe.matmul(ps[0:B, 0, 0:heads * TAPS], kp_t[:], kg_w2[:], start=True, stop=True).then_inc(sem["k_made"], 1)
                pe.wait_ge(sem["k_ready"], 1)
                for b in range(B):
                    mm = pe.matmul(ps[:, 1 + b // 2, (b % 2) * 256:(b % 2) * 256 + heads * TAPS],
                                   keep.identity[0:B, b:b + 1].to_broadcast([B, P]),
                                   kernels[:].rearrange("b h n -> b (h n)"), start=True, stop=True)
                mm.then_inc(sem["taps_made"], 1)

            @block.scalar
            def _(act):
                act.wait_ge(sem["gelu_in"], 1)
                act.activation(eh[:], eh[:], ACT.Gelu).then_inc(sem["eh_ready"], 1)
                act.wait_ge(sem["inner_made"], 1)
                act.wait_ge(sem["ctx_loaded"], 64)
                act.activation(inner_act[:], ps[0:inner, 2, 0:B * C], ACT.Gelu, bias=ctx_b1[:, 0:1])\
                    .then_inc(sem["inner_ready"], 1)
                act.wait_ge(sem["aw_centred"], 1)
                act.activation(aw[:], aw[:], ACT.Exp).then_inc(sem["aw_exp"], 1)
                act.wait_ge(sem["kp_gelu_in"], 1)
                act.activation(kp[:], kp[:], ACT.Gelu).then_inc(sem["kp_ready"], 1)
                act.wait_ge(sem["k_centred"], 1)
                act.activation(kernels[:], kernels[:], ACT.Exp).then_inc(sem["k_exp"], 1)

            @block.vector
            def _(dve):
                steps = Tally(sem["eh_steps"])

                def then(instruction):
                    steps.add(instruction)
                    steps.wait(dve)

                dve.wait_ge(sem["hist_made"], 1)
                then(dve.tensor_tensor(eh[:], ps[:, 0, :].rearrange("p (u n) -> p u n", u=2),
                                       hist_rows[:, 0:1, :].to_broadcast([P, 2, wide]), ALU.add))
                for u in range(2):
                    steps.add(dve.bn_stats(stats[:, u, :], eh[:, u, :]))
                steps.wait(dve)
                for u in range(2):
                    steps.add(dve.bn_aggr(moments[:, u, :], stats[:, u, :]))
                steps.wait(dve)
                dve.tensor_scalar(rstd[:, :, 0], moments[:, :, 1], EPS, None, ALU.add).then_inc(sem["var_ready"], 1)
                dve.wait_ge(sem["rstd_ready"], 1)
                for u in range(2):
                    steps.add(dve.tensor_scalar(eh[:, u, :], eh[:, u, :], moments[:, u, 0:1], rstd[:, u, :],
                                                ALU.subtract, ALU.mult))
                steps.wait(dve)
                then(dve.tensor_tensor(eh[:], eh[:], hist_rows[:, 1:2, :].to_broadcast([P, 2, wide]), ALU.mult))
                dve.tensor_tensor(eh[:], eh[:], hist_rows[:, 2:3, :].to_broadcast([P, 2, wide]), ALU.add)\
                    .then_inc(sem["gelu_in"], 1)
                dve.wait_ge(sem["eh_turned"], 1)
                dve.tensor_copy(eh_t[:].rearrange("p c u k -> p (c u k)"), ps[:, 1, :]).then_inc(sem["eh_kept"], 1)
                combine.add_tile(dve, 0)
                dve.wait_ge(sem["aw_made"], 1)
                then(dve.tensor_scalar(aw[:].rearrange("p b k -> p (b k)"), ps[0:1, 3, 0:B * C], ctx_b2[:, 0:1], None,
                                       ALU.add))
                then(dve.tensor_reduce(aw_top[:], aw[:], AX, ALU.max))
                dve.tensor_tensor(aw[:], aw[:], aw_top[:, :, None].to_broadcast([1, B, C]), ALU.subtract)\
                    .then_inc(sem["aw_centred"], 1)
                dve.wait_ge(sem["aw_exp"], 1)
                then(dve.tensor_reduce(aw_sum[:], aw[:], AX, ALU.add))
                then(dve.reciprocal(aw_top[:], aw_sum[:]))
                dve.tensor_tensor(aw[:], aw[:], aw_top[:, :, None].to_broadcast([1, B, C]), ALU.mult)\
                    .then_inc(sem["aw_ready"], 1)
                combine.add_tile(dve, 1)
                combine.add_tile(dve, 2)
                dve.wait_ge(sem["cols_made"], 1)
                dve.wait_ge(sem["ones_set"], 4)
                for u in range(2):
                    dve.tensor_scalar(aw_cols[:, u, :], ones[:], ps[:, 4, u:u + 1], None, ALU.mult)\
                        .then_inc(sem["cols_ready"], 1)
                combine.add_tile(dve, 3)
                combine.add_tile(dve, 4)
                dve.wait_ge(sem["cc_made"], 1)
                dve.tensor_copy(cc_t[:].rearrange("p c b -> p (c b)"), ps[:, 5, 0:2 * B]).then_inc(sem["cc_ready"], 1)
                combine.add_tile(dve, 5)
                dve.wait_ge(sem["kp_made"], 1)
                dve.wait_ge(sem["kg_loaded"], 96)
                then(dve.tensor_tensor(kp[:], ps[0:B, 6, 0:D], kg_rows[:, 0, :], ALU.add))
                then(dve.bn_stats(kp_stats[:], kp[:]))
                then(dve.bn_aggr(kp_moments[:], kp_stats[:]))
                dve.tensor_scalar(kp_rstd[:], kp_moments[:, 1:2], EPS, None, ALU.add).then_inc(sem["kp_var"], 1)
                combine.add_tile(dve, 6)
                dve.wait_ge(sem["kp_rstd_ready"], 1)
                then(dve.tensor_scalar(kp[:], kp[:], kp_moments[:, 0:1], kp_rstd[:, 0:1], ALU.subtract, ALU.mult))
                then(dve.tensor_tensor(kp[:], kp[:], kg_rows[:, 1, :], ALU.mult))
                dve.tensor_tensor(kp[:], kp[:], kg_rows[:, 2, :], ALU.add).then_inc(sem["kp_gelu_in"], 1)
                combine.add_tile(dve, 7)
                dve.wait_ge(sem["kp_turned"], 1)
                dve.tensor_copy(kp_t[:], ps[:, 7, 0:B]).then_inc(sem["kp_kept"], 1)
                dve.wait_ge(combine.added, CHOSEN * NT)
                for t in range(NT // 2):
                    rows.stats_of_tile(dve, t)
                dve.wait_ge(sem["k_made"], 1)
                flat = kernels[:].rearrange("b h n -> b (h n)")
                then(dve.tensor_tensor(flat, ps[0:B, 0, 0:heads * TAPS], kg_b2[:], ALU.add))
                then(dve.tensor_reduce(k_top[:], kernels[:], AX, ALU.max))
                dve.tensor_tensor(kernels[:], kernels[:], k_top[:, :, None].to_broadcast([B, heads, TAPS]),
                                  ALU.subtract).then_inc(sem["k_centred"], 1)
                for t in range(NT // 2, NT):
                    rows.stats_of_tile(dve, t)
                dve.wait_ge(sem["k_exp"], 1)
                then(dve.tensor_reduce(k_sum[:], kernels[:], AX, ALU.add))
                then(dve.reciprocal(k_top[:], k_sum[:]))
                dve.tensor_tensor(kernels[:], kernels[:], k_top[:, :, None].to_broadcast([B, heads, TAPS]), ALU.mult)\
                    .then_inc(sem["k_ready"], 1)
                rows.join_stats(dve)
                dve.wait_ge(sem["taps_made"], 1)
                for n in range(2):
                    dve.tensor_copy(taps[:, 2 * n:2 * n + 2, :, :].rearrange("p b h n -> p b (h n)"),
                                    ps[:, 1 + n, :].rearrange("p (b n) -> p b n", b=2)[:, :, 0:heads * TAPS])\
                        .then_inc(sem["taps_ready"], 1)


def conv_attention_any_mask(nc, a, keep, name, taps, gate, rows):
    heads, wide = 16, 8
    scale = float(wide) ** -0.5
    with Scope(nc, name) as s:
        ps = s.psum("ps", [P, 8, 512])
        norm = Normed(s, keep, ps[:, 0], ps[:, 1], rows=rows)
        wq, wk, wv, proj = (s.sb(n, [P, D]) for n in ("wq", "wk", "wv", "proj"))
        proj_rows, head_mask = s.sb("proj_rows", [P, D]), s.sb("head_mask", [P, heads])
        mask_u8, masked, open_ = s.sb("mask_u8", [P, 2, S], U8), s.sb("masked", [P, 2, S]), s.sb("open", [P, 2, S])
        bands, edge = s.sb("bands", [P, 3, P]), s.sb("edge", [P, 2, P])
        q_t, k_t, v = s.sb("q_t", [P, S]), s.sb("k_t", [P, S]), s.sb("v", [P, 2, D])
        k_spread = s.sb("k_spread", [P, heads, S])
        scored = s.sb("scored", [P, 2, S + 2])
        along, tmp = s.sb("along", [P, 3, P]), s.sb("tmp", [P, 3, P])
        over_edge = s.sb("over_edge", [P, 2, 3, P])
        e, e_t = s.sb("e", [P, 2, S]), s.sb("e_t", [P, 2, 2, P])
        top, total, inverse = s.sb("top", [P, 2]), s.sb("total", [P, 2]), s.sb("inverse", [P, 2])
        mixed, mixed_t = s.sb("mixed", [P, 2, D]), s.sb("mixed_t", [P, 2, P])
        change = s.sb("change", [P, 2, D])
        names = ["loaded", "mask_loaded", "tables", "tables_done", "q_made", "q_kept", "v_kept", "k_ready",
                 "spread", "scores_made", "scored_ready", "kernel_steps", "kernel_ready", "conv_made", "biased", "topped",
                 "exp_done", "turned", "turned_kept", "mixed_made", "inverted", "band_made", "mixed_ready", "mixed_turned",
                 "mixed_kept", "out_made", "changed", "x_done"]
        sem = {n: s.sem(n) for n in names}
        with s.block() as block:

            @block.sync
            def _(sp):
                with sp.If(keep.mask_is_odd(sp) > 0):
                    for to, w in zip((wq, wk, wv, proj), ("Wq", "Wk", "Wv", "proj_W")):
                        sp.dma_start(to[:], a["L3_xattn_" + w]).then_inc(sem["loaded"], 16)
                    sp.dma_start(proj_rows[:], row(a["L3_xattn_proj_b"]).to_broadcast([P, D])).then_inc(sem["loaded"], 16)
                    sp.dma_start(mask_u8[:], a["mask_SxS_bc0"].rearrange("(u i) j -> i u j", i=P))\
                        .then_inc(sem["mask_loaded"], 16)

            @block.gpsimd
            def _(pool):
                with pool.If(keep.mask_is_odd(pool) > 0):
                    norm.gpsimd(pool)
                    tables = Tally(sem["tables"])
                    tables.add(pool.memset(head_mask[:], 1.0))
                    tables.add(pool.memset(bands[:], 0.0))
                    tables.add(pool.memset(edge[:], 0.0))
                    tables.add(pool.memset(scored[:], 0.0))
                    tables.wait(pool)
                    tables.add(pool.affine_select(out=head_mask[:], in_=head_mask[:], compare_op=ALU.is_ge, fill=0.0,
                                                  base=0, pattern=[[-wide, heads]], channel_multiplier=1))
                    tables.wait(pool)
                    pool.affine_select(out=head_mask[:], in_=head_mask[:], compare_op=ALU.is_ge, fill=0.0, base=wide - 1,
                                       pattern=[[wide, heads]], channel_multiplier=-1).then_inc(sem["tables_done"], 1)
                    for n in range(3):
                        pool.affine_select(out=bands[:, n, :], in_=bands[:, n, :], compare_op=ALU.not_equal, fill=1.0,
                                           base=1 - n, pattern=[[-1, P]], channel_multiplier=1)\
                            .then_inc(sem["tables_done"], 1)
                    for n, base in enumerate((P - 1, 1 - P)):
                        pool.affine_select(out=edge[:, n, :], in_=edge[:, n, :], compare_op=ALU.not_equal, fill=1.0,
                                           base=base, pattern=[[-1, P]], channel_multiplier=1)\
                            .then_inc(sem["tables_done"], 1)

            @block.tensor
            def _(pe):
                with pe.If(keep.mask_is_odd(pe) > 0):
                    norm.tensor(pe)
                    for free in ("conv_made", "turned", "mixed_made"):
                        pe.sem_inc(sem[free], 1)
                    pe.wait_ge(sem["loaded"], 80)
                    pe.wait_ge(norm.xt_ready, 2)
                    with pe.Fori(0, B) as b:
                        xt = norm.xt[:, bass.ds(2 * b, 2), :].rearrange("p t k -> p (t k)")
                        pe.wait_ge(sem["x_done"], b + 1)
                        pe.matmul(ps[:, 2, 0:S], wq[:], xt, start=True, stop=True)
                        pe.matmul(ps[:, 2, S:2 * S], wk[:], xt, start=True, stop=True)
                        pe.matmul(ps[:, 3, 0:S], wv[:], xt, start=True, stop=True).then_inc(sem["q_made"], 1)
                        pe.wait_ge(sem["q_kept"], 3 * (b + 1))
                        for u in range(2):
                            mm = pe.transpose(ps[:, 4, u * D:(u + 1) * D], e[:, 0, u * P:(u + 1) * P], keep.identity[:])
                        mm.then_inc(sem["q_made"], 1)
                        with pe.Fori(0, heads) as h:
                            n = b * heads + h
                            pe.wait_ge(sem["spread"], b + 1)
                            pe.wait_ge(sem["v_kept"], b + 1)
                            pe.wait_ge(sem["scored_ready"], n + 1)
                            for u in range(2):
                                mm = pe.matmul(ps[:, 5, u * S:(u + 1) * S], q_t[:, u * P:(u + 1) * P],
                                               k_spread[:, bass.ds(h, 1), :].rearrange("p a j -> p (a j)"),
                                               start=True, stop=True)
                            mm.then_inc(sem["scores_made"], 1)
                            pe.wait_ge(sem["scored_ready"], n + 2)
                            pe.wait_ge(sem["kernel_ready"], 3 * (n + 1))
                            for u in range(2):
                                to = ps[:, 6, u * S:(u + 1) * S]
                                for c in range(3):
                                    pe.matmul(to, along[:, c, :], scored[:, u, c:c + S], start=(c == 0), stop=False)
                                for c in range(3):
                                    mm = pe.matmul(to, over_edge[:, u, c, :], scored[:, 1 - u, c:c + S], start=False,
                                                   stop=(c == 2))
                            mm.then_inc(sem["conv_made"], 1)
                            pe.wait_ge(sem["exp_done"], 2 * (n + 1))
                            for u in range(2):
                                for j in range(2):
                                    mm = pe.transpose(ps[:, 7, (2 * u + j) * P:(2 * u + j + 1) * P],
                                                      e[:, u, j * P:(j + 1) * P], keep.identity[:])
                            mm.then_inc(sem["turned"], 1)
                            pe.wait_ge(sem["turned_kept"], n + 1)
                            for u in range(2):
                                for j in range(2):
                                    mm = pe.matmul(ps[:, 4, u * wide:(u + 1) * wide], e_t[:, u, j, :],
                                                   v[:, j, bass.ds(h * wide, wide)], start=(j == 0), stop=(j == 1))
                            mm.then_inc(sem["mixed_made"], 1)
                        pe.wait_ge(sem["mixed_ready"], 2 * heads * (b + 1) + 1)
                        for u in range(2):
                            mm = pe.transpose(ps[:, 2, u * P:(u + 1) * P], mixed[:, u, :], keep.identity[:])
                        mm.then_inc(sem["mixed_turned"], 1)
                        pe.wait_ge(sem["mixed_kept"], b + 1)
                        for u in range(2):
                            mm = pe.matmul(ps[:, 3, u * D:(u + 1) * D], mixed_t[:, u, :], proj[:], start=True, stop=True)
                        mm.then_inc(sem["out_made"], 1)

            @block.scalar
            def _(act):
                with act.If(keep.mask_is_odd(act) > 0):
                    norm.scalar(act)
                    act.wait_ge(sem["loaded"], 80)
                    with act.Fori(0, B * heads) as n:
                        act.wait_ge(sem["topped"], n + 1)
                        act.wait_ge(sem["mixed_made"], n + 1)
                        for u in range(2):
                            act.activation(e[:, u, :], e[:, u, :], ACT.Exp, bias=top[:, u:u + 1],
                                           accum_out=total[:, u:u + 1]).then_inc(sem["exp_done"], 1)

            @block.vector
            def _(dve):
                with dve.If(keep.mask_is_odd(dve) > 0):
                    norm.vector(dve)
                    for free in ("x_done", "scored_ready", "mixed_ready"):
                        dve.sem_inc(sem[free], 1)
                    steps = Tally(sem["kernel_steps"])

                    def then(instruction):
                        steps.add(instruction)
                        steps.wait(dve)

                    dve.wait_ge(sem["mask_loaded"], 16)
                    then(dve.tensor_copy(masked[:], mask_u8[:]))
                    then(dve.tensor_scalar(open_[:], masked[:], -1.0, 1.0, ALU.mult, ALU.add))
                    then(dve.tensor_scalar(masked[:], masked[:], -1e30, None, ALU.mult))
                    dve.wait_ge(sem["tables_done"], 6)
                    with dve.Fori(0, B) as b:
                        dve.wait_ge(sem["q_made"], 2 * b + 1)
                        dve.tensor_scalar(q_t[:], ps[:, 2, 0:S], scale, None, ALU.mult).then_inc(sem["q_kept"], 1)
                        dve.tensor_copy(k_t[:], ps[:, 2, S:2 * S]).then_inc(sem["q_kept"], 1)
                        dve.tensor_copy(e[:, 0, :], ps[:, 3, 0:S]).then_inc(sem["q_kept"], 1)
                        dve.wait_ge(sem["q_kept"], 3 * (b + 1))
                        dve.tensor_tensor(k_spread[:], k_t[:, None, :].to_broadcast([P, heads, S]),
                                          head_mask[:, :, None].to_broadcast([P, heads, S]), ALU.mult)\
                            .then_inc(sem["spread"], 1)
                        dve.wait_ge(sem["q_made"], 2 * b + 2)
                        dve.tensor_copy(v[:].rearrange("p u d -> p (u d)"), ps[:, 4, 0:2 * D]).then_inc(sem["v_kept"], 1)
                        with dve.Fori(0, heads) as h:
                            n = b * heads + h
                            def tap(k):
                                return taps[:, bass.ds(b, 1), bass.ds(h, 1), 3 * k:3 * k + 3].rearrange(
                                    "p x y c -> p (x y c)")[:, :, None].to_broadcast([P, 3, P])

                            def spread(to, table, k):
                                return dve.tensor_tensor(to, table.to_broadcast([P, 3, P]), tap(k), ALU.mult)

                            dve.wait_ge(sem["conv_made"], n + 1)
                            spread(along[:], bands[:, 0:1, :], 0).then_inc(sem["band_made"], 1)
                            spread(tmp[:], bands[:, 1:2, :], 1).then_inc(sem["band_made"], 1)
                            dve.wait_ge(sem["band_made"], 4 * n + 2)
                            dve.tensor_tensor(along[:], along[:], tmp[:], ALU.add).then_inc(sem["band_made"], 1)
                            dve.wait_ge(sem["band_made"], 4 * n + 3)
                            spread(tmp[:], bands[:, 2:3, :], 2).then_inc(sem["band_made"], 1)
                            dve.wait_ge(sem["band_made"], 4 * n + 4)
                            dve.tensor_tensor(along[:], along[:], tmp[:], ALU.add).then_inc(sem["kernel_ready"], 1)
                            spread(over_edge[:, 0], edge[:, 0:1, :], 2).then_inc(sem["kernel_ready"], 1)
                            spread(over_edge[:, 1], edge[:, 1:2, :], 0).then_inc(sem["kernel_ready"], 1)
                            dve.wait_ge(sem["scores_made"], n + 1)
                            dve.tensor_tensor(scored[:, :, 1:S + 1], ps[:, 5, :].rearrange("p (u j) -> p u j", u=2),
                                              open_[:], ALU.mult).then_inc(sem["scored_ready"], 1)
                            dve.wait_ge(sem["conv_made"], n + 2)
                            dve.wait_ge(sem["turned"], n + 1)
                            dve.tensor_tensor(e[:], ps[:, 6, :].rearrange("p (u j) -> p u j", u=2), masked[:], ALU.add)\
                                .then_inc(sem["biased"], 1)
                            dve.wait_ge(sem["biased"], n + 1)
                            dve.tensor_reduce(top[:], e[:], AX, ALU.max, negate=True).then_inc(sem["topped"], 1)
                            dve.wait_ge(sem["turned"], n + 2)
                            dve.tensor_copy(e_t[:].rearrange("p u j k -> p (u j k)"), ps[:, 7, :])\
                                .then_inc(sem["turned_kept"], 1)
                            dve.wait_ge(sem["mixed_ready"], 2 * n + 1)
                            dve.reciprocal(inverse[:], total[:]).then_inc(sem["inverted"], 1)
                            dve.wait_ge(sem["inverted"], n + 1)
                            dve.wait_ge(sem["mixed_made"], n + 2)
                            for u in range(2):
                                dve.tensor_scalar(mixed[:, u, bass.ds(h * wide, wide)], ps[:, 4, u * wide:(u + 1) * wide],
                                                  inverse[:, u:u + 1], None, ALU.mult).then_inc(sem["mixed_ready"], 1)
                        dve.wait_ge(sem["mixed_turned"], b + 1)
                        dve.tensor_copy(mixed_t[:].rearrange("p u k -> p (u k)"), ps[:, 2, 0:2 * P])\
                            .then_inc(sem["mixed_kept"], 1)
                        dve.wait_ge(sem["out_made"], b + 1)
                        dve.tensor_tensor(change[:], ps[:, 3, 0:2 * D].rearrange("p (u d) -> p u d", u=2),
                                          proj_rows[:, None, :].to_broadcast([P, 2, D]), ALU.add).then_inc(sem["changed"], 1)
                        dve.wait_ge(sem["changed"], b + 1)
                        xb = keep.x[:, bass.ds(2 * b, 2), :]
                        dve.scalar_tensor_tensor(out=xb, in0=change[:], scalar=gate, in1=xb, op0=ALU.mult, op1=ALU.add)\
                            .then_inc(sem["x_done"], 1)


def check_mask(nc, a, keep, name):
    with Scope(nc, name) as s:
        mask_u8, given, causal = s.sb("mask_u8", [P, 2, S], U8), s.sb("given", [P, 2, S]), s.sb("causal", [P, 2, S])
        ones, off = s.sb("ones", [P, 1]), s.sb("off", [P, 1])
        ps = s.psum("ps", [1, 1])
        names = ["loaded", "ones_set", "causal_set", "causal_made", "steps", "off_ready", "off_counted", "flagged"]
        sem = {n: s.sem(n) for n in names}
        with s.block() as block:

            @block.sync
            def _(sp):
                sp.dma_start(mask_u8[:], a["mask_SxS_bc0"].rearrange("(u i) j -> i u j", i=P)).then_inc(sem["loaded"], 16)

            @block.gpsimd
            def _(pool):
                pool.memset(ones[:], 1.0).then_inc(sem["ones_set"], 1)
                pool.memset(causal[:], 1.0).then_inc(sem["causal_set"], 1)
                pool.wait_ge(sem["causal_set"], 1)
                pool.affine_select(out=causal[:], in_=causal[:], compare_op=ALU.is_ge, fill=0.0, base=-1,
                                   pattern=[[-P, 2], [1, S]], channel_multiplier=-1).then_inc(sem["causal_made"], 1)

            @block.tensor
            def _(pe):
                pe.wait_ge(sem["ones_set"], 1)
                pe.wait_ge(sem["off_ready"], 1)
                pe.matmul(ps[:], off[:], ones[:], start=True, stop=True).then_inc(sem["off_counted"], 1)

            @block.vector
            def _(dve):
                steps = Tally(sem["steps"])
                dve.wait_ge(sem["loaded"], 16)
                steps.add(dve.tensor_copy(given[:], mask_u8[:]))
                steps.wait(dve)
                dve.wait_ge(sem["causal_made"], 1)
                steps.add(dve.tensor_tensor(given[:], given[:], causal[:], ALU.not_equal))
                steps.wait(dve)
                dve.tensor_reduce(off[:], given[:].rearrange("p u j -> p (u j)"), AX, ALU.max)\
                    .then_inc(sem["off_ready"], 1)
                dve.wait_ge(sem["off_counted"], 1)
                dve.tensor_scalar(keep.odd_mask[:], ps[:], 1.0, None, ALU.min).then_inc(sem["flagged"], 1)
                dve.wait_ge(sem["flagged"], 1)


def conv_attention_causal(nc, a, keep, name, taps, gate, rows):
    heads, wide, R, G = 16, 8, 4, 4
    scale = float(wide) ** -0.5
    closest = [(shift, tap_a) for shift in range(4) for tap_a in (-1, 0, 1)
               if abs(tap_a - shift) <= 1 or abs(tap_a - shift + 1) <= 1]
    rows3 = 3 * R * wide
    units = [(b, t, j) for b in range(B) for t, j in ((0, 0), (1, 0), (1, 1))]
    with Scope(nc, name) as s:
        ps = s.psum("ps", [P, 8, 512])
        norm = Normed(s, keep, ps[:, 0], ps[:, 1], True, rows)
        xt = norm.xt
        wq, wk, wv, proj, bias = (s.sb(n, [P, D]) for n in ("wq", "wk", "wv", "proj", "bias"))
        head_mask = s.sb("head_mask", [P, heads])
        near_taps = s.sb("near_taps", [P, B, len(closest), 2, heads])
        w_wide = s.sb("w_wide", [P, 2, G, 3, R * wide])
        own_row, own_head = s.sb("own_row", [rows3, R, 3, 3]), s.sb("own_head", [rows3, R])
        row_taps, tap_parts = s.sb("row_taps", [rows3, B * G, 3]), s.sb("tap_parts", [rows3, B * G, R * 9])
        below, one_below, zeros = s.sb("below", [P, P]), s.sb("one_below", [P, 1]), s.sb("zeros", [P, P])
        q_f, k_f = s.sb("q_f", [P, B, S + 2]), s.sb("k_f", [P, B, S + 5])
        products = s.sb("products", [P, 2, 4, S + 2])
        queries, keys = s.sb("queries", [rows3, G, B, S]), s.sb("keys", [rows3, G, B, S + 2])
        one_shift = s.sb("one_shift", [rows3, G, S])
        keys_summed, keys_apart = s.sb("keys_summed", [rows3, G, S]), s.sb("keys_apart", [rows3, 2, G, R, S])
        v, v_before = s.sb("v", [P, NT, heads, wide + 1]), s.sb("v_before", [P, NT, heads, wide + 1])
        near = s.sb("near", [P, NT, 2, heads])
        near_e = s.sb("near_e", [P, NT, 2, heads])
        near_v = s.sb("near_v", [P, 4, 2, heads, wide + 1])
        top = s.sb("top", [P, len(units), heads])
        tmp_top = s.sb("tmp_top", [P, B, 3, heads])
        e, e_t = s.sb("e", [P, 2, G, R, P]), s.sb("e_t", [P, 2, G, R, P])
        acc = s.sb("acc", [P, len(units), heads, wide + 1])
        inverse = s.sb("inverse", [P, NT, heads])
        mixed, mixed_t, change = s.sb("mixed", [P, NT, D]), s.sb("mixed_t", [P, 2, P]), norm.xn
        names = ["loaded", "padded", "tables", "tables_made", "widened", "taps_steps", "taps_taken", "jobs_made", "act_read",
                 "dve_read", "key_steps_dve", "key_steps_pool", "keys_ready_dve", "keys_ready_pool", "products_made",
                 "near_kept", "misc_made",
                 "misc_read", "scores_made", "scores_read", "maxed", "centred", "near_centred", "exp_done", "near_exp",
                 "near_steps", "near_ready", "turned", "turned_kept", "pv_made", "acc_made", "gap_ready", "gap_exp",
                 "joined", "inverted", "mixed_ready", "biased_x", "x_done"]
        sem = {n: s.sem(n) for n in names}

        jobs = ([("keys", 0, g, "dve_read") for g in range(G)] + [("queries", 0, g, "act_read") for g in range(G)]
                + [("q_f", half, 0, "act_read") for half in range(2)] + [("k_f", half, 0, "dve_read") for half in range(2)]
                + [("v", half, before, "act_read") for before in range(2) for half in range(2)]
                + [("keys", 1, g, "dve_read") for g in range(G)] + [("queries", 1, g, "act_read") for g in range(G)])

        def read_by_then(j):
            return sem[jobs[j][3]], sum(job[3] == jobs[j][3] for job in jobs[:j + 1])

        def bank(j):
            return ps[:, (j + 2) % 8]

        uses, plan = [("near", 0)], []
        for b in range(B):
            near_next = ("near", b + 1) if b + 1 < B else None
            last = [("turn", b - 1), ("project", b - 1)] if b else [None, None]
            plan += [[None, None, near_next, None], [None, last[0], None, last[1]], [None, None, None, None]]
        uses += [use for places in plan for use in places if use] + [("turn", B - 1), ("project", B - 1)]

        def spread_keys(engine, steps, ready, b):
            if b >= 2:
                engine.wait_ge(sem["scores_made"], G * 3 * (b - 1))
            if b >= 2:
                engine.wait_ge(ready, G * (b - 1))
            for c in range(3):
                tap = row_taps[:, b * G:(b + 1) * G, c:c + 1].to_broadcast([rows3, G, S])
                to = one_shift if c else keys_summed
                steps.add(engine.tensor_tensor(to[:], keys[:, :, b, c:c + S], tap, ALU.mult))
                steps.wait(engine)
                if c:
                    steps.add(engine.tensor_tensor(keys_summed[:], keys_summed[:], one_shift[:], ALU.add))
                    steps.wait(engine)
            for g in range(G):
                engine.tensor_tensor(keys_apart[:, b % 2, g], keys_summed[:, g:g + 1].to_broadcast([rows3, R, S]),
                                     own_head[:, :, None].to_broadcast([rows3, R, S]), ALU.mult).then_inc(ready, 1)

        near_pairs = sum(abs(tap_a - shift + x) <= 1 for shift, tap_a in closest for x in range(2))
        near_tables = 14 + B * near_pairs

        with s.block() as block:

            @block.sync
            def _(sp):
                with sp.If(keep.mask_is_odd(sp) < 1):
                    for to, w in zip((wq, wk, wv, proj), ("Wq", "Wk", "Wv", "proj_W")):
                        sp.dma_start(to[:], a["L3_xattn_" + w]).then_inc(sem["loaded"], 16)
                    sp.dma_start(bias[:], row(a["L3_xattn_proj_b"]).to_broadcast([P, D])).then_inc(sem["loaded"], 16)
                    sp.wait_ge(sem["loaded"], 80)

            @block.gpsimd
            def _(pool):
                with pool.If(keep.mask_is_odd(pool) < 1):
                    steps = Tally(sem["tables"])
                    pads = (xt[:, :, 0:1], xt[:, :, S + 1:S + 2], q_f[:, :, 0:1], q_f[:, :, S + 1:S + 2], k_f[:, :, 0:4],
                            k_f[:, :, S + 4:S + 5], keys[:, :, :, 0:1], keys[:, :, :, S + 1:S + 2],
                            queries[0:32, :, :, 0:1], queries[64:96, :, :, S - 1:S])
                    for n, pad in enumerate(pads):
                        if n >= 6:
                            pool.wait_ge(sem["padded"], n)
                        pool.memset(pad, 0.0).then_inc(sem["padded"], 1)
                    pool.wait_ge(sem["padded"], 10)
                    norm.gpsimd(pool)
                    steps.add(pool.memset(own_row[:], 1.0))
                    steps.add(pool.memset(own_head[:], 0.0))
                    steps.wait(pool)
                    steps.add(pool.affine_select(out=own_row[:], in_=own_row[:], compare_op=ALU.is_ge, fill=0.0, base=0,
                                                 pattern=[[-wide, R], [-wide * R, 3], [0, 3]], channel_multiplier=1))
                    steps.wait(pool)
                    steps.add(pool.affine_select(out=own_row[:], in_=own_row[:], compare_op=ALU.is_ge, fill=0.0,
                                                 base=wide - 1, pattern=[[wide, R], [wide * R, 3], [0, 3]],
                                                 channel_multiplier=-1))
                    steps.wait(pool)
                    for at in range(3):
                        steps.add(pool.tensor_tensor(own_head[:], own_head[:], own_row[:, :, at, 0], ALU.add))
                        steps.wait(pool)
                    steps.add(pool.memset(head_mask[:], 1.0))
                    steps.add(pool.memset(zeros[:], 0.0))
                    steps.add(pool.memset(near_taps[:], 0.0))
                    steps.add(pool.memset(v[:, :, :, wide:wide + 1], 1.0))
                    steps.add(pool.memset(v_before[:, :, :, wide:wide + 1], 1.0))
                    steps.wait(pool)
                    pool.affine_select(out=below[:], in_=zeros[:], compare_op=ALU.is_ge, fill=-1e30, base=-2,
                                       pattern=[[-1, P]], channel_multiplier=1).then_inc(sem["tables_made"], 1)
                    pool.affine_select(out=one_below[:], in_=zeros[:, 0:1], compare_op=ALU.not_equal, fill=-1e30,
                                       base=0, pattern=[[0, 1]], channel_multiplier=1).then_inc(sem["tables_made"], 1)
                    steps.add(pool.affine_select(out=head_mask[:], in_=head_mask[:], compare_op=ALU.is_ge, fill=0.0,
                                                 base=0, pattern=[[-wide, heads]], channel_multiplier=1))
                    steps.wait(pool)
                    steps.add(pool.affine_select(out=head_mask[:], in_=head_mask[:], compare_op=ALU.is_ge, fill=0.0,
                                                 base=wide - 1, pattern=[[wide, heads]], channel_multiplier=-1))
                    steps.wait(pool)
                    for n, (shift, tap_a) in enumerate(closest):
                        for below_by in range(2):
                            tap_c = tap_a - shift + below_by
                            if abs(tap_c) <= 1:
                                at = 3 * (tap_a + 1) + tap_c + 1
                                for b in range(B):
                                    steps.add(pool.tensor_tensor(
                                        near_taps[:, b, n, below_by, :], taps[:, b, :, at], head_mask[:], ALU.mult))
                    steps.wait(pool)

                    def near_values(b, t):
                        n = 2 * b + t
                        pool.wait_ge(sem["near_exp"], n + 1)
                        pool.wait_ge(sem["act_read"], 10)
                        if n >= 4:
                            pool.wait_ge(sem["acc_made"], 3 * ((n - 4) // 2) + (3 if t else 1))
                        near_steps = Tally(sem["near_steps"])
                        near_steps.n = 2 * n
                        for below_by, rows in enumerate((v, v_before)):
                            near_steps.add(pool.tensor_tensor(
                                near_v[:, n % 4, below_by], rows[:, n],
                                near_e[:, n, below_by, :, None].to_broadcast([P, heads, wide + 1]), ALU.mult))
                        near_steps.wait(pool)
                        pool.tensor_tensor(near_v[:, n % 4, 0], near_v[:, n % 4, 0], near_v[:, n % 4, 1], ALU.add)\
                            .then_inc(sem["near_ready"], 1)

                    def join(b):
                        n = 3 * b + 1
                        joined = Tally(sem["joined"])
                        joined.n = 3 * b
                        pool.wait_ge(sem["gap_exp"], b + 1)
                        pool.wait_ge(sem["acc_made"], n + 2)
                        for k in range(2):
                            joined.add(pool.tensor_tensor(
                                acc[:, n + k], acc[:, n + k],
                                tmp_top[:, b, k, :, None].to_broadcast([P, heads, wide + 1]), ALU.mult))
                        joined.wait(pool)
                        joined.add(pool.tensor_tensor(acc[:, n + 1], acc[:, n + 1], acc[:, n], ALU.add))

                    def add_change(b):
                        pool.wait_ge(sem["misc_read"], uses.index(("project", b)) + 1)
                        pool.wait_ge(sem["biased_x"], 1)
                        pool.tensor_tensor(keep.x[:, 2 * b:2 * b + 2], keep.x[:, 2 * b:2 * b + 2],
                                           change[:, 2 * b:2 * b + 2], ALU.add).then_inc(sem["x_done"], 1)

                    key_steps = Tally(sem["key_steps_pool"])
                    for b in range(B):
                        near_values(b, 0)
                        if b + 1 < B:
                            if b == 0:
                                pool.wait_ge(sem["taps_taken"], 1)
                                pool.wait_ge(sem["dve_read"], 10)
                            spread_keys(pool, key_steps, sem["keys_ready_pool"], b + 1)
                        if b:
                            add_change(b - 1)
                        near_values(b, 1)
                        join(b)
                    add_change(B - 1)

            @block.tensor
            def _(pe):
                with pe.If(keep.mask_is_odd(pe) < 1):
                    norm.tensor(pe)
                    pe.wait_ge(sem["loaded"], 80)
                    pe.wait_ge(sem["padded"], 10)
                    pe.wait_ge(sem["widened"], 2)
                    pe.wait_ge(norm.xt_ready, 1)
                    for n, (what, half, which, _) in enumerate(jobs):
                        if n == 6:
                            pe.wait_ge(norm.xt_ready, 2)
                        if n >= 8:
                            pe.wait_ge(*read_by_then(n - 8))
                        of_batches = xt[:, 2 * half:2 * half + 2, 1:S + 1]
                        if what in ("keys", "queries"):
                            mm = pe.matmul(bank(n)[0:rows3], w_wide[:, what == "keys", which].rearrange("p a d -> p (a d)"),
                                           of_batches, start=True, stop=True)
                        elif what in ("q_f", "k_f"):
                            mm = pe.matmul(bank(n), (wq if what == "q_f" else wk)[:], of_batches, start=True, stop=True)
                        else:
                            for t in range(4):
                                at = (t % 2) * P + 1 - which
                                mm = pe.matmul(bank(n)[:, t * D:(t + 1) * D], xt[:, 2 * half + t // 2, at:at + P], wv[:],
                                               start=True, stop=True)
                        mm.then_inc(sem["jobs_made"], 1)

                    def misc(use):
                        if use:
                            {"near": near_scores, "turn": turn_mixed, "project": project}[use[0]](uses.index(use))

                    def near_scores(use):
                        b = uses[use][1]
                        if use:
                            pe.wait_ge(sem["misc_read"], use)
                        else:
                            pe.wait_ge(*read_by_then(len(jobs) - 4))
                            pe.wait_ge(sem["tables"], near_tables)
                        pe.wait_ge(sem["products_made"], 4 * (b + 1))
                        for t in range(2):
                            for n, (shift, tap_a) in enumerate(closest):
                                at = t * P + 1 + tap_a
                                mm = pe.matmul(ps[:, 6, t * 2 * heads:(t + 1) * 2 * heads],
                                               products[:, b % 2, shift, at:at + P],
                                               near_taps[:, b, n].rearrange("p x h -> p (x h)"),
                                               start=(n == 0), stop=(n == len(closest) - 1))
                        mm.then_inc(sem["misc_made"], 1)

                    def turn_mixed(use):
                        b = uses[use][1]
                        pe.wait_ge(sem["misc_read"], use)
                        pe.wait_ge(sem["mixed_ready"], 2 * (b + 1))
                        for t in range(2):
                            mm = pe.transpose(ps[:, 6, t * P:(t + 1) * P], mixed[:, 2 * b + t, :], keep.identity[:])
                        mm.then_inc(sem["misc_made"], 1)

                    def project(use):
                        b = uses[use][1]
                        pe.wait_ge(sem["misc_read"], use)
                        for t in range(2):
                            mm = pe.matmul(ps[:, 6, t * D:(t + 1) * D], mixed_t[:, t, :], proj[:],
                                           start=True, stop=True)
                        mm.then_inc(sem["misc_made"], 1)

                    def scores(n):
                        b, t, j = units[n]
                        if b:
                            pe.wait_ge(sem["keys_ready_pool"], G * b)
                        else:
                            pe.wait_ge(sem["keys_ready_dve"], G)
                            pe.wait_ge(sem["act_read"], 14)
                            pe.wait_ge(sem["dve_read"], 10)
                        for g in range(G):
                            if n:
                                pe.wait_ge(sem["scores_read"], G * (n - 1) + g + 1)
                            pe.matmul(ps[:, g, :].rearrange("p (r k) -> p r k", r=R), queries[:, g, b, t * P:(t + 1) * P],
                                      keys_apart[:, b % 2, g, :, j * P:(j + 1) * P], start=True, stop=True)\
                                .then_inc(sem["scores_made"], 1)

                    def turn(n):
                        for g in range(G):
                            if g % 2 == 0:
                                pe.wait_ge(sem["exp_done"], 2 * n + g // 2 + 1)
                            if G * n + g >= 2:
                                pe.wait_ge(sem["turned_kept"], G * n + g - 1)
                            for r in range(R):
                                mm = pe.transpose(ps[:, 4 + g % 2, r * P:(r + 1) * P], e[:, n % 2, g, r, :],
                                                  keep.identity[:])
                            mm.then_inc(sem["turned"], 1)

                    def values(n):
                        b, t, j = units[n]
                        if n:
                            pe.wait_ge(sem["acc_made"], n)
                        for h in range(heads):
                            if h % R == 0:
                                pe.wait_ge(sem["turned_kept"], G * n + h // R + 1)
                            mm = pe.matmul(ps[:, 7, (wide + 1) * h:(wide + 1) * (h + 1)], e_t[:, n % 2, h // R, h % R, :],
                                           v[:, 2 * b + j, h, :], start=True, stop=True)
                        mm.then_inc(sem["pv_made"], 1)

                    scores(0)
                    misc(uses[0])
                    for n in range(len(units)):
                        misc(plan[n][0])
                        if n + 1 < len(units):
                            scores(n + 1)
                        misc(plan[n][1])
                        turn(n)
                        misc(plan[n][2])
                        values(n)
                        misc(plan[n][3])
                    misc(uses[-2])
                    misc(uses[-1])

            @block.scalar
            def _(act):
                with act.If(keep.mask_is_odd(act) < 1):
                    norm.scalar(act)
                    act.wait_ge(sem["padded"], 10)
                    for n, (what, half, which, reader) in enumerate(jobs):
                        if reader != "act_read":
                            continue
                        act.wait_ge(sem["jobs_made"], n + 1)
                        batches = bank(n).rearrange("p (b i) -> p b i", b=2)
                        if what == "queries":
                            for x, (to, at) in enumerate(((slice(1, S), slice(0, S - 1)), (slice(0, S), slice(0, S)),
                                                          (slice(0, S - 1), slice(1, S)))):
                                done = act.activation(queries[32 * x:32 * x + 32, which, 2 * half:2 * half + 2, to],
                                                      batches[32 * x:32 * x + 32, :, at], ACT.Copy, scale=scale)
                        elif what == "q_f":
                            done = act.activation(q_f[:, 2 * half:2 * half + 2, 1:S + 1], batches, ACT.Copy, scale=scale)
                        else:
                            if not which and not half:
                                act.wait_ge(sem["tables"], 12)
                            done = act.activation((v_before if which else v)[:, 4 * half:4 * half + 4, :, 0:wide],
                                                  bank(n).rearrange("p (t h d) -> p t h d", t=4, d=wide), ACT.Copy)
                        done.then_inc(sem["act_read"], 1)

                    def misc(use):
                        if not use:
                            return
                        kind, b = use
                        act.wait_ge(sem["misc_made"], uses.index(use) + 1)
                        if kind == "near":
                            act.activation(near[:, 2 * b:2 * b + 2].rearrange("p t x h -> p (t x h)"),
                                           ps[:, 6, 0:4 * heads], ACT.Copy).then_inc(sem["misc_read"], 1)
                        elif kind == "turn":
                            act.activation(mixed_t[:].rearrange("p t k -> p (t k)"), ps[:, 6, 0:2 * P],
                                           ACT.Copy).then_inc(sem["misc_read"], 1)
                        else:
                            act.activation(change[:, 2 * b:2 * b + 2].rearrange("p t k -> p (t k)"), ps[:, 6, 0:2 * D],
                                           ACT.Copy, scale=gate).then_inc(sem["misc_read"], 1)

                    def exp(n):
                        b, t, j = units[n]
                        for half in range(2):
                            act.wait_ge(sem["centred"], R * n + 2 * half + 2)
                            act.activation(e[:, n % 2, 2 * half:2 * half + 2], e[:, n % 2, 2 * half:2 * half + 2], ACT.Exp)\
                                .then_inc(sem["exp_done"], 1)
                        if t == j:
                            act.wait_ge(sem["near_centred"], 2 * b + t + 1)
                            act.activation(near_e[:, 2 * b + t], near_e[:, 2 * b + t], ACT.Exp)\
                                .then_inc(sem["near_exp"], 1)
                        if (t, j) == (1, 1):
                            act.wait_ge(sem["gap_ready"], b + 1)
                            act.activation(tmp_top[:, b, 0:2], tmp_top[:, b, 0:2], ACT.Exp).then_inc(sem["gap_exp"], 1)

                    def keep_turned(n):
                        for g in range(G):
                            act.wait_ge(sem["turned"], G * n + g + 1)
                            if n >= 2:
                                act.wait_ge(sem["pv_made"], n - 1)
                            act.activation(e_t[:, n % 2, g].rearrange("p r k -> p (r k)"), ps[:, 4 + g % 2, :], ACT.Copy)\
                                .then_inc(sem["turned_kept"], 1)

                    misc(uses[0])
                    exp(0)
                    for n in range(len(units)):
                        misc(plan[n][0])
                        misc(plan[n][1])
                        keep_turned(n)
                        misc(plan[n][2])
                        if n + 1 < len(units):
                            exp(n + 1)
                        misc(plan[n][3])
                    misc(uses[-2])
                    misc(uses[-1])

            @block.vector
            def _(dve):
                with dve.If(keep.mask_is_odd(dve) < 1):
                    norm.vector(dve)
                    dve.wait_ge(sem["loaded"], 80)
                    for n, w in enumerate((wq, wk)):
                        dve.tensor_copy(w_wide[:, n], w[:].rearrange("p (g d) -> p g d", g=G)[:, :, None, :].to_broadcast(
                            [P, G, 3, R * wide])).then_inc(sem["widened"], 1)
                    dve.wait_ge(sem["padded"], 10)
                    dve.wait_ge(sem["tables"], 4)
                    dve.tensor_tensor(tap_parts[:], taps[0:rows3].rearrange("p b (g r) n -> p (b g) (r n)", g=G),
                                      own_row[:, None].rearrange("p x r a c -> p x (r a c)").to_broadcast(
                                          [rows3, B * G, R * 9]), ALU.mult).then_inc(sem["taps_steps"], 1)
                    dve.wait_ge(sem["taps_steps"], 1)
                    dve.tensor_reduce(row_taps[:], tap_parts[:].rearrange("p x (y c) -> p x c y", c=3), AX, ALU.add)\
                        .then_inc(sem["taps_taken"], 1)

                    def products_of(b):
                        if b >= 2:
                            dve.wait_ge(sem["misc_made"], uses.index(("near", b - 2)) + 1)
                        for shift in range(4):
                            dve.tensor_tensor(products[:, b % 2, shift], q_f[:, b], k_f[:, b, 3 - shift:3 - shift + S + 2],
                                              ALU.mult).then_inc(sem["products_made"], 1)

                    for n, (what, half, which, reader) in enumerate(jobs):
                        if reader != "dve_read":
                            continue
                        if (what, half, which) == ("keys", 1, 0):
                            dve.wait_ge(sem["taps_taken"], 1)
                            dve.wait_ge(sem["tables"], 7)
                            dve.wait_ge(sem["dve_read"], 6)
                            spread_keys(dve, Tally(sem["key_steps_dve"]), sem["keys_ready_dve"], 0)
                            dve.wait_ge(sem["act_read"], 6)
                            products_of(0)
                        dve.wait_ge(sem["jobs_made"], n + 1)
                        to = (keys[:, which, 2 * half:2 * half + 2, 1:S + 1] if what == "keys" else
                              k_f[:, 2 * half:2 * half + 2, 4:S + 4])
                        dve.tensor_copy(to, bank(n)[0:rows3 if what == "keys" else P].rearrange("p (b i) -> p b i", b=2))\
                            .then_inc(sem["dve_read"], 1)
                    dve.wait_ge(sem["tables_made"], 2)
                    maxed = Tally(sem["maxed"])

                    def centre(n):
                        b, t, j = units[n]
                        if n % 3 == 0:
                            dve.wait_ge(sem["misc_read"], uses.index(("near", b)) + 1)
                            dve.tensor_scalar(near[0:1, 2 * b, 1, :], near[0:1, 2 * b, 1, :], -1e30, None, ALU.add)\
                                .then_inc(sem["near_kept"], 1)
                            dve.wait_ge(sem["near_kept"], b + 1)
                        if n >= 2:
                            dve.wait_ge(sem["turned"], R * (n - 1))
                        banks = [ps[:, g, :].rearrange("p (r k) -> p r k", r=R) for g in range(G)]
                        scored = [e[:, n % 2, g] for g in range(G)] if t == j else banks
                        for g in range(G):
                            dve.wait_ge(sem["scores_made"], G * n + g + 1)
                            if t == j:
                                dve.tensor_tensor(scored[g], banks[g], below[:, None, :].to_broadcast([P, R, P]), ALU.add)\
                                    .then_inc(sem["scores_read"], 1)
                            else:
                                maxed.add(dve.tensor_scalar(banks[g][:, :, P - 1], banks[g][:, :, P - 1], one_below[:], None,
                                                            ALU.add))
                        if t == j:
                            dve.wait_ge(sem["scores_read"], R * (n + 1))
                        maxed.wait(dve)
                        for g in range(G):
                            maxed.add(dve.tensor_reduce(top[:, n, R * g:R * (g + 1)], scored[g], AX, ALU.max))
                        maxed.wait(dve)
                        if t == j:
                            for x in range(2):
                                maxed.add(dve.tensor_tensor(top[:, n], top[:, n], near[:, 2 * b + t, x], ALU.max))
                                maxed.wait(dve)
                        for g in range(G):
                            done = dve.tensor_tensor(e[:, n % 2, g], scored[g],
                                                     top[:, n, R * g:R * (g + 1), None].to_broadcast([P, R, P]),
                                                     ALU.subtract)
                            done.then_inc(sem["centred"], 1)
                        if t != j:
                            dve.wait_ge(sem["centred"], R * (n + 1))
                            dve.sem_inc(sem["scores_read"], R)
                        if t == j:
                            dve.tensor_tensor(near_e[:, 2 * b + t], near[:, 2 * b + t],
                                              top[:, n:n + 1].to_broadcast([P, 2, heads]), ALU.subtract)\
                                .then_inc(sem["near_centred"], 1)
                        if (t, j) == (1, 1):
                            maxed.add(dve.tensor_tensor(tmp_top[:, b, 2], top[:, n - 1], top[:, n], ALU.max))
                            maxed.wait(dve)
                            dve.tensor_tensor(tmp_top[:, b, 0:2], top[:, n - 1:n + 1],
                                              tmp_top[:, b, 2:3].to_broadcast([P, 2, heads]), ALU.subtract)\
                                .then_inc(sem["gap_ready"], 1)

                    def gather(n):
                        b, t, j = units[n]
                        dve.wait_ge(sem["pv_made"], n + 1)
                        flat = acc[:, n].rearrange("p h d -> p (h d)")
                        if t == j:
                            dve.wait_ge(sem["near_ready"], 2 * b + t + 1)
                            dve.tensor_tensor(flat, ps[:, 7, 0:heads * (wide + 1)],
                                              near_v[:, (2 * b + t) % 4, 0].rearrange("p h d -> p (h d)"), ALU.add)\
                                .then_inc(sem["acc_made"], 1)
                        else:
                            dve.tensor_copy(flat, ps[:, 7, 0:heads * (wide + 1)]).then_inc(sem["acc_made"], 1)

                    def normalise(n):
                        b, t, j = units[n]
                        m = 2 * b + t
                        if t:
                            dve.wait_ge(sem["joined"], 3 * (b + 1))
                        else:
                            dve.wait_ge(sem["acc_made"], n + 1)
                        dve.reciprocal(inverse[:, m], acc[:, n, :, wide]).then_inc(sem["inverted"], 1)
                        dve.wait_ge(sem["inverted"], m + 1)
                        dve.tensor_tensor(mixed[:, m].rearrange("p (h d) -> p h d", h=heads), acc[:, n, :, 0:wide],
                                          inverse[:, m, :, None].to_broadcast([P, heads, wide]), ALU.mult).then_inc(sem["mixed_ready"], 1)

                    centre(0)
                    products_of(1)
                    for n in range(len(units)):
                        if n + 1 < len(units):
                            centre(n + 1)
                        if n == 0:
                            dve.wait_ge(norm.xn_ready, NT)
                            dve.scalar_tensor_tensor(out=keep.x[:], in0=bias[:, None, :].to_broadcast([P, NT, D]),
                                                     scalar=gate, in1=keep.x[:], op0=ALU.mult, op1=ALU.add)\
                                .then_inc(sem["biased_x"], 1)
                        gather(n)
                        if n % 3 == 0:
                            if n:
                                normalise(n - 1)
                            normalise(n)
                        if n % 3 == 1 and n // 3 + 2 < B:
                            products_of(n // 3 + 2)
                    normalise(len(units) - 1)



class Keep:

    def __init__(self, nc, s):
        self.x = s.sb("x", [P, NT, D])
        self.ctx_t = s.sb("ctx_t", [P, B * C])
        self.identity = s.sb("identity", [P, P])
        self.gates = s.sb("gates", [P, 2 * B])
        self.neg_half = s.sb("neg_half", [P, 16])
        self.iota = s.sb("iota", [P, P])
        self.iota_tiles = s.sb("iota_tiles", [P, NT])
        self.token = s.sb("token", [P, NT])
        self.odd_mask = s.sb("odd_mask", [1, 1], I32)
        self.x_loaded = s.sem("x_loaded")
        self.routes = [Routes(nc, s, f"ffn{n + 1}", n) for n in range(3)]
        self.gathered = [s.gpsimd_dma_sem(f"gathered{u}") for u in range(4)]
        self.got = [s.gpsimd_dma_sem(f"got{k}{t}") for t in range(NT) for k in range(CHOSEN)]

    def mask_is_odd(self, engine):
        return engine.value_load(self.odd_mask[0:1, 0:1], min_val=0, max_val=1)


def latent_operands(nc, a, keep, name, scores_rhs, values_rhs, score_bias, wq, bias_q, scale, out_bias_rows,
                    gather):
    heads = 16
    wide = D // heads
    with Scope(nc, name) as s:
        wk, wv = s.sb("wk", [P, D]), s.sb("wv", [P, D])
        ctx_twice = s.sb("ctx_twice", [P, B, 2, C])
        bias_k, head_mask, k_t = s.sb("bias_k", [P, 1]), s.sb("head_mask", [P, heads]), s.sb("k_t", [P, B * C])
        ps = s.psum("ps", [P, 2, 512])
        names = ["weights_loaded", "bias_loaded", "mask_loaded", "ones_set", "lower_cut", "mask_made", "k_made",
                 "k_kept", "v_made", "rhs_zeroed", "v_kept", "k_spread", "ones_placed", "q_scaled", "ctx_doubled",
                 "out_bias_loaded"]
        sem = {n: s.sem(n) for n in names}
        with s.block() as block:

            @block.sync
            def _(sp):
                sp.dma_start(wk[:], a["L2_xattn_Wk"]).then_inc(sem["weights_loaded"], 16)
                sp.dma_start(wv[:], a["L2_xattn_Wv"]).then_inc(sem["weights_loaded"], 16)
                sp.dma_start(wq[:], a["L2_xattn_Wq"]).then_inc(sem["weights_loaded"], 16)
                sp.dma_start(score_bias[:].rearrange("p b k -> p (b k)"),
                             a["mask_Bx1x1xS2_ff0"].rearrange("b x y k -> (x y) (b k)").to_broadcast([P, B * C]))\
                    .then_inc(sem["mask_loaded"], 16)
                sp.wait_ge(sem["mask_loaded"], 16)
                for to, v in ((bias_k, "L2_xattn_bk"), (bias_q, "L2_xattn_bq")):
                    sp.dma_start(to[:], a[v].rearrange("(p c) -> p c", c=1)).then_inc(sem["bias_loaded"], 16)
                sp.dma_start(out_bias_rows[:], row(a["L2_xattn_bv"]).to_broadcast([P, D]))\
                    .then_inc(sem["out_bias_loaded"], 16)
                sp.wait_ge(sem["out_bias_loaded"], 16)
                sp.wait_ge(sem["weights_loaded"], 48)

            @block.gpsimd
            def _(pool):
                pool.memset(head_mask[:], 1.0).then_inc(sem["ones_set"], 1)
                pool.wait_ge(sem["ones_set"], 1)
                pool.affine_select(out=head_mask[:], in_=head_mask[:], compare_op=ALU.is_ge, fill=0.0, base=0,
                                   pattern=[[-wide, heads]], channel_multiplier=1).then_inc(sem["lower_cut"], 1)
                pool.wait_ge(sem["lower_cut"], 1)
                pool.affine_select(out=head_mask[:], in_=head_mask[:], compare_op=ALU.is_ge, fill=0.0, base=wide - 1,
                                   pattern=[[wide, heads]], channel_multiplier=-1).then_inc(sem["mask_made"], 1)
                gather(pool)
                pool.wait_ge(sem["rhs_zeroed"], 1)
                pool.wait_ge(sem["mask_made"], 1)
                for e in range(2):
                    if e:
                        pool.wait_ge(sem["ones_placed"], e)
                    pool.memset(values_rhs[e * C:(e + 1) * C, :, :, 2 * wide + e:2 * wide + e + 1], 1.0)\
                        .then_inc(sem["ones_placed"], 1)
                pool.wait_ge(sem["ones_placed"], 2)

            @block.tensor
            def _(pe):
                pe.wait_ge(sem["weights_loaded"], 48)
                pe.matmul(ps[:, 0, 0:B * C], wk[:], keep.ctx_t[:], start=True, stop=True).then_inc(sem["k_made"], 1)
                pe.wait_ge(sem["ctx_doubled"], 1)
                for b in range(B):
                    mm = pe.matmul(ps[:, 1, b * D:(b + 1) * D], ctx_twice[:, b, :, :].rearrange("p e k -> p (e k)"),
                                   wv[:], start=True, stop=True)
                mm.then_inc(sem["v_made"], 1)

            @block.scalar
            def _(act):
                act.wait_ge(sem["bias_loaded"], 32)
                act.activation(bias_q[:], bias_q[:], ACT.Copy, scale=scale).then_inc(sem["q_scaled"], 1)
                act.wait_ge(sem["v_made"], 1)
                act.wait_ge(sem["rhs_zeroed"], 1)
                for e in range(2):
                    rows = slice(e * C, (e + 1) * C)
                    act.activation(values_rhs[rows, :, :, e * wide:(e + 1) * wide],
                                   ps[rows, 1, :].rearrange("r (b p e d) -> r b p e d", b=B, e=2, d=wide)[:, :, :, e, :],
                                   ACT.Copy).then_inc(sem["v_kept"], 1)

            @block.vector
            def _(dve):
                dve.memset(values_rhs[:], 0.0).then_inc(sem["rhs_zeroed"], 1)
                dve.tensor_copy(ctx_twice[:], keep.ctx_t[:].rearrange("p (b k) -> p b k", b=B)[:, :, None, :]
                                .to_broadcast([P, B, 2, C])).then_inc(sem["ctx_doubled"], 1)
                dve.wait_ge(sem["k_made"], 1)
                dve.wait_ge(sem["bias_loaded"], 32)
                dve.tensor_scalar(k_t[:], ps[:, 0, 0:B * C], bias_k[:, 0:1], None, ALU.add).then_inc(sem["k_kept"], 1)
                dve.wait_ge(sem["k_kept"], 1)
                dve.wait_ge(sem["mask_made"], 1)
                for b in range(B):
                    dve.tensor_tensor(scores_rhs[:, b, :].rearrange("p (h k) -> p h k", h=heads),
                                      k_t[:, None, b * C:(b + 1) * C].to_broadcast([P, heads, C]),
                                      head_mask[:, :, None].to_broadcast([P, heads, C]), ALU.mult)\
                        .then_inc(sem["k_spread"], 1)


class Normed:

    def __init__(self, s, keep, bank_a, bank_b, padded=False, rows=None):
        self.keep, self.banks, self.padded = keep, (bank_a, bank_b), padded
        self.xn, self.xt = s.sb("xn", [P, NT, D]), s.sb("xt", [P, B, S + 2] if padded else [P, NT, P])
        self.rows, self.rows_given = rows or RowStats(keep, s), rows is not None
        self.xn_ready, self.xn_turned, self.xt_ready = s.sem("xn_ready"), s.sem("xn_turned"), s.sem("xt_ready")

    def vector(self, dve):
        rows = self.rows
        if not self.rows_given:
            rows.vector(dve)
        dve.wait_ge(rows.rstd_ready, 1)
        for t in range(NT):
            dve.tensor_scalar(self.xn[:, t, :], self.keep.x[:, t, :], rows.moments[:, t, 0:1], rows.rstd[:, t:t + 1],
                              ALU.subtract, ALU.mult).then_inc(self.xn_ready, 1)

    def gpsimd(self, pool):
        if not self.rows_given:
            self.rows.gpsimd(pool)

    def tensor(self, pe):
        for t in range(NT):
            pe.wait_ge(self.xn_ready, t + 1)
            mm = pe.transpose(self.banks[t // 4][:, (t % 4) * P:(t % 4 + 1) * P], self.xn[:, t, :],
                              self.keep.identity[:])
            if t % 4 == 3:
                mm.then_inc(self.xn_turned, 1)

    def scalar(self, act):
        for n in range(2):
            act.wait_ge(self.xn_turned, n + 1)
            if self.padded:
                act.activation(self.xt[:, 2 * n:2 * n + 2, 1:S + 1], self.banks[n].rearrange("p (b k) -> p b k", b=2),
                               ACT.Copy).then_inc(self.xt_ready, 1)
            else:
                act.activation(self.xt[:, 4 * n:4 * n + 4, :].rearrange("p t k -> p (t k)"), self.banks[n][:],
                               ACT.Copy).then_inc(self.xt_ready, 1)


def lora_ffn(nc, a, keep, name, gate):
    with Scope(nc, name) as s:
        ps = s.psum("ps", [P, 8, 512])
        norm = Normed(s, keep, ps[:, 0], ps[:, 1])
        w1, w1_t = s.sb("w1", [P, 4, D]), s.sb("w1_t", [P, 4, P])
        w2, w2_t = s.sb("w2", [P, 4, P]), s.sb("w2_t", [P, 4, D])
        b1_rows, b1, b2 = s.sb("b1_rows", [4, P]), s.sb("b1", [P, 4]), s.sb("b2", [P, D])
        scale, odd = s.sb("scale", [P, 1]), s.sb("odd", [P, B, 8])
        w1_own, w2_own = s.sb("w1_own", [P, 2, 4, P]), s.sb("w2_own", [P, 2, 4, D])
        hidden, change = s.sb("hidden", [P, 2, 4, S]), s.sb("change", [P, 2, 2, D])
        names = ["loaded", "w_turned", "w_kept", "b1_turned", "b1_kept", "odd_scaled", "even_made", "own_made",
                 "hidden_made", "gelu_done", "out_made", "change_made", "x_done"]
        sem = {n: s.sem(n) for n in names}
        with s.block() as block:

            @block.sync
            def _(sp):
                sp.dma_start(w1[:], a["L0_ffn_W1"].rearrange("(j h) d -> h j d", h=P)).then_inc(sem["loaded"], 16)
                sp.dma_start(w2[:], a["L0_ffn_W2"].rearrange("o (g c) -> o g c", c=P)).then_inc(sem["loaded"], 16)
                sp.dma_start(b1_rows[:], a["L0_ffn_b1"].rearrange("(j h) -> j h", h=P)).then_inc(sem["loaded"], 16)
                sp.dma_start(b2[:], row(a["L0_ffn_b2"]).to_broadcast([P, D])).then_inc(sem["loaded"], 16)
                sp.dma_start(scale[:], row(a["L0_ffn_scale"]).to_broadcast([P, 1])).then_inc(sem["loaded"], 16)

            @block.gpsimd
            def _(pool):
                norm.gpsimd(pool)

            @block.tensor
            def _(pe):
                pe.wait_ge(sem["loaded"], 80)
                for j in range(4):
                    pe.transpose(ps[:, 2, j * P:(j + 1) * P], w1[:, j, :], keep.identity[:])
                    mm = pe.transpose(ps[:, 3, j * P:(j + 1) * P], w2[:, j, :], keep.identity[:])
                mm.then_inc(sem["w_turned"], 1)
                pe.transpose(ps[:, 4, 0:4], b1_rows[:], keep.identity[0:4, 0:4]).then_inc(sem["b1_turned"], 1)
                norm.tensor(pe)

                def even(b):
                    if b == 0:
                        pe.wait_ge(sem["w_kept"], 2)
                    else:
                        pe.wait_ge(sem["own_made"], 8 * b)
                    for j in range(8):
                        mm = pe.matmul(ps[:, 2 + j // 4, (j % 4) * D:(j % 4 + 1) * D],
                                       keep.identity[:, 1 + 2 * j:2 + 2 * j].to_broadcast([P, P]),
                                       norm.xn[:, 2 * b, :], start=True, stop=True)
                    mm.then_inc(sem["even_made"], 1)

                def up(b):
                    pe.wait_ge(sem["own_made"], 8 * (b + 1))
                    pe.wait_ge(norm.xt_ready, 2)
                    if b >= 1:
                        pe.wait_ge(sem["gelu_done"], 4 * b)
                    for j in range(4):
                        mm = pe.matmul(ps[:, 4 + j // 2, (j % 2) * S:(j % 2 + 1) * S], w1_own[:, b % 2, j, :],
                                       norm.xt[:, 2 * b:2 * b + 2, :].rearrange("p t k -> p (t k)"),
                                       start=True, stop=True)
                    mm.then_inc(sem["hidden_made"], 1)

                def down(b):
                    pe.wait_ge(sem["gelu_done"], 4 * (b + 1))
                    if b >= 2:
                        pe.wait_ge(sem["change_made"], b - 1)
                    for u in range(2):
                        for g in range(4):
                            mm = pe.matmul(ps[:, 6 + b % 2, u * D:(u + 1) * D],
                                           hidden[:, b % 2, g, u * P:(u + 1) * P], w2_own[:, b % 2, g, :],
                                           start=(g == 0), stop=(g == 3))
                    mm.then_inc(sem["out_made"], 1)

                pe.wait_ge(sem["b1_kept"], 1)
                even(0)
                for b in range(B):
                    up(b)
                    if b + 1 < B:
                        even(b + 1)
                    down(b)

            @block.scalar
            def _(act):
                act.wait_ge(sem["b1_turned"], 1)
                act.activation(b1[:], ps[:, 4, 0:4], ACT.Copy).then_inc(sem["b1_kept"], 1)
                norm.scalar(act)
                act.wait_ge(sem["b1_kept"], 1)
                for b in range(B):
                    act.wait_ge(sem["hidden_made"], b + 1)
                    if b >= 2:
                        act.wait_ge(sem["out_made"], b - 1)
                    for j in range(4):
                        act.activation(hidden[:, b % 2, j, :], ps[:, 4 + j // 2, (j % 2) * S:(j % 2 + 1) * S],
                                       ACT.Gelu, bias=b1[:, j:j + 1]).then_inc(sem["gelu_done"], 1)

            @block.vector
            def _(dve):
                dve.wait_ge(sem["w_turned"], 1)
                dve.tensor_copy(w1_t[:].rearrange("p j h -> p (j h)"), ps[:, 2]).then_inc(sem["w_kept"], 1)
                dve.tensor_copy(w2_t[:].rearrange("p j h -> p (j h)"), ps[:, 3]).then_inc(sem["w_kept"], 1)
                norm.vector(dve)
                dve.wait_ge(norm.xt_ready, 2)
                for b in range(B):
                    dve.tensor_scalar(odd[:, b, :], norm.xt[:, 2 * b, 2:18:2], scale[:, 0:1], None, ALU.mult)\
                        .then_inc(sem["odd_scaled"], 1)

                def own(b):
                    dve.wait_ge(sem["odd_scaled"], B)
                    dve.wait_ge(sem["w_kept"], 2)
                    dve.wait_ge(sem["even_made"], b + 1)
                    if b >= 2:
                        dve.wait_ge(sem["out_made"], b - 1)
                    for j in range(4):
                        dve.scalar_tensor_tensor(out=w1_own[:, b % 2, j, :], in0=ps[:, 2, j * D:(j + 1) * D],
                                                 scalar=odd[:, b, j:j + 1], in1=w1_t[:, j, :], op0=ALU.mult,
                                                 op1=ALU.add).then_inc(sem["own_made"], 1)
                    for m in range(4):
                        cols = slice(32 * m, 32 * m + 32)
                        dve.scalar_tensor_tensor(
                            out=w2_own[:, b % 2, :, cols],
                            in0=ps[:, 3, m * D:(m + 1) * D].rearrange("c (o g) -> c g o", g=4),
                            scalar=odd[:, b, 4 + m:5 + m], in1=w2_t[:, :, cols], op0=ALU.mult,
                            op1=ALU.add).then_inc(sem["own_made"], 1)

                def update(b):
                    dve.wait_ge(sem["out_made"], b + 1)
                    dve.tensor_tensor(change[:, b % 2], ps[:, 6 + b % 2, 0:2 * D].rearrange("p (u d) -> p u d", u=2),
                                      b2[:, None, :].to_broadcast([P, 2, D]), ALU.add).then_inc(sem["change_made"], 1)
                    dve.wait_ge(sem["change_made"], b + 1)
                    dve.scalar_tensor_tensor(out=keep.x[:, 2 * b:2 * b + 2, :], in0=change[:, b % 2], scalar=gate,
                                             in1=keep.x[:, 2 * b:2 * b + 2, :], op0=ALU.mult, op1=ALU.add)\
                        .then_inc(sem["x_done"], 1)

                own(0)
                for b in range(B):
                    if b + 1 < B:
                        own(b + 1)
                    update(b)


class GeluWeights:

    def __init__(self, s):
        self.w1, self.w2 = s.sb("w1", [P, EXPERTS, 512]), s.sb("w2", [P, EXPERTS, 4, 512])
        self.w3, self.b3 = s.sb("w3", [P, EXPERTS, 4, D]), s.sb("b3", [P, EXPERTS, D])
        self.b_rows, self.b = s.sb("b_rows", [2 * EXPERTS * 4, P]), s.sb("b", [P, 2 * EXPERTS * 4])
        self.loaded = s.sem("loaded")


def load_gelu_weights(a, w, sp):
    for n, v in enumerate(("L1_ffn_b1", "L1_ffn_b2")):
        sp.dma_start(w.b_rows[32 * n:32 * n + 32, :], a[v].rearrange("e (c d) -> (e c) d", d=P)).then_inc(w.loaded, 16)
    sp.dma_start(w.b3[:], a["L1_ffn_b3"].rearrange("(o e) d -> o e d", o=1).to_broadcast([P, EXPERTS, D]))\
        .then_inc(w.loaded, 16)
    sp.dma_start(w.w1[:], a["L1_ffn_W1"].rearrange("e d h -> d e h")).then_inc(w.loaded, 16)
    sp.dma_start(w.w3[:], a["L1_ffn_W3"].rearrange("e (c d) h -> d e c h", d=P)).then_inc(w.loaded, 16)
    sp.dma_start(w.w2[:], a["L1_ffn_W2"].rearrange("e (c d) h -> d e c h", d=P)).then_inc(w.loaded, 16)


def turn_expert_biases(nc, keep, name, w):
    with Scope(nc, name) as s:
        ps = s.psum("ps", [P, 512])
        turned, kept = s.sem("turned"), s.sem("kept")
        with s.block() as block:

            @block.tensor
            def _(pe):
                pe.wait_ge(w.loaded, 96)
                pe.transpose(ps[:, 0:64], w.b_rows[:], keep.identity[0:64, 0:64]).then_inc(turned, 1)

            @block.vector
            def _(dve):
                dve.wait_ge(turned, 1)
                dve.tensor_copy(w.b[:], ps[:, 0:64]).then_inc(kept, 1)


def program(nc, a, out):
    with Scope(nc, "keep") as s:
        keep = Keep(nc, s)

        def gate(kind, layer):
            return keep.gates[:, B * kind + layer:B * kind + layer + 1]

        with Scope(nc, "experts1") as own:
            w = GeluWeights(own)
            with Scope(nc, "heads1") as early:
                heads1 = HeadWeights(early, [a[f"L1_xattn_{n}"] for n in ("WQ", "WK", "WV", "WO")],
                                     [a[f"L1_xattn_{n}"] for n in ("bQ", "bK", "bV")], a["L1_xattn_bO"])

                def load_layer1(sp):
                    heads1.load(sp)
                    load_gelu_weights(a, w, sp)

                with Scope(nc, "attention0") as q:
                    heads0 = HeadWeights(q, [a[f"L0_xattn_{n}_kernel"] for n in ("query", "key", "value", "projection")],
                                         None, a["L0_xattn_projection_bias"])
                    with Together(nc):
                        check_mask(nc, a, keep, "mask")
                        setup(nc, a, keep, heads0)
                    scores_rhs, values_rhs = q.sb("scores_rhs", [P, B, 16 * C]), q.sb("values_rhs", [P, B, 8, D])
                    rows = RowStats(keep, q)
                    with Together(nc) as block:
                        block.vector(rows.vector)
                        head_operands(nc, keep, "operands0", heads0, 0.125, scores_rhs, values_rhs, None, load_layer1)
                        block.gpsimd(rows.gpsimd)
                    cross_attention(nc, a, keep, "core0", scores_rhs, values_rhs, None, heads0.out_bias_rows, gate(0, 0),
                                    rows)
                lora_ffn(nc, a, keep, "ffn0", gate(1, 0))
                with Scope(nc, "attention1") as q:
                    scores_rhs, values_rhs = q.sb("scores_rhs", [P, B, 16 * C]), q.sb("values_rhs", [P, B, 8, D])
                    score_bias = q.sb("score_bias", [P, B, 16 * C])
                    rows = RowStats(keep, q)
                    with Together(nc) as block:
                        block.vector(rows.vector)
                        head_operands(nc, keep, "operands1", heads1, 0.125, scores_rhs, values_rhs, score_bias)
                        block.gpsimd(rows.gpsimd)
                    cross_attention(nc, a, keep, "core1", scores_rhs, values_rhs, score_bias, heads1.out_bias_rows,
                                    gate(0, 1), rows)
            turn_expert_biases(nc, keep, "biases1", w)
            route(nc, keep, "route1", keep.routes[0], a["L1_ffn_expert_tokens"], gate(1, 1), False)
            gelu_experts(nc, keep, "experts1", keep.routes[0], w.w1, w.w2, w.w3, w.b[:, 0:32], w.b[:, 32:64], w.b3)
        with Scope(nc, "experts23") as own:
            w_in3, w_out3 = own.sb("w_in3", [P, EXPERTS, 512]), own.sb("w_out3", [P, EXPERTS, 2, D])
            taps = own.sb("taps", [P, B, 16, TAPS])
            loaded3, rows3 = own.sem("loaded3"), RowStats(keep, own)
            with Scope(nc, "kernels") as conv:
                conv_weights = ConvWeights(conv)
                with Scope(nc, "experts2") as experts2:
                    w_in2, w_out2 = experts2.sb("w_in2", [P, EXPERTS, 1024]), experts2.sb("w_out2", [P, EXPERTS, 4, D])
                    with Scope(nc, "raw2") as raw:
                        gate_up, down = raw.sb("gate_up", [P, EXPERTS, 8, D]), raw.sb("down", [P, EXPERTS, 512])
                        keep.raw_loaded = [raw.sem("gate_up_loaded"), raw.sem("down_loaded")]

                        def load_layers23(sp):
                            sp.dma_start(gate_up[:], a["L2_ffn_gate_up_proj"].rearrange("e (c i) h -> i e c h", i=P))\
                                .then_inc(keep.raw_loaded[0], 16)
                            sp.dma_start(down[:], a["L2_ffn_down_proj"].rearrange("e h i -> h e i"))\
                                .then_inc(keep.raw_loaded[1], 16)
                            conv_weights.load(a, sp)
                            for n, v in enumerate(("gate", "up")):
                                sp.dma_start(w_in3[:, :, 256 * n:256 * (n + 1)], a[f"L3_ffn_{v}_w"].rearrange("e d i -> d e i"))\
                                    .then_inc(loaded3, 16)
                            sp.dma_start(w_out3[:], a["L3_ffn_down_w"].rearrange("e (c i) d -> i e c d", i=P))\
                                .then_inc(loaded3, 16)

                        with Scope(nc, "attention2") as q:
                            scores_rhs, values_rhs = q.sb("scores_rhs", [P, B, 16 * C]), q.sb("values_rhs", [P, B, 8, 18])
                            score_bias, wq = q.sb("score_bias", [P, B, C]), q.sb("wq", [P, D])
                            bias_q, out_bias = q.sb("bias_q", [P, 1]), q.sb("out_bias", [P, D])
                            rows = RowStats(keep, q)
                            with Together(nc) as block, Scope(nc, "combine1") as c:
                                combine = Combine(keep, c, keep.routes[0])
                                latent_operands(nc, a, keep, "operands2", scores_rhs, values_rhs, score_bias, wq, bias_q,
                                                8 ** -0.5, out_bias, combine.gather)
                                combine.add(block, rows)
                            cross_attention(nc, a, keep, "core2", scores_rhs, values_rhs, score_bias, out_bias,
                                            gate(0, 2), rows, (wq[:], bias_q[:]), 8 ** -0.5, load_layers23)
                        with Together(nc):
                            turn_gated_weights(nc, a, keep, "weights2", gate_up, down, w_in2, w_out2)
                            route(nc, keep, "route2", keep.routes[1], a["L2_ffn_gate_w"], gate(1, 2), True)
                    gated_experts(nc, keep, "gated2", keep.routes[1], w_in2, w_out2)
                with Together(nc), Scope(nc, "combine2") as c:
                    conv_kernels(nc, keep, "kernels3", conv_weights, taps, Combine(keep, c, keep.routes[1]), rows3)
            conv_attention_any_mask(nc, a, keep, "masked3", taps, gate(0, 3), rows3)
            conv_attention_causal(nc, a, keep, "causal3", taps, gate(0, 3), rows3)
            with nc.Block() as block:

                @block.tensor
                def _(pe):
                    pe.wait_ge(loaded3, 48)

            route(nc, keep, "route3", keep.routes[2], a["L3_ffn_router_w"], gate(1, 3), True)
            gated_experts(nc, keep, "gated3", keep.routes[2], w_in3, w_out3)
        with Together(nc) as block, Scope(nc, "combine3") as c:
            combine = Combine(keep, c, keep.routes[2], out)
            block.gpsimd(combine.gather)
            combine.add(block)


def kernel(**inputs):
    import concourse.bacc as bacc
    from concourse.bass_utils import run_bass_kernel_spmd

    nc = bacc.Bacc("TRN2", target_bir_lowering=False, num_devices=1)
    arrays, a = {}, {}
    for name, value in inputs.items():
        value = np.ascontiguousarray(value)
        if not value.shape:
            value = value.reshape(1)
        arrays["in_" + name] = value
        a[name] = nc.dram_tensor("in_" + name, value.shape, mybir.dt.from_np(value.dtype), kind="ExternalInput").ap()
    out = nc.dram_tensor("out", (B, S, D), F32, kind="ExternalOutput").ap()
    program(nc, a, out)
    return run_bass_kernel_spmd(nc, [arrays], core_ids=[0]).results[0]["out"]
```
